# Optimizing a Trainium2 kernel written in Bass

```python
import numpy as np
import jax
import jax.numpy as jnp

def _softmax(x, axis=-1):
    return jax.nn.softmax(x, axis=axis)

def _gelu(x):
    return jax.nn.gelu(x, approximate=True)

def _silu(x):
    return jax.nn.silu(x)

def _sigmoid(x):
    return jax.nn.sigmoid(x)

def _layernorm(x, axis=-1, eps=1e-05):
    m = jnp.mean(x, axis=axis, keepdims=True)
    v = jnp.var(x, axis=axis, keepdims=True)
    return (x - m) / jnp.sqrt(v + eps)

def _scatter_add(tgt, idx, src, axis=0):
    return tgt.at[idx].add(src)

def _segment_sum(src, seg, n):
    return jax.ops.segment_sum(src, seg, n)
kernel_name = 'mk_decoder_preln_d4_seqx_r8_5da453'

def setup_inputs(seed: int=0):
    np.random.seed(seed)
    _w = jnp.asarray

    def _rec_inputs():
        import jax
        import jax.numpy as jnp
        _rk = jax.random.key(seed)
        x = 7.22e-05 + 1 * jax.random.normal(jax.random.fold_in(_rk, 1), (32, 128, 128), jnp.float32)
        _lenS = 128 - jax.random.randint(jax.random.fold_in(_rk, 7), (32,), 0, max(1, 128 // 4) + 1, jnp.int32)
        _lenS2 = 128 - jax.random.randint(jax.random.fold_in(_rk, 8), (32,), 0, max(1, 128 // 4) + 1, jnp.int32)
        _ctx_1024P = jax.random.normal(jax.random.fold_in(_rk, 11), (32, 16, 128), jnp.float32)
        _ctx_1024c = jax.random.dirichlet(jax.random.fold_in(_rk, 511), 0.3 * jnp.ones((16,), jnp.float32), (32, 128))
        _ctx_1024t = jnp.einsum('bsk,bkd->bsd', _ctx_1024c, _ctx_1024P)
        _ctx_1024t = _ctx_1024t * jax.lax.rsqrt(jnp.mean(jnp.square(_ctx_1024t)) + 1e-12) * 0.953939
        ctx_1024 = 4.13588e-05 + 0.999923 * (_ctx_1024t + 0.3 * jax.random.normal(jax.random.fold_in(_rk, 611), (32, 128, 128), jnp.float32))
        _validS = jnp.arange(128)[None, :] < _lenS[:, None]
        _validS2 = jnp.arange(128)[None, :] < _lenS2[:, None]
        _causal = jnp.tril(jnp.ones((128, 128), dtype=bool))
        mask_BxS2_ik0 = jnp.where(jnp.broadcast_to(_validS2[:, :], (32, 128)), 0, 1).astype(jnp.int32)
        mask_BxSxS2_fk0 = jnp.where(jnp.broadcast_to(_validS2[:, None, :], (32, 128, 128)), 1.1111111640930176, 0.0).astype(jnp.float32)
        return (x, ctx_1024, mask_BxS2_ik0, mask_BxSxS2_fk0)
    x, ctx_1024, mask_BxS2_ik0, mask_BxSxS2_fk0 = _rec_inputs()

    def _L0_attn_setup():
        import jax, jax.numpy as jnp
        import numpy as np
        DT_MIN, DT_MAX = (0.001, 0.1)
        CHUNK = 64
        key = jax.random.key(seed)
        ks = jax.random.split(key, 8)
        b, L, D = (2, 512, 128)
        d_inner, d_state, nheads, K = (256, 128, 32, 4)
        conv_dim = d_inner + 2 * d_state
        d_in_proj = 2 * d_inner + 2 * d_state + nheads
        f32 = jnp.float32
        return {'x': jax.random.normal(ks[0], (b, L, D), f32), 'in_proj_w': jax.random.normal(ks[1], (d_in_proj, D), f32) * D ** (-0.5), 'conv_w': jax.random.normal(ks[2], (conv_dim, K), f32) * 0.3, 'conv_b': jnp.zeros((conv_dim,), f32), 'dt_bias': jax.random.normal(ks[3], (nheads,), f32) * 0.5, 'A_log': jnp.log(jax.random.uniform(ks[4], (nheads,), f32, 1.0, 16.0)), 'D_skip': jnp.ones((nheads,), f32), 'norm_w': jnp.ones((d_inner,), f32), 'out_proj_w': jax.random.normal(ks[5], (D, d_inner), f32) * d_inner ** (-0.5), 'ln_w': jnp.ones((D,), f32), 'ln_b': jnp.zeros((D,), f32)}
    _L0_attn_all = _L0_attn_setup()
    _L0_attn_in = {k: v for k, v in _L0_attn_all.items() if k in ('in_proj_w', 'conv_w', 'conv_b', 'dt_bias', 'A_log', 'D_skip', 'norm_w', 'out_proj_w', 'ln_w', 'ln_b')}
    del _L0_attn_all

    def _L0_xattn_setup():
        import jax, jax.numpy as jnp
        import numpy as np
        HEADS = 8
        DIM_HEAD = 64
        key = jax.random.key(seed)
        ks = jax.random.split(key, 9)
        B, N1, N2, D = (4, 256, 256, 128)
        inner = HEADS * DIM_HEAD
        s_in = 1.0 / np.sqrt(D)
        s_inner = 1.0 / np.sqrt(inner)
        return {'x1': jax.random.normal(ks[0], (B, N1, D), jnp.float32), 'x2': jax.random.normal(ks[1], (B, N2, D), jnp.float32), 'Wq1': jax.random.normal(ks[2], (D, inner), jnp.float32) * s_in, 'Wk1': jax.random.normal(ks[3], (D, inner), jnp.float32) * s_in, 'Wv1': jax.random.normal(ks[4], (D, inner), jnp.float32) * s_in, 'Wk2': jax.random.normal(ks[5], (D, inner), jnp.float32) * s_in, 'Wv2': jax.random.normal(ks[6], (D, inner), jnp.float32) * s_in, 'Wo': jax.random.normal(ks[7], (inner, D), jnp.float32) * s_inner, 'bo': jnp.zeros((D,), jnp.float32)}
    _L0_xattn_all = _L0_xattn_setup()
    _L0_xattn_in = {k: v for k, v in _L0_xattn_all.items() if k in ('Wq1', 'Wk1', 'Wv1', 'Wk2', 'Wv2', 'Wo', 'bo')}
    del _L0_xattn_all

    def _L0_ffn_setup():
        import jax, jax.numpy as jnp
        import numpy as np
        E = 16
        K = 4
        NG = 4
        TG = 2
        SCALE = 2.5
        NORM_TOPK = True
        H = 128
        I = 64
        SH_I = I * 2
        B, S = (2, 256)
        key = jax.random.key(seed)
        ks = jax.random.split(key, 9)

        def w(k, shape, fan_in):
            return jax.random.normal(k, shape, jnp.float32) * (1.0 / np.sqrt(fan_in))
        return {'hidden_states': jax.random.normal(ks[0], (B, S, H), jnp.float32), 'gate_w': w(ks[1], (E, H), H), 'gate_bias': jnp.zeros((E,), jnp.float32), 'Wg': w(ks[2], (E, I, H), H), 'Wu': w(ks[3], (E, I, H), H), 'Wd': w(ks[4], (E, H, I), I), 'Ws_g': w(ks[5], (SH_I, H), H), 'Ws_u': w(ks[6], (SH_I, H), H), 'Ws_d': w(ks[7], (H, SH_I), SH_I)}
    _L0_ffn_all = _L0_ffn_setup()
    _L0_ffn_in = {k: v for k, v in _L0_ffn_all.items() if k in ('gate_w', 'gate_bias', 'Wg', 'Wu', 'Wd', 'Ws_g', 'Ws_u', 'Ws_d')}
    del _L0_ffn_all

    def _L1_attn_setup():
        import jax, jax.numpy as jnp
        import numpy as np
        N_EMBD = 128
        N_HEAD = 16
        HEAD_DIM = N_EMBD // N_HEAD
        LATENT_DIM = N_EMBD // 2
        B, T = (4, 256)
        key = jax.random.key(seed)
        ks = jax.random.split(key, 5)

        def init(k, fan_in, fan_out):
            bound = 1.0 / np.sqrt(fan_in)
            return jax.random.uniform(k, (fan_in, fan_out), jnp.float32, -bound, bound)
        return {'x': jax.random.normal(ks[0], (B, T, N_EMBD), jnp.float32), 'Wc_down': init(ks[1], N_EMBD, LATENT_DIM), 'Wq_up': init(ks[2], LATENT_DIM, N_EMBD), 'Wkv_up': init(ks[3], LATENT_DIM, 2 * HEAD_DIM), 'Wc_proj': init(ks[4], N_EMBD, N_EMBD)}
    _L1_attn_all = _L1_attn_setup()
    _L1_attn_in = {k: v for k, v in _L1_attn_all.items() if k in ('Wc_down', 'Wq_up', 'Wkv_up', 'Wc_proj')}
    del _L1_attn_all

    def _L1_xattn_setup():
        import jax, jax.numpy as jnp
        import numpy as np
        EMBED = 128
        HEADS = 16
        HEAD_DIM = EMBED // HEADS
        B, S = (4, 256)
        key = jax.random.key(seed)
        ks = jax.random.split(key, 12)
        sc = 1.0 / np.sqrt(EMBED)
        inp = {'query': jax.random.normal(ks[0], (B, S, EMBED), jnp.float32), 'keys': jax.random.normal(ks[1], (B, S, EMBED), jnp.float32), 'values': jax.random.normal(ks[2], (B, S, EMBED), jnp.float32), 'mask': jax.random.randint(ks[3], (B, S), 0, 2, jnp.int32), 'Wq': jax.random.normal(ks[4], (EMBED, EMBED), jnp.float32) * sc, 'bq': jnp.zeros((EMBED,), jnp.float32), 'Wk': jax.random.normal(ks[5], (EMBED, EMBED), jnp.float32) * sc, 'bk': jnp.zeros((EMBED,), jnp.float32), 'Wv': jax.random.normal(ks[6], (EMBED, EMBED), jnp.float32) * sc, 'bv': jnp.zeros((EMBED,), jnp.float32), 'Wo': jax.random.normal(ks[7], (EMBED, EMBED), jnp.float32) * sc, 'bo': jnp.zeros((EMBED,), jnp.float32)}
        return inp
    _L1_xattn_all = _L1_xattn_setup()
    _L1_xattn_in = {k: v for k, v in _L1_xattn_all.items() if k in ('Wq', 'bq', 'Wk', 'bk', 'Wv', 'bv', 'Wo', 'bo')}
    del _L1_xattn_all

    def _L1_ffn_setup():
        import jax, jax.numpy as jnp
        import numpy as np
        B, F, D, H, E, K = (4, 256, 128, 256, 8, 2)
        key = jax.random.key(seed)
        ks = jax.random.split(key, 9)
        sc = lambda k, shape, fan_in: jax.random.normal(k, shape, jnp.float32) * fan_in ** (-0.5)
        return {'x': jax.random.normal(ks[0], (B, F, D), jnp.float32), 'rw1': sc(ks[1], (D, D), D), 'rb1': jnp.zeros((D,), jnp.float32), 'rw2': sc(ks[2], (D, E), D), 'rb2': jnp.zeros((E,), jnp.float32), 'ew1': sc(ks[3], (E, D, H), D), 'eb1': jnp.zeros((E, H), jnp.float32), 'ew2': sc(ks[4], (E, H, D), H), 'eb2': jnp.zeros((E, D), jnp.float32)}
    _L1_ffn_all = _L1_ffn_setup()
    _L1_ffn_in = {k: v for k, v in _L1_ffn_all.items() if k in ('rw1', 'rb1', 'rw2', 'rb2', 'ew1', 'eb1', 'ew2', 'eb2')}
    del _L1_ffn_all

    def _L2_attn_setup():
        import jax, jax.numpy as jnp
        import numpy as np
        DIM = 128
        B, S = (4, 512)
        key = jax.random.key(seed)
        ks = jax.random.split(key, 7)
        s = 1.0 / np.sqrt(DIM)
        return {'x': jax.random.normal(ks[0], (B, S, DIM), dtype=jnp.float32), 'wq': jax.random.uniform(ks[1], (DIM, DIM), minval=-s, maxval=s, dtype=jnp.float32), 'bq': jax.random.uniform(ks[2], (DIM,), minval=-s, maxval=s, dtype=jnp.float32), 'wk': jax.random.uniform(ks[3], (DIM, DIM), minval=-s, maxval=s, dtype=jnp.float32), 'bk': jax.random.uniform(ks[4], (DIM,), minval=-s, maxval=s, dtype=jnp.float32), 'wv': jax.random.uniform(ks[5], (DIM, DIM), minval=-s, maxval=s, dtype=jnp.float32), 'bv': jax.random.uniform(ks[6], (DIM,), minval=-s, maxval=s, dtype=jnp.float32)}
    _L2_attn_all = _L2_attn_setup()
    _L2_attn_in = {k: v for k, v in _L2_attn_all.items() if k in ('wq', 'bq', 'wk', 'bk', 'wv', 'bv')}
    del _L2_attn_all

    def _L2_xattn_setup():
        import jax, jax.numpy as jnp
        import numpy as np
        import math
        B, S, E = (2, 256, 128)
        H = 16
        DK = E // H
        MAX_DIST = 256

        def _split_heads(x):
            b, s, _ = x.shape
            return x.reshape(b, s, H, DK).transpose(0, 2, 1, 3)
        key = jax.random.key(seed)
        ks = jax.random.split(key, 9)
        sc = 1.0 / math.sqrt(E)
        return {'key': jax.random.normal(ks[0], (B, S, E), jnp.float32), 'query': jax.random.normal(ks[1], (B, S, E), jnp.float32), 'value': jax.random.normal(ks[2], (B, S, E), jnp.float32), 'wq': jax.random.normal(ks[3], (E, E), jnp.float32) * sc, 'wk': jax.random.normal(ks[4], (E, E), jnp.float32) * sc, 'wv': jax.random.normal(ks[5], (E, E), jnp.float32) * sc, 'fc_w': jax.random.normal(ks[6], (E, E), jnp.float32) * sc, 'fc_b': jax.random.normal(ks[7], (E,), jnp.float32) * sc, 'rel_table': jax.random.normal(ks[8], (2 * MAX_DIST - 1, H), jnp.float32) * 0.02}
    _L2_xattn_all = _L2_xattn_setup()
    _L2_xattn_in = {k: v for k, v in _L2_xattn_all.items() if k in ('wq', 'wk', 'wv', 'fc_w', 'fc_b', 'rel_table')}
    del _L2_xattn_all

    def _L2_ffn_setup():
        import jax, jax.numpy as jnp
        import numpy as np
        DIM = 128
        HID = 512
        NUM_EXPERTS = 8
        TOP_K = 2
        ALPHA = 2.0
        B, S = (4, 256)

        def _swiglu(x, wu, wg, wd):
            up = x @ wu
            g = x @ wg
            gate = jax.nn.sigmoid(g) * g
            return up * gate @ wd
        key = jax.random.key(seed)
        ks = jax.random.split(key, 8)
        x = jax.random.normal(ks[0], (B, S, DIM), dtype=jnp.float32)
        Wr = jax.random.normal(ks[1], (DIM, NUM_EXPERTS), dtype=jnp.float32) * 0.02
        Wu = jax.random.normal(ks[2], (NUM_EXPERTS - 1, DIM, HID), dtype=jnp.float32) * 0.02
        Wg = jax.random.normal(ks[3], (NUM_EXPERTS - 1, DIM, HID), dtype=jnp.float32) * 0.02
        Wd = jax.random.normal(ks[4], (NUM_EXPERTS - 1, HID, DIM), dtype=jnp.float32) * 0.002
        Wu_s = jax.random.normal(ks[5], (DIM, HID), dtype=jnp.float32) * 0.02
        Wg_s = jax.random.normal(ks[6], (DIM, HID), dtype=jnp.float32) * 0.02
        Wd_s = jax.random.normal(ks[7], (HID, DIM), dtype=jnp.float32) * 0.002
        return {'x': x, 'Wr': Wr, 'Wu': Wu, 'Wg': Wg, 'Wd': Wd, 'Wu_s': Wu_s, 'Wg_s': Wg_s, 'Wd_s': Wd_s}
    _L2_ffn_all = _L2_ffn_setup()
    _L2_ffn_in = {k: v for k, v in _L2_ffn_all.items() if k in ('Wr', 'Wu', 'Wg', 'Wd', 'Wu_s', 'Wg_s', 'Wd_s')}
    del _L2_ffn_all

    def _L3_attn_setup():
        import jax, jax.numpy as jnp
        import numpy as np
        D_MODEL = 128
        N_HEADS = 16
        NUM_PATTERN = 32
        HEAD_DIM = D_MODEL // N_HEADS

        def sparsemax(z):
            S = z.shape[-1]
            z_sorted = -jnp.sort(-z, axis=-1)
            cum = jnp.cumsum(z_sorted, axis=-1)
            k = jnp.arange(1, S + 1, dtype=z.dtype)
            support = 1.0 + k * z_sorted > cum
            k_sup = jnp.sum(support, axis=-1, keepdims=True)
            cum_sel = jnp.take_along_axis(cum, k_sup - 1, axis=-1)
            tau = (cum_sel - 1.0) / k_sup.astype(z.dtype)
            return jnp.maximum(z - tau, 0.0)
        key = jax.random.key(seed)
        ks = jax.random.split(key, 10)
        s = 1.0 / np.sqrt(D_MODEL)
        inp = {'query': jax.random.normal(ks[0], (8, 512, D_MODEL), dtype=jnp.float32), 'key_param': jax.random.normal(ks[1], (1, NUM_PATTERN, D_MODEL), dtype=jnp.float32), 'Wq': jax.random.normal(ks[2], (D_MODEL, N_HEADS * HEAD_DIM), dtype=jnp.float32) * s, 'bq': jnp.zeros((N_HEADS * HEAD_DIM,), dtype=jnp.float32), 'Wk': jax.random.normal(ks[3], (D_MODEL, N_HEADS * HEAD_DIM), dtype=jnp.float32) * s, 'bk': jnp.zeros((N_HEADS * HEAD_DIM,), dtype=jnp.float32), 'Wv': jax.random.normal(ks[4], (N_HEADS * HEAD_DIM, N_HEADS * HEAD_DIM), dtype=jnp.float32) * s, 'bv': jnp.zeros((N_HEADS * HEAD_DIM,), dtype=jnp.float32), 'Wo': jax.random.normal(ks[5], (N_HEADS * HEAD_DIM, D_MODEL), dtype=jnp.float32) * s, 'bo': jnp.zeros((D_MODEL,), dtype=jnp.float32)}
        return inp
    _L3_attn_all = _L3_attn_setup()
    _L3_attn_in = {k: v for k, v in _L3_attn_all.items() if k in ('key_param', 'Wq', 'bq', 'Wk', 'bk', 'Wv', 'bv', 'Wo', 'bo')}
    del _L3_attn_all

    def _L3_xattn_setup():
        import jax, jax.numpy as jnp
        import numpy as np
        B, S, E = (8, 256, 128)
        DROPOUT_P = 0.1
        key = jax.random.key(seed)
        kq, kk, kv, km, kw, kb = jax.random.split(key, 6)
        query = jax.random.normal(kq, (B, S, E), dtype=jnp.float32)
        key_t = jax.random.normal(kk, (B, S, E), dtype=jnp.float32)
        value = jax.random.normal(kv, (B, S, E), dtype=jnp.float32)
        keep = jax.random.bernoulli(km, 1.0 - DROPOUT_P, (B, S, S))
        dropout_mask = keep.astype(jnp.float32) / (1.0 - DROPOUT_P)
        Wout = jax.random.normal(kw, (E, E), dtype=jnp.float32) * E ** (-0.5)
        bout = jax.random.normal(kb, (E,), dtype=jnp.float32) * 0.01
        return {'query': query, 'key': key_t, 'value': value, 'dropout_mask': dropout_mask, 'Wout': Wout, 'bout': bout, 'inv_scale_factor': 32}
    _L3_xattn_all = _L3_xattn_setup()
    _L3_xattn_in = {k: v for k, v in _L3_xattn_all.items() if k in ('Wout', 'bout')}
    del _L3_xattn_all

    def _L3_ffn_setup():
        import jax, jax.numpy as jnp
        import numpy as np
        B, S, IN, OUT = (4, 1024, 128, 128)
        EPS = 1e-06

        def _xla_quantized_matmul(x2d, weight_q, weight_scale):
            amax = jnp.max(jnp.abs(x2d), axis=-1, keepdims=True)
            x_scale = jnp.maximum(amax, EPS) / 127.0
            x_q = jnp.clip(jnp.round(x2d / x_scale), -128, 127).astype(jnp.int8)
            acc = jax.lax.dot_general(x_q, weight_q, (((1,), (1,)), ((), ())), preferred_element_type=jnp.int32)
            return acc.astype(jnp.float32) * x_scale * weight_scale[None, :]
        key = jax.random.key(seed)
        k1, k2, k3, k4 = jax.random.split(key, 4)
        x = jax.random.normal(k1, (B, S, IN), dtype=jnp.float32)
        weight_q = jax.random.randint(k2, (OUT, IN), -128, 128, dtype=jnp.int32).astype(jnp.int8)
        weight_scale = jax.random.uniform(k3, (OUT,), dtype=jnp.float32, minval=0.001, maxval=0.01)
        bias = jax.random.normal(k4, (OUT,), dtype=jnp.float32) * 0.01
        return {'x': x, 'weight_q': weight_q, 'weight_scale': weight_scale, 'bias': bias}
    _L3_ffn_all = _L3_ffn_setup()
    _L3_ffn_in = {k: v for k, v in _L3_ffn_all.items() if k in ('weight_q', 'weight_scale', 'bias')}
    del _L3_ffn_all
    return {'x': x, 'ctx_1024': ctx_1024, 'mask_BxS2_ik0': mask_BxS2_ik0, 'mask_BxSxS2_fk0': mask_BxSxS2_fk0, 'L0_attn_in_proj_w': _L0_attn_in['in_proj_w'], 'L0_attn_conv_w': _L0_attn_in['conv_w'], 'L0_attn_conv_b': _L0_attn_in['conv_b'], 'L0_attn_dt_bias': _L0_attn_in['dt_bias'], 'L0_attn_A_log': _L0_attn_in['A_log'], 'L0_attn_D_skip': _L0_attn_in['D_skip'], 'L0_attn_norm_w': _L0_attn_in['norm_w'], 'L0_attn_out_proj_w': _L0_attn_in['out_proj_w'], 'L0_attn_ln_w': _L0_attn_in['ln_w'], 'L0_attn_ln_b': _L0_attn_in['ln_b'], 'L0_xattn_Wq1': _L0_xattn_in['Wq1'], 'L0_xattn_Wk1': _L0_xattn_in['Wk1'], 'L0_xattn_Wv1': _L0_xattn_in['Wv1'], 'L0_xattn_Wk2': _L0_xattn_in['Wk2'], 'L0_xattn_Wv2': _L0_xattn_in['Wv2'], 'L0_xattn_Wo': _L0_xattn_in['Wo'], 'L0_xattn_bo': _L0_xattn_in['bo'], 'L0_ffn_gate_w': _L0_ffn_in['gate_w'], 'L0_ffn_gate_bias': _L0_ffn_in['gate_bias'], 'L0_ffn_Wg': _L0_ffn_in['Wg'], 'L0_ffn_Wu': _L0_ffn_in['Wu'], 'L0_ffn_Wd': _L0_ffn_in['Wd'], 'L0_ffn_Ws_g': _L0_ffn_in['Ws_g'], 'L0_ffn_Ws_u': _L0_ffn_in['Ws_u'], 'L0_ffn_Ws_d': _L0_ffn_in['Ws_d'], 'L1_attn_Wc_down': _L1_attn_in['Wc_down'], 'L1_attn_Wq_up': _L1_attn_in['Wq_up'], 'L1_attn_Wkv_up': _L1_attn_in['Wkv_up'], 'L1_attn_Wc_proj': _L1_attn_in['Wc_proj'], 'L1_xattn_Wq': _L1_xattn_in['Wq'], 'L1_xattn_bq': _L1_xattn_in['bq'], 'L1_xattn_Wk': _L1_xattn_in['Wk'], 'L1_xattn_bk': _L1_xattn_in['bk'], 'L1_xattn_Wv': _L1_xattn_in['Wv'], 'L1_xattn_bv': _L1_xattn_in['bv'], 'L1_xattn_Wo': _L1_xattn_in['Wo'], 'L1_xattn_bo': _L1_xattn_in['bo'], 'L1_ffn_rw1': _L1_ffn_in['rw1'], 'L1_ffn_rb1': _L1_ffn_in['rb1'], 'L1_ffn_rw2': _L1_ffn_in['rw2'], 'L1_ffn_rb2': _L1_ffn_in['rb2'], 'L1_ffn_ew1': _L1_ffn_in['ew1'], 'L1_ffn_eb1': _L1_ffn_in['eb1'], 'L1_ffn_ew2': _L1_ffn_in['ew2'], 'L1_ffn_eb2': _L1_ffn_in['eb2'], 'L2_attn_wq': _L2_attn_in['wq'], 'L2_attn_bq': _L2_attn_in['bq'], 'L2_attn_wk': _L2_attn_in['wk'], 'L2_attn_bk': _L2_attn_in['bk'], 'L2_attn_wv': _L2_attn_in['wv'], 'L2_attn_bv': _L2_attn_in['bv'], 'L2_xattn_wq': _L2_xattn_in['wq'], 'L2_xattn_wk': _L2_xattn_in['wk'], 'L2_xattn_wv': _L2_xattn_in['wv'], 'L2_xattn_fc_w': _L2_xattn_in['fc_w'], 'L2_xattn_fc_b': _L2_xattn_in['fc_b'], 'L2_xattn_rel_table': _L2_xattn_in['rel_table'], 'L2_ffn_Wr': _L2_ffn_in['Wr'], 'L2_ffn_Wu': _L2_ffn_in['Wu'], 'L2_ffn_Wg': _L2_ffn_in['Wg'], 'L2_ffn_Wd': _L2_ffn_in['Wd'], 'L2_ffn_Wu_s': _L2_ffn_in['Wu_s'], 'L2_ffn_Wg_s': _L2_ffn_in['Wg_s'], 'L2_ffn_Wd_s': _L2_ffn_in['Wd_s'], 'L3_attn_key_param': _L3_attn_in['key_param'], 'L3_attn_Wq': _L3_attn_in['Wq'], 'L3_attn_bq': _L3_attn_in['bq'], 'L3_attn_Wk': _L3_attn_in['Wk'], 'L3_attn_bk': _L3_attn_in['bk'], 'L3_attn_Wv': _L3_attn_in['Wv'], 'L3_attn_bv': _L3_attn_in['bv'], 'L3_attn_Wo': _L3_attn_in['Wo'], 'L3_attn_bo': _L3_attn_in['bo'], 'L3_xattn_Wout': _L3_xattn_in['Wout'], 'L3_xattn_bout': _L3_xattn_in['bout'], 'L3_ffn_weight_q': _L3_ffn_in['weight_q'], 'L3_ffn_weight_scale': _L3_ffn_in['weight_scale'], 'L3_ffn_bias': _L3_ffn_in['bias']}

def reference(x, ctx_1024, mask_BxS2_ik0, mask_BxSxS2_fk0, L0_attn_in_proj_w, L0_attn_conv_w, L0_attn_conv_b, L0_attn_dt_bias, L0_attn_A_log, L0_attn_D_skip, L0_attn_norm_w, L0_attn_out_proj_w, L0_attn_ln_w, L0_attn_ln_b, L0_xattn_Wq1, L0_xattn_Wk1, L0_xattn_Wv1, L0_xattn_Wk2, L0_xattn_Wv2, L0_xattn_Wo, L0_xattn_bo, L0_ffn_gate_w, L0_ffn_gate_bias, L0_ffn_Wg, L0_ffn_Wu, L0_ffn_Wd, L0_ffn_Ws_g, L0_ffn_Ws_u, L0_ffn_Ws_d, L1_attn_Wc_down, L1_attn_Wq_up, L1_attn_Wkv_up, L1_attn_Wc_proj, L1_xattn_Wq, L1_xattn_bq, L1_xattn_Wk, L1_xattn_bk, L1_xattn_Wv, L1_xattn_bv, L1_xattn_Wo, L1_xattn_bo, L1_ffn_rw1, L1_ffn_rb1, L1_ffn_rw2, L1_ffn_rb2, L1_ffn_ew1, L1_ffn_eb1, L1_ffn_ew2, L1_ffn_eb2, L2_attn_wq, L2_attn_bq, L2_attn_wk, L2_attn_bk, L2_attn_wv, L2_attn_bv, L2_xattn_wq, L2_xattn_wk, L2_xattn_wv, L2_xattn_fc_w, L2_xattn_fc_b, L2_xattn_rel_table, L2_ffn_Wr, L2_ffn_Wu, L2_ffn_Wg, L2_ffn_Wd, L2_ffn_Wu_s, L2_ffn_Wg_s, L2_ffn_Wd_s, L3_attn_key_param, L3_attn_Wq, L3_attn_bq, L3_attn_Wk, L3_attn_bk, L3_attn_Wv, L3_attn_bv, L3_attn_Wo, L3_attn_bo, L3_xattn_Wout, L3_xattn_bout, L3_ffn_weight_q, L3_ffn_weight_scale, L3_ffn_bias):
    import jax
    import jax.numpy as jnp

    def _L0_attn_ref(x, in_proj_w, conv_w, conv_b, dt_bias, A_log, D_skip, norm_w, out_proj_w, ln_w, ln_b):
        import jax, jax.numpy as jnp
        import numpy as np
        DT_MIN, DT_MAX = (0.001, 0.1)
        CHUNK = 64
        b, L, d_model = x.shape
        d_inner = norm_w.shape[0]
        nheads = A_log.shape[0]
        hd = d_inner // nheads
        conv_dim = conv_w.shape[0]
        d_state = (conv_dim - d_inner) // 2
        Q = CHUNK
        c = L // Q
        zxbcdt = jnp.einsum('bld,kd->blk', x, in_proj_w)
        z = zxbcdt[..., :d_inner]
        xBC = zxbcdt[..., d_inner:d_inner + conv_dim]
        dt_raw = zxbcdt[..., d_inner + conv_dim:]
        K = conv_w.shape[1]
        xp = jnp.pad(xBC, ((0, 0), (K - 1, 0), (0, 0)))
        conv = sum((xp[:, k:k + L, :] * conv_w[:, k] for k in range(K))) + conv_b
        xBC = jax.nn.silu(conv)
        x_ssm = xBC[..., :d_inner]
        Bm = xBC[..., d_inner:d_inner + d_state]
        Cm = xBC[..., d_inner + d_state:]
        dt = DT_MIN + (DT_MAX - DT_MIN) * jax.nn.sigmoid(dt_raw + dt_bias)
        A = -jnp.exp(A_log)
        xh = x_ssm.reshape(b, c, Q, nheads, hd)
        dtc = dt.reshape(b, c, Q, nheads)
        x_dt = xh * dtc[..., None]
        dA = jnp.einsum('bcqh,h->bhcq', dtc, A)
        Acum = jnp.cumsum(dA, axis=-1)
        Bc = Bm.reshape(b, c, Q, d_state)
        Cc = Cm.reshape(b, c, Q, d_state)
        seg = Acum[..., :, None] - Acum[..., None, :]
        mask = jnp.tril(jnp.ones((Q, Q), bool))
        Lmat = jnp.exp(jnp.where(mask, seg, -jnp.inf))
        Yd = jnp.einsum('bcqn,bcsn,bhcqs,bcshp->bcqhp', Cc, Bc, Lmat, x_dt)
        decay_states = jnp.exp(Acum[..., -1:] - Acum)
        states = jnp.einsum('bcqn,bhcq,bcqhp->bchpn', Bc, decay_states, x_dt)
        chunk_decay = jnp.exp(Acum[..., -1])

        def step(carry, inp):
            st, dec = inp
            return (dec[..., None, None] * carry + st, carry)
        _, prevs = jax.lax.scan(step, jnp.zeros((b, nheads, hd, d_state), x.dtype), (jnp.moveaxis(states, 1, 0), jnp.moveaxis(chunk_decay, 2, 0)))
        prevs = jnp.moveaxis(prevs, 0, 1)
        Yo = jnp.einsum('bcqn,bchpn,bhcq->bcqhp', Cc, prevs, jnp.exp(Acum))
        Y = (Yd + Yo).reshape(b, L, nheads, hd) + D_skip[None, None, :, None] * xh.reshape(b, L, nheads, hd)
        y = Y.reshape(b, L, d_inner)
        y = y * jax.nn.silu(z)
        y = y * jax.lax.rsqrt(jnp.mean(y * y, axis=-1, keepdims=True) + 1e-05) * norm_w
        out = jnp.einsum('bli,di->bld', y, out_proj_w)
        mu = jnp.mean(out, axis=-1, keepdims=True)
        var = jnp.mean((out - mu) ** 2, axis=-1, keepdims=True)
        ln = (out - mu) * jax.lax.rsqrt(var + 1e-05) * ln_w + ln_b
        return x + ln

    def _L0_xattn_ref(x1, x2, Wq1, Wk1, Wv1, Wk2, Wv2, Wo, bo):
        import jax, jax.numpy as jnp
        import numpy as np
        HEADS = 8
        DIM_HEAD = 64
        h, d = (HEADS, DIM_HEAD)
        scale = d ** (-0.5)
        B, N1, _ = x1.shape
        N2 = x2.shape[1]

        def split_heads(t, n):
            return t.reshape(B, n, h, d)
        q1 = split_heads(x1 @ Wq1, N1)
        k1 = split_heads(x1 @ Wk1, N1)
        v1 = split_heads(x1 @ Wv1, N1)
        k2 = split_heads(x2 @ Wk2, N2)
        v2 = split_heads(x2 @ Wv2, N2)
        k = jnp.concatenate([k1, k2], axis=1)
        v = jnp.concatenate([v1, v2], axis=1)
        sim = jnp.einsum('bihd,bjhd->bhij', q1.astype(jnp.float32), k.astype(jnp.float32)) * scale
        attn = jax.nn.softmax(sim, axis=-1)
        out = jnp.einsum('bhij,bjhd->bihd', attn, v)
        out = out.reshape(B, N1, h * d)
        return out @ Wo + bo

    def _L0_ffn_ref(hidden_states, gate_w, gate_bias, Wg, Wu, Wd, Ws_g, Ws_u, Ws_d):
        import jax, jax.numpy as jnp
        import numpy as np
        E = 16
        K = 4
        NG = 4
        TG = 2
        SCALE = 2.5
        NORM_TOPK = True
        H = 128
        I = 64
        SH_I = I * 2
        B, S = (2, 256)
        x = hidden_states
        b, s, h = x.shape
        n = b * s
        xf = x.reshape(n, h)
        logits = xf @ gate_w.T
        scores = jax.nn.sigmoid(logits)
        sfc = scores + gate_bias
        epg = E // NG
        grp = sfc.reshape(n, NG, epg)
        g_scores = jax.lax.top_k(grp, 2)[0].sum(-1)
        _, gidx = jax.lax.top_k(g_scores, TG)
        gmask = jax.nn.one_hot(gidx, NG, dtype=sfc.dtype).sum(1)
        emask = jnp.repeat(gmask, epg, axis=1)
        masked = jnp.where(emask > 0, sfc, -jnp.inf)
        _, topk_idx = jax.lax.top_k(masked, K)
        topk_w = jnp.take_along_axis(scores, topk_idx, axis=1)
        if K > 1 and NORM_TOPK:
            topk_w = topk_w / (topk_w.sum(-1, keepdims=True) + 1e-20)
        topk_w = topk_w * SCALE
        cw = (jax.nn.one_hot(topk_idx, E, dtype=topk_w.dtype) * topk_w[..., None]).sum(1)
        hg = jnp.einsum('nh,eih->nei', xf, Wg)
        hu = jnp.einsum('nh,eih->nei', xf, Wu)
        act = jax.nn.silu(hg) * hu
        y = jnp.einsum('nei,ne,ehi->nh', act, cw, Wd)
        shared = jax.nn.silu(xf @ Ws_g.T) * (xf @ Ws_u.T) @ Ws_d.T
        y = y + shared
        return (x + y.reshape(b, s, h)).astype(hidden_states.dtype)

    def _L1_attn_ref(x, Wc_down, Wq_up, Wkv_up, Wc_proj):
        import jax, jax.numpy as jnp
        import numpy as np
        N_EMBD = 128
        N_HEAD = 16
        HEAD_DIM = N_EMBD // N_HEAD
        LATENT_DIM = N_EMBD // 2
        B, T = (4, 256)
        Bsz, Tlen, C = x.shape
        latent = x @ Wc_down
        q = (latent @ Wq_up).reshape(Bsz, Tlen, N_HEAD, HEAD_DIM)
        kv = latent @ Wkv_up
        k, v = (kv[..., :HEAD_DIM], kv[..., HEAD_DIM:])
        scale = 1.0 / np.sqrt(HEAD_DIM)
        att = jnp.einsum('bthd,bsd->bhts', q, k) * scale
        causal = jnp.tril(jnp.ones((Tlen, Tlen), dtype=bool))
        att = jnp.where(causal[None, None], att, -jnp.inf)
        att = jax.nn.softmax(att, axis=-1)
        y = jnp.einsum('bhts,bsd->bthd', att, v).reshape(Bsz, Tlen, C)
        return y @ Wc_proj

    def _L1_xattn_ref(query, keys, values, mask, Wq, bq, Wk, bk, Wv, bv, Wo, bo):
        import jax, jax.numpy as jnp
        import numpy as np
        EMBED = 128
        HEADS = 16
        HEAD_DIM = EMBED // HEADS
        B, S = (4, 256)
        N, Lq, _ = query.shape
        Lk = keys.shape[1]
        q = (query @ Wq.T + bq).reshape(N, Lq, HEADS, HEAD_DIM).transpose(0, 2, 1, 3)
        k = (keys @ Wk.T + bk).reshape(N, Lk, HEADS, HEAD_DIM).transpose(0, 2, 1, 3)
        v = (values @ Wv.T + bv).reshape(N, Lk, HEADS, HEAD_DIM).transpose(0, 2, 1, 3)
        energy = jnp.einsum('bhqd,bhkd->bhqk', q, k)
        energy = jnp.where(mask[:, None, None, :] == 0, jnp.float32(-1e+20), energy)
        attention = jax.nn.softmax(energy / np.sqrt(HEAD_DIM), axis=-1)
        out = jnp.einsum('bhqk,bhkd->bhqd', attention, v)
        out = out.transpose(0, 2, 1, 3).reshape(N, Lq, EMBED)
        return out @ Wo.T + bo

    def _L1_ffn_ref(x, rw1, rb1, rw2, rb2, ew1, eb1, ew2, eb2):
        import jax, jax.numpy as jnp
        import numpy as np
        B, F, D, H, E, K = (4, 256, 128, 256, 8, 2)
        b, f, d = x.shape
        t = x.reshape(b * f, d)
        logits = jax.nn.silu(t @ rw1 + rb1) @ rw2 + rb2
        vals, idx = jax.lax.top_k(logits, K)
        rows = jnp.arange(t.shape[0])[:, None]
        masked = jnp.full_like(logits, -jnp.inf).at[rows, idx].set(vals)
        w = jax.nn.softmax(masked, axis=1)
        eh = jax.nn.silu(jnp.einsum('td,edh->teh', t, ew1) + eb1[None])
        eo = jnp.einsum('teh,ehd->ted', eh, ew2) + eb2[None]
        y = t + jnp.einsum('te,ted->td', w, eo)
        return y.reshape(b, f, d)

    def _L2_attn_ref(x, wq, bq, wk, bk, wv, bv):
        import jax, jax.numpy as jnp
        import numpy as np
        DIM = 128
        B, S = (4, 512)
        scale = x.shape[-1] ** (-0.5)
        q = x @ wq.T + bq
        k = x @ wk.T + bk
        v = x @ wv.T + bv
        scores = jnp.einsum('bqd,bkd->bqk', q, k) * scale
        attn = jax.nn.softmax(scores, axis=-1)
        return jnp.einsum('bqk,bkd->bqd', attn, v)

    def _L2_xattn_ref(key, query, value, wq, wk, wv, fc_w, fc_b, rel_table):
        import jax, jax.numpy as jnp
        import numpy as np
        import math
        B, S, E = (2, 256, 128)
        H = 16
        DK = E // H
        MAX_DIST = 256

        def _split_heads(x):
            b, s, _ = x.shape
            return x.reshape(b, s, H, DK).transpose(0, 2, 1, 3)
        b, s, _ = query.shape
        k = _split_heads(key @ wk.T)
        q = _split_heads(query @ wq.T)
        v = _split_heads(value @ wv.T)
        ctx = jnp.arange(s)[:, None]
        mem = jnp.arange(s)[None, :]
        rel = jnp.clip(mem - ctx, -MAX_DIST + 1, MAX_DIST - 1) + MAX_DIST - 1
        bias = rel_table[rel]
        bias = bias.transpose(2, 0, 1)[None]
        scores = jnp.einsum('bhqd,bhkd->bhqk', q, k) / math.sqrt(DK)
        scores = scores + bias
        attn = jax.nn.softmax(scores, axis=-1)
        out = jnp.einsum('bhqk,bhkd->bhqd', attn, v)
        out = out.transpose(0, 2, 1, 3).reshape(b, s, E)
        return out @ fc_w.T + fc_b

    def _L2_ffn_ref(x, Wr, Wu, Wg, Wd, Wu_s, Wg_s, Wd_s):
        import jax, jax.numpy as jnp
        import numpy as np
        DIM = 128
        HID = 512
        NUM_EXPERTS = 8
        TOP_K = 2
        ALPHA = 2.0
        B, S = (4, 256)

        def _swiglu(x, wu, wg, wd):
            up = x @ wu
            g = x @ wg
            gate = jax.nn.sigmoid(g) * g
            return up * gate @ wd
        logits = x @ Wr
        probs = jax.nn.softmax(logits, axis=-1)
        topk_vals, topk_idx = jax.lax.top_k(probs, TOP_K)
        out = jnp.zeros_like(x)
        for i in range(TOP_K - 1):
            p = topk_vals[..., i:i + 1]
            ind = topk_idx[..., i]
            acc = jnp.zeros_like(x)
            for j in range(NUM_EXPERTS - 1):
                mask = (ind == j).astype(x.dtype)[..., None]
                acc = acc + _swiglu(x, Wu[j], Wg[j], Wd[j]) * mask
            out = out + ALPHA * p * acc
        out = out + _swiglu(x, Wu_s, Wg_s, Wd_s)
        return out

    def _L3_attn_ref(query, key_param, Wq, bq, Wk, bk, Wv, bv, Wo, bo):
        import jax, jax.numpy as jnp
        import numpy as np
        D_MODEL = 128
        N_HEADS = 16
        NUM_PATTERN = 32
        HEAD_DIM = D_MODEL // N_HEADS

        def sparsemax(z):
            S = z.shape[-1]
            z_sorted = -jnp.sort(-z, axis=-1)
            cum = jnp.cumsum(z_sorted, axis=-1)
            k = jnp.arange(1, S + 1, dtype=z.dtype)
            support = 1.0 + k * z_sorted > cum
            k_sup = jnp.sum(support, axis=-1, keepdims=True)
            cum_sel = jnp.take_along_axis(cum, k_sup - 1, axis=-1)
            tau = (cum_sel - 1.0) / k_sup.astype(z.dtype)
            return jnp.maximum(z - tau, 0.0)
        B, L, _ = query.shape
        S = key_param.shape[1]
        H, E = (N_HEADS, HEAD_DIM)
        D = HEAD_DIM
        k = jnp.broadcast_to(key_param, (B, S, D_MODEL))
        queries = (query @ Wq + bq).reshape(B, L, H, E)
        keys_flat = k @ Wk + bk
        values = (keys_flat @ Wv + bv).reshape(B, S, H, D)
        keys = keys_flat.reshape(B, S, H, E)
        scale = 1.0 / np.sqrt(E)
        scores = jnp.einsum('blhe,bshe->bhls', queries, keys)
        A = sparsemax(scale * scores)
        out = jnp.einsum('bhls,bshd->blhd', A, values)
        out = jnp.transpose(out, (0, 2, 1, 3)).reshape(B, L, H * D)
        return out @ Wo + bo

    def _L3_xattn_ref(query, key, value, dropout_mask, Wout, bout, inv_scale_factor):
        import jax, jax.numpy as jnp
        import numpy as np
        B, S, E = (8, 256, 128)
        DROPOUT_P = 0.1
        scores = jnp.einsum('bqd,bkd->bqk', query, key) / jnp.float32(inv_scale_factor)
        probs = jax.nn.softmax(scores, axis=-1)
        probs = probs * dropout_mask
        attn = jnp.einsum('bqk,bkd->bqd', probs, value)
        return jnp.einsum('bqd,ed->bqe', attn, Wout) + bout

    def _L3_ffn_ref(x, weight_q, weight_scale, bias):
        import jax, jax.numpy as jnp
        import numpy as np
        B, S, IN, OUT = (4, 1024, 128, 128)
        EPS = 1e-06

        def _xla_quantized_matmul(x2d, weight_q, weight_scale):
            amax = jnp.max(jnp.abs(x2d), axis=-1, keepdims=True)
            x_scale = jnp.maximum(amax, EPS) / 127.0
            x_q = jnp.clip(jnp.round(x2d / x_scale), -128, 127).astype(jnp.int8)
            acc = jax.lax.dot_general(x_q, weight_q, (((1,), (1,)), ((), ())), preferred_element_type=jnp.int32)
            return acc.astype(jnp.float32) * x_scale * weight_scale[None, :]
        orig_shape = x.shape
        x2d = x.reshape(-1, orig_shape[-1])
        out = _xla_quantized_matmul(x2d, weight_q, weight_scale)
        out = out.reshape(*orig_shape[:-1], out.shape[-1])
        out = out + bias
        return out
    x = x + _L0_attn_ref(_layernorm(x, axis=-1), L0_attn_in_proj_w, L0_attn_conv_w, L0_attn_conv_b, L0_attn_dt_bias, L0_attn_A_log, L0_attn_D_skip, L0_attn_norm_w, L0_attn_out_proj_w, L0_attn_ln_w, L0_attn_ln_b)
    x = x + _L0_xattn_ref(_layernorm(x, axis=-1), ctx_1024, L0_xattn_Wq1, L0_xattn_Wk1, L0_xattn_Wv1, L0_xattn_Wk2, L0_xattn_Wv2, L0_xattn_Wo, L0_xattn_bo)
    x = x + _L0_ffn_ref(_layernorm(x, axis=-1), L0_ffn_gate_w, L0_ffn_gate_bias, L0_ffn_Wg, L0_ffn_Wu, L0_ffn_Wd, L0_ffn_Ws_g, L0_ffn_Ws_u, L0_ffn_Ws_d)
    x = x + _L1_attn_ref(_layernorm(x, axis=-1), L1_attn_Wc_down, L1_attn_Wq_up, L1_attn_Wkv_up, L1_attn_Wc_proj)
    x = x + _L1_xattn_ref(_layernorm(x, axis=-1), ctx_1024, ctx_1024, mask_BxS2_ik0, L1_xattn_Wq, L1_xattn_bq, L1_xattn_Wk, L1_xattn_bk, L1_xattn_Wv, L1_xattn_bv, L1_xattn_Wo, L1_xattn_bo)
    x = x + _L1_ffn_ref(_layernorm(x, axis=-1), L1_ffn_rw1, L1_ffn_rb1, L1_ffn_rw2, L1_ffn_rb2, L1_ffn_ew1, L1_ffn_eb1, L1_ffn_ew2, L1_ffn_eb2)
    x = x + _L2_attn_ref(_layernorm(x, axis=-1), L2_attn_wq, L2_attn_bq, L2_attn_wk, L2_attn_bk, L2_attn_wv, L2_attn_bv)
    x = x + _L2_xattn_ref(ctx_1024, _layernorm(x, axis=-1), ctx_1024, L2_xattn_wq, L2_xattn_wk, L2_xattn_wv, L2_xattn_fc_w, L2_xattn_fc_b, L2_xattn_rel_table)
    x = x + _L2_ffn_ref(_layernorm(x, axis=-1), L2_ffn_Wr, L2_ffn_Wu, L2_ffn_Wg, L2_ffn_Wd, L2_ffn_Wu_s, L2_ffn_Wg_s, L2_ffn_Wd_s)
    x = x + _L3_attn_ref(_layernorm(x, axis=-1), L3_attn_key_param, L3_attn_Wq, L3_attn_bq, L3_attn_Wk, L3_attn_bk, L3_attn_Wv, L3_attn_bv, L3_attn_Wo, L3_attn_bo)
    x = x + _L3_xattn_ref(_layernorm(x, axis=-1), ctx_1024, ctx_1024, mask_BxSxS2_fk0, L3_xattn_Wout, L3_xattn_bout, 32)
    x = x + _L3_ffn_ref(_layernorm(x, axis=-1), L3_ffn_weight_q, L3_ffn_weight_scale, L3_ffn_bias)
    return x

_drawn_inputs = setup_inputs


def setup_inputs(seed=0):
    import zlib

    import numpy as np

    out = dict(_drawn_inputs(seed))
    spreads = {'L0_attn_conv_b': (0.0, 0.1),
     'L0_attn_D_skip': (1.0, 0.2),
     'L0_attn_norm_w': (1.0, 0.2),
     'L0_attn_ln_w': (1.0, 0.2),
     'L0_attn_ln_b': (0.0, 0.1),
     'L0_xattn_bo': (0.0, 0.1),
     'L0_ffn_gate_bias': (0.0, 0.1),
     'L1_xattn_bq': (0.0, 2.0),
     'L1_xattn_bk': (0.0, 2.0),
     'L1_xattn_bv': (0.0, 0.515),
     'L1_xattn_bo': (0.0, 0.49),
     'L1_ffn_rb1': (0.0, 0.277),
     'L1_ffn_rb2': (0.0, 0.1),
     'L1_ffn_eb1': (0.0, 0.683),
     'L1_ffn_eb2': (0.0, 0.43),
     'L3_attn_bq': (0.0, 0.549),
     'L3_attn_bk': (0.0, 0.315),
     'L3_attn_bv': (0.0, 0.358),
     'L3_attn_bo': (0.0, 0.369)}
    factors = {'L1_attn_Wc_down': 3.331,
     'L1_attn_Wq_up': 8.0,
     'L1_attn_Wkv_up': 3.669,
     'L1_attn_Wc_proj': 3.399,
     'L2_attn_wq': 7.958,
     'L2_attn_bq': 25.381,
     'L2_attn_wk': 7.882,
     'L2_attn_bk': 200.0,
     'L2_attn_bv': 4.368,
     'L2_xattn_fc_b': 2.68,
     'L2_xattn_rel_table': 181.002,
     'L2_ffn_Wr': 8.0,
     'L2_ffn_Wu': 8.0,
     'L2_ffn_Wg': 8.0,
     'L2_ffn_Wd': 8.0,
     'L2_ffn_Wu_s': 8.0,
     'L2_ffn_Wg_s': 8.0,
     'L2_ffn_Wd_s': 8.0,
     'L3_xattn_bout': 44.954,
     'L3_ffn_bias': 62.263}
    for name, (base, spread) in spreads.items():
        noise = np.random.default_rng([zlib.crc32(name.encode()), seed]).standard_normal(out[name].shape)
        drawn = base * np.exp(spread * noise) if base else spread * noise
        out[name] = jnp.asarray(drawn.astype(out[name].dtype))
    for name, factor in factors.items():
        out[name] = (out[name] * factor).astype(out[name].dtype)
    return out
```

```python
import concourse.bass as bass
import concourse.mybir as mybir
import numpy as np
from contextlib import ExitStack

F32 = mybir.dt.float32
BF16 = mybir.dt.bfloat16
ALU = mybir.AluOpType
ACT = mybir.ActivationFunctionType
AX = mybir.AxisListType

NB = 32
T = 128
D = 128
GROUP = 4
NG = NB // GROUP
BANK = 512
LN_EPS = 1e-5
MASKED = -1e20


class Layer:

    def __init__(self, nc, ctx, name):
        self.nc, self.ctx, self.name, self.sems = nc, ctx, name, []
        ctx.callback(self.close)

    def close(self):
        self.nc.clear_and_free_semaphores(self.sems)
        self.nc.all_engine_barrier()

    def sbuf(self, name, shape, dtype=F32):
        return self.ctx.enter_context(self.nc.sbuf_tensor(f"{self.name}_{name}", shape, dtype))

    def psum(self, name, shape, dtype=F32):
        return self.ctx.enter_context(self.nc.psum_tensor(f"{self.name}_{name}", shape, dtype))

    def sem(self, name):
        handle = self.nc.alloc_semaphore(f"{self.name}_{name}")
        self.sems.append(handle)
        return handle


class Order:

    def __init__(self, eng, sem):
        self.eng, self.sem, self.n, self.base = eng, sem, 0, 0

    def then(self, ins):
        self.n += 1
        ins.then_inc(self.sem, 1)
        self.eng.wait_ge(self.sem, self.base + self.n)


def groups(eng, order, body, n=NG):
    body(0, True)
    if order is not None:
        per, order.n = order.n, 0
    with eng.Fori(1, n) as i:
        if order is not None:
            order.base = i * per
            order.n = 0
        body(i, False)


def bcast(ap, shape, axis):
    return ap.unsqueeze(axis).broadcast_to(shape)


def layernorm_stats(nc, dve, order, x, i, stats, moments, pad, count=GROUP):
    for u in range(count):
        last = nc.vector.bn_stats(stats[:, u, :], x[:, i * count + u, :])
    order.then(last)
    nc.vector.memset(pad[:, :], 0.0)
    for u in range(count):
        last = nc.vector.bn_aggr(moments[:, u, :], stats[:, u, :])
    order.then(last)
    return nc.vector.tensor_scalar(moments[:, :, 1], moments[:, :, 1], LN_EPS, None, ALU.add)


def layernorm_rstd(nc, pool, stats_ready, i, minus_half, moments, rstd):
    pool.wait_ge(stats_ready, i + 1)
    return nc.gpsimd.tensor_tensor(rstd[:, :], moments[:, :, 1], minus_half[:, 0:moments.shape[1]], ALU.pow)


def layernorm_apply(nc, x, i, moments, rstd, h, count=GROUP):
    for u in range(count):
        last = nc.vector.tensor_scalar(h[:, u, :], x[:, i * count + u, :], moments[:, u, 0:1], rstd[:, u:u + 1],
                                       ALU.subtract, ALU.mult)
    return last
HEADS = 16
HD = D // HEADS
HALF = HEADS // 2
UNITS = 2 * GROUP


def attention16(nc, name, x, const, w, loaded, ctx_t=None, latent=False, causal=False, key_mask=None,
                rel_bias=False, qkv_bias=False, out_bias=False):
    scale = float(HD) ** -0.5
    with ExitStack() as ctx:
        L = Layer(nc, ctx, name)
        stats = L.sbuf("stats", [T, GROUP, 6])
        moments = L.sbuf("moments", [T, GROUP, 2])
        pad = L.sbuf("pad", [T, 1])
        rstd = L.sbuf("rstd", [T, GROUP])
        h = L.sbuf("h", [T, GROUP, D])
        h_t = L.sbuf("h_t", [D, GROUP * T])
        lat_t = L.sbuf("lat_t", [64, GROUP * T])
        q_t = L.sbuf("q_t", [D, GROUP * T])
        k_t = L.sbuf("k_t", [D, GROUP * T])
        c_t = L.sbuf("c_t", [D, 2, GROUP * T])
        v = L.sbuf("v", [T, GROUP, HEADS, HD + 1])
        spread = L.sbuf("spread", [D, 2, HEADS, T])
        probs = L.sbuf("probs", [T, 2, HALF, T])
        probs_t = L.sbuf("probs_t", [T, 2, HALF, T])
        top = L.sbuf("top", [T, 2, HALF])
        rec = L.sbuf("rec", [T, HALF])
        heads_out = L.sbuf("heads_out", [T, GROUP, D])
        heads_t = L.sbuf("heads_t", [D, GROUP * T])
        update = L.sbuf("update", [T, GROUP, D])
        p_score = [L.psum(f"p_score{n}", [T, 2, 4, T]) for n in range(2)]
        p_trans = L.psum("p_trans", [T, 2, 4, T])
        p_pv = L.psum("p_pv", [T, BANK])
        p_misc = L.psum("p_misc", [T, BANK])

        ctx_in = L.sem("ctx_in")
        stats_ready = L.sem("stats_ready")
        rstd_ready = L.sem("rstd_ready")
        normed = L.sem("normed")
        trans = L.sem("trans")
        h_t_ready = L.sem("h_t_ready")
        lat_done = L.sem("lat_done")
        lat_ready = L.sem("lat_ready")
        proj = L.sem("proj")
        q_ready = L.sem("q_ready")
        k_ready = L.sem("k_ready")
        v_ready = L.sem("v_ready")
        spread_ready = L.sem("spread_ready")
        scored = L.sem("scored")
        shifted = L.sem("shifted")
        expd = L.sem("expd")
        turned = L.sem("turned")
        turned_out = L.sem("turned_out")
        weighed = L.sem("weighed")
        divided = L.sem("divided")
        out_t = L.sem("out_t")
        out_t_ready = L.sem("out_t_ready")
        out_done = L.sem("out_done")
        added = L.sem("added")
        dve_order = L.sem("dve_order")
        setup = L.sem("setup")
        flipped = L.sem("flipped")
        scaled_bq = L.sbuf("scaled_bq", [D, 1])
        if rel_bias:
            bias = L.sbuf("bias", [T, HEADS, T])
        if causal:
            causal_b = L.sbuf("causal_b", [T, T], BF16)
            ident_b = L.sbuf("ident_b", [T, T], BF16)
        if key_mask is not None:
            mask_f = L.sbuf("mask_f", [1, GROUP * T], BF16)
            ones_b = L.sbuf("ones_b", [1, T], BF16)

        with nc.Block() as block:
            if ctx_t is not None:
                @block.sync
                def _(sp):
                    def body(i, first):
                        if not first:
                            sp.wait_ge(proj, 3 * i)
                        sp.dma_start(c_t[:, 0, :], ctx_t[:, bass.ts(i, GROUP * T)]).then_inc(ctx_in, 16)
                    groups(sp, None, body)

            @block.tensor
            def _(pe):
                if rel_bias:
                    pe.wait_ge(loaded, w["n"])
                    for n in range(4):
                        last = nc.tensor.matmul(p_score[n // 2][:, n % 2, :, :], const["flip"][:, :],
                                                w["rel"][:, 4 * n:4 * n + 4, :], start=True, stop=True)
                    last.then_inc(flipped, 1)
                    pe.wait_ge(setup, 1)
                else:
                    pe.wait_ge(loaded, w["n"])
                    pe.wait_ge(setup, 1)

                def body(i, first):
                    pe.wait_ge(normed, i + 1)
                    if not first:
                        pe.wait_ge(added, i)
                    for u in range(GROUP):
                        last = nc.tensor.transpose(p_misc[:, u * T:(u + 1) * T], h[:, u, :], const["ident"][:, :])
                    last.then_inc(trans, 1)
                    pe.wait_ge(h_t_ready, i + 1)
                    source_q = h_t
                    source_kv, kd = (c_t[:, 0, :], D) if ctx_t is not None else (h_t[:, :], D)
                    if latent:
                        nc.tensor.matmul(p_pv[0:64, :], w["down"][:, :], h_t[:, :], start=True, stop=True)\
                            .then_inc(lat_done, 1)
                        pe.wait_ge(lat_ready, i + 1)
                        source_q, source_kv, kd = lat_t, lat_t[:, :], 64
                    nc.tensor.matmul(p_score[0][:, 0, :, :], w["wq"][0:kd, :], source_q[0:kd, :], start=True, stop=True)\
                        .then_inc(proj, 1)
                    if ctx_t is not None:
                        pe.wait_ge(ctx_in, (i + 1) * 16)
                    nc.tensor.matmul(p_score[0][:, 1, :, :], w["wk"][0:kd, :], source_kv, start=True, stop=True)\
                        .then_inc(proj, 1)
                    for u in range(GROUP):
                        last = nc.tensor.matmul(p_score[1][:, 0, u, :], source_kv[:, u * T:(u + 1) * T],
                                                w["wv"][0:kd, :], start=True, stop=True)
                    last.then_inc(proj, 1)
                    pe.wait_ge(q_ready, i + 1)
                    pe.wait_ge(k_ready, i + 1)
                    pe.wait_ge(v_ready, i + 1)

                    def scores(n):
                        u, half = n // 2, n % 2
                        pe.wait_ge(spread_ready, i * GROUP + u + 1)
                        if n >= 2:
                            pe.wait_ge(shifted, i * UNITS + n - 1)
                        for j in range(2):
                            out = p_score[n % 2][:, j, :, :]
                            masks = causal or key_mask is not None
                            if causal:
                                nc.tensor.matmul(out, ident_b[:, :], bcast(causal_b[:, :], [T, 4, T], 1),
                                                 start=True, stop=False)
                            if key_mask is not None:
                                nc.tensor.matmul(out, ones_b[0:1, :], bcast(mask_f[0:1, u * T:(u + 1) * T], [1, 4, T], 1),
                                                 start=True, stop=False)
                            head = half * HALF + 4 * j
                            last = nc.tensor.matmul(out, q_t[:, u * T:(u + 1) * T], spread[:, u % 2, head:head + 4, :],
                                                    start=not masks, stop=True)
                        last.then_inc(scored, 1)

                    def transposes(n):
                        pe.wait_ge(expd, i * UNITS + n + 1)
                        if n >= 1:
                            pe.wait_ge(turned_out, i * UNITS + n)
                        for k in range(HALF):
                            last = nc.tensor.transpose(p_trans[:, k // 4, k % 4, :], probs[:, n % 2, k, :],
                                                       const["ident"][:, :])
                        last.then_inc(turned, 1)

                    def values(n):
                        u, half = n // 2, n % 2
                        pe.wait_ge(turned_out, i * UNITS + n + 1)
                        if n >= 1:
                            pe.wait_ge(divided, i * UNITS + n)
                        for k in range(HALF):
                            last = nc.tensor.matmul(p_pv[:, k * (HD + 1):(k + 1) * (HD + 1)], probs_t[:, n % 2, k, :],
                                                    v[:, u, half * HALF + k, :], start=True, stop=True)
                        last.then_inc(weighed, 1)

                    scores(0)
                    for n in range(UNITS):
                        if n + 1 < UNITS:
                            scores(n + 1)
                        if n >= 1:
                            values(n - 1)
                        transposes(n)
                    values(UNITS - 1)

                    pe.wait_ge(divided, (i + 1) * UNITS)
                    for u in range(GROUP):
                        last = nc.tensor.transpose(p_misc[:, u * T:(u + 1) * T], heads_out[:, u, :], const["ident"][:, :])
                    last.then_inc(out_t, 1)
                    pe.wait_ge(out_t_ready, i + 1)
                    for u in range(GROUP):
                        last = nc.tensor.matmul(p_misc[:, u * D:(u + 1) * D], heads_t[:, u * T:(u + 1) * T],
                                                w["wo"][:, :], start=True, stop=True)
                    last.then_inc(out_done, 1)
                groups(pe, None, body)

            @block.scalar
            def _(act):
                act.wait_ge(loaded, w["n"])

                def body(i, first):
                    act.wait_ge(trans, i + 1)
                    nc.scalar.copy(h_t[:, :], p_misc[:, :]).then_inc(h_t_ready, 1)
                    if latent:
                        act.wait_ge(lat_done, i + 1)
                        nc.scalar.copy(lat_t[:, :], p_pv[0:64, :]).then_inc(lat_ready, 1)
                    act.wait_ge(proj, i * 3 + 1)
                    if qkv_bias:
                        act.wait_ge(setup, 1)
                        nc.scalar.activation(q_t[:, :], p_score[0][:, 0, :, :], ACT.Identity, bias=scaled_bq[:, 0:1],
                                             scale=scale).then_inc(q_ready, 1)
                    else:
                        nc.scalar.activation(q_t[:, :], p_score[0][:, 0, :, :], ACT.Copy, scale=scale)\
                            .then_inc(q_ready, 1)
                    act.wait_ge(proj, i * 3 + 2)
                    if not first:
                        act.wait_ge(spread_ready, i * GROUP)
                    if qkv_bias:
                        nc.scalar.activation(k_t[:, :], p_score[0][:, 1, :, :], ACT.Identity, bias=w["bk"][:, 0:1])\
                            .then_inc(k_ready, 1)
                    else:
                        nc.scalar.copy(k_t[:, :], p_score[0][:, 1, :, :]).then_inc(k_ready, 1)

                    def turn_out(n):
                        act.wait_ge(turned, i * UNITS + n + 1)
                        if n >= 2:
                            act.wait_ge(weighed, i * UNITS + n - 1)
                        nc.scalar.copy(probs_t[:, n % 2, 0:4, :], p_trans[:, 0, :, :])
                        nc.scalar.copy(probs_t[:, n % 2, 4:8, :], p_trans[:, 1, :, :]).then_inc(turned_out, 1)

                    for n in range(UNITS):
                        act.wait_ge(shifted, i * UNITS + n + 1)
                        nc.scalar.activation(probs[:, n % 2, :, :], probs[:, n % 2, :, :], ACT.Exp).then_inc(expd, 1)
                        if n >= 1:
                            turn_out(n - 1)
                    turn_out(UNITS - 1)
                    act.wait_ge(out_t, i + 1)
                    nc.scalar.copy(heads_t[:, :], p_misc[:, :]).then_inc(out_t_ready, 1)
                groups(act, None, body)

            @block.vector
            def _(dve):
                order = Order(dve, dve_order)
                dve.wait_ge(loaded, w["n"])
                if causal:
                    nc.vector.tensor_copy(causal_b[:, :], const["causal"][:, :])
                    nc.vector.tensor_copy(ident_b[:, :], const["ident"][:, :])
                if key_mask is not None:
                    nc.vector.memset(ones_b[:, :], 1.0)
                if qkv_bias:
                    nc.vector.tensor_scalar(scaled_bq[:, :], w["bq"][:, :], scale, None, ALU.mult)
                if rel_bias:
                    dve.wait_ge(flipped, 1)
                    for n in range(4):
                        nc.vector.tensor_copy(bias[:, 4 * n:4 * n + 4, :], p_score[n // 2][:, n % 2, :, :])
                nc.vector.memset(v[:, :, :, :], 1.0).then_inc(setup, 1)
                dve.wait_ge(setup, 1)

                def body(i, first):
                    if not first:
                        dve.wait_ge(added, i)
                        dve.wait_ge(trans, i)
                    layernorm_stats(nc, dve, order, x, i, stats, moments, pad).then_inc(stats_ready, 1)
                    dve.wait_ge(rstd_ready, i + 1)
                    layernorm_apply(nc, x, i, moments, rstd, h).then_inc(normed, 1)
                    dve.wait_ge(proj, 3 * i + 3)
                    if not first:
                        dve.wait_ge(weighed, i * UNITS)
                    if key_mask is not None:
                        nc.vector.tensor_scalar(mask_f[:, :], w["mask"][0:1, bass.ts(i, GROUP * T)], 0.0, MASKED,
                                                ALU.is_equal, ALU.mult)
                    if qkv_bias:
                        nc.vector.tensor_tensor(v[:, :, :, 0:HD], p_score[1][:, 0, :, :].rearrange("p u (h d) -> p u h d", d=HD),
                                                bcast(w["bv"][:, :].rearrange("p (h d) -> p h d", d=HD), [T, GROUP, HEADS, HD], 1),
                                                ALU.add).then_inc(v_ready, 1)
                    else:
                        nc.vector.tensor_copy(v[:, :, :, 0:HD], p_score[1][:, 0, :, :].rearrange("p u (h d) -> p u h d", d=HD))\
                            .then_inc(v_ready, 1)

                    def shift(n):
                        u, half = n // 2, n % 2
                        dve.wait_ge(scored, i * UNITS + n + 1)
                        if n >= 2:
                            dve.wait_ge(turned, i * UNITS + n - 1)
                        s = p_score[n % 2][:, :, :, :].rearrange("p a b k -> p (a b) k")
                        p = probs[:, n % 2, :, :]
                        if rel_bias:
                            order.then(nc.vector.tensor_tensor(p, s, bias[:, half * HALF:(half + 1) * HALF, :], ALU.add))
                            s = p
                        order.then(nc.vector.tensor_reduce(top[:, n % 2, :], s, AX.X, ALU.max))
                        nc.vector.tensor_tensor(p, s, bcast(top[:, n % 2, :], [T, HALF, T], 2), ALU.subtract)\
                            .then_inc(shifted, 1)

                    def divide(n):
                        u, half = n // 2, n % 2
                        dve.wait_ge(weighed, i * UNITS + n + 1)
                        o = p_pv[:, 0:HALF * (HD + 1)].rearrange("p (h d) -> p h d", d=HD + 1)
                        order.then(nc.vector.reciprocal(rec[:, :], o[:, :, HD]))
                        if not first and n == 0:
                            dve.wait_ge(out_t, i)
                        nc.vector.tensor_tensor(
                            heads_out[:, u, half * (D // 2):(half + 1) * (D // 2)].rearrange("p (h d) -> p h d", d=HD),
                            o[:, :, 0:HD], bcast(rec[:, :], [T, HALF, HD], 2), ALU.mult).then_inc(divided, 1)

                    for n in range(UNITS):
                        shift(n)
                        if n >= 2:
                            divide(n - 2)
                    divide(UNITS - 2)
                    divide(UNITS - 1)
                    dve.wait_ge(out_done, i + 1)
                    out = p_misc[:, :].rearrange("p (u d) -> p u d", d=D)
                    if out_bias:
                        order.then(nc.vector.tensor_tensor(update[:, :, :], out, bcast(w["bo"][:, :], [T, GROUP, D], 1), ALU.add))
                        out = update[:, :, :]
                    xs = x[:, bass.ts(i, GROUP), :]
                    nc.vector.tensor_tensor(xs, xs, out, ALU.add).then_inc(added, 1)
                groups(dve, order, body)

            @block.gpsimd
            def _(pool):
                def body(i, first):
                    layernorm_rstd(nc, pool, stats_ready, i, const["minus_half"], moments, rstd).then_inc(rstd_ready, 1)
                    pool.wait_ge(k_ready, i + 1)
                    for u in range(GROUP):
                        if not first:
                            pool.wait_ge(scored, i * UNITS + 2 * u - 2)
                        elif u >= 2:
                            pool.wait_ge(scored, 2 * u - 2)
                        nc.gpsimd.tensor_tensor(spread[:, u % 2, :, :], bcast(k_t[:, u * T:(u + 1) * T], [D, HEADS, T], 1),
                                                bcast(const["head_of"][:, :], [D, HEADS, T], 2), ALU.mult)\
                            .then_inc(spread_ready, 1)
                groups(pool, None, body)


def attention8(nc, name, x, const, w, loaded, ctx_t):
    HEADS8, HD8, KEYS, BLOCKS = 8, 64, 2 * T, 4
    with ExitStack() as ctx:
        L = Layer(nc, ctx, name)
        stats = L.sbuf("stats", [T, GROUP, 6])
        moments = L.sbuf("moments", [T, GROUP, 2])
        pad = L.sbuf("pad", [T, 1])
        rstd = L.sbuf("rstd", [T, GROUP])
        h = L.sbuf("h", [T, GROUP, D])
        h_t = L.sbuf("h_t", [D, GROUP * T])
        c_t = L.sbuf("c_t", [D, GROUP * T])
        q_t = L.sbuf("q_t", [T, BLOCKS, GROUP * T])
        keys = L.sbuf("keys", [T, BLOCKS, 2, GROUP, KEYS])
        v = L.sbuf("v", [T, GROUP, 2, HEADS8, HD8 + 1])
        probs = L.sbuf("probs", [T, 2, 4, KEYS])
        probs_t = L.sbuf("probs_t", [T, 2, 8, T])
        top = L.sbuf("top", [T, 2, 4])
        rec = L.sbuf("rec", [T, 4])
        heads_out = L.sbuf("heads_out", [T, GROUP, BLOCKS, T])
        heads_t = L.sbuf("heads_t", [T, BLOCKS, GROUP * T])
        update = L.sbuf("update", [T, GROUP, D])
        p_score = [L.psum(f"p_score{n}", [T, 2, BANK]) for n in range(2)]
        p_trans = L.psum("p_trans", [T, 2, 4, T])
        p_pv = L.psum("p_pv", [T, BANK])
        p_misc = L.psum("p_misc", [T, BANK])

        ctx_in = L.sem("ctx_in")
        stats_ready = L.sem("stats_ready")
        rstd_ready = L.sem("rstd_ready")
        normed = L.sem("normed")
        trans = L.sem("trans")
        h_t_ready = L.sem("h_t_ready")
        qk_done = L.sem("qk_done")
        qk_ready = L.sem("qk_ready")
        v_done = L.sem("v_done")
        v_ready = L.sem("v_ready")
        scored = L.sem("scored")
        shifted = L.sem("shifted")
        expd = L.sem("expd")
        turned = L.sem("turned")
        turned_out = L.sem("turned_out")
        weighed = L.sem("weighed")
        divided = L.sem("divided")
        out_t = L.sem("out_t")
        out_t_ready = L.sem("out_t_ready")
        out_done = L.sem("out_done")
        added = L.sem("added")
        dve_order = L.sem("dve_order")
        setup = L.sem("setup")
        NQK, NV = 3 * BLOCKS, 2 * GROUP

        with nc.Block() as block:
            @block.sync
            def _(sp):
                def body(i, first):
                    if not first:
                        sp.wait_ge(qk_done, i * NQK)
                    sp.dma_start(c_t[:, :], ctx_t[:, bass.ts(i, GROUP * T)]).then_inc(ctx_in, 16)
                groups(sp, None, body)

            @block.tensor
            def _(pe):
                pe.wait_ge(loaded, w["n"])
                pe.wait_ge(setup, 2)

                def body(i, first):
                    pe.wait_ge(normed, i + 1)
                    if not first:
                        pe.wait_ge(added, i)
                    for u in range(GROUP):
                        last = nc.tensor.transpose(p_misc[:, u * T:(u + 1) * T], h[:, u, :], const["ident"][:, :])
                    last.then_inc(trans, 1)
                    pe.wait_ge(h_t_ready, i + 1)
                    pe.wait_ge(ctx_in, (i + 1) * 16)
                    for j in range(NQK):
                        block_n, what = j // 3, j % 3
                        if j >= 2:
                            pe.wait_ge(qk_ready, i * NQK + j - 1)
                        weights = (w["wq"], w["wk1"], w["wk2"])[what][:, block_n * T:(block_n + 1) * T]
                        nc.tensor.matmul(p_score[0][:, j % 2, :], weights, (h_t, h_t, c_t)[what][:, :],
                                         start=True, stop=True).then_inc(qk_done, 1)
                        if j < NV:
                            u, of_ctx = j // 2, j % 2
                            if j >= 2:
                                pe.wait_ge(v_ready, i * NV + j - 1)
                            nc.tensor.matmul(p_score[1][:, j % 2, :], (h_t, c_t)[of_ctx][:, u * T:(u + 1) * T],
                                             (w["wv1"], w["wv2"])[of_ctx][:, :], start=True, stop=True).then_inc(v_done, 1)
                    pe.wait_ge(qk_ready, (i + 1) * NQK)
                    pe.wait_ge(v_ready, (i + 1) * NV)

                    def scores(n):
                        u, half = n // 2, n % 2
                        if n >= 2:
                            pe.wait_ge(shifted, i * UNITS + n - 1)
                        for j in range(2):
                            block_n = 2 * half + j
                            last = nc.tensor.matmul(p_score[n % 2][:, j, :], q_t[:, block_n, u * T:(u + 1) * T],
                                                    keys[:, block_n, :, u, :], start=True, stop=True)
                        last.then_inc(scored, 1)

                    def transposes(n):
                        pe.wait_ge(expd, i * UNITS + n + 1)
                        if n >= 1:
                            pe.wait_ge(turned_out, i * UNITS + n)
                        for k in range(8):
                            last = nc.tensor.transpose(p_trans[:, k // 4, k % 4, :],
                                                       probs[:, n % 2, k // 2, (k % 2) * T:(k % 2 + 1) * T],
                                                       const["ident"][:, :])
                        last.then_inc(turned, 1)

                    def values(n):
                        u, half = n // 2, n % 2
                        pe.wait_ge(turned_out, i * UNITS + n + 1)
                        if n >= 1:
                            pe.wait_ge(divided, i * UNITS + n)
                        for k in range(8):
                            head, part = k // 2, k % 2
                            last = nc.tensor.matmul(p_pv[:, head * (HD8 + 1):(head + 1) * (HD8 + 1)],
                                                    probs_t[:, n % 2, k, :], v[:, u, part, 4 * half + head, :],
                                                    start=(part == 0), stop=(part == 1))
                        last.then_inc(weighed, 1)

                    scores(0)
                    for n in range(UNITS):
                        if n + 1 < UNITS:
                            scores(n + 1)
                        if n >= 1:
                            values(n - 1)
                        transposes(n)
                    values(UNITS - 1)
                    pe.wait_ge(divided, (i + 1) * UNITS)
                    for b in range(BLOCKS):
                        for u in range(GROUP):
                            last = nc.tensor.transpose(p_score[b // 2][:, b % 2, u * T:(u + 1) * T], heads_out[:, u, b, :],
                                                       const["ident"][:, :])
                        last.then_inc(out_t, 1)
                    pe.wait_ge(out_t_ready, (i + 1) * BLOCKS)
                    for u in range(GROUP):
                        for b in range(BLOCKS):
                            last = nc.tensor.matmul(p_misc[:, u * D:(u + 1) * D], heads_t[:, b, u * T:(u + 1) * T],
                                                    w["wo"][:, b, :], start=(b == 0), stop=(b == BLOCKS - 1))
                    last.then_inc(out_done, 1)
                groups(pe, None, body)

            @block.scalar
            def _(act):
                act.wait_ge(loaded, w["n"])
                act.wait_ge(setup, 2)

                def body(i, first):
                    act.wait_ge(trans, i + 1)
                    nc.scalar.copy(h_t[:, :], p_misc[:, :]).then_inc(h_t_ready, 1)
                    for j in range(NQK):
                        block_n, what = j // 3, j % 3
                        act.wait_ge(qk_done, i * NQK + j + 1)
                        src = p_score[0][:, j % 2, :]
                        if what == 0:
                            nc.scalar.activation(q_t[:, block_n, :], src, ACT.Copy, scale=float(HD8) ** -0.5)\
                                .then_inc(qk_ready, 1)
                        else:
                            for half in range(2):
                                part = slice(64 * half, 64 * half + 64)
                                last = nc.scalar.copy(keys[part, block_n, half, :, (what - 1) * T:what * T],
                                                      src[part, :].rearrange("p (u k) -> p u k", k=T))
                            last.then_inc(qk_ready, 1)

                    def turn_out(n):
                        act.wait_ge(turned, i * UNITS + n + 1)
                        if n >= 2:
                            act.wait_ge(weighed, i * UNITS + n - 1)
                        nc.scalar.copy(probs_t[:, n % 2, 0:4, :], p_trans[:, 0, :, :])
                        nc.scalar.copy(probs_t[:, n % 2, 4:8, :], p_trans[:, 1, :, :]).then_inc(turned_out, 1)

                    for n in range(UNITS):
                        act.wait_ge(shifted, i * UNITS + n + 1)
                        nc.scalar.activation(probs[:, n % 2, :, :], probs[:, n % 2, :, :], ACT.Exp).then_inc(expd, 1)
                        if n >= 1:
                            turn_out(n - 1)
                    turn_out(UNITS - 1)
                    for b in range(BLOCKS):
                        act.wait_ge(out_t, i * BLOCKS + b + 1)
                        nc.scalar.copy(heads_t[:, b, :], p_score[b // 2][:, b % 2, :]).then_inc(out_t_ready, 1)
                groups(act, None, body)

            @block.vector
            def _(dve):
                order = Order(dve, dve_order)
                dve.wait_ge(loaded, w["n"])
                nc.vector.memset(v[:, :, :, :, :].rearrange("p a b c d -> p (a b c d)"), 1.0).then_inc(setup, 1)
                dve.wait_ge(setup, 2)

                def body(i, first):
                    if not first:
                        dve.wait_ge(added, i)
                        dve.wait_ge(trans, i)
                    layernorm_stats(nc, dve, order, x, i, stats, moments, pad).then_inc(stats_ready, 1)
                    dve.wait_ge(rstd_ready, i + 1)
                    layernorm_apply(nc, x, i, moments, rstd, h).then_inc(normed, 1)
                    for j in range(NV):
                        dve.wait_ge(v_done, i * NV + j + 1)
                        nc.vector.tensor_copy(v[:, j // 2, j % 2, :, 0:HD8],
                                              p_score[1][:, j % 2, :].rearrange("p (h d) -> p h d", d=HD8))\
                            .then_inc(v_ready, 1)

                    def shift(n):
                        dve.wait_ge(scored, i * UNITS + n + 1)
                        if n >= 2:
                            dve.wait_ge(turned, i * UNITS + n - 1)
                        s = p_score[n % 2][:, :, :].rearrange("p a (b k) -> p (a b) k", k=KEYS)
                        order.then(nc.vector.tensor_reduce(top[:, n % 2, :], s, AX.X, ALU.max))
                        nc.vector.tensor_tensor(probs[:, n % 2, :, :], s, bcast(top[:, n % 2, :], [T, 4, KEYS], 2),
                                                ALU.subtract).then_inc(shifted, 1)

                    def divide(n):
                        u, half = n // 2, n % 2
                        dve.wait_ge(weighed, i * UNITS + n + 1)
                        o = p_pv[:, 0:4 * (HD8 + 1)].rearrange("p (h d) -> p h d", d=HD8 + 1)
                        order.then(nc.vector.reciprocal(rec[:, :], o[:, :, HD8]))
                        out = heads_out[:, u, 2 * half:2 * half + 2, :].rearrange("p b (h d) -> p (b h) d", d=HD8)
                        nc.vector.tensor_tensor(out, o[:, :, 0:HD8], bcast(rec[:, :], [T, 4, HD8], 2), ALU.mult)\
                            .then_inc(divided, 1)

                    for n in range(UNITS):
                        shift(n)
                        if n >= 2:
                            divide(n - 2)
                    divide(UNITS - 2)
                    divide(UNITS - 1)
                    dve.wait_ge(out_done, i + 1)
                    out = p_misc[:, :].rearrange("p (u d) -> p u d", d=D)
                    order.then(nc.vector.tensor_tensor(update[:, :, :], out, bcast(w["bo"][:, :], [T, GROUP, D], 1), ALU.add))
                    xs = x[:, bass.ts(i, GROUP), :]
                    nc.vector.tensor_tensor(xs, xs, update[:, :, :], ALU.add).then_inc(added, 1)
                groups(dve, order, body)

            @block.gpsimd
            def _(pool):
                nc.gpsimd.memset(keys[:, :, :, :, :].rearrange("p a b c d -> p (a b c d)"), 0.0).then_inc(setup, 1)

                def body(i, first):
                    layernorm_rstd(nc, pool, stats_ready, i, const["minus_half"], moments, rstd).then_inc(rstd_ready, 1)
                groups(pool, None, body)


NEG = -1e30


def pick_first_largest(nc, order, vals, falling, best, best_rank, chosen):
    shape = list(vals.shape)
    axis = len(shape) - 1
    order.then(nc.vector.tensor_reduce(best, vals, AX.X, ALU.max))
    order.then(nc.vector.tensor_tensor(chosen, vals, bcast(best, shape, axis), ALU.is_equal))
    order.then(nc.vector.tensor_tensor(chosen, chosen, falling, ALU.mult))
    order.then(nc.vector.tensor_reduce(best_rank, chosen, AX.X, ALU.max))
    order.then(nc.vector.tensor_tensor(chosen, chosen, bcast(best_rank, shape, axis), ALU.is_equal))


def experts(nc, name, x, const, w, loaded, kind):
    gated = kind != "top2"
    n_exp = 16 if kind == "groups" else 8
    per = {"groups": 1, "top2": 2, "top1": 4}[kind]
    n_weights = {"groups": 8, "top2": 8, "top1": 7}[kind]
    shared = {"groups": 1, "top2": 0, "top1": 4}[kind]
    steps = n_weights * per + shared
    with ExitStack() as ctx:
        L = Layer(nc, ctx, name)
        stats = L.sbuf("stats", [T, GROUP, 6])
        moments = L.sbuf("moments", [T, GROUP, 2])
        pad = L.sbuf("pad", [T, 1])
        rstd = L.sbuf("rstd", [T, GROUP])
        h = L.sbuf("h", [T, GROUP, D])
        h_t = L.sbuf("h_t", [D, GROUP * T])
        r1 = L.sbuf("r1", [D, GROUP * T])
        score = L.sbuf("score", [T, GROUP, n_exp])
        left = L.sbuf("left", [T, GROUP, n_exp])
        raw = L.sbuf("raw", [T, GROUP, n_exp])
        chosen = L.sbuf("chosen", [T, GROUP, n_exp])
        picked = L.sbuf("picked", [T, GROUP, n_exp])
        best = L.sbuf("best", [T, GROUP, 4])
        best_rank = L.sbuf("best_rank", [T, GROUP, 4])
        g_score = L.sbuf("g_score", [T, GROUP, 4])
        g_chosen = L.sbuf("g_chosen", [T, GROUP, 4])
        g_picked = L.sbuf("g_picked", [T, GROUP, 4])
        total = L.sbuf("total", [T, GROUP])
        weight = L.sbuf("weight", [T, GROUP, n_exp])
        weight_t = L.sbuf("weight_t", [n_exp, GROUP * T])
        h_w = L.sbuf("h_w", [D, 2, GROUP * T])
        act_out = L.sbuf("act_out", [D, 2, GROUP * T])
        prod = L.sbuf("prod", [D, GROUP * T])
        hidden = L.sbuf("hidden", [D, 2, GROUP * T])
        out_t = L.sbuf("out_t", [D, GROUP * T])
        p_misc = L.psum("p_misc", [T, BANK])
        p_route = L.psum("p_route", [T, BANK])
        p_spread = L.psum("p_spread", [T, BANK])
        p_out = L.psum("p_out", [T, BANK])
        p_gate = [L.psum(f"p_gate{n}", [T, BANK]) for n in range(2)]
        p_up = [L.psum(f"p_up{n}", [T, BANK]) for n in range(2)] if gated else None

        stats_ready = L.sem("stats_ready")
        rstd_ready = L.sem("rstd_ready")
        normed = L.sem("normed")
        trans = L.sem("trans")
        h_t_ready = L.sem("h_t_ready")
        r1_done = L.sem("r1_done")
        r1_ready = L.sem("r1_ready")
        logits = L.sem("logits")
        route_in = L.sem("route_in")
        route_out = L.sem("route_out")
        routed = L.sem("routed")
        routed_t = L.sem("routed_t")
        weight_t_ready = L.sem("weight_t_ready")
        spread = L.sem("spread")
        spread_used = L.sem("spread_used")
        gate = L.sem("gate")
        acted = L.sem("acted")
        hidden_ready = L.sem("hidden_ready")
        down = L.sem("down")
        out_t_ready = L.sem("out_t_ready")
        out_done = L.sem("out_done")
        added = L.sem("added")
        dve_order = L.sem("dve_order")
        weighs_input = kind == "top1"

        with nc.Block() as block:
            @block.tensor
            def _(pe):
                pe.wait_ge(loaded, w["n"])

                def body(i, first):
                    pe.wait_ge(normed, i + 1)
                    if not first:
                        pe.wait_ge(added, i)
                    for u in range(GROUP):
                        last = nc.tensor.transpose(p_misc[:, u * T:(u + 1) * T], h[:, u, :], const["ident"][:, :])
                    last.then_inc(trans, 1)
                    pe.wait_ge(h_t_ready, i + 1)
                    source = h_t
                    if kind == "top2":
                        nc.tensor.matmul(p_gate[0][:, :], w["rw1"][:, :], h_t[:, :], start=True, stop=True)\
                            .then_inc(r1_done, 1)
                        pe.wait_ge(r1_ready, i + 1)
                        source = r1
                    for u in range(GROUP):
                        last = nc.tensor.matmul(p_route[:, u * n_exp:(u + 1) * n_exp], source[:, u * T:(u + 1) * T],
                                                w["router"][:, :], start=True, stop=True)
                    last.then_inc(logits, 1)
                    pe.wait_ge(routed, i + 1)
                    for u in range(GROUP):
                        last = nc.tensor.transpose(p_misc[0:n_exp, u * T:(u + 1) * T], weight[:, u, :], const["ident"][:, :])
                    last.then_inc(routed_t, 1)
                    pe.wait_ge(weight_t_ready, i + 1)

                    def spread_weight(e):
                        if e >= 1:
                            pe.wait_ge(spread_used, i * n_weights + e)
                        nc.tensor.matmul(p_spread[:, :], w["pick"][:, e, :], weight_t[:, :], start=True, stop=True)\
                            .then_inc(spread, 1)

                    def gate_step(s):
                        e = s // per
                        if e < n_weights and s % per == 0 and not weighs_input:
                            spread_weight(e)
                        if weighs_input and e < n_weights and s % per == 0:
                            if e == 0:
                                spread_weight(0)
                            if e + 1 < n_weights:
                                pe.wait_ge(spread_used, i * n_weights + e + 1)
                                spread_weight(e + 1)
                            else:
                                pe.wait_ge(spread_used, i * n_weights + e + 1)
                        if s >= 2:
                            pe.wait_ge(acted, i * steps + s - 1)
                        out = nc.tensor.matmul(p_gate[s % 2][:, :], w["wg"][:, s, :], h_t[:, :], start=True, stop=True)
                        if gated:
                            if s >= 2:
                                pe.wait_ge(hidden_ready, i * steps + s - 1)
                            source = h_w[:, e % 2, :] if weighs_input and e < n_weights else h_t[:, :]
                            out = nc.tensor.matmul(p_up[s % 2][:, :], w["wu"][:, s, :], source, start=True, stop=True)
                        out.then_inc(gate, 1)

                    def down_step(s):
                        pe.wait_ge(hidden_ready, i * steps + s + 1)
                        nc.tensor.matmul(p_out[:, :], w["wd"][:, s, :], hidden[:, s % 2, :], start=(s == 0),
                                         stop=(s == steps - 1 and kind != "top2")).then_inc(down, 1)

                    gate_step(0)
                    for s in range(steps):
                        if s + 1 < steps:
                            gate_step(s + 1)
                        down_step(s)
                    if kind == "top2":
                        nc.tensor.matmul(p_out[:, :], w["eb2"][:, :], weight_t[:, :], start=False, stop=True)\
                            .then_inc(down, 1)
                    pe.wait_ge(out_t_ready, i + 1)
                    for u in range(GROUP):
                        last = nc.tensor.transpose(p_misc[:, u * D:(u + 1) * D], out_t[:, u * T:(u + 1) * T],
                                                   const["ident"][:, :])
                    last.then_inc(out_done, 1)
                groups(pe, None, body)

            n_down = steps + (kind == "top2")

            @block.scalar
            def _(act):
                act.wait_ge(loaded, w["n"])

                def body(i, first):
                    act.wait_ge(trans, i + 1)
                    nc.scalar.copy(h_t[:, :], p_misc[:, :]).then_inc(h_t_ready, 1)
                    if kind == "top2":
                        act.wait_ge(r1_done, i + 1)
                        nc.scalar.activation(r1[:, :], p_gate[0][:, :], ACT.Silu, bias=w["rb1"][:, 0:1])\
                            .then_inc(r1_ready, 1)
                    if kind == "groups":
                        act.wait_ge(logits, i + 1)
                        nc.scalar.activation(score[:, :, :], p_route[:, 0:GROUP * n_exp], ACT.Sigmoid)\
                            .then_inc(route_out, 1)
                    else:
                        act.wait_ge(route_in, i + 1)
                        nc.scalar.activation(score[:, :, :], left[:, :, :], ACT.Exp).then_inc(route_out, 1)
                    act.wait_ge(routed_t, i + 1)
                    nc.scalar.copy(weight_t[:, :], p_misc[0:n_exp, :]).then_inc(weight_t_ready, 1)
                    for s in range(steps):
                        act.wait_ge(gate, i * steps + s + 1)
                        if s >= 2:
                            act.wait_ge(hidden_ready, i * steps + s - 1)
                        bias = {"bias": w["eb1"][:, s:s + 1]} if kind == "top2" else {}
                        nc.scalar.activation(act_out[:, s % 2, :], p_gate[s % 2][:, :], ACT.Silu, **bias)\
                            .then_inc(acted, 1)
                    act.wait_ge(down, (i + 1) * n_down)
                    nc.scalar.copy(out_t[:, :], p_out[:, :]).then_inc(out_t_ready, 1)
                groups(act, None, body)

            @block.vector
            def _(dve):
                order = Order(dve, dve_order)
                dve.wait_ge(loaded, w["n"])

                def route_groups(i):
                    falling = const["falling16"]
                    order.then(nc.vector.tensor_tensor(raw[:, :, :], score[:, :, :],
                                                       bcast(w["gate_bias"][:, :], [T, GROUP, n_exp], 1), ALU.add))
                    by_group = lambda t: t[:, :, :].rearrange("p u (g e) -> p (u g) e", e=4)
                    flat = lambda t: t[:, :, :].rearrange("p u g -> p (u g)")
                    fall4 = bcast(const["falling4"][:, :], [T, 4 * GROUP, 4], 1)
                    pick_first_largest(nc, order, by_group(raw), fall4, flat(best), flat(best_rank), by_group(chosen))
                    order.then(nc.vector.scalar_tensor_tensor(left[:, :, :], chosen[:, :, :], NEG, raw[:, :, :],
                                                              ALU.mult, ALU.add))
                    order.then(nc.vector.tensor_reduce(flat(g_score), by_group(left), AX.X, ALU.max))
                    order.then(nc.vector.tensor_tensor(flat(g_score), flat(g_score), flat(best), ALU.add))
                    for n in range(2):
                        pick_first_largest(nc, order, g_score[:, :, :], bcast(const["falling4"][:, :], [T, GROUP, 4], 1),
                                           best[:, :, 0], best_rank[:, :, 0], g_chosen[:, :, :])
                        if n == 0:
                            order.then(nc.vector.tensor_copy(g_picked[:, :, :], g_chosen[:, :, :]))
                            order.then(nc.vector.scalar_tensor_tensor(g_score[:, :, :], g_chosen[:, :, :], NEG,
                                                                      g_score[:, :, :], ALU.mult, ALU.add))
                        else:
                            order.then(nc.vector.tensor_tensor(g_picked[:, :, :], g_picked[:, :, :], g_chosen[:, :, :],
                                                               ALU.add))
                    order.then(nc.vector.tensor_scalar(g_picked[:, :, :], g_picked[:, :, :], 1.0, -NEG,
                                                       ALU.subtract, ALU.mult))
                    order.then(nc.vector.tensor_tensor(by_group(left), by_group(raw),
                                                       bcast(flat(g_picked), [T, 4 * GROUP, 4], 2), ALU.add))
                    for n in range(4):
                        pick_first_largest(nc, order, left[:, :, :], bcast(falling[:, :], [T, GROUP, n_exp], 1),
                                           best[:, :, 0], best_rank[:, :, 0], chosen[:, :, :])
                        if n == 0:
                            order.then(nc.vector.tensor_copy(picked[:, :, :], chosen[:, :, :]))
                        else:
                            order.then(nc.vector.tensor_tensor(picked[:, :, :], picked[:, :, :], chosen[:, :, :], ALU.add))
                        if n < 3:
                            order.then(nc.vector.scalar_tensor_tensor(left[:, :, :], chosen[:, :, :], 2 * NEG,
                                                                      left[:, :, :], ALU.mult, ALU.add))
                    order.then(nc.vector.tensor_tensor(weight[:, :, :], score[:, :, :], picked[:, :, :], ALU.mult))
                    order.then(nc.vector.tensor_reduce(total[:, :], weight[:, :, :], AX.X, ALU.add))
                    order.then(nc.vector.tensor_scalar(total[:, :], total[:, :], 1e-20, None, ALU.add))
                    order.then(nc.vector.reciprocal(total[:, :], total[:, :]))
                    order.then(nc.vector.tensor_scalar(total[:, :], total[:, :], 2.5, None, ALU.mult))

                def route_top(i, count):
                    seen = bcast(const["falling8"][:, :], [T, GROUP, n_exp], 1)
                    p_logit = p_route[:, 0:GROUP * n_exp].rearrange("p (u e) -> p u e", e=n_exp)
                    if kind == "top2":
                        order.then(nc.vector.tensor_tensor(raw[:, :, :], p_logit, bcast(w["rb2"][:, :], [T, GROUP, n_exp], 1),
                                                           ALU.add))
                    else:
                        order.then(nc.vector.tensor_copy(raw[:, :, :], p_logit))
                    order.then(nc.vector.tensor_reduce(best[:, :, 0], raw[:, :, :], AX.X, ALU.max))
                    nc.vector.tensor_tensor(left[:, :, :], raw[:, :, :], bcast(best[:, :, 0], [T, GROUP, n_exp], 2),
                                            ALU.subtract).then_inc(route_in, 1)
                    for n in range(count):
                        pick_first_largest(nc, order, raw[:, :, :], seen, best[:, :, 1], best_rank[:, :, 1],
                                           chosen[:, :, :])
                        if n == 0:
                            order.then(nc.vector.tensor_copy(picked[:, :, :], chosen[:, :, :]))
                            if count == 2:
                                order.then(nc.vector.scalar_tensor_tensor(raw[:, :, :], chosen[:, :, :], NEG, raw[:, :, :],
                                                                          ALU.mult, ALU.add))
                        else:
                            order.then(nc.vector.tensor_tensor(picked[:, :, :], picked[:, :, :], chosen[:, :, :], ALU.add))
                    dve.wait_ge(route_out, i + 1)
                    order.then(nc.vector.tensor_tensor(weight[:, :, :], score[:, :, :], picked[:, :, :], ALU.mult))
                    over = weight if count == 2 else score
                    order.then(nc.vector.tensor_reduce(total[:, :], over[:, :, :], AX.X, ALU.add))
                    order.then(nc.vector.reciprocal(total[:, :], total[:, :]))
                    if count == 1:
                        order.then(nc.vector.tensor_scalar(total[:, :], total[:, :], 2.0, None, ALU.mult))

                def body(i, first):
                    if not first:
                        dve.wait_ge(added, i)
                        dve.wait_ge(trans, i)
                    layernorm_stats(nc, dve, order, x, i, stats, moments, pad).then_inc(stats_ready, 1)
                    dve.wait_ge(rstd_ready, i + 1)
                    layernorm_apply(nc, x, i, moments, rstd, h).then_inc(normed, 1)
                    if kind == "groups":
                        dve.wait_ge(route_out, i + 1)
                        route_groups(i)
                    else:
                        dve.wait_ge(logits, i + 1)
                        route_top(i, 2 if kind == "top2" else 1)
                    nc.vector.tensor_tensor(weight[:, :, :], weight[:, :, :], bcast(total[:, :], [T, GROUP, n_exp], 2),
                                            ALU.mult).then_inc(routed, 1)

                    def weigh_input(e):
                        dve.wait_ge(spread, i * n_weights + e + 1)
                        if e >= 2:
                            dve.wait_ge(gate, i * steps + (e - 1) * per)
                        nc.vector.tensor_tensor(h_w[:, e % 2, :], h_t[:, :], p_spread[:, :], ALU.mult)\
                            .then_inc(spread_used, 1)

                    if weighs_input:
                        dve.wait_ge(h_t_ready, i + 1)
                        weigh_input(0)
                        weigh_input(1)
                    for s in range(steps):
                        e = s // per
                        dve.wait_ge(acted, i * steps + s + 1)
                        if s >= 2:
                            dve.wait_ge(down, i * n_down + s - 1)
                        if weighs_input:
                            nc.vector.tensor_tensor(hidden[:, s % 2, :], act_out[:, s % 2, :], p_up[s % 2][:, :], ALU.mult)\
                                .then_inc(hidden_ready, 1)
                            if s % per == per - 1 and e + 2 < n_weights:
                                weigh_input(e + 2)
                        elif e >= n_weights:
                            nc.vector.tensor_tensor(hidden[:, s % 2, :], act_out[:, s % 2, :], p_up[s % 2][:, :], ALU.mult)\
                                .then_inc(hidden_ready, 1)
                        else:
                            a = act_out[:, s % 2, :]
                            if gated:
                                order.then(nc.vector.tensor_tensor(prod[:, :], a, p_up[s % 2][:, :], ALU.mult))
                                a = prod[:, :]
                            dve.wait_ge(spread, i * n_weights + e + 1)
                            ins = nc.vector.tensor_tensor(hidden[:, s % 2, :], a, p_spread[:, :], ALU.mult)
                            ins.then_inc(hidden_ready, 1)
                            if s % per == per - 1:
                                nc.vector.memset(pad[:, :], 0.0).then_inc(spread_used, 1)
                    dve.wait_ge(out_done, i + 1)
                    xs = x[:, bass.ts(i, GROUP), :]
                    if kind != "top1":
                        order.then(nc.vector.tensor_tensor(xs, xs, h[:, :, :], ALU.add))
                    nc.vector.tensor_tensor(xs, xs, p_misc[:, :].rearrange("p (u d) -> p u d", d=D), ALU.add)\
                        .then_inc(added, 1)
                groups(dve, order, body)

            @block.gpsimd
            def _(pool):
                def body(i, first):
                    layernorm_rstd(nc, pool, stats_ready, i, const["minus_half"], moments, rstd).then_inc(rstd_ready, 1)
                groups(pool, None, body)


def attention1(nc, name, x, const, w, loaded, aps, cross):
    scale = 1.0 / 32.0 if cross else float(D) ** -0.5
    with ExitStack() as ctx:
        L = Layer(nc, ctx, name)
        stats = L.sbuf("stats", [T, GROUP, 6])
        moments = L.sbuf("moments", [T, GROUP, 2])
        pad = L.sbuf("pad", [T, 1])
        rstd = L.sbuf("rstd", [T, GROUP])
        h = L.sbuf("h", [T, GROUP, D])
        h_t = L.sbuf("h_t", [D, GROUP * T])
        q_t = L.sbuf("q_t", [D, GROUP * T])
        k_t = L.sbuf("k_t", [D, 2, GROUP * T])
        v = L.sbuf("v", [T, 2, GROUP, D])
        drop = L.sbuf("drop", [T, 2, GROUP, T])
        probs = L.sbuf("probs", [T, GROUP, T])
        probs_t = L.sbuf("probs_t", [T, GROUP * T])
        top = L.sbuf("top", [T, GROUP])
        total = L.sbuf("total", [T, GROUP])
        att = L.sbuf("att", [T, GROUP, D])
        att_t = L.sbuf("att_t", [D, GROUP * T])
        p_misc = L.psum("p_misc", [T, BANK])
        p_q = L.psum("p_q", [T, BANK])
        p_k = L.psum("p_k", [T, BANK])
        p_v = L.psum("p_v", [T, BANK])
        p_score = L.psum("p_score", [T, GROUP, T])
        p_trans = L.psum("p_trans", [T, BANK])
        p_out = L.psum("p_out", [T, GROUP, D])

        inputs_in = L.sem("inputs_in")
        stats_ready = L.sem("stats_ready")
        rstd_ready = L.sem("rstd_ready")
        normed = L.sem("normed")
        trans = L.sem("trans")
        h_t_ready = L.sem("h_t_ready")
        proj = L.sem("proj")
        q_ready = L.sem("q_ready")
        k_ready = L.sem("k_ready")
        v_ready = L.sem("v_ready")
        scored = L.sem("scored")
        shifted = L.sem("shifted")
        expd = L.sem("expd")
        summed = L.sem("summed")
        turned = L.sem("turned")
        turned_out = L.sem("turned_out")
        weighed = L.sem("weighed")
        divided = L.sem("divided")
        att_turned = L.sem("att_turned")
        att_t_ready = L.sem("att_t_ready")
        out_done = L.sem("out_done")
        added = L.sem("added")
        dve_order = L.sem("dve_order")

        with nc.Block() as block:
            if cross:
                @block.sync
                def _(sp):
                    def load_group(i, slot):
                        sp.dma_start(k_t[:, slot, :], aps["ctx_t"][:, bass.ts(i, GROUP * T)]).then_inc(inputs_in, 16)
                        sp.dma_start(v[:, slot, :, :], aps["ctx"][:, bass.ts(i, GROUP), :]).then_inc(inputs_in, 16)
                        sp.dma_start(drop[:, slot, :, :], aps["drop"][:, bass.ts(i, GROUP), :]).then_inc(inputs_in, 16)

                    def body(i, first):
                        if not first:
                            sp.wait_ge(weighed, i)
                        load_group(i, 0)
                    groups(sp, None, body)

            @block.tensor
            def _(pe):
                pe.wait_ge(loaded, w["n"])

                def body(i, first):
                    pe.wait_ge(normed, i + 1)
                    if not first:
                        pe.wait_ge(added, i)
                    for u in range(GROUP):
                        last = nc.tensor.transpose(p_misc[:, u * T:(u + 1) * T], h[:, u, :], const["ident"][:, :])
                    last.then_inc(trans, 1)
                    pe.wait_ge(h_t_ready, i + 1)
                    if cross:
                        pe.wait_ge(inputs_in, (i + 1) * 48)
                        queries = h_t
                    else:
                        nc.tensor.matmul(p_q[:, :], w["wq"][:, :], h_t[:, :], start=True, stop=True).then_inc(proj, 1)
                        nc.tensor.matmul(p_k[:, :], w["wk"][:, :], h_t[:, :], start=True, stop=True).then_inc(proj, 1)
                        for u in range(GROUP):
                            last = nc.tensor.matmul(p_v[:, u * D:(u + 1) * D], h_t[:, u * T:(u + 1) * T], w["wv"][:, :],
                                                    start=True, stop=True)
                        last.then_inc(proj, 1)
                        pe.wait_ge(q_ready, i + 1)
                        pe.wait_ge(k_ready, i + 1)
                        queries = q_t
                    for u in range(GROUP):
                        last = nc.tensor.matmul(p_score[:, u, :], queries[:, u * T:(u + 1) * T],
                                                k_t[:, 0, u * T:(u + 1) * T], start=True, stop=True)
                    last.then_inc(scored, 1)
                    pe.wait_ge(summed, i + 1)
                    for u in range(GROUP):
                        last = nc.tensor.transpose(p_trans[:, u * T:(u + 1) * T], probs[:, u, :], const["ident"][:, :])
                    last.then_inc(turned, 1)
                    pe.wait_ge(turned_out, i + 1)
                    if not cross:
                        pe.wait_ge(v_ready, i + 1)
                    for u in range(GROUP):
                        last = nc.tensor.matmul(p_out[:, u, :], probs_t[:, u * T:(u + 1) * T], v[:, 0, u, :],
                                                start=True, stop=True)
                    last.then_inc(weighed, 1)
                    if cross:
                        pe.wait_ge(divided, i + 1)
                        for u in range(GROUP):
                            last = nc.tensor.transpose(p_misc[:, u * T:(u + 1) * T], att[:, u, :], const["ident"][:, :])
                        last.then_inc(att_turned, 1)
                        pe.wait_ge(att_t_ready, i + 1)
                        for u in range(GROUP):
                            last = nc.tensor.matmul(p_misc[:, u * D:(u + 1) * D], att_t[:, u * T:(u + 1) * T],
                                                    w["wo"][:, :], start=True, stop=True)
                        last.then_inc(out_done, 1)
                groups(pe, None, body)

            @block.scalar
            def _(act):
                act.wait_ge(loaded, w["n"])

                def body(i, first):
                    act.wait_ge(trans, i + 1)
                    nc.scalar.copy(h_t[:, :], p_misc[:, :]).then_inc(h_t_ready, 1)
                    if not cross:
                        act.wait_ge(proj, 3 * i + 1)
                        nc.scalar.activation(q_t[:, :], p_q[:, :], ACT.Identity, bias=w["bq"][:, 0:1]).then_inc(q_ready, 1)
                        act.wait_ge(proj, 3 * i + 2)
                        nc.scalar.activation(k_t[:, 0, :], p_k[:, :], ACT.Identity, bias=w["bk"][:, 0:1])\
                            .then_inc(k_ready, 1)
                    act.wait_ge(shifted, i + 1)
                    nc.scalar.activation(probs[:, :, :], probs[:, :, :], ACT.Exp, scale=scale).then_inc(expd, 1)
                    act.wait_ge(turned, i + 1)
                    nc.scalar.copy(probs_t[:, :], p_trans[:, :]).then_inc(turned_out, 1)
                    if cross:
                        act.wait_ge(att_turned, i + 1)
                        nc.scalar.copy(att_t[:, :], p_misc[:, :]).then_inc(att_t_ready, 1)
                groups(act, None, body)

            @block.vector
            def _(dve):
                order = Order(dve, dve_order)
                dve.wait_ge(loaded, w["n"])

                def body(i, first):
                    if not first:
                        dve.wait_ge(added, i)
                        dve.wait_ge(trans, i)
                    layernorm_stats(nc, dve, order, x, i, stats, moments, pad).then_inc(stats_ready, 1)
                    dve.wait_ge(rstd_ready, i + 1)
                    layernorm_apply(nc, x, i, moments, rstd, h).then_inc(normed, 1)
                    if not cross:
                        dve.wait_ge(proj, 3 * i + 3)
                        nc.vector.tensor_tensor(v[:, 0, :, :], p_v[:, :].rearrange("p (u d) -> p u d", d=D),
                                                bcast(w["bv"][:, :], [T, GROUP, D], 1), ALU.add).then_inc(v_ready, 1)
                    dve.wait_ge(scored, i + 1)
                    order.then(nc.vector.tensor_reduce(top[:, :], p_score[:, :, :], AX.X, ALU.max))
                    nc.vector.tensor_tensor(probs[:, :, :], p_score[:, :, :], bcast(top[:, :], [T, GROUP, T], 2),
                                            ALU.subtract).then_inc(shifted, 1)
                    dve.wait_ge(expd, i + 1)
                    if cross:
                        order.then(nc.vector.tensor_reduce(total[:, :], probs[:, :, :], AX.X, ALU.add))
                        dve.wait_ge(inputs_in, (i + 1) * 48)
                        nc.vector.tensor_tensor(probs[:, :, :], probs[:, :, :], drop[:, 0, :, :], ALU.mult)\
                            .then_inc(summed, 1)
                    else:
                        nc.vector.tensor_reduce(total[:, :], probs[:, :, :], AX.X, ALU.add).then_inc(summed, 1)
                        dve.wait_ge(summed, i + 1)
                    order.then(nc.vector.reciprocal(total[:, :], total[:, :]))
                    dve.wait_ge(weighed, i + 1)
                    ins = nc.vector.tensor_tensor(att[:, :, :], p_out[:, :, :], bcast(total[:, :], [T, GROUP, D], 2),
                                                  ALU.mult)
                    xs = x[:, bass.ts(i, GROUP), :]
                    if cross:
                        ins.then_inc(divided, 1)
                        dve.wait_ge(out_done, i + 1)
                        order.then(nc.vector.tensor_tensor(att[:, :, :], p_misc[:, :].rearrange("p (u d) -> p u d", d=D),
                                                           bcast(w["bo"][:, :], [T, GROUP, D], 1), ALU.add))
                    else:
                        order.then(ins)
                    nc.vector.tensor_tensor(xs, xs, att[:, :, :], ALU.add).then_inc(added, 1)
                groups(dve, order, body)

            @block.gpsimd
            def _(pool):
                def body(i, first):
                    layernorm_rstd(nc, pool, stats_ready, i, const["minus_half"], moments, rstd).then_inc(rstd_ready, 1)
                groups(pool, None, body)


def state_space(nc, name, x, const, w, loaded):
    NH, P8, NC = 32, 8, 4
    QH = 8
    NU = GROUP * NH // QH
    TAPS = 4
    with ExitStack() as ctx:
        L = Layer(nc, ctx, name)
        stats = L.sbuf("stats", [T, GROUP, 6])
        moments = L.sbuf("moments", [T, GROUP, 2])
        pad = L.sbuf("pad", [T, 1])
        rstd = L.sbuf("rstd", [T, GROUP])
        h = L.sbuf("h", [T, GROUP, D])
        h_t = L.sbuf("h_t", [D, GROUP * T])
        padded = L.sbuf("padded", [T, NC, GROUP, T + TAPS - 1])
        conv = L.sbuf("conv", [T, NC, GROUP, T])
        gate = L.sbuf("gate", [T, 2, GROUP * T])
        dt = L.sbuf("dt", [T, GROUP, NH])
        da = L.sbuf("da", [T, GROUP, NH])
        neg_a = L.sbuf("neg_a", [T, NH])
        cum = L.sbuf("cum", [T, GROUP, NH])
        cum_t = L.sbuf("cum_t", [NH, GROUP * T])
        cb = L.sbuf("cb", [T, GROUP, T])
        xs_t = L.sbuf("xs_t", [T, GROUP, 2 * T])
        ident_b = L.sbuf("ident_b", [T, T], BF16)
        future_b = L.sbuf("future_b", [T, T], BF16)
        xdt_own = L.sbuf("xdt_own", [T, 2, NH * T])
        decay = L.sbuf("decay", [T, 2, QH, T])
        mix = L.sbuf("mix", [T, 2, QH, T])
        y = L.sbuf("y", [T, 2, GROUP * T])
        sq = L.sbuf("sq", [T, 2, GROUP * T])
        out_w = L.sbuf("out_w", [T, 2, D])
        ones = L.sbuf("ones", [T, 2])
        ms = L.sbuf("ms", [T, GROUP])
        rms = L.sbuf("rms", [T, GROUP])
        o = L.sbuf("o", [T, GROUP, D])
        p_a = L.psum("p_a", [T, BANK])
        p_b = L.psum("p_b", [T, BANK])
        p_seg = [L.psum(f"p_seg{n}", [T, 2, BANK]) for n in range(2)]
        p_y = L.psum("p_y", [T, 2, BANK])
        stats_ready = L.sem("stats_ready")
        rstd_ready = L.sem("rstd_ready")
        normed = L.sem("normed")
        trans = L.sem("trans")
        h_t_ready = L.sem("h_t_ready")
        conv_in = L.sem("conv_in")
        padded_ready = L.sem("padded_ready")
        convolved = L.sem("convolved")
        conv_ready = L.sem("conv_ready")
        z_done = L.sem("z_done")
        gate_ready = L.sem("gate_ready")
        dt_done = L.sem("dt_done")
        dt_in = L.sem("dt_in")
        dt_sig = L.sem("dt_sig")
        da_ready = L.sem("da_ready")
        cum_done = L.sem("cum_done")
        cum_ready = L.sem("cum_ready")
        cum_t_ready = L.sem("cum_t_ready")
        cb_done = L.sem("cb_done")
        cb_ready = L.sem("cb_ready")
        x_turned = L.sem("x_turned")
        xs_ready = L.sem("xs_ready")
        own_ready = L.sem("own_ready")
        seg_done = L.sem("seg_done")
        seg_ready = L.sem("seg_ready")
        decay_ready = L.sem("decay_ready")
        mix_ready = L.sem("mix_ready")
        mixed = L.sem("mixed")
        y_ready = L.sem("y_ready")
        sq_ready = L.sem("sq_ready")
        ms_done = L.sem("ms_done")
        ms_ready = L.sem("ms_ready")
        rms_ready = L.sem("rms_ready")
        out_done = L.sem("out_done")
        added = L.sem("added")
        dve_order = L.sem("dve_order")
        setup = L.sem("setup")

        with nc.Block() as block:
            @block.tensor
            def _(pe):
                pe.wait_ge(loaded, w["n"])
                pe.wait_ge(setup, 4)

                def body(i, first):
                    pe.wait_ge(normed, i + 1)
                    if not first:
                        pe.wait_ge(added, i)
                    for u in range(GROUP):
                        last = nc.tensor.transpose(p_a[:, u * T:(u + 1) * T], h[:, u, :], const["ident"][:, :])
                    last.then_inc(trans, 1)
                    pe.wait_ge(h_t_ready, i + 1)
                    for c in range(NC):
                        nc.tensor.matmul(p_seg[c // 2][:, c % 2, :], w["conv_in"][:, c * T:(c + 1) * T], h_t[:, :],
                                         start=True, stop=True).then_inc(conv_in, 1)
                    for b in range(2):
                        nc.tensor.matmul(p_y[:, b, :], w["z_in"][:, b * T:(b + 1) * T], h_t[:, :], start=True, stop=True)\
                            .then_inc(z_done, 1)
                    for u in range(GROUP):
                        last = nc.tensor.matmul(p_a[:, u * NH:(u + 1) * NH], h_t[:, u * T:(u + 1) * T], w["dt_in"][:, :],
                                                start=True, stop=True)
                    last.then_inc(dt_done, 1)
                    pe.wait_ge(da_ready, i + 1)
                    nc.tensor.matmul(p_a[:, 0:GROUP * NH], w["upto"][:, :], da[:, :, :], start=True, stop=True)
                    for u in range(GROUP):
                        last = nc.tensor.matmul(p_b[0:NH, u * T:(u + 1) * T], da[:, u, :], w["upto"][:, :],
                                                start=True, stop=True)
                    last.then_inc(cum_done, 1)
                    pe.wait_ge(cum_ready, i + 1)
                    pe.wait_ge(conv_ready, NC * (i + 1))
                    for u in range(GROUP):
                        last = nc.tensor.matmul(p_a[:, u * T:(u + 1) * T], conv[:, 2, u, :], conv[:, 3, u, :],
                                                start=True, stop=True)
                    last.then_inc(cb_done, 1)
                    for b in range(2):
                        for u in range(GROUP):
                            last = nc.tensor.transpose(p_seg[1][:, b, u * T:(u + 1) * T], conv[:, b, u, :],
                                                       const["ident"][:, :])
                    last.then_inc(x_turned, 1)
                    pe.wait_ge(cum_t_ready, i + 1)
                    pe.wait_ge(gate_ready, 2 * (i + 1))

                    def segments(n):
                        u, part = n // 4, n % 4
                        if n == 1:
                            pe.wait_ge(xs_ready, i + 1)
                        if n >= 2:
                            pe.wait_ge(seg_ready, i * NU + n - 1)
                        for half in range(2):
                            nc.tensor.matmul(p_seg[n % 2][:, half, :], ident_b[:, :], bcast(future_b[:, :], [T, 4, T], 1),
                                             start=True, stop=False)
                            for k in range(4):
                                last = nc.tensor.matmul(p_seg[n % 2][:, half, k * T:(k + 1) * T],
                                                        w["pick"][:, part * QH + 4 * half + k, :],
                                                        cum_t[:, u * T:(u + 1) * T], start=False, stop=(k == 3))
                        last.then_inc(seg_done, 1)

                    def mixing(n):
                        u, part = n // 4, n % 4
                        pe.wait_ge(mix_ready, i * NU + n + 1)
                        if part == 0:
                            pe.wait_ge(own_ready, i * GROUP + u + 1)
                        for k in range(QH):
                            head = part * QH + k
                            last = nc.tensor.matmul(p_y[:, part // 2, u * T:(u + 1) * T],
                                                    xdt_own[:, u % 2, head * T:(head + 1) * T], mix[:, n % 2, k, :],
                                                    start=(head % 16 == 0), stop=(head % 16 == 15))
                        last.then_inc(mixed, 1)

                    segments(0)
                    for n in range(NU):
                        if n + 1 < NU:
                            segments(n + 1)
                        mixing(n)
                    pe.wait_ge(y_ready, 2 * (i + 1))
                    pe.wait_ge(sq_ready, 2 * (i + 1))
                    for u in range(GROUP):
                        for b in range(2):
                            last = nc.tensor.matmul(p_b[:, 2 * u:2 * u + 2], sq[:, b, u * T:(u + 1) * T], ones[:, :],
                                                    start=(b == 0), stop=(b == 1))
                    last.then_inc(ms_done, 1)
                    pe.wait_ge(cb_ready, i + 1)
                    for u in range(GROUP):
                        for b in range(2):
                            last = nc.tensor.matmul(p_a[:, u * D:(u + 1) * D], y[:, b, u * T:(u + 1) * T], out_w[:, b, :],
                                                    start=(b == 0), stop=(b == 1))
                    last.then_inc(out_done, 1)
                groups(pe, None, body)

            @block.scalar
            def _(act):
                act.wait_ge(loaded, w["n"])
                nc.scalar.activation(neg_a[:, :], w["a_log"][:, :], ACT.Exp).then_inc(setup, 1)
                act.wait_ge(setup, 4)

                def body(i, first):
                    act.wait_ge(trans, i + 1)
                    nc.scalar.copy(h_t[:, :], p_a[:, :]).then_inc(h_t_ready, 1)
                    for c in range(NC):
                        act.wait_ge(conv_in, NC * i + c + 1)
                        nc.scalar.copy(padded[:, c, :, TAPS - 1:], p_seg[c // 2][:, c % 2, :].rearrange("p (u t) -> p u t", t=T))\
                            .then_inc(padded_ready, 1)
                    for b in range(2):
                        act.wait_ge(z_done, 2 * i + b + 1)
                        nc.scalar.activation(gate[:, b, :], p_y[:, b, :], ACT.Silu).then_inc(gate_ready, 1)
                    for c in range(NC):
                        act.wait_ge(convolved, NC * i + c + 1)
                        nc.scalar.activation(conv[:, c, :, :], conv[:, c, :, :], ACT.Silu).then_inc(conv_ready, 1)
                    act.wait_ge(dt_in, i + 1)
                    nc.scalar.activation(dt[:, :, :], dt[:, :, :], ACT.Sigmoid).then_inc(dt_sig, 1)
                    act.wait_ge(cum_done, i + 1)
                    nc.scalar.copy(cum_t[:, :], p_b[0:NH, :]).then_inc(cum_t_ready, 1)
                    for n in range(NU):
                        act.wait_ge(seg_ready, i * NU + n + 1)
                        nc.scalar.activation(decay[:, n % 2, :, :], decay[:, n % 2, :, :], ACT.Exp).then_inc(decay_ready, 1)
                    for b in range(2):
                        act.wait_ge(y_ready, 2 * i + b + 1)
                        nc.scalar.activation(sq[:, b, :], y[:, b, :], ACT.Square).then_inc(sq_ready, 1)
                groups(act, None, body)

            @block.vector
            def _(dve):
                order = Order(dve, dve_order)
                dve.wait_ge(loaded, w["n"])
                nc.vector.memset(ones[:, :], 1.0)
                nc.vector.tensor_copy(ident_b[:, :], const["ident"][:, :])
                nc.vector.tensor_scalar(future_b[:, :], w["upto"][:, :], 1.0, -NEG, ALU.subtract, ALU.mult)
                nc.vector.memset(padded[:, :, :, :].rearrange("p c u t -> p (c u t)"), 0.0)
                nc.vector.tensor_tensor(out_w[:, :, :], w["out_w"][:, :, :], bcast(w["norm_w"][:, :], [T, 2, D], 2), ALU.mult)\
                    .then_inc(setup, 1)
                dve.wait_ge(setup, 3)
                nc.vector.tensor_scalar(neg_a[:, :], neg_a[:, :], -1.0, None, ALU.mult).then_inc(setup, 1)
                dve.wait_ge(setup, 4)

                def body(i, first):
                    if not first:
                        dve.wait_ge(added, i)
                        dve.wait_ge(trans, i)
                    layernorm_stats(nc, dve, order, x, i, stats, moments, pad).then_inc(stats_ready, 1)
                    dve.wait_ge(rstd_ready, 2 * i + 1)
                    layernorm_apply(nc, x, i, moments, rstd, h).then_inc(normed, 1)
                    for c in range(NC):
                        dve.wait_ge(padded_ready, NC * i + c + 1)
                        order.then(nc.vector.tensor_scalar(conv[:, c, :, :], padded[:, c, :, 0:T], w["conv_w"][:, c, 0:1],
                                                           w["conv_b"][:, c:c + 1], ALU.mult, ALU.add))
                        for k in range(1, TAPS):
                            ins = nc.vector.scalar_tensor_tensor(conv[:, c, :, :], padded[:, c, :, k:k + T],
                                                                 w["conv_w"][:, c, k:k + 1], conv[:, c, :, :],
                                                                 ALU.mult, ALU.add)
                            if k < TAPS - 1:
                                order.then(ins)
                        ins.then_inc(convolved, 1)
                    dve.wait_ge(dt_done, i + 1)
                    nc.vector.tensor_tensor(dt[:, :, :], p_a[:, 0:GROUP * NH].rearrange("p (u h) -> p u h", h=NH),
                                            bcast(w["dt_bias"][:, :], [T, GROUP, NH], 1), ALU.add).then_inc(dt_in, 1)
                    dve.wait_ge(dt_sig, i + 1)
                    order.then(nc.vector.tensor_scalar(dt[:, :, :], dt[:, :, :], 0.1 - 0.001, 0.001, ALU.mult, ALU.add))
                    nc.vector.tensor_tensor(da[:, :, :], dt[:, :, :], bcast(neg_a[:, :], [T, GROUP, NH], 1), ALU.mult)\
                        .then_inc(da_ready, 1)
                    dve.wait_ge(cum_done, i + 1)
                    nc.vector.tensor_copy(cum[:, :, :], p_a[:, 0:GROUP * NH]).then_inc(cum_ready, 1)
                    dve.wait_ge(cb_done, i + 1)
                    nc.vector.tensor_copy(cb[:, :, :], p_a[:, :]).then_inc(cb_ready, 1)
                    dve.wait_ge(x_turned, i + 1)
                    if not first:
                        dve.wait_ge(own_ready, GROUP * i)
                    for b in range(2):
                        last = nc.vector.tensor_copy(xs_t[:, :, b * T:(b + 1) * T],
                                                     p_seg[1][:, b, :].rearrange("p (u c) -> p u c", u=GROUP))
                    last.then_inc(xs_ready, 1)
                    dve.wait_ge(cum_ready, i + 1)
                    dve.wait_ge(cb_ready, i + 1)

                    def subtract(n):
                        u, part = n // 4, n % 4
                        dve.wait_ge(seg_done, i * NU + n + 1)
                        nc.vector.tensor_tensor(decay[:, n % 2, :, :], p_seg[n % 2][:, :, :].rearrange("p b (k t) -> p (b k) t", t=T),
                                                bcast(cum[:, u, part * QH:(part + 1) * QH], [T, QH, T], 2), ALU.subtract)\
                            .then_inc(seg_ready, 1)

                    def combine(n):
                        u = n // 4
                        dve.wait_ge(decay_ready, i * NU + n + 1)
                        if n >= 2:
                            dve.wait_ge(mixed, i * NU + n - 1)
                        nc.vector.tensor_tensor(mix[:, n % 2, :, :], decay[:, n % 2, :, :],
                                                bcast(cb[:, u, :], [T, QH, T], 1), ALU.mult).then_inc(mix_ready, 1)

                    subtract(0)
                    for n in range(NU):
                        if n + 1 < NU:
                            if n >= 1:
                                dve.wait_ge(mix_ready, i * NU + n)
                            subtract(n + 1)
                        combine(n)
                    dve.wait_ge(mixed, (i + 1) * NU)
                    for b in range(2):
                        order.then(nc.vector.scalar_tensor_tensor(y[:, b, :], conv[:, b, :, :].rearrange("p u t -> p (u t)"),
                                                                  w["d_skip"][:, b:b + 1], p_y[:, b, :], ALU.mult, ALU.add))
                        nc.vector.tensor_tensor(y[:, b, :], y[:, b, :], gate[:, b, :], ALU.mult).then_inc(y_ready, 1)
                    dve.wait_ge(ms_done, i + 1)
                    nc.vector.tensor_scalar(ms[:, :], p_b[:, 0:2 * GROUP].rearrange("p (u two) -> p u two", two=2)[:, :, 0],
                                            1.0 / 256.0, 1e-5, ALU.mult, ALU.add).then_inc(ms_ready, 1)
                    dve.wait_ge(rms_ready, i + 1)
                    dve.wait_ge(out_done, i + 1)
                    order.then(nc.vector.tensor_tensor(o[:, :, :], p_a[:, :].rearrange("p (u d) -> p u d", d=D),
                                                       bcast(rms[:, :], [T, GROUP, D], 2), ALU.mult))
                    layernorm_stats(nc, dve, order, o, 0, stats, moments, pad).then_inc(stats_ready, 1)
                    dve.wait_ge(rstd_ready, 2 * i + 2)
                    order.then(layernorm_apply(nc, o, 0, moments, rstd, o))
                    order.then(nc.vector.tensor_tensor(o[:, :, :], o[:, :, :], bcast(w["ln_w"][:, :], [T, GROUP, D], 1), ALU.mult))
                    order.then(nc.vector.tensor_tensor(o[:, :, :], o[:, :, :], bcast(w["ln_b"][:, :], [T, GROUP, D], 1), ALU.add))
                    order.then(nc.vector.tensor_tensor(o[:, :, :], o[:, :, :], h[:, :, :], ALU.add))
                    xs = x[:, bass.ts(i, GROUP), :]
                    nc.vector.tensor_tensor(xs, xs, o[:, :, :], ALU.add).then_inc(added, 1)
                groups(dve, order, body)

            @block.gpsimd
            def _(pool):
                nc.gpsimd.memset(xdt_own[:, :, :].rearrange("p a b -> p (a b)"), 0.0).then_inc(setup, 1)
                pool.wait_ge(setup, 4)

                def body(i, first):
                    layernorm_rstd(nc, pool, stats_ready, 2 * i, const["minus_half"], moments, rstd).then_inc(rstd_ready, 1)
                    pool.wait_ge(xs_ready, i + 1)
                    for u in range(GROUP):
                        if not first:
                            pool.wait_ge(mixed, i * NU + 4 * (u - 1))
                        elif u >= 2:
                            pool.wait_ge(mixed, 4 * (u - 1))
                        for b in range(2):
                            dst = xdt_own[:, u % 2, b * 16 * T:(b + 1) * 16 * T]
                            dst = bass.AP(dst.tensor, dst.offset, [dst.ap[0], [T + P8, 16], [1, P8]])
                            last = nc.gpsimd.tensor_tensor(
                                dst, xs_t[:, u, b * T:(b + 1) * T].rearrange("p (h d) -> p h d", d=P8),
                                bcast(dt[:, u, 16 * b:16 * b + 16], [T, 16, P8], 2), ALU.mult)
                        last.then_inc(own_ready, 1)
                    pool.wait_ge(ms_ready, i + 1)
                    nc.gpsimd.tensor_tensor(rms[:, :], ms[:, :], const["minus_half"][:, 0:GROUP], ALU.pow).then_inc(rms_ready, 1)
                    layernorm_rstd(nc, pool, stats_ready, 2 * i + 1, const["minus_half"], moments, rstd).then_inc(rstd_ready, 1)
                groups(pool, None, body)


def sparse_attention(nc, name, x, const, w, loaded):
    S = 32
    ROWS = GROUP * HEADS
    LI = 16
    scale = float(HD) ** -0.5
    with ExitStack() as ctx:
        L = Layer(nc, ctx, name)
        stats = L.sbuf("stats", [T, GROUP, 6])
        moments = L.sbuf("moments", [T, GROUP, 2])
        pad = L.sbuf("pad", [T, 1])
        rstd = L.sbuf("rstd", [T, GROUP])
        h = L.sbuf("h", [T, GROUP, D])
        h_t = L.sbuf("h_t", [D, GROUP * T])
        q_t = L.sbuf("q_t", [D, GROUP * T])
        scaled_bq = L.sbuf("scaled_bq", [D, 1])
        k_t = L.sbuf("k_t", [D, S])
        k_rep = L.sbuf("k_rep", [D, 4, S])
        keys = L.sbuf("keys", [D, HEADS, S])
        vals = L.sbuf("vals", [T, D])
        vals_own = L.sbuf("vals_own", [T, 4, D])
        z = L.sbuf("z", [T, ROWS, S])
        srt = [L.sbuf(f"srt{n}", [T, ROWS, S]) for n in range(2)]
        starts = L.sbuf("starts", [T, ROWS, S])
        tau = L.sbuf("tau", [T, ROWS])
        a_t = L.sbuf("a_t", [T, 4, GROUP * T])
        o_t = L.sbuf("o_t", [D, GROUP * T])
        apart = L.sbuf("apart", [D, 2, LI, T])
        out = L.sbuf("out", [T, GROUP, D])
        p_misc = L.psum("p_misc", [T, BANK])
        p_q = L.psum("p_q", [T, BANK])
        p_out = L.psum("p_out", [T, GROUP, D])
        p_s = [L.psum(f"p_s{n}", [T, BANK]) for n in range(4)]
        stats_ready = L.sem("stats_ready")
        rstd_ready = L.sem("rstd_ready")
        normed = L.sem("normed")
        trans = L.sem("trans")
        h_t_ready = L.sem("h_t_ready")
        proj = L.sem("proj")
        q_ready = L.sem("q_ready")
        scored = L.sem("scored")
        z_ready = L.sem("z_ready")
        shifted = L.sem("shifted")
        clipped = L.sem("clipped")
        turned = L.sem("turned")
        turned_out = L.sem("turned_out")
        weighed = L.sem("weighed")
        o_t_ready = L.sem("o_t_ready")
        apart_ready = L.sem("apart_ready")
        out_done = L.sem("out_done")
        added = L.sem("added")
        dve_order = L.sem("dve_order")
        kv_done = L.sem("kv_done")
        kv_ready = L.sem("kv_ready")

        def blocks(t, size):
            return t[:, :, :].rearrange("p r s -> p (r s)").rearrange("p (b e) -> p b e", e=size)

        with nc.Block() as block:
            @block.tensor
            def _(pe):
                pe.wait_ge(loaded, w["n"])
                nc.tensor.matmul(p_misc[:, 0:S], w["wk"][:, :], w["key_t"][:, :], start=True, stop=True)\
                    .then_inc(kv_done, 1)
                pe.wait_ge(kv_ready, 2)
                nc.tensor.matmul(p_misc[:, 0:D], k_rep[:, :, :], w["wv"][:, :], start=True, stop=True).then_inc(kv_done, 1)
                pe.wait_ge(kv_ready, 3)

                def body(i, first):
                    pe.wait_ge(normed, i + 1)
                    if not first:
                        pe.wait_ge(added, i)
                    for u in range(GROUP):
                        last = nc.tensor.transpose(p_misc[:, u * T:(u + 1) * T], h[:, u, :], const["ident"][:, :])
                    last.then_inc(trans, 1)
                    pe.wait_ge(h_t_ready, i + 1)
                    nc.tensor.matmul(p_q[:, :], w["wq"][:, :], h_t[:, :], start=True, stop=True).then_inc(proj, 1)
                    pe.wait_ge(q_ready, i + 1)
                    for u in range(GROUP):
                        nc.tensor.matmul(p_s[u][:, :], q_t[:, u * T:(u + 1) * T], keys[:, :, :], start=True, stop=True)\
                            .then_inc(scored, 1)
                    pe.wait_ge(clipped, i + 1)
                    for b in range(4):
                        for u in range(GROUP):
                            row = u * HEADS + 4 * b
                            last = nc.tensor.transpose(p_s[b][:, u * T:(u + 1) * T], z[:, row:row + 4, :],
                                                       const["ident"][:, :])
                        last.then_inc(turned, 1)
                    for b in range(4):
                        pe.wait_ge(turned_out, 4 * i + b + 1)
                        last = nc.tensor.matmul(p_q[:, :], vals_own[:, b, :], a_t[:, b, :], start=(b == 0), stop=(b == 3))
                    last.then_inc(weighed, 1)
                    for u in range(GROUP):
                        pe.wait_ge(apart_ready, GROUP * i + u + 1)
                        for li in range(LI):
                            last = nc.tensor.matmul(p_out[:, u, :], apart[:, u % 2, li, :], w["wo"][:, li, :],
                                                    start=(li == 0), stop=(li == LI - 1))
                        last.then_inc(out_done, 1)
                groups(pe, None, body)

            @block.scalar
            def _(act):
                act.wait_ge(kv_ready, 3)

                def body(i, first):
                    act.wait_ge(trans, i + 1)
                    nc.scalar.copy(h_t[:, :], p_misc[:, :]).then_inc(h_t_ready, 1)
                    act.wait_ge(proj, i + 1)
                    nc.scalar.activation(q_t[:, :], p_q[:, :], ACT.Identity, bias=scaled_bq[:, 0:1], scale=scale)\
                        .then_inc(q_ready, 1)
                    for u in range(GROUP):
                        act.wait_ge(scored, GROUP * i + u + 1)
                        nc.scalar.copy(z[:, u * HEADS:(u + 1) * HEADS, :], p_s[u][:, :]).then_inc(z_ready, 1)
                    act.wait_ge(shifted, i + 1)
                    nc.scalar.activation(z[:, :, :], z[:, :, :], ACT.Relu).then_inc(clipped, 1)
                    for b in range(4):
                        act.wait_ge(turned, 4 * i + b + 1)
                        nc.scalar.copy(a_t[:, b, :], p_s[b][:, :]).then_inc(turned_out, 1)
                    act.wait_ge(weighed, i + 1)
                    nc.scalar.copy(o_t[:, :], p_q[:, :]).then_inc(o_t_ready, 1)
                groups(act, None, body)

            @block.vector
            def _(dve):
                order = Order(dve, dve_order)
                dve.wait_ge(loaded, w["n"])
                nc.vector.tensor_scalar(scaled_bq[:, :], w["bq"][:, :], scale, None, ALU.mult)
                nc.vector.memset(starts[:, :, :], 1.0).then_inc(kv_ready, 1)
                dve.wait_ge(kv_ready, 1)
                nc.vector.memset(starts[:, :, 0:1], 0.0)
                dve.wait_ge(kv_done, 1)
                order.then(nc.vector.tensor_scalar(k_t[:, :], p_misc[:, 0:S], w["bk"][:, 0:1], None, ALU.add))
                nc.vector.tensor_copy(k_rep[:, :, :], bcast(k_t[:, :], [D, 4, S], 1)).then_inc(kv_ready, 1)
                nc.vector.tensor_tensor(keys[:, :, :], bcast(k_t[:, :], [D, HEADS, S], 1),
                                        bcast(const["head_of"][:, :], [D, HEADS, S], 2), ALU.mult)
                dve.wait_ge(kv_done, 2)
                order.then(nc.vector.tensor_tensor(vals[:, :], p_misc[:, 0:D], w["bv"][:, :], ALU.add))
                nc.vector.tensor_tensor(vals_own[:, :, :], bcast(vals[:, :], [T, 4, D], 1), w["own"][:, :, :], ALU.mult)\
                    .then_inc(kv_ready, 1)
                setup_steps = order.n
                order.n = 0

                def body(i, first):
                    order.base = order.base + setup_steps
                    if not first:
                        dve.wait_ge(added, i)
                        dve.wait_ge(trans, i)
                    layernorm_stats(nc, dve, order, x, i, stats, moments, pad).then_inc(stats_ready, 1)
                    dve.wait_ge(rstd_ready, i + 1)
                    layernorm_apply(nc, x, i, moments, rstd, h).then_inc(normed, 1)
                    dve.wait_ge(z_ready, GROUP * (i + 1))
                    src, dst, at = z, srt[0], 0
                    size = 2
                    while size <= S:
                        step = size // 2
                        while step:
                            if 2 * step == size:
                                a, b = blocks(src, size)[:, :, 0:step], blocks(src, size)[:, :, size - 1:step - 1:-1]
                                da, db = blocks(dst, size)[:, :, 0:step], blocks(dst, size)[:, :, size - 1:step - 1:-1]
                            else:
                                a, b = blocks(src, 2 * step)[:, :, 0:step], blocks(src, 2 * step)[:, :, step:2 * step]
                                da, db = blocks(dst, 2 * step)[:, :, 0:step], blocks(dst, 2 * step)[:, :, step:2 * step]
                            nc.vector.tensor_tensor(da, a, b, ALU.max)
                            order.then(nc.vector.tensor_tensor(db, a, b, ALU.min))
                            at = 1 - at
                            src, dst = dst, srt[at]
                            step //= 2
                        size *= 2
                    flat = lambda t: t[:, :, :].rearrange("p r s -> p (r s)")
                    order.then(nc.vector.tensor_tensor_scan(flat(dst), flat(starts), flat(src), 0.0, ALU.mult, ALU.add))
                    order.then(nc.vector.scalar_tensor_tensor(src[:, :, :], dst[:, :, :], 1.0,
                                                              bcast(w["inv"][:, :], [T, ROWS, S], 1),
                                                              ALU.subtract, ALU.mult))
                    order.then(nc.vector.tensor_reduce(tau[:, :], src[:, :, :], AX.X, ALU.max))
                    nc.vector.tensor_tensor(z[:, :, :], z[:, :, :], bcast(tau[:, :], [T, ROWS, S], 2), ALU.subtract)\
                        .then_inc(shifted, 1)
                    dve.wait_ge(out_done, GROUP * (i + 1))
                    order.then(nc.vector.tensor_tensor(out[:, :, :], p_out[:, :, :], bcast(w["bo"][:, :], [T, GROUP, D], 1),
                                                       ALU.add))
                    xs = x[:, bass.ts(i, GROUP), :]
                    nc.vector.tensor_tensor(xs, xs, out[:, :, :], ALU.add).then_inc(added, 1)
                groups(dve, order, body)

            @block.gpsimd
            def _(pool):
                def body(i, first):
                    layernorm_rstd(nc, pool, stats_ready, i, const["minus_half"], moments, rstd).then_inc(rstd_ready, 1)
                    pool.wait_ge(o_t_ready, i + 1)
                    for u in range(GROUP):
                        if not first:
                            pool.wait_ge(out_done, GROUP * i + u - 1)
                        elif u >= 2:
                            pool.wait_ge(out_done, u - 1)
                        nc.gpsimd.tensor_tensor(
                            apart[:, u % 2, :, :].rearrange("p l (h o) -> p l h o", h=HEADS),
                            o_t[:, u * T:(u + 1) * T].rearrange("p (o l) -> p l o", l=LI).unsqueeze(2)
                            .broadcast_to([D, LI, HEADS, T // LI]),
                            const["head_of"][:, :].unsqueeze(1).unsqueeze(3).broadcast_to([D, LI, HEADS, T // LI]),
                            ALU.mult).then_inc(apart_ready, 1)
                groups(pool, None, body)


def quantized(nc, name, x, const, w, loaded):
    MAGIC = 12582912.0
    with ExitStack() as ctx:
        L = Layer(nc, ctx, name)
        stats = L.sbuf("stats", [T, GROUP, 6])
        moments = L.sbuf("moments", [T, GROUP, 2])
        pad = L.sbuf("pad", [T, 1])
        rstd = L.sbuf("rstd", [T, GROUP])
        h = L.sbuf("h", [T, GROUP, D])
        mag = L.sbuf("mag", [T, GROUP, D])
        q = L.sbuf("q", [T, GROUP, D])
        q_t = L.sbuf("q_t", [D, GROUP * T], BF16)
        wq = L.sbuf("wq", [D, D], BF16)
        amax = L.sbuf("amax", [T, GROUP])
        scale = L.sbuf("scale", [T, GROUP])
        out = L.sbuf("out", [T, GROUP, D])
        p_t = L.psum("p_t", [T, BANK])
        p_out = L.psum("p_out", [T, GROUP, D])
        stats_ready = L.sem("stats_ready")
        rstd_ready = L.sem("rstd_ready")
        normed = L.sem("normed")
        mag_ready = L.sem("mag_ready")
        rounded = L.sem("rounded")
        trans = L.sem("trans")
        q_t_ready = L.sem("q_t_ready")
        out_done = L.sem("out_done")
        added = L.sem("added")
        dve_order = L.sem("dve_order")
        setup = L.sem("setup")
        with nc.Block() as block:
            @block.tensor
            def _(pe):
                pe.wait_ge(setup, 1)

                def body(i, first):
                    pe.wait_ge(rounded, i + 1)
                    for u in range(GROUP):
                        last = nc.tensor.transpose(p_t[:, u * T:(u + 1) * T], q[:, u, :], const["ident"][:, :])
                    last.then_inc(trans, 1)
                    pe.wait_ge(q_t_ready, i + 1)
                    if not first:
                        pe.wait_ge(added, i)
                    for u in range(GROUP):
                        last = nc.tensor.matmul(p_out[:, u, :], q_t[:, u * T:(u + 1) * T], wq[:, :], start=True, stop=True)
                    last.then_inc(out_done, 1)
                groups(pe, None, body)

            @block.scalar
            def _(act):
                def body(i, first):
                    act.wait_ge(normed, i + 1)
                    nc.scalar.activation(mag[:, :, :], h[:, :, :], ACT.Abs).then_inc(mag_ready, 1)
                    act.wait_ge(trans, i + 1)
                    nc.scalar.copy(q_t[:, :], p_t[:, :]).then_inc(q_t_ready, 1)
                groups(act, None, body)

            @block.vector
            def _(dve):
                order = Order(dve, dve_order)
                dve.wait_ge(loaded, w["n"])
                nc.vector.tensor_copy(wq[:, :], w["wq"][:, :]).then_inc(setup, 1)

                def body(i, first):
                    if not first:
                        dve.wait_ge(added, i)
                        dve.wait_ge(trans, i)
                    layernorm_stats(nc, dve, order, x, i, stats, moments, pad).then_inc(stats_ready, 1)
                    dve.wait_ge(rstd_ready, i + 1)
                    layernorm_apply(nc, x, i, moments, rstd, h).then_inc(normed, 1)
                    dve.wait_ge(mag_ready, i + 1)
                    order.then(nc.vector.tensor_reduce(amax[:, :], mag[:, :, :], AX.X, ALU.max))
                    order.then(nc.vector.tensor_scalar(amax[:, :], amax[:, :], 1e-6, None, ALU.max))
                    order.then(nc.vector.tensor_scalar(scale[:, :], amax[:, :], 1.0 / 127.0, None, ALU.mult))
                    order.then(nc.vector.reciprocal(amax[:, :], scale[:, :]))
                    order.then(nc.vector.tensor_tensor(q[:, :, :], h[:, :, :], bcast(amax[:, :], [T, GROUP, D], 2),
                                                       ALU.mult))
                    order.then(nc.vector.tensor_scalar(q[:, :, :], q[:, :, :], MAGIC, MAGIC, ALU.add, ALU.subtract))
                    nc.vector.tensor_scalar(q[:, :, :], q[:, :, :], 127.0, -128.0, ALU.min, ALU.max).then_inc(rounded, 1)
                    dve.wait_ge(out_done, i + 1)
                    order.then(nc.vector.tensor_tensor(out[:, :, :], p_out[:, :, :], bcast(scale[:, :], [T, GROUP, D], 2),
                                                       ALU.mult))
                    order.then(nc.vector.tensor_tensor(out[:, :, :], out[:, :, :], bcast(w["scale"][:, :], [T, GROUP, D], 1),
                                                       ALU.mult))
                    order.then(nc.vector.tensor_tensor(out[:, :, :], out[:, :, :], bcast(w["bias"][:, :], [T, GROUP, D], 1),
                                                       ALU.add))
                    xs = x[:, bass.ts(i, GROUP), :]
                    nc.vector.tensor_tensor(xs, xs, out[:, :, :], ALU.add).then_inc(added, 1)
                groups(dve, order, body)

            @block.gpsimd
            def _(pool):
                def body(i, first):
                    layernorm_rstd(nc, pool, stats_ready, i, const["minus_half"], moments, rstd).then_inc(rstd_ready, 1)
                groups(pool, None, body)


def layer3(nc, x, const, w, loaded, aps):
    attention16(nc, "l3", x, {**const, "causal": w["causal"]}, w, loaded, latent=True, causal=True)


def layer4(nc, x, const, w, loaded, aps):
    attention16(nc, "l4", x, const, w, loaded, ctx_t=aps["ctx_t"], key_mask=True, qkv_bias=True, out_bias=True)


def layer7(nc, x, const, w, loaded, aps):
    with ExitStack() as ctx:
        rel = ctx.enter_context(nc.sbuf_tensor("l7_rel", [T, HEADS, T], F32))
        table = aps["rel_table"]
        rel_in = ctx.enter_context(nc.semaphore("rel_in"))
        with nc.Block() as block:
            @block.sync
            def _(sp):
                for head in range(HEADS):
                    src = bass.AP(table.tensor, head * 511 + 128, [[1, T], [1, T]])
                    sp.dma_start(rel[:, head, :], src).then_inc(rel_in, 16)
                sp.wait_ge(rel_in, 16 * HEADS)
        attention16(nc, "l7", x, {**const, "flip": w["flip"]}, {**w, "rel": rel}, loaded, ctx_t=aps["ctx_t"],
                    rel_bias=True, out_bias=True)


def layer2(nc, x, const, w, loaded, aps):
    experts(nc, "l2", x, const, w, loaded, "groups")


def layer5(nc, x, const, w, loaded, aps):
    experts(nc, "l5", x, const, w, loaded, "top2")


def layer8(nc, x, const, w, loaded, aps):
    experts(nc, "l8", x, const, w, loaded, "top1")


def layer1(nc, x, const, w, loaded, aps):
    attention8(nc, "l1", x, const, w, loaded, aps["ctx_t"])


def layer6(nc, x, const, w, loaded, aps):
    attention1(nc, "l6", x, const, w, loaded, aps, cross=False)


def layer10(nc, x, const, w, loaded, aps):
    attention1(nc, "l10", x, const, w, loaded, aps, cross=True)


def layer11(nc, x, const, w, loaded, aps):
    quantized(nc, "l11", x, const, w, loaded)


def layer0(nc, x, const, w, loaded, aps):
    state_space(nc, "l0", x, const, w, loaded)


def layer9(nc, x, const, w, loaded, aps):
    sparse_attention(nc, "l9", x, const, w, loaded)


LAYERS = {0: layer0, 9: layer9, 1: layer1, 6: layer6, 10: layer10, 11: layer11, 2: layer2, 3: layer3, 4: layer4, 5: layer5, 7: layer7, 8: layer8}


TABLE = [
    (-1, "ident", "ident", 0, False),
    (-1, "head_of", "head_of", 0, False),
    (-1, "minus_half", "minus_half", 0, False),
    (-1, "falling4", "falling4", T, True),
    (-1, "falling8", "falling8", T, True),
    (-1, "falling16", "falling16", T, True),
    (0, "conv_in", "mam_conv_in", 0, False),
    (0, "z_in", "mam_z_in", 0, False),
    (0, "dt_in", "mam_dt_in", 0, False),
    (0, "conv_w", "mam_conv_w", 0, False),
    (0, "conv_b", "mam_conv_b", 0, False),
    (0, "dt_bias", "mam_dt_bias", T, True),
    (0, "a_log", "mam_a_log", T, True),
    (0, "d_skip", "mam_d_skip", 0, False),
    (0, "norm_w", "mam_norm_w", 0, False),
    (0, "out_w", "mam_out_w", 0, False),
    (0, "ln_w", "mam_ln_w", T, True),
    (0, "ln_b", "mam_ln_b", T, True),
    (0, "upto", "mam_upto", 0, False),
    (0, "pick", "mam_pick", 0, False),
    (9, "key_t", "l3a_key", 0, False),
    (9, "wq", "L3_attn_Wq", 0, False),
    (9, "wk", "L3_attn_Wk", 0, False),
    (9, "wv", "L3_attn_Wv", 0, False),
    (9, "wo", "l3a_wo", 0, False),
    (9, "bq", "l3a_bq", 0, False),
    (9, "bk", "l3a_bk", 0, False),
    (9, "bv", "l3a_bv", T, True),
    (9, "bo", "l3a_bo", T, True),
    (9, "own", "l3a_own", 0, False),
    (9, "inv", "l3a_inv", T, True),
    (1, "wq", "L0_xattn_Wq1", 0, False),
    (1, "wk1", "L0_xattn_Wk1", 0, False),
    (1, "wk2", "L0_xattn_Wk2", 0, False),
    (1, "wv1", "L0_xattn_Wv1", 0, False),
    (1, "wv2", "L0_xattn_Wv2", 0, False),
    (1, "wo", "l0x_wo", 0, False),
    (1, "bo", "l0x_bo", T, True),
    (2, "router", "l0f_router", 0, False),
    (2, "gate_bias", "l0f_bias", T, True),
    (2, "pick", "l0f_pick", 0, False),
    (2, "wg", "l0f_wg", 0, False),
    (2, "wu", "l0f_wu", 0, False),
    (2, "wd", "l0f_wd", 0, False),
    (5, "rw1", "L1_ffn_rw1", 0, False),
    (5, "rb1", "l1f_rb1", 0, False),
    (5, "router", "L1_ffn_rw2", 0, False),
    (5, "rb2", "l1f_rb2", T, True),
    (5, "pick", "pick8", 0, False),
    (5, "wg", "l1f_w1", 0, False),
    (5, "eb1", "l1f_eb1", 0, False),
    (5, "wd", "l1f_w2", 0, False),
    (5, "eb2", "L1_ffn_eb2", 0, False),
    (6, "wq", "l2a_wq", 0, False),
    (6, "wk", "l2a_wk", 0, False),
    (6, "wv", "l2a_wv", 0, False),
    (6, "bq", "l2a_bq", 0, False),
    (6, "bk", "l2a_bk", 0, False),
    (6, "bv", "l2a_bv", T, True),
    (10, "wo", "l3x_wo", 0, False),
    (10, "bo", "l3x_bo", T, True),
    (11, "wq", "l3f_wq", 0, False),
    (11, "scale", "l3f_scale", T, True),
    (11, "bias", "l3f_bias", T, True),
    (8, "router", "L2_ffn_Wr", 0, False),
    (8, "pick", "pick8", 0, False),
    (8, "wg", "l2f_wg", 0, False),
    (8, "wu", "l2f_wu", 0, False),
    (8, "wd", "l2f_wd", 0, False),
    (3, "causal", "causal", 0, False),
    (3, "down", "L1_attn_Wc_down", 0, False),
    (3, "wq", "L1_attn_Wq_up", 0, False),
    (3, "wk", "l1_wk", 0, False),
    (3, "wv", "l1_wv", 0, False),
    (3, "wo", "L1_attn_Wc_proj", 0, False),
    (4, "wq", "l1x_wq", 0, False),
    (4, "wk", "l1x_wk", 0, False),
    (4, "wv", "l1x_wv", 0, False),
    (4, "wo", "l1x_wo", 0, False),
    (4, "bq", "l1x_bq", 0, False),
    (4, "bk", "l1x_bk", 0, False),
    (4, "bv", "l1x_bv", T, True),
    (4, "bo", "l1x_bo", T, True),
    (4, "mask", "mask", 0, False),
    (7, "wq", "l2x_wq", 0, False),
    (7, "wk", "l2x_wk", 0, False),
    (7, "wv", "l2x_wv", 0, False),
    (7, "wo", "l2x_wo", 0, False),
    (7, "bo", "l2x_bo", T, True),
    (7, "flip", "flip", 0, False),
]


def lay_out(a):
    c = np.ascontiguousarray
    a = {k: np.asarray(v) for k, v in a.items()}
    o = {"x": c(a["x"].transpose(1, 0, 2)), "ctx_t": c(a["ctx_1024"].transpose(2, 0, 1).reshape(D, NB * T))}
    o["ident"] = np.eye(T, dtype=np.float32)
    o["minus_half"] = np.full((T, 8), -0.5, np.float32)
    o["flip"] = c(np.eye(T, dtype=np.float32)[::-1])
    o["causal"] = np.where(np.tril(np.ones((T, T), bool)), 0.0, -1e30).astype(np.float32)
    o["head_of"] = c(np.repeat(np.eye(HEADS, dtype=np.float32), HD, axis=0))
    for n in ("L1_attn_Wc_down", "L1_attn_Wq_up", "L1_attn_Wc_proj"):
        o[n] = a[n]
    o["l1_wk"] = np.tile(a["L1_attn_Wkv_up"][:, :HD], (1, HEADS))
    o["l1_wv"] = np.tile(a["L1_attn_Wkv_up"][:, HD:], (1, HEADS))
    for n in "qkvo":
        o[f"l1x_w{n}"] = c(a[f"L1_xattn_W{n}"].T)
    o["l1x_bq"], o["l1x_bk"] = a["L1_xattn_bq"].reshape(D, 1), a["L1_xattn_bk"].reshape(D, 1)
    o["l1x_bv"], o["l1x_bo"] = a["L1_xattn_bv"].reshape(1, D), a["L1_xattn_bo"].reshape(1, D)
    o["mask"] = a["mask_BxS2_ik0"].reshape(1, NB * T)
    for n in "qkv":
        o[f"l2x_w{n}"] = c(a[f"L2_xattn_w{n}"].T)
    o["l2x_wo"], o["l2x_bo"] = c(a["L2_xattn_fc_w"].T), a["L2_xattn_fc_b"].reshape(1, D)
    o["rel_table"] = c(a["L2_xattn_rel_table"].T)
    for n in (4, 8, 16):
        o[f"falling{n}"] = np.arange(n, 0, -1, dtype=np.float32).reshape(1, n)
    o["pick8"] = np.repeat(np.eye(8, dtype=np.float32)[:, :, None], T, axis=2)
    o["l0f_pick"] = c(np.repeat(np.eye(16, dtype=np.float32), 64, axis=1).reshape(16, 8, T))
    o["l0f_router"] = c(a["L0_ffn_gate_w"].T)
    o["l0f_bias"] = a["L0_ffn_gate_bias"].reshape(1, 16)
    for n, s in (("g", "Ws_g"), ("u", "Ws_u")):
        both = np.concatenate([a[f"L0_ffn_W{n}"].reshape(8, T, D), a[f"L0_ffn_{s}"][None]])
        o[f"l0f_w{n}"] = c(both.transpose(2, 0, 1))
    both = np.concatenate([a["L0_ffn_Wd"].transpose(0, 2, 1).reshape(8, T, D), a["L0_ffn_Ws_d"].T[None]])
    o["l0f_wd"] = c(both.transpose(1, 0, 2))
    for n in ("L1_ffn_rw1", "L1_ffn_rw2", "L1_ffn_eb2", "L2_ffn_Wr"):
        o[n] = a[n]
    o["l1f_rb1"], o["l1f_rb2"] = a["L1_ffn_rb1"].reshape(D, 1), a["L1_ffn_rb2"].reshape(1, 8)
    o["l1f_w1"] = c(a["L1_ffn_ew1"].transpose(1, 0, 2).reshape(D, 16, T))
    o["l1f_eb1"] = c(a["L1_ffn_eb1"].reshape(16, T).T)
    o["l1f_w2"] = c(a["L1_ffn_ew2"].reshape(16, T, D).transpose(1, 0, 2))
    for n in "gu":
        both = np.concatenate([a[f"L2_ffn_W{n}"], a[f"L2_ffn_W{n}_s"][None]])
        o[f"l2f_w{n}"] = c(both.transpose(1, 0, 2).reshape(D, 32, T))
    both = np.concatenate([a["L2_ffn_Wd"], a["L2_ffn_Wd_s"][None]])
    o["l2f_wd"] = c(both.reshape(32, T, D).transpose(1, 0, 2))
    for n in ("Wq1", "Wk1", "Wk2", "Wv1", "Wv2"):
        o[f"L0_xattn_{n}"] = a[f"L0_xattn_{n}"]
    o["l0x_wo"], o["l0x_bo"] = c(a["L0_xattn_Wo"].reshape(4, T, D).transpose(1, 0, 2)), a["L0_xattn_bo"].reshape(1, D)
    for n in "qkv":
        o[f"l2a_w{n}"] = c(a[f"L2_attn_w{n}"].T)
    o["l2a_bq"], o["l2a_bk"] = a["L2_attn_bq"].reshape(D, 1), a["L2_attn_bk"].reshape(D, 1)
    o["l2a_bv"] = a["L2_attn_bv"].reshape(1, D)
    o["l3x_wo"], o["l3x_bo"] = c(a["L3_xattn_Wout"].T), a["L3_xattn_bout"].reshape(1, D)
    o["ctx"] = c(a["ctx_1024"].transpose(1, 0, 2))
    o["drop"] = c(a["mask_BxSxS2_fk0"].transpose(1, 0, 2))
    o["l3f_wq"] = c(a["L3_ffn_weight_q"].T.astype(np.int32))
    o["l3f_scale"], o["l3f_bias"] = a["L3_ffn_weight_scale"].reshape(1, D), a["L3_ffn_bias"].reshape(1, D)
    w_in = a["L0_attn_in_proj_w"].T
    o["mam_z_in"], o["mam_conv_in"], o["mam_dt_in"] = c(w_in[:, :256]), c(w_in[:, 256:768]), c(w_in[:, 768:])
    o["mam_conv_w"] = c(a["L0_attn_conv_w"].reshape(4, T, 4).transpose(1, 0, 2))
    o["mam_conv_b"] = c(a["L0_attn_conv_b"].reshape(4, T).T)
    o["mam_dt_bias"], o["mam_a_log"] = a["L0_attn_dt_bias"].reshape(1, 32), a["L0_attn_A_log"].reshape(1, 32)
    o["mam_d_skip"] = c(np.repeat(a["L0_attn_D_skip"], 8).reshape(2, T).T)
    o["mam_norm_w"] = c(a["L0_attn_norm_w"].reshape(2, T).T)
    o["mam_out_w"] = c(a["L0_attn_out_proj_w"].T.reshape(2, T, D).transpose(1, 0, 2))
    o["mam_ln_w"], o["mam_ln_b"] = a["L0_attn_ln_w"].reshape(1, D), a["L0_attn_ln_b"].reshape(1, D)
    o["mam_upto"] = np.triu(np.ones((T, T), np.float32))
    o["mam_pick"] = np.repeat(np.eye(32, dtype=np.float32)[:, :, None], T, axis=2)
    o["l3a_key"] = c(a["L3_attn_key_param"][0].T)
    for n in "qkv":
        o[f"L3_attn_W{n}"] = a[f"L3_attn_W{n}"]
    o["l3a_wo"] = c(np.tile(a["L3_attn_Wo"].reshape(16, HD, D).transpose(1, 0, 2), (HEADS, 1, 1)))
    o["l3a_bq"], o["l3a_bk"] = a["L3_attn_bq"].reshape(D, 1), a["L3_attn_bk"].reshape(D, 1)
    o["l3a_bv"], o["l3a_bo"] = a["L3_attn_bv"].reshape(1, D), a["L3_attn_bo"].reshape(1, D)
    head = np.arange(T)[:, None, None] // 32 + 4 * np.arange(4)[None, :, None]
    o["l3a_own"] = (head == np.arange(D)[None, None, :] // HD).astype(np.float32)
    o["l3a_inv"] = (1.0 / np.arange(1, 33)).astype(np.float32).reshape(1, 32)
    return o


def load(nc, aps, table, ctx, layers, x=None):
    tiles, loaded, counts = {}, {}, {}
    jobs = []
    for layer, key, name, parts, wide in table:
        if layer not in layers:
            continue
        ap = aps[name]
        dt = ap.dtype
        shape = [parts if wide else ap.shape[0]] + list(ap.shape[1:])
        t = ctx.enter_context(nc.sbuf_tensor(f"w{layer}_{key}", shape, dt))
        tiles.setdefault(layer, {})[key] = t
        counts[layer] = counts.get(layer, 0) + 16
        jobs.append((layer, t, ap, wide))
    for layer in counts:
        loaded[layer] = ctx.enter_context(nc.semaphore(f"loaded{layer}"))
        tiles[layer]["n"] = counts[layer]
    with nc.Block() as block:
        @block.sync
        def _(sp):
            if x is not None:
                sp.dma_start(x[:, :, :], aps["x"]).then_inc(loaded[-1], 16)
            for layer, t, ap, wide in jobs:
                src = ap
                if wide:
                    src = ap.partition_broadcast(T)
                    src = src.rearrange("p o d -> p (o d)") if len(src.shape) == 3 else src
                sp.dma_start(t[tuple(slice(None) for _ in t.shape)], src).then_inc(loaded[layer], 16)
            if x is not None:
                sp.wait_ge(loaded[-1], counts[-1] + 16)
    return tiles, loaded


ACTS = ((0, 1, 2), (3, 4, 5), (6, 7, 8), (9, 10, 11))


def build(nc, aps, phases=tuple(range(12))):
    with ExitStack() as ctx:
        x = ctx.enter_context(nc.sbuf_tensor("x_res", [T, NB, D], F32))
        tiles, _ = load(nc, aps, TABLE, ctx, (-1,), x)
        const = tiles[-1]
        for act in ACTS:
            act = [p for p in act if p in phases]
            if act:
                with ExitStack() as act_ctx:
                    tiles, loaded = load(nc, aps, TABLE, act_ctx, act)
                    for p in act:
                        LAYERS[p](nc, x, const, tiles[p], loaded[p], aps)
        done = ctx.enter_context(nc.semaphore("done"))
        with nc.Block() as block:
            @block.sync
            def _(sp):
                sp.dma_start(aps["out"], x[:, :, :]).then_inc(done, 16)
                sp.wait_ge(done, 16)


def kernel(**inputs):
    import concourse.bacc as bacc
    from concourse.bass_utils import run_bass_kernel_spmd

    arrays = lay_out(inputs)
    used = {row[2] for row in TABLE} | {"x", "ctx_t", "ctx", "drop", "rel_table"}
    nc = bacc.Bacc("TRN2", target_bir_lowering=False, num_devices=1)
    ins, aps = {}, {}
    for name in sorted(used):
        array = np.ascontiguousarray(arrays[name])
        ins[f"in_{name}"] = array
        aps[name] = nc.dram_tensor(f"in_{name}", array.shape, mybir.dt.from_np(array.dtype), kind="ExternalInput").ap()
    aps["out"] = nc.dram_tensor("out", (T, NB, D), F32, kind="ExternalOutput").ap()
    build(nc, aps)
    result = run_bass_kernel_spmd(nc, [ins], core_ids=[0])
    return np.ascontiguousarray(result.results[0]["out"].transpose(1, 0, 2))
```

```python
import concourse.bass as bass
import concourse.mybir as mybir
import numpy as np
from contextlib import ExitStack

F32 = mybir.dt.float32
BF16 = mybir.dt.bfloat16
ALU = mybir.AluOpType
ACT = mybir.ActivationFunctionType
AX = mybir.AxisListType

NB = 32
T = 128
D = 128
GROUP = 4
NG = NB // GROUP
BANK = 512
LN_EPS = 1e-5
MASKED = -1e20


class Layer:

    def __init__(self, nc, ctx, name):
        self.nc, self.ctx, self.name, self.sems = nc, ctx, name, []
        ctx.callback(self.close)

    def close(self):
        self.nc.clear_and_free_semaphores(self.sems)
        self.nc.all_engine_barrier()

    def sbuf(self, name, shape, dtype=F32):
        return self.ctx.enter_context(self.nc.sbuf_tensor(f"{self.name}_{name}", shape, dtype))

    def psum(self, name, shape, dtype=F32):
        return self.ctx.enter_context(self.nc.psum_tensor(f"{self.name}_{name}", shape, dtype))

    def sem(self, name):
        handle = self.nc.alloc_semaphore(f"{self.name}_{name}")
        self.sems.append(handle)
        return handle


class Order:

    def __init__(self, eng, sem):
        self.eng, self.sem, self.n, self.base = eng, sem, 0, 0

    def then(self, ins):
        self.n += 1
        ins.then_inc(self.sem, 1)
        self.eng.wait_ge(self.sem, self.base + self.n)


def groups(eng, order, body, n=NG):
    body(0, True)
    if order is not None:
        per, order.n = order.n, 0
    with eng.Fori(1, n) as i:
        if order is not None:
            order.base = i * per
            order.n = 0
        body(i, False)


def pipelined(eng, order, start, body, per=None):
    start()
    before = order.n if order is not None else 0
    body(0, 0, False)
    if order is not None:
        base = order.n
        per = base - before if per is None else per
    with eng.Fori(0, NG // 2 - 1) as k:
        if order is not None:
            order.base, order.n = base + k * (2 * per), 0
        body(k * 2 + 1, 1, False)
        body(k * 2 + 2, 0, False)
        assert order is None or order.n == 2 * per
    if order is not None:
        order.base, order.n = base + (NG // 2 - 1) * 2 * per, 0
    body(NG - 1, 1, True)


def split_high(nc, src, high, parts):
    nc.scalar.copy(high[:, :], src[0:96, :])
    return nc.scalar.copy(parts[0:32, :], src[0:32, :])


def split_rest(nc, order, src, high, rest, middle, parts):
    order.then(nc.vector.tensor_tensor(rest[:, :], src[0:96, :], high[:, :], ALU.subtract))
    nc.vector.tensor_copy(parts[32:64, :], rest[32:64, :])
    order.then(nc.vector.tensor_copy(middle[64:96, :], rest[64:96, :]))
    return nc.vector.tensor_tensor(parts[64:96, :], rest[64:96, :], middle[64:96, :], ALU.subtract)


def bcast(ap, shape, axis):
    return ap.unsqueeze(axis).broadcast_to(shape)


def layernorm_stats(nc, dve, order, x, i, stats, moments, pad, count=GROUP):
    for u in range(count):
        last = nc.vector.bn_stats(stats[:, u, :], x[:, i * count + u, :])
    order.then(last)
    nc.vector.memset(pad[:, :], 0.0)
    for u in range(count):
        last = nc.vector.bn_aggr(moments[:, u, :], stats[:, u, :])
    order.then(last)
    return nc.vector.tensor_scalar(moments[:, :, 1], moments[:, :, 1], LN_EPS, None, ALU.add)


def layernorm_rstd(nc, pool, stats_ready, i, minus_half, moments, rstd):
    pool.wait_ge(stats_ready, i + 1)
    return nc.gpsimd.tensor_tensor(rstd[:, :], moments[:, :, 1], minus_half[:, 0:moments.shape[1]], ALU.pow)


def layernorm_apply(nc, x, i, moments, rstd, h, count=GROUP):
    for u in range(count):
        last = nc.vector.tensor_scalar(h[:, u, :], x[:, i * count + u, :], moments[:, u, 0:1], rstd[:, u:u + 1],
                                       ALU.subtract, ALU.mult)
    return last
HEADS = 16
HD = D // HEADS
HALF = HEADS // 2
UNITS = 2 * GROUP


def attention16(nc, name, x, const, w, loaded, ctx_t=None, latent=False, causal=False, key_mask=None,
                rel_bias=False, qkv_bias=False, out_bias=False):
    scale = float(HD) ** -0.5
    with ExitStack() as ctx:
        L = Layer(nc, ctx, name)
        stats = L.sbuf("stats", [T, GROUP, 6])
        moments = L.sbuf("moments", [T, GROUP, 2])
        pad = L.sbuf("pad", [T, 1])
        rstd = L.sbuf("rstd", [T, GROUP])
        h = L.sbuf("h", [T, GROUP, D])
        h_t = L.sbuf("h_t", [D, GROUP * T])
        lat_t = L.sbuf("lat_t", [64, GROUP * T])
        q_t = L.sbuf("q_t", [D, 2, GROUP * T])
        k_t = L.sbuf("k_t", [D, 2, GROUP * T])
        c_t = L.sbuf("c_t", [D, GROUP * T])
        v = L.sbuf("v", [T, 2 * GROUP, HEADS, HD + 1])
        spread = L.sbuf("spread", [D, 2, HEADS, T])
        probs = L.sbuf("probs", [T, 2, HALF, T])
        probs_t = L.sbuf("probs_t", [T, 2, HALF, T])
        top = L.sbuf("top", [T, 2, HALF])
        rec = L.sbuf("rec", [T, HALF])
        heads_out = L.sbuf("heads_out", [T, 2 * GROUP, D])
        heads_t = L.sbuf("heads_t", [D, GROUP * T])
        update = L.sbuf("update", [T, GROUP, D])
        p_score = [L.psum(f"p_score{n}", [T, 2, 4, T]) for n in range(2)]
        p_trans = L.psum("p_trans", [T, 2, 4, T])
        p_pv = L.psum("p_pv", [T, BANK])
        p_misc = L.psum("p_misc", [T, BANK])

        ctx_in = L.sem("ctx_in")
        stats_ready = L.sem("stats_ready")
        rstd_ready = L.sem("rstd_ready")
        normed = L.sem("normed")
        trans = L.sem("trans")
        h_t_ready = L.sem("h_t_ready")
        lat_done = L.sem("lat_done")
        lat_ready = L.sem("lat_ready")
        proj = L.sem("proj")
        q_ready = L.sem("q_ready")
        k_ready = L.sem("k_ready")
        v_ready = L.sem("v_ready")
        spread_ready = L.sem("spread_ready")
        scored = L.sem("scored")
        shifted = L.sem("shifted")
        expd = L.sem("expd")
        turned = L.sem("turned")
        turned_out = L.sem("turned_out")
        weighed = L.sem("weighed")
        divided = L.sem("divided")
        out_t = L.sem("out_t")
        out_t_ready = L.sem("out_t_ready")
        out_done = L.sem("out_done")
        added = L.sem("added")
        biased = L.sem("biased")
        dve_order = L.sem("dve_order")
        setup = L.sem("setup")
        flipped = L.sem("flipped")
        scaled_bq = L.sbuf("scaled_bq", [D, 1])
        if rel_bias:
            bias = L.sbuf("bias", [T, HEADS, T])
        if causal:
            causal_b = L.sbuf("causal_b", [T, T], BF16)
            ident_b = L.sbuf("ident_b", [T, T], BF16)
        if key_mask is not None:
            mask_f = L.sbuf("mask_f", [1, 2, GROUP * T], BF16)
            ones_b = L.sbuf("ones_b", [1, T], BF16)

        masks = causal or key_mask is not None
        started = lambda i: not (isinstance(i, int) and i == 0)
        if latent:
            TURN_H, LATENT, QUERIES, KEYS, VALUES, TURN_OUT, PROJECT = 0, 2, 3, 4, 5, 6, 7
        else:
            TURN_H, LATENT, QUERIES, KEYS, VALUES, TURN_OUT, PROJECT = 1, None, 2, 3, 4, 5, 6

        with nc.Block() as block:
            if ctx_t is not None:
                @block.sync
                def _(sp):
                    def body(i, first):
                        if not first:
                            sp.wait_ge(proj, 3 * i)
                        sp.dma_start(c_t[:, :], ctx_t[:, bass.ts(i, GROUP * T)]).then_inc(ctx_in, 16)
                    groups(sp, None, body)

            @block.tensor
            def _(pe):
                pe.wait_ge(loaded, w["n"])
                if rel_bias:
                    for n in range(4):
                        last = nc.tensor.matmul(p_score[n // 2][:, n % 2, :, :], const["flip"][:, :],
                                                w["rel"][:, 4 * n:4 * n + 4, :], start=True, stop=True)
                    last.then_inc(flipped, 1)
                pe.wait_ge(setup, 1)
                source_kv, kd = (c_t, D) if ctx_t is not None else (lat_t, 64) if latent else (h_t, D)
                source_q = lat_t if latent else h_t

                def turn_h(j):
                    pe.wait_ge(normed, j + 1)
                    for u in range(GROUP):
                        last = nc.tensor.transpose(p_misc[:, u * T:(u + 1) * T], h[:, u, :], const["ident"][:, :])
                    last.then_inc(trans, 1)

                def latent_down(j):
                    pe.wait_ge(h_t_ready, j + 1)
                    nc.tensor.matmul(p_misc[0:64, :], w["down"][:, :], h_t[:, :], start=True, stop=True)\
                        .then_inc(lat_done, 1)

                def queries(j):
                    pe.wait_ge(lat_ready if latent else h_t_ready, j + 1)
                    nc.tensor.matmul(p_misc[:, :], w["wq"][0:kd, :], source_q[0:kd, :], start=True, stop=True)\
                        .then_inc(proj, 1)

                def keys(j):
                    pe.wait_ge(q_ready, j + 1)
                    if ctx_t is not None:
                        pe.wait_ge(ctx_in, (j + 1) * 16)
                    nc.tensor.matmul(p_misc[:, :], w["wk"][0:kd, :], source_kv[0:kd, :], start=True, stop=True)\
                        .then_inc(proj, 1)

                def value_rows(j):
                    pe.wait_ge(k_ready, j + 1)
                    for u in range(GROUP):
                        last = nc.tensor.matmul(p_misc[:, u * T:(u + 1) * T], source_kv[0:kd, u * T:(u + 1) * T],
                                                w["wv"][0:kd, :], start=True, stop=True)
                    last.then_inc(proj, 1)

                def turn_out(j, q):
                    pe.wait_ge(divided, (j + 1) * UNITS)
                    for u in range(GROUP):
                        last = nc.tensor.transpose(p_misc[:, u * T:(u + 1) * T], heads_out[:, q * GROUP + u, :],
                                                   const["ident"][:, :])
                    last.then_inc(out_t, 1)

                def project(j):
                    pe.wait_ge(out_t_ready, j + 1)
                    for u in range(GROUP):
                        last = nc.tensor.matmul(p_misc[:, u * D:(u + 1) * D], heads_t[:, u * T:(u + 1) * T],
                                                w["wo"][:, :], start=True, stop=True)
                    last.then_inc(out_done, 1)

                def scores(i, n, q):
                    u, half, g = n // 2, n % 2, i * UNITS + n
                    pe.wait_ge(spread_ready, i * GROUP + u + 1)
                    if not isinstance(g, int) or g >= 2:
                        pe.wait_ge(shifted, g - 1)
                    for j in range(2):
                        out = p_score[n % 2][:, j, :, :]
                        if causal:
                            nc.tensor.matmul(out, ident_b[:, :], bcast(causal_b[:, :], [T, 4, T], 1), start=True, stop=False)
                        if key_mask is not None:
                            nc.tensor.matmul(out, ones_b[0:1, :], bcast(mask_f[0:1, q, u * T:(u + 1) * T], [1, 4, T], 1),
                                             start=True, stop=False)
                        head = half * HALF + 4 * j
                        last = nc.tensor.matmul(out, q_t[:, q, u * T:(u + 1) * T], spread[:, u % 2, head:head + 4, :],
                                                start=not masks, stop=True)
                    last.then_inc(scored, 1)

                def transposes(i, n):
                    g = i * UNITS + n
                    pe.wait_ge(expd, g + 1)
                    if not isinstance(g, int) or g >= 1:
                        pe.wait_ge(turned_out, g)
                    for k in range(HALF):
                        last = nc.tensor.transpose(p_trans[:, k // 4, k % 4, :], probs[:, n % 2, k, :], const["ident"][:, :])
                    last.then_inc(turned, 1)

                def values(i, n, q):
                    u, half, g = n // 2, n % 2, i * UNITS + n
                    pe.wait_ge(turned_out, g + 1)
                    if not isinstance(g, int) or g >= 1:
                        pe.wait_ge(divided, g)
                    for k in range(HALF):
                        last = nc.tensor.matmul(p_pv[:, k * (HD + 1):(k + 1) * (HD + 1)], probs_t[:, n % 2, k, :],
                                                v[:, q * GROUP + u, half * HALF + k, :], start=True, stop=True)
                    last.then_inc(weighed, 1)

                def start():
                    turn_h(0)
                    if latent:
                        latent_down(0)
                    queries(0)
                    keys(0)
                    value_rows(0)
                    pe.wait_ge(v_ready, 1)
                    scores(0, 0, 0)

                def body(i, p, last_group):
                    for n in range(UNITS):
                        if n + 1 < UNITS:
                            scores(i, n + 1, p)
                        elif not last_group:
                            pe.wait_ge(v_ready, i + 2)
                            scores(i + 1, 0, 1 - p)
                        if n >= 1:
                            values(i, n - 1, p)
                        elif started(i):
                            values(i - 1, UNITS - 1, 1 - p)
                        transposes(i, n)
                        if not last_group:
                            if n == TURN_H:
                                pe.wait_ge(shifted, i * UNITS + 1)
                                turn_h(i + 1)
                            if n == LATENT and latent:
                                latent_down(i + 1)
                            if n == QUERIES:
                                queries(i + 1)
                            if n == KEYS:
                                keys(i + 1)
                            if n == VALUES:
                                value_rows(i + 1)
                        if n == TURN_OUT and started(i):
                            if not last_group:
                                pe.wait_ge(v_ready, i + 2)
                            else:
                                pe.wait_ge(added, i - 1)
                            turn_out(i - 1, 1 - p)
                        if n == PROJECT and started(i):
                            project(i - 1)
                pipelined(pe, None, start, body)
                values(NG - 1, UNITS - 1, 1)
                pe.wait_ge(added, NG - 1)
                turn_out(NG - 1, 1)
                project(NG - 1)

            @block.scalar
            def _(act):
                act.wait_ge(loaded, w["n"])
                act.wait_ge(setup, 1)

                def copy_h(j):
                    act.wait_ge(trans, j + 1)
                    nc.scalar.copy(h_t[:, :], p_misc[:, :]).then_inc(h_t_ready, 1)

                def copy_latent(j):
                    act.wait_ge(lat_done, j + 1)
                    nc.scalar.copy(lat_t[:, :], p_misc[0:64, :]).then_inc(lat_ready, 1)

                def copy_queries(j, q):
                    act.wait_ge(proj, j * 3 + 1)
                    if qkv_bias:
                        nc.scalar.activation(q_t[:, q, :], p_misc[:, :], ACT.Identity, bias=scaled_bq[:, 0:1], scale=scale)\
                            .then_inc(q_ready, 1)
                    else:
                        nc.scalar.activation(q_t[:, q, :], p_misc[:, :], ACT.Copy, scale=scale).then_inc(q_ready, 1)

                def copy_keys(j, q):
                    act.wait_ge(proj, j * 3 + 2)
                    if qkv_bias:
                        nc.scalar.activation(k_t[:, q, :], p_misc[:, :], ACT.Identity, bias=w["bk"][:, 0:1]).then_inc(k_ready, 1)
                    else:
                        nc.scalar.copy(k_t[:, q, :], p_misc[:, :]).then_inc(k_ready, 1)

                def copy_turned(i, n):
                    g = i * UNITS + n
                    act.wait_ge(turned, g + 1)
                    if not isinstance(g, int) or g >= 2:
                        act.wait_ge(weighed, g - 1)
                    nc.scalar.copy(probs_t[:, n % 2, 0:4, :], p_trans[:, 0, :, :])
                    nc.scalar.copy(probs_t[:, n % 2, 4:8, :], p_trans[:, 1, :, :]).then_inc(turned_out, 1)

                def copy_out(j):
                    act.wait_ge(out_t, j + 1)
                    nc.scalar.copy(heads_t[:, :], p_misc[:, :]).then_inc(out_t_ready, 1)

                def start():
                    copy_h(0)
                    if latent:
                        copy_latent(0)
                    copy_queries(0, 0)
                    copy_keys(0, 0)

                def body(i, p, last_group):
                    for n in range(UNITS):
                        act.wait_ge(shifted, i * UNITS + n + 1)
                        nc.scalar.activation(probs[:, n % 2, :, :], probs[:, n % 2, :, :], ACT.Exp).then_inc(expd, 1)
                        if n >= 1:
                            copy_turned(i, n - 1)
                        elif started(i):
                            copy_turned(i - 1, UNITS - 1)
                        if not last_group:
                            if n == TURN_H + 1:
                                copy_h(i + 1)
                            if latent and n == LATENT + 1:
                                copy_latent(i + 1)
                            if n == QUERIES + 1:
                                copy_queries(i + 1, 1 - p)
                            if n == KEYS + 1:
                                copy_keys(i + 1, 1 - p)
                        if n == TURN_OUT + 1 and started(i):
                            copy_out(i - 1)
                pipelined(act, None, start, body)
                copy_turned(NG - 1, UNITS - 1)
                copy_out(NG - 1)

            @block.vector
            def _(dve):
                order = Order(dve, dve_order)
                dve.wait_ge(loaded, w["n"])
                if causal:
                    nc.vector.tensor_copy(causal_b[:, :], const["causal"][:, :])
                    nc.vector.tensor_copy(ident_b[:, :], const["ident"][:, :])
                if key_mask is not None:
                    nc.vector.memset(ones_b[:, :], 1.0)
                if qkv_bias:
                    nc.vector.tensor_scalar(scaled_bq[:, :], w["bq"][:, :], scale, None, ALU.mult)
                if rel_bias:
                    dve.wait_ge(flipped, 1)
                    for n in range(4):
                        nc.vector.tensor_copy(bias[:, 4 * n:4 * n + 4, :], p_score[n // 2][:, n % 2, :, :])
                nc.vector.memset(v[:, :, :, :], 1.0).then_inc(setup, 1)
                dve.wait_ge(setup, 1)

                def norm_stats(j):
                    layernorm_stats(nc, dve, order, x, j, stats, moments, pad).then_inc(stats_ready, 1)

                def norm_apply(j):
                    dve.wait_ge(rstd_ready, j + 1)
                    layernorm_apply(nc, x, j, moments, rstd, h).then_inc(normed, 1)

                def copy_values(j, q):
                    if key_mask is not None:
                        nc.vector.tensor_scalar(mask_f[:, q, :], w["mask"][0:1, bass.ts(j, GROUP * T)], 0.0, MASKED,
                                                ALU.is_equal, ALU.mult)
                    dve.wait_ge(proj, 3 * j + 3)
                    dst = v[:, q * GROUP:(q + 1) * GROUP, :, 0:HD]
                    src = p_misc[:, :].rearrange("p (u h d) -> p u h d", u=GROUP, d=HD)
                    if qkv_bias:
                        nc.vector.tensor_tensor(dst, src, bcast(w["bv"][:, :].rearrange("p (h d) -> p h d", d=HD),
                                                                [T, GROUP, HEADS, HD], 1), ALU.add).then_inc(v_ready, 1)
                    else:
                        nc.vector.tensor_copy(dst, src).then_inc(v_ready, 1)

                def shift(i, n):
                    u, half, g = n // 2, n % 2, i * UNITS + n
                    dve.wait_ge(scored, g + 1)
                    if not isinstance(g, int) or g >= 2:
                        dve.wait_ge(turned, g - 1)
                    s = p_score[n % 2][:, :, :, :].rearrange("p a b k -> p (a b) k")
                    p = probs[:, n % 2, :, :]
                    if rel_bias:
                        order.then(nc.vector.tensor_tensor(p, s, bias[:, half * HALF:(half + 1) * HALF, :], ALU.add))
                        s = p
                    order.then(nc.vector.tensor_reduce(top[:, n % 2, :], s, AX.X, ALU.max))
                    nc.vector.tensor_tensor(p, s, bcast(top[:, n % 2, :], [T, HALF, T], 2), ALU.subtract)\
                        .then_inc(shifted, 1)

                def divide(i, n, q):
                    u, half, g = n // 2, n % 2, i * UNITS + n
                    dve.wait_ge(weighed, g + 1)
                    o = p_pv[:, 0:HALF * (HD + 1)].rearrange("p (h d) -> p h d", d=HD + 1)
                    order.then(nc.vector.reciprocal(rec[:, :], o[:, :, HD]))
                    nc.vector.tensor_tensor(
                        heads_out[:, q * GROUP + u, half * (D // 2):(half + 1) * (D // 2)].rearrange("p (h d) -> p h d", d=HD),
                        o[:, :, 0:HD], bcast(rec[:, :], [T, HALF, HD], 2), ALU.mult).then_inc(divided, 1)

                def add_output(j):
                    dve.wait_ge(out_done, j + 1)
                    out = p_misc[:, :].rearrange("p (u d) -> p u d", d=D)
                    xs = x[:, bass.ts(j, GROUP), :]
                    if out_bias:
                        nc.vector.tensor_tensor(update[:, :, :], out, bcast(w["bo"][:, :], [T, GROUP, D], 1), ALU.add)\
                            .then_inc(biased, 1)
                        dve.wait_ge(biased, j + 1)
                        out = update[:, :, :]
                    nc.vector.tensor_tensor(xs, xs, out, ALU.add).then_inc(added, 1)

                def start():
                    norm_stats(0)
                    norm_apply(0)
                    copy_values(0, 0)

                def body(i, p, last_group):
                    for n in range(UNITS):
                        shift(i, n)
                        if n >= 2:
                            divide(i, n - 2, p)
                        elif started(i):
                            divide(i - 1, UNITS - 2 + n, 1 - p)
                        if n == 0 and not last_group:
                            norm_stats(i + 1)
                            norm_apply(i + 1)
                        if n == VALUES + 1 and not last_group:
                            copy_values(i + 1, 1 - p)
                        if n == UNITS - 1 and started(i):
                            add_output(i - 1)
                pipelined(dve, order, start, body, per=2 + UNITS * (3 if rel_bias else 2))
                divide(NG - 1, UNITS - 2, 1)
                divide(NG - 1, UNITS - 1, 1)
                add_output(NG - 1)

            @block.gpsimd
            def _(pool):
                def norm_scale(j):
                    layernorm_rstd(nc, pool, stats_ready, j, const["minus_half"], moments, rstd).then_inc(rstd_ready, 1)

                def spread_keys(i, u, q):
                    if not isinstance(i, int) or i > 0:
                        pool.wait_ge(scored, i * UNITS + 2 * u - 2)
                    elif u >= 2:
                        pool.wait_ge(scored, 2 * u - 2)
                    nc.gpsimd.tensor_tensor(spread[:, u % 2, :, :], bcast(k_t[:, q, u * T:(u + 1) * T], [D, HEADS, T], 1),
                                            bcast(const["head_of"][:, :], [D, HEADS, T], 2), ALU.mult)\
                        .then_inc(spread_ready, 1)

                def start():
                    norm_scale(0)
                    pool.wait_ge(k_ready, 1)
                    spread_keys(0, 0, 0)
                    spread_keys(0, 1, 0)

                def body(i, p, last_group):
                    if not last_group:
                        norm_scale(i + 1)
                    spread_keys(i, 2, p)
                    spread_keys(i, 3, p)
                    if not last_group:
                        pool.wait_ge(k_ready, i + 2)
                        spread_keys(i + 1, 0, 1 - p)
                        spread_keys(i + 1, 1, 1 - p)
                pipelined(pool, None, start, body)


def attention8(nc, name, x, const, w, loaded, ctx_t):
    HEADS8, HD8, KEYS, BLOCKS = 8, 64, 2 * T, 4
    with ExitStack() as ctx:
        L = Layer(nc, ctx, name)
        stats = L.sbuf("stats", [T, GROUP, 6])
        moments = L.sbuf("moments", [T, GROUP, 2])
        pad = L.sbuf("pad", [T, 1])
        rstd = L.sbuf("rstd", [T, GROUP])
        h = L.sbuf("h", [T, GROUP, D])
        h_t = L.sbuf("h_t", [D, GROUP * T])
        c_t = L.sbuf("c_t", [D, GROUP * T])
        q_t = L.sbuf("q_t", [T, BLOCKS, GROUP * T])
        keys = L.sbuf("keys", [T, BLOCKS, 2, GROUP, KEYS])
        v = L.sbuf("v", [T, GROUP, 2, HEADS8, HD8 + 1])
        probs = L.sbuf("probs", [T, 2, 4, KEYS])
        probs_t = L.sbuf("probs_t", [T, 2, 8, T])
        top = L.sbuf("top", [T, 2, 4])
        rec = L.sbuf("rec", [T, 4])
        heads_out = L.sbuf("heads_out", [T, GROUP, BLOCKS, T])
        heads_t = L.sbuf("heads_t", [T, BLOCKS, GROUP * T])
        update = L.sbuf("update", [T, GROUP, D])
        p_score = [L.psum(f"p_score{n}", [T, 2, BANK]) for n in range(2)]
        p_trans = L.psum("p_trans", [T, 2, 4, T])
        p_pv = L.psum("p_pv", [T, BANK])
        p_misc = L.psum("p_misc", [T, BANK])

        ctx_in = L.sem("ctx_in")
        stats_ready = L.sem("stats_ready")
        rstd_ready = L.sem("rstd_ready")
        normed = L.sem("normed")
        trans = L.sem("trans")
        h_t_ready = L.sem("h_t_ready")
        qk_done = L.sem("qk_done")
        qk_ready = L.sem("qk_ready")
        v_done = L.sem("v_done")
        v_ready = L.sem("v_ready")
        scored = L.sem("scored")
        shifted = L.sem("shifted")
        expd = L.sem("expd")
        turned = L.sem("turned")
        turned_out = L.sem("turned_out")
        weighed = L.sem("weighed")
        divided = L.sem("divided")
        out_t = L.sem("out_t")
        out_t_ready = L.sem("out_t_ready")
        out_done = L.sem("out_done")
        added = L.sem("added")
        dve_order = L.sem("dve_order")
        setup = L.sem("setup")
        NQK, NV = 3 * BLOCKS, 2 * GROUP

        with nc.Block() as block:
            @block.sync
            def _(sp):
                def body(i, first):
                    if not first:
                        sp.wait_ge(qk_done, i * NQK)
                    sp.dma_start(c_t[:, :], ctx_t[:, bass.ts(i, GROUP * T)]).then_inc(ctx_in, 16)
                groups(sp, None, body)

            @block.tensor
            def _(pe):
                pe.wait_ge(loaded, w["n"])
                pe.wait_ge(setup, 2)

                def body(i, first):
                    pe.wait_ge(normed, i + 1)
                    if not first:
                        pe.wait_ge(added, i)
                    for u in range(GROUP):
                        last = nc.tensor.transpose(p_misc[:, u * T:(u + 1) * T], h[:, u, :], const["ident"][:, :])
                    last.then_inc(trans, 1)
                    pe.wait_ge(h_t_ready, i + 1)
                    pe.wait_ge(ctx_in, (i + 1) * 16)
                    for j in range(NQK):
                        block_n, what = j // 3, j % 3
                        if j >= 2:
                            pe.wait_ge(qk_ready, i * NQK + j - 1)
                        weights = (w["wq"], w["wk1"], w["wk2"])[what][:, block_n * T:(block_n + 1) * T]
                        nc.tensor.matmul(p_score[0][:, j % 2, :], weights, (h_t, h_t, c_t)[what][:, :],
                                         start=True, stop=True).then_inc(qk_done, 1)
                        if j < NV:
                            u, of_ctx = j // 2, j % 2
                            if j >= 2:
                                pe.wait_ge(v_ready, i * NV + j - 1)
                            nc.tensor.matmul(p_score[1][:, j % 2, :], (h_t, c_t)[of_ctx][:, u * T:(u + 1) * T],
                                             (w["wv1"], w["wv2"])[of_ctx][:, :], start=True, stop=True).then_inc(v_done, 1)
                    pe.wait_ge(qk_ready, (i + 1) * NQK)
                    pe.wait_ge(v_ready, (i + 1) * NV)

                    def scores(n):
                        u, half = n // 2, n % 2
                        if n >= 2:
                            pe.wait_ge(shifted, i * UNITS + n - 1)
                        for j in range(2):
                            block_n = 2 * half + j
                            last = nc.tensor.matmul(p_score[n % 2][:, j, :], q_t[:, block_n, u * T:(u + 1) * T],
                                                    keys[:, block_n, :, u, :], start=True, stop=True)
                        last.then_inc(scored, 1)

                    def transposes(n):
                        pe.wait_ge(expd, i * UNITS + n + 1)
                        if n >= 1:
                            pe.wait_ge(turned_out, i * UNITS + n)
                        for k in range(8):
                            last = nc.tensor.transpose(p_trans[:, k // 4, k % 4, :],
                                                       probs[:, n % 2, k // 2, (k % 2) * T:(k % 2 + 1) * T],
                                                       const["ident"][:, :])
                        last.then_inc(turned, 1)

                    def values(n):
                        u, half = n // 2, n % 2
                        pe.wait_ge(turned_out, i * UNITS + n + 1)
                        if n >= 1:
                            pe.wait_ge(divided, i * UNITS + n)
                        for k in range(8):
                            head, part = k // 2, k % 2
                            last = nc.tensor.matmul(p_pv[:, head * (HD8 + 1):(head + 1) * (HD8 + 1)],
                                                    probs_t[:, n % 2, k, :], v[:, u, part, 4 * half + head, :],
                                                    start=(part == 0), stop=(part == 1))
                        last.then_inc(weighed, 1)

                    scores(0)
                    for n in range(UNITS):
                        if n + 1 < UNITS:
                            scores(n + 1)
                        if n >= 1:
                            values(n - 1)
                        transposes(n)
                    values(UNITS - 1)
                    pe.wait_ge(divided, (i + 1) * UNITS)
                    for b in range(BLOCKS):
                        for u in range(GROUP):
                            last = nc.tensor.transpose(p_score[b // 2][:, b % 2, u * T:(u + 1) * T], heads_out[:, u, b, :],
                                                       const["ident"][:, :])
                        last.then_inc(out_t, 1)
                    pe.wait_ge(out_t_ready, (i + 1) * BLOCKS)
                    for u in range(GROUP):
                        for b in range(BLOCKS):
                            last = nc.tensor.matmul(p_misc[:, u * D:(u + 1) * D], heads_t[:, b, u * T:(u + 1) * T],
                                                    w["wo"][:, b, :], start=(b == 0), stop=(b == BLOCKS - 1))
                    last.then_inc(out_done, 1)
                groups(pe, None, body)

            @block.scalar
            def _(act):
                act.wait_ge(loaded, w["n"])
                act.wait_ge(setup, 2)

                def body(i, first):
                    act.wait_ge(trans, i + 1)
                    nc.scalar.copy(h_t[:, :], p_misc[:, :]).then_inc(h_t_ready, 1)
                    for j in range(NQK):
                        block_n, what = j // 3, j % 3
                        act.wait_ge(qk_done, i * NQK + j + 1)
                        src = p_score[0][:, j % 2, :]
                        if what == 0:
                            nc.scalar.activation(q_t[:, block_n, :], src, ACT.Copy, scale=float(HD8) ** -0.5)\
                                .then_inc(qk_ready, 1)
                        else:
                            for half in range(2):
                                part = slice(64 * half, 64 * half + 64)
                                last = nc.scalar.copy(keys[part, block_n, half, :, (what - 1) * T:what * T],
                                                      src[part, :].rearrange("p (u k) -> p u k", k=T))
                            last.then_inc(qk_ready, 1)

                    def turn_out(n):
                        act.wait_ge(turned, i * UNITS + n + 1)
                        if n >= 2:
                            act.wait_ge(weighed, i * UNITS + n - 1)
                        nc.scalar.copy(probs_t[:, n % 2, 0:4, :], p_trans[:, 0, :, :])
                        nc.scalar.copy(probs_t[:, n % 2, 4:8, :], p_trans[:, 1, :, :]).then_inc(turned_out, 1)

                    for n in range(UNITS):
                        act.wait_ge(shifted, i * UNITS + n + 1)
                        nc.scalar.activation(probs[:, n % 2, :, :], probs[:, n % 2, :, :], ACT.Exp).then_inc(expd, 1)
                        if n >= 1:
                            turn_out(n - 1)
                    turn_out(UNITS - 1)
                    for b in range(BLOCKS):
                        act.wait_ge(out_t, i * BLOCKS + b + 1)
                        nc.scalar.copy(heads_t[:, b, :], p_score[b // 2][:, b % 2, :]).then_inc(out_t_ready, 1)
                groups(act, None, body)

            @block.vector
            def _(dve):
                order = Order(dve, dve_order)
                dve.wait_ge(loaded, w["n"])
                nc.vector.memset(v[:, :, :, :, :].rearrange("p a b c d -> p (a b c d)"), 1.0).then_inc(setup, 1)
                dve.wait_ge(setup, 2)

                def body(i, first):
                    if not first:
                        dve.wait_ge(added, i)
                        dve.wait_ge(trans, i)
                    layernorm_stats(nc, dve, order, x, i, stats, moments, pad).then_inc(stats_ready, 1)
                    dve.wait_ge(rstd_ready, i + 1)
                    layernorm_apply(nc, x, i, moments, rstd, h).then_inc(normed, 1)
                    for j in range(NV):
                        dve.wait_ge(v_done, i * NV + j + 1)
                        nc.vector.tensor_copy(v[:, j // 2, j % 2, :, 0:HD8],
                                              p_score[1][:, j % 2, :].rearrange("p (h d) -> p h d", d=HD8))\
                            .then_inc(v_ready, 1)

                    def shift(n):
                        dve.wait_ge(scored, i * UNITS + n + 1)
                        if n >= 2:
                            dve.wait_ge(turned, i * UNITS + n - 1)
                        s = p_score[n % 2][:, :, :].rearrange("p a (b k) -> p (a b) k", k=KEYS)
                        order.then(nc.vector.tensor_reduce(top[:, n % 2, :], s, AX.X, ALU.max))
                        nc.vector.tensor_tensor(probs[:, n % 2, :, :], s, bcast(top[:, n % 2, :], [T, 4, KEYS], 2),
                                                ALU.subtract).then_inc(shifted, 1)

                    def divide(n):
                        u, half = n // 2, n % 2
                        dve.wait_ge(weighed, i * UNITS + n + 1)
                        o = p_pv[:, 0:4 * (HD8 + 1)].rearrange("p (h d) -> p h d", d=HD8 + 1)
                        order.then(nc.vector.reciprocal(rec[:, :], o[:, :, HD8]))
                        out = heads_out[:, u, 2 * half:2 * half + 2, :].rearrange("p b (h d) -> p (b h) d", d=HD8)
                        nc.vector.tensor_tensor(out, o[:, :, 0:HD8], bcast(rec[:, :], [T, 4, HD8], 2), ALU.mult)\
                            .then_inc(divided, 1)

                    for n in range(UNITS):
                        shift(n)
                        if n >= 2:
                            divide(n - 2)
                    divide(UNITS - 2)
                    divide(UNITS - 1)
                    dve.wait_ge(out_done, i + 1)
                    out = p_misc[:, :].rearrange("p (u d) -> p u d", d=D)
                    order.then(nc.vector.tensor_tensor(update[:, :, :], out, bcast(w["bo"][:, :], [T, GROUP, D], 1), ALU.add))
                    xs = x[:, bass.ts(i, GROUP), :]
                    nc.vector.tensor_tensor(xs, xs, update[:, :, :], ALU.add).then_inc(added, 1)
                groups(dve, order, body)

            @block.gpsimd
            def _(pool):
                nc.gpsimd.memset(keys[:, :, :, :, :].rearrange("p a b c d -> p (a b c d)"), 0.0).then_inc(setup, 1)

                def body(i, first):
                    layernorm_rstd(nc, pool, stats_ready, i, const["minus_half"], moments, rstd).then_inc(rstd_ready, 1)
                groups(pool, None, body)


NEG = -1e30


def pick_first_largest(nc, order, vals, falling, best, best_rank, chosen):
    shape = list(vals.shape)
    axis = len(shape) - 1
    order.then(nc.vector.tensor_reduce(best, vals, AX.X, ALU.max))
    order.then(nc.vector.tensor_tensor(chosen, vals, bcast(best, shape, axis), ALU.is_equal))
    order.then(nc.vector.tensor_tensor(chosen, chosen, falling, ALU.mult))
    order.then(nc.vector.tensor_reduce(best_rank, chosen, AX.X, ALU.max))
    order.then(nc.vector.tensor_tensor(chosen, chosen, bcast(best_rank, shape, axis), ALU.is_equal))


def experts(nc, name, x, const, w, loaded, kind):
    gated = kind != "top2"
    n_exp = 16 if kind == "groups" else 8
    per = {"groups": 1, "top2": 2, "top1": 4}[kind]
    n_weights = {"groups": 8, "top2": 8, "top1": 7}[kind]
    shared = {"groups": 1, "top2": 0, "top1": 4}[kind]
    steps = n_weights * per + shared
    at = {"groups": dict(trans=1, r1=0, logits=3, route=(5, 5, 6, 6, 7, 7, 8, 8), act_h=2, act_r1=0, act_route=4),
          "top2": dict(trans=1, r1=3, logits=5, route=(6, 8, 9, 11), act_h=2, act_r1=4, act_route=8),
          "top1": dict(trans=1, r1=0, logits=4, route=(6, 8, 11), act_h=2, act_r1=0, act_route=8)}[kind]
    turn_at = {"groups": steps - 1, "top2": 13, "top1": 14}[kind]
    with ExitStack() as ctx:
        L = Layer(nc, ctx, name)
        stats = L.sbuf("stats", [T, GROUP, 6])
        moments = L.sbuf("moments", [T, GROUP, 2])
        pad = L.sbuf("pad", [T, 1])
        rstd = L.sbuf("rstd", [T, GROUP])
        h = L.sbuf("h", [T, GROUP, D])
        h_t = L.sbuf("h_t", [D, 2, GROUP * T])
        r1 = L.sbuf("r1", [D, GROUP * T])
        score = L.sbuf("score", [T, GROUP, n_exp])
        left = L.sbuf("left", [T, GROUP, n_exp])
        raw = L.sbuf("raw", [T, GROUP, n_exp])
        chosen = L.sbuf("chosen", [T, GROUP, n_exp])
        picked = L.sbuf("picked", [T, GROUP, n_exp])
        best = L.sbuf("best", [T, GROUP, 4])
        best_rank = L.sbuf("best_rank", [T, GROUP, 4])
        g_score = L.sbuf("g_score", [T, GROUP, 4])
        g_chosen = L.sbuf("g_chosen", [T, GROUP, 4])
        g_picked = L.sbuf("g_picked", [T, GROUP, 4])
        total = L.sbuf("total", [T, GROUP])
        weight = L.sbuf("weight", [T, GROUP, n_exp])
        weight3 = L.sbuf("weight3", [T, GROUP, 3, 32])
        high = L.sbuf("high", [96, GROUP * T], BF16)
        rest = L.sbuf("rest", [96, GROUP * T])
        middle = L.sbuf("middle", [96, GROUP * T], BF16)
        parts = [L.sbuf(f"parts{n}", [96, GROUP * T], BF16) for n in range(2)]
        pick = L.sbuf("pick", [96, n_weights, T], BF16)
        eb2 = L.sbuf("eb2", [96, D]) if kind == "top2" else None
        weight_t = L.sbuf("weight_t", [n_exp, 2, GROUP * T]) if kind == "top2" else None
        h_w = L.sbuf("h_w", [D, 2, GROUP * T])
        act_out = L.sbuf("act_out", [D, 2, GROUP * T])
        prod = L.sbuf("prod", [D, 2, GROUP * T])
        hidden = L.sbuf("hidden", [D, 2, GROUP * T])
        out_t = L.sbuf("out_t", [D, GROUP * T])
        p_misc = L.psum("p_misc", [T, BANK])
        p_route = L.psum("p_route", [T, BANK])
        p_spread = L.psum("p_spread", [T, BANK])
        p_out = L.psum("p_out", [T, BANK])
        p_gate = [L.psum(f"p_gate{n}", [T, BANK]) for n in range(2)]
        p_up = [L.psum(f"p_up{n}", [T, BANK]) for n in range(2)] if gated else None

        stats_ready = L.sem("stats_ready")
        rstd_ready = L.sem("rstd_ready")
        normed = L.sem("normed")
        x_h = L.sem("x_h")
        trans = L.sem("trans")
        h_t_ready = L.sem("h_t_ready")
        r1_done = L.sem("r1_done")
        r1_ready = L.sem("r1_ready")
        logits = L.sem("logits")
        route_in = L.sem("route_in")
        route_out = L.sem("route_out")
        routed = L.sem("routed")
        routed_t = L.sem("routed_t")
        high_ready = L.sem("high_ready")
        parts_ready = L.sem("parts_ready")
        spread = L.sem("spread")
        spread_used = L.sem("spread_used")
        gate = L.sem("gate")
        acted = L.sem("acted")
        hidden_ready = L.sem("hidden_ready")
        down = L.sem("down")
        out_t_ready = L.sem("out_t_ready")
        out_done = L.sem("out_done")
        added = L.sem("added")
        dve_order = L.sem("dve_order")
        setup = L.sem("setup")
        weighs_input = kind == "top1"
        n_down = steps + (kind == "top2")

        with nc.Block() as block:
            @block.tensor
            def _(pe):
                pe.wait_ge(loaded, w["n"])
                pe.wait_ge(setup, 1)

                def turn_h(j, q):
                    pe.wait_ge(normed, j + 1)
                    for u in range(GROUP):
                        last = nc.tensor.transpose(p_misc[:, u * T:(u + 1) * T], h[:, u, :], const["ident"][:, :])
                    last.then_inc(trans, 1)

                def route_first(j, q):
                    pe.wait_ge(h_t_ready, j + 1)
                    nc.tensor.matmul(p_route[:, :], w["rw1"][:, :], h_t[:, q, :], start=True, stop=True)\
                        .then_inc(r1_done, 1)

                def route_logits(j, q):
                    source = h_t[:, q, :]
                    if kind == "top2":
                        pe.wait_ge(r1_ready, j + 1)
                        source = r1[:, :]
                    else:
                        pe.wait_ge(h_t_ready, j + 1)
                    for u in range(GROUP):
                        last = nc.tensor.matmul(p_route[:, u * n_exp:(u + 1) * n_exp], source[:, u * T:(u + 1) * T],
                                                w["router"][:, :], start=True, stop=True)
                    last.then_inc(logits, 1)

                def turn_weights(j):
                    pe.wait_ge(routed, j + 1)
                    for u in range(GROUP):
                        last = nc.tensor.transpose(p_misc[0:96, u * T:(u + 1) * T],
                                                   weight3[:, u, :, :].rearrange("p r e -> p (r e)"), const["ident"][:, :])
                    last.then_inc(routed_t, 1)

                def start():
                    turn_h(0, 0)
                    if kind == "top2":
                        route_first(0, 0)
                    route_logits(0, 0)
                    turn_weights(0)

                def output(i):
                    pe.wait_ge(out_t_ready, i + 1)
                    for u in range(GROUP):
                        last = nc.tensor.transpose(p_misc[:, u * D:(u + 1) * D], out_t[:, u * T:(u + 1) * T],
                                                   const["ident"][:, :])
                    last.then_inc(out_done, 1)

                def body(i, p, last_group):
                    pe.wait_ge(parts_ready, i + 1)

                    def spread_weight(e):
                        if e >= 1:
                            pe.wait_ge(spread_used, i * n_weights + e)
                        nc.tensor.matmul(p_spread[:, :], pick[:, e, :], parts[p][:, :], start=True, stop=True)\
                            .then_inc(spread, 1)

                    def gate_step(s):
                        e = s // per
                        if e < n_weights and s % per == 0:
                            if weighs_input:
                                if e == 0:
                                    spread_weight(0)
                                if e + 1 < n_weights:
                                    spread_weight(e + 1)
                                pe.wait_ge(spread_used, i * n_weights + e + 1)
                        if s >= 2:
                            pe.wait_ge(acted, i * steps + s - 1)
                        out = nc.tensor.matmul(p_gate[s % 2][:, :], w["wg"][:, s, :], h_t[:, p, :], start=True, stop=True)
                        if gated:
                            if s >= 2:
                                pe.wait_ge(hidden_ready, i * steps + s - 1)
                            source = h_w[:, e % 2, :] if weighs_input and e < n_weights else h_t[:, p, :]
                            out = nc.tensor.matmul(p_up[s % 2][:, :], w["wu"][:, s, :], source, start=True, stop=True)
                        out.then_inc(gate, 1)
                        if e < n_weights and s % per == 0 and not weighs_input:
                            spread_weight(e)

                    def down_step(s):
                        pe.wait_ge(hidden_ready, i * steps + s + 1)
                        nc.tensor.matmul(p_out[:, :], w["wd"][:, s, :], hidden[:, s % 2, :], start=(s == 0),
                                         stop=(s == steps - 1 and kind != "top2")).then_inc(down, 1)

                    gate_step(0)
                    for s in range(steps):
                        if s + 1 < steps:
                            gate_step(s + 1)
                        if s == 0 and not (isinstance(i, int) and i == 0):
                            pe.wait_ge(out_t_ready, i)
                        down_step(s)
                        if s == 0 and not (isinstance(i, int) and i == 0):
                            output(i - 1)
                        if last_group:
                            continue
                        if s == at["trans"]:
                            if not (isinstance(i, int) and i == 0):
                                pe.wait_ge(added, i)
                            turn_h(i + 1, 1 - p)
                        if kind == "top2" and s == at["r1"]:
                            route_first(i + 1, 1 - p)
                        if s == at["logits"]:
                            route_logits(i + 1, 1 - p)
                        if s == turn_at:
                            turn_weights(i + 1)
                    if kind == "top2":
                        nc.tensor.matmul(p_out[:, :], w["eb2"][:, :], weight_t[:, p, :], start=False, stop=True)\
                            .then_inc(down, 1)
                pipelined(pe, None, start, body)
                output(NG - 1)

            @block.scalar
            def _(act):
                act.wait_ge(loaded, w["n"])

                def copy_h(j, q):
                    act.wait_ge(trans, j + 1)
                    nc.scalar.copy(h_t[:, q, :], p_misc[:, :]).then_inc(h_t_ready, 1)

                def route_first(j):
                    act.wait_ge(r1_done, j + 1)
                    nc.scalar.activation(r1[:, :], p_route[:, :], ACT.Silu, bias=w["rb1"][:, 0:1]).then_inc(r1_ready, 1)

                def route_function(j):
                    if kind == "groups":
                        act.wait_ge(logits, j + 1)
                        nc.scalar.activation(score[:, :, :], p_route[:, 0:GROUP * n_exp], ACT.Sigmoid)\
                            .then_inc(route_out, 1)
                    else:
                        act.wait_ge(route_in, j + 1)
                        nc.scalar.activation(score[:, :, :], left[:, :, :], ACT.Exp).then_inc(route_out, 1)

                def split(j, q):
                    act.wait_ge(routed_t, j + 1)
                    if kind == "top2":
                        nc.scalar.copy(weight_t[:, q, :], p_misc[0:n_exp, :])
                    split_high(nc, p_misc, high, parts[q]).then_inc(high_ready, 1)

                def start():
                    copy_h(0, 0)
                    if kind == "top2":
                        route_first(0)
                    route_function(0)
                    split(0, 0)

                def body(i, p, last_group):
                    for s in range(steps):
                        act.wait_ge(gate, i * steps + s + 1)
                        if s >= 2:
                            act.wait_ge(hidden_ready, i * steps + s - 1)
                        bias = {"bias": w["eb1"][:, s:s + 1]} if kind == "top2" else {}
                        nc.scalar.activation(act_out[:, s % 2, :], p_gate[s % 2][:, :], ACT.Silu, **bias)\
                            .then_inc(acted, 1)
                        if last_group:
                            continue
                        if s == at["act_h"]:
                            copy_h(i + 1, 1 - p)
                        if kind == "top2" and s == at["act_r1"]:
                            route_first(i + 1)
                        if s == at["act_route"]:
                            route_function(i + 1)
                        if s == turn_at + 1:
                            split(i + 1, 1 - p)
                    act.wait_ge(down, (i + 1) * n_down)
                    nc.scalar.copy(out_t[:, :], p_out[:, :]).then_inc(out_t_ready, 1)
                    if not last_group and turn_at + 1 >= steps:
                        split(i + 1, 1 - p)
                pipelined(act, None, start, body)

            @block.vector
            def _(dve):
                order = Order(dve, dve_order)
                dve.wait_ge(loaded, w["n"])
                nc.vector.memset(weight3[:, :, :, :].rearrange("p u r e -> p (u r e)"), 0.0)
                nc.vector.tensor_copy(pick[:, :, :], w["pick"][:, :, :]).then_inc(setup, 1)
                dve.wait_ge(setup, 1)

                def route_groups(j, part):
                    falling = bcast(const["falling16"][:, :], [T, GROUP, n_exp], 1)
                    by_group = lambda t: t[:, :, :].rearrange("p u (g e) -> p (u g) e", e=4)
                    flat = lambda t: t[:, :, :].rearrange("p u g -> p (u g)")
                    if part == 0:
                        dve.wait_ge(route_out, j + 1)
                        order.then(nc.vector.tensor_tensor(raw[:, :, :], score[:, :, :],
                                                           bcast(w["gate_bias"][:, :], [T, GROUP, n_exp], 1), ALU.add))
                        fall4 = bcast(const["falling4"][:, :], [T, 4 * GROUP, 4], 1)
                        pick_first_largest(nc, order, by_group(raw), fall4, flat(best), flat(best_rank), by_group(chosen))
                        order.then(nc.vector.scalar_tensor_tensor(left[:, :, :], chosen[:, :, :], NEG, raw[:, :, :],
                                                                  ALU.mult, ALU.add))
                        order.then(nc.vector.tensor_reduce(flat(g_score), by_group(left), AX.X, ALU.max))
                        order.then(nc.vector.tensor_tensor(flat(g_score), flat(g_score), flat(best), ALU.add))
                    elif part in (1, 2):
                        pick_first_largest(nc, order, g_score[:, :, :], bcast(const["falling4"][:, :], [T, GROUP, 4], 1),
                                           best[:, :, 0], best_rank[:, :, 0], g_chosen[:, :, :])
                        if part == 1:
                            order.then(nc.vector.tensor_copy(g_picked[:, :, :], g_chosen[:, :, :]))
                            order.then(nc.vector.scalar_tensor_tensor(g_score[:, :, :], g_chosen[:, :, :], NEG,
                                                                      g_score[:, :, :], ALU.mult, ALU.add))
                        else:
                            order.then(nc.vector.tensor_tensor(g_picked[:, :, :], g_picked[:, :, :], g_chosen[:, :, :],
                                                               ALU.add))
                            order.then(nc.vector.tensor_scalar(g_picked[:, :, :], g_picked[:, :, :], 1.0, -NEG,
                                                               ALU.subtract, ALU.mult))
                            order.then(nc.vector.tensor_tensor(by_group(left), by_group(raw),
                                                               bcast(flat(g_picked), [T, 4 * GROUP, 4], 2), ALU.add))
                    elif part < 7:
                        pick_first_largest(nc, order, left[:, :, :], falling, best[:, :, 0], best_rank[:, :, 0],
                                           chosen[:, :, :])
                        if part == 3:
                            order.then(nc.vector.tensor_copy(picked[:, :, :], chosen[:, :, :]))
                        else:
                            order.then(nc.vector.tensor_tensor(picked[:, :, :], picked[:, :, :], chosen[:, :, :], ALU.add))
                        if part < 6:
                            order.then(nc.vector.scalar_tensor_tensor(left[:, :, :], chosen[:, :, :], 2 * NEG,
                                                                      left[:, :, :], ALU.mult, ALU.add))
                    else:
                        order.then(nc.vector.tensor_tensor(weight[:, :, :], score[:, :, :], picked[:, :, :], ALU.mult))
                        order.then(nc.vector.tensor_reduce(total[:, :], weight[:, :, :], AX.X, ALU.add))
                        order.then(nc.vector.tensor_scalar(total[:, :], total[:, :], 1e-20, None, ALU.add))
                        order.then(nc.vector.reciprocal(total[:, :], total[:, :]))
                        order.then(nc.vector.tensor_scalar(total[:, :], total[:, :], 2.5, None, ALU.mult))
                        write_weights()

                def route_top(j, part, count):
                    falling = bcast(const["falling8"][:, :], [T, GROUP, n_exp], 1)
                    if part == 0:
                        dve.wait_ge(logits, j + 1)
                        p_logit = p_route[:, 0:GROUP * n_exp].rearrange("p (u e) -> p u e", e=n_exp)
                        if kind == "top2":
                            order.then(nc.vector.tensor_tensor(raw[:, :, :], p_logit,
                                                               bcast(w["rb2"][:, :], [T, GROUP, n_exp], 1), ALU.add))
                        else:
                            order.then(nc.vector.tensor_copy(raw[:, :, :], p_logit))
                        order.then(nc.vector.tensor_reduce(best[:, :, 0], raw[:, :, :], AX.X, ALU.max))
                        nc.vector.tensor_tensor(left[:, :, :], raw[:, :, :], bcast(best[:, :, 0], [T, GROUP, n_exp], 2),
                                                ALU.subtract).then_inc(route_in, 1)
                    elif part <= count:
                        pick_first_largest(nc, order, raw[:, :, :], falling, best[:, :, 1], best_rank[:, :, 1],
                                           chosen[:, :, :])
                        if part == 1:
                            order.then(nc.vector.tensor_copy(picked[:, :, :], chosen[:, :, :]))
                            if count == 2:
                                order.then(nc.vector.scalar_tensor_tensor(raw[:, :, :], chosen[:, :, :], NEG, raw[:, :, :],
                                                                          ALU.mult, ALU.add))
                        else:
                            order.then(nc.vector.tensor_tensor(picked[:, :, :], picked[:, :, :], chosen[:, :, :], ALU.add))
                    else:
                        dve.wait_ge(route_out, j + 1)
                        order.then(nc.vector.tensor_tensor(weight[:, :, :], score[:, :, :], picked[:, :, :], ALU.mult))
                        over = weight if count == 2 else score
                        order.then(nc.vector.tensor_reduce(total[:, :], over[:, :, :], AX.X, ALU.add))
                        order.then(nc.vector.reciprocal(total[:, :], total[:, :]))
                        if count == 1:
                            order.then(nc.vector.tensor_scalar(total[:, :], total[:, :], 2.0, None, ALU.mult))
                        write_weights()

                def write_weights():
                    order.then(nc.vector.tensor_tensor(weight[:, :, :], weight[:, :, :],
                                                       bcast(total[:, :], [T, GROUP, n_exp], 2), ALU.mult))
                    nc.vector.tensor_copy(weight3[:, :, :, 0:n_exp], weight[:, :, :].unsqueeze(2)
                                          .broadcast_to([T, GROUP, 3, n_exp])).then_inc(routed, 1)

                def route(j, part):
                    if kind == "groups":
                        route_groups(j, part)
                    else:
                        route_top(j, part, 2 if kind == "top2" else 1)

                def norm_stats(j):
                    layernorm_stats(nc, dve, order, x, j, stats, moments, pad).then_inc(stats_ready, 1)

                def norm_apply(j):
                    dve.wait_ge(rstd_ready, j + 1)
                    layernorm_apply(nc, x, j, moments, rstd, h).then_inc(normed, 1)
                    if kind != "top1":
                        dve.wait_ge(normed, j + 1)
                        xs = x[:, bass.ts(j, GROUP), :]
                        nc.vector.tensor_tensor(xs, xs, h[:, :, :], ALU.add).then_inc(x_h, 1)

                def split(j, q):
                    dve.wait_ge(high_ready, j + 1)
                    split_rest(nc, order, p_misc, high, rest, middle, parts[q]).then_inc(parts_ready, 1)

                def start():
                    norm_stats(0)
                    norm_apply(0)
                    for part in range(len(at["route"])):
                        route(0, part)
                    split(0, 0)

                def add_output(i):
                    dve.wait_ge(out_done, i + 1)
                    if kind != "top1":
                        dve.wait_ge(x_h, i + 1)
                    xs = x[:, bass.ts(i, GROUP), :]
                    nc.vector.tensor_tensor(xs, xs, p_misc[:, :].rearrange("p (u d) -> p u d", d=D), ALU.add)\
                        .then_inc(added, 1)

                def body(i, p, last_group):
                    def weigh_input(e):
                        dve.wait_ge(spread, i * n_weights + e + 1)
                        if e >= 2:
                            dve.wait_ge(gate, i * steps + (e - 1) * per)
                        nc.vector.tensor_tensor(h_w[:, e % 2, :], h_t[:, p, :], p_spread[:, :], ALU.mult)\
                            .then_inc(spread_used, 1)

                    if not last_group:
                        norm_stats(i + 1)
                    if weighs_input:
                        dve.wait_ge(h_t_ready, i + 1)
                        weigh_input(0)
                        weigh_input(1)
                    for s in range(steps):
                        e = s // per
                        dve.wait_ge(acted, i * steps + s + 1)
                        if s >= 2:
                            dve.wait_ge(down, i * n_down + s - 1)
                        if weighs_input or e >= n_weights:
                            nc.vector.tensor_tensor(hidden[:, s % 2, :], act_out[:, s % 2, :], p_up[s % 2][:, :], ALU.mult)\
                                .then_inc(hidden_ready, 1)
                            if weighs_input and s % per == per - 1 and e + 2 < n_weights:
                                weigh_input(e + 2)
                        else:
                            a = act_out[:, s % 2, :]
                            if gated:
                                order.then(nc.vector.tensor_tensor(prod[:, s % 2, :], a, p_up[s % 2][:, :], ALU.mult))
                                a = prod[:, s % 2, :]
                            dve.wait_ge(spread, i * n_weights + e + 1)
                            nc.vector.tensor_tensor(hidden[:, s % 2, :], a, p_spread[:, :], ALU.mult)\
                                .then_inc(hidden_ready, 1)
                            if s % per == per - 1:
                                nc.vector.memset(pad[:, :], 0.0).then_inc(spread_used, 1)
                        if s == 0 and not (isinstance(i, int) and i == 0):
                            add_output(i - 1)
                        if last_group:
                            continue
                        if s == 0:
                            norm_apply(i + 1)
                        for part, where in enumerate(at["route"]):
                            if s == where:
                                route(i + 1, part)
                        if s == turn_at + 2:
                            split(i + 1, 1 - p)
                    if not last_group and turn_at + 2 >= steps:
                        split(i + 1, 1 - p)
                pipelined(dve, order, start, body)
                add_output(NG - 1)

            @block.gpsimd
            def _(pool):
                def body(i, first):
                    layernorm_rstd(nc, pool, stats_ready, i, const["minus_half"], moments, rstd).then_inc(rstd_ready, 1)
                groups(pool, None, body)


def attention1(nc, name, x, const, w, loaded, aps, cross):
    scale = 1.0 / 32.0 if cross else float(D) ** -0.5
    with ExitStack() as ctx:
        L = Layer(nc, ctx, name)
        stats = L.sbuf("stats", [T, GROUP, 6])
        moments = L.sbuf("moments", [T, GROUP, 2])
        pad = L.sbuf("pad", [T, 1])
        rstd = L.sbuf("rstd", [T, GROUP])
        h = L.sbuf("h", [T, GROUP, D])
        h_t = L.sbuf("h_t", [D, GROUP * T])
        q_t = L.sbuf("q_t", [D, GROUP * T])
        k_t = L.sbuf("k_t", [D, 2, GROUP * T])
        v = L.sbuf("v", [T, 2, GROUP, D])
        drop = L.sbuf("drop", [T, 2, GROUP, T])
        probs = L.sbuf("probs", [T, GROUP, T])
        probs_t = L.sbuf("probs_t", [T, GROUP * T])
        top = L.sbuf("top", [T, GROUP])
        total = L.sbuf("total", [T, GROUP])
        att = L.sbuf("att", [T, GROUP, D])
        att_t = L.sbuf("att_t", [D, GROUP * T])
        p_misc = L.psum("p_misc", [T, BANK])
        p_q = L.psum("p_q", [T, BANK])
        p_k = L.psum("p_k", [T, BANK])
        p_v = L.psum("p_v", [T, BANK])
        p_score = L.psum("p_score", [T, GROUP, T])
        p_trans = L.psum("p_trans", [T, BANK])
        p_out = L.psum("p_out", [T, GROUP, D])

        inputs_in = L.sem("inputs_in")
        stats_ready = L.sem("stats_ready")
        rstd_ready = L.sem("rstd_ready")
        normed = L.sem("normed")
        trans = L.sem("trans")
        h_t_ready = L.sem("h_t_ready")
        proj = L.sem("proj")
        q_ready = L.sem("q_ready")
        k_ready = L.sem("k_ready")
        v_ready = L.sem("v_ready")
        scored = L.sem("scored")
        shifted = L.sem("shifted")
        expd = L.sem("expd")
        summed = L.sem("summed")
        turned = L.sem("turned")
        turned_out = L.sem("turned_out")
        weighed = L.sem("weighed")
        divided = L.sem("divided")
        att_turned = L.sem("att_turned")
        att_t_ready = L.sem("att_t_ready")
        out_done = L.sem("out_done")
        added = L.sem("added")
        dve_order = L.sem("dve_order")

        with nc.Block() as block:
            if cross:
                @block.sync
                def _(sp):
                    def load_group(i, slot):
                        sp.dma_start(k_t[:, slot, :], aps["ctx_t"][:, bass.ts(i, GROUP * T)]).then_inc(inputs_in, 16)
                        sp.dma_start(v[:, slot, :, :], aps["ctx"][:, bass.ts(i, GROUP), :]).then_inc(inputs_in, 16)
                        sp.dma_start(drop[:, slot, :, :], aps["drop"][:, bass.ts(i, GROUP), :]).then_inc(inputs_in, 16)

                    def body(i, first):
                        if not first:
                            sp.wait_ge(weighed, i)
                        load_group(i, 0)
                    groups(sp, None, body)

            @block.tensor
            def _(pe):
                pe.wait_ge(loaded, w["n"])

                def body(i, first):
                    pe.wait_ge(normed, i + 1)
                    if not first:
                        pe.wait_ge(added, i)
                    for u in range(GROUP):
                        last = nc.tensor.transpose(p_misc[:, u * T:(u + 1) * T], h[:, u, :], const["ident"][:, :])
                    last.then_inc(trans, 1)
                    pe.wait_ge(h_t_ready, i + 1)
                    if cross:
                        pe.wait_ge(inputs_in, (i + 1) * 48)
                        queries = h_t
                    else:
                        nc.tensor.matmul(p_q[:, :], w["wq"][:, :], h_t[:, :], start=True, stop=True).then_inc(proj, 1)
                        nc.tensor.matmul(p_k[:, :], w["wk"][:, :], h_t[:, :], start=True, stop=True).then_inc(proj, 1)
                        for u in range(GROUP):
                            last = nc.tensor.matmul(p_v[:, u * D:(u + 1) * D], h_t[:, u * T:(u + 1) * T], w["wv"][:, :],
                                                    start=True, stop=True)
                        last.then_inc(proj, 1)
                        pe.wait_ge(q_ready, i + 1)
                        pe.wait_ge(k_ready, i + 1)
                        queries = q_t
                    for u in range(GROUP):
                        last = nc.tensor.matmul(p_score[:, u, :], queries[:, u * T:(u + 1) * T],
                                                k_t[:, 0, u * T:(u + 1) * T], start=True, stop=True)
                    last.then_inc(scored, 1)
                    pe.wait_ge(summed, i + 1)
                    for u in range(GROUP):
                        last = nc.tensor.transpose(p_trans[:, u * T:(u + 1) * T], probs[:, u, :], const["ident"][:, :])
                    last.then_inc(turned, 1)
                    pe.wait_ge(turned_out, i + 1)
                    if not cross:
                        pe.wait_ge(v_ready, i + 1)
                    for u in range(GROUP):
                        last = nc.tensor.matmul(p_out[:, u, :], probs_t[:, u * T:(u + 1) * T], v[:, 0, u, :],
                                                start=True, stop=True)
                    last.then_inc(weighed, 1)
                    if cross:
                        pe.wait_ge(divided, i + 1)
                        for u in range(GROUP):
                            last = nc.tensor.transpose(p_misc[:, u * T:(u + 1) * T], att[:, u, :], const["ident"][:, :])
                        last.then_inc(att_turned, 1)
                        pe.wait_ge(att_t_ready, i + 1)
                        for u in range(GROUP):
                            last = nc.tensor.matmul(p_misc[:, u * D:(u + 1) * D], att_t[:, u * T:(u + 1) * T],
                                                    w["wo"][:, :], start=True, stop=True)
                        last.then_inc(out_done, 1)
                groups(pe, None, body)

            @block.scalar
            def _(act):
                act.wait_ge(loaded, w["n"])

                def body(i, first):
                    act.wait_ge(trans, i + 1)
                    nc.scalar.copy(h_t[:, :], p_misc[:, :]).then_inc(h_t_ready, 1)
                    if not cross:
                        act.wait_ge(proj, 3 * i + 1)
                        nc.scalar.activation(q_t[:, :], p_q[:, :], ACT.Identity, bias=w["bq"][:, 0:1]).then_inc(q_ready, 1)
                        act.wait_ge(proj, 3 * i + 2)
                        nc.scalar.activation(k_t[:, 0, :], p_k[:, :], ACT.Identity, bias=w["bk"][:, 0:1])\
                            .then_inc(k_ready, 1)
                    act.wait_ge(shifted, i + 1)
                    nc.scalar.activation(probs[:, :, :], probs[:, :, :], ACT.Exp, scale=scale).then_inc(expd, 1)
                    act.wait_ge(turned, i + 1)
                    nc.scalar.copy(probs_t[:, :], p_trans[:, :]).then_inc(turned_out, 1)
                    if cross:
                        act.wait_ge(att_turned, i + 1)
                        nc.scalar.copy(att_t[:, :], p_misc[:, :]).then_inc(att_t_ready, 1)
                groups(act, None, body)

            @block.vector
            def _(dve):
                order = Order(dve, dve_order)
                dve.wait_ge(loaded, w["n"])

                def body(i, first):
                    if not first:
                        dve.wait_ge(added, i)
                        dve.wait_ge(trans, i)
                    layernorm_stats(nc, dve, order, x, i, stats, moments, pad).then_inc(stats_ready, 1)
                    dve.wait_ge(rstd_ready, i + 1)
                    layernorm_apply(nc, x, i, moments, rstd, h).then_inc(normed, 1)
                    if not cross:
                        dve.wait_ge(proj, 3 * i + 3)
                        nc.vector.tensor_tensor(v[:, 0, :, :], p_v[:, :].rearrange("p (u d) -> p u d", d=D),
                                                bcast(w["bv"][:, :], [T, GROUP, D], 1), ALU.add).then_inc(v_ready, 1)
                    dve.wait_ge(scored, i + 1)
                    order.then(nc.vector.tensor_reduce(top[:, :], p_score[:, :, :], AX.X, ALU.max))
                    nc.vector.tensor_tensor(probs[:, :, :], p_score[:, :, :], bcast(top[:, :], [T, GROUP, T], 2),
                                            ALU.subtract).then_inc(shifted, 1)
                    dve.wait_ge(expd, i + 1)
                    if cross:
                        order.then(nc.vector.tensor_reduce(total[:, :], probs[:, :, :], AX.X, ALU.add))
                        dve.wait_ge(inputs_in, (i + 1) * 48)
                        nc.vector.tensor_tensor(probs[:, :, :], probs[:, :, :], drop[:, 0, :, :], ALU.mult)\
                            .then_inc(summed, 1)
                    else:
                        nc.vector.tensor_reduce(total[:, :], probs[:, :, :], AX.X, ALU.add).then_inc(summed, 1)
                        dve.wait_ge(summed, i + 1)
                    order.then(nc.vector.reciprocal(total[:, :], total[:, :]))
                    dve.wait_ge(weighed, i + 1)
                    ins = nc.vector.tensor_tensor(att[:, :, :], p_out[:, :, :], bcast(total[:, :], [T, GROUP, D], 2),
                                                  ALU.mult)
                    xs = x[:, bass.ts(i, GROUP), :]
                    if cross:
                        ins.then_inc(divided, 1)
                        dve.wait_ge(out_done, i + 1)
                        order.then(nc.vector.tensor_tensor(att[:, :, :], p_misc[:, :].rearrange("p (u d) -> p u d", d=D),
                                                           bcast(w["bo"][:, :], [T, GROUP, D], 1), ALU.add))
                    else:
                        order.then(ins)
                    nc.vector.tensor_tensor(xs, xs, att[:, :, :], ALU.add).then_inc(added, 1)
                groups(dve, order, body)

            @block.gpsimd
            def _(pool):
                def body(i, first):
                    layernorm_rstd(nc, pool, stats_ready, i, const["minus_half"], moments, rstd).then_inc(rstd_ready, 1)
                groups(pool, None, body)


def state_space(nc, name, x, const, w, loaded):
    NH, P8, NC = 32, 8, 4
    QH = 8
    NU = GROUP * NH // QH
    TAPS = 4
    with ExitStack() as ctx:
        L = Layer(nc, ctx, name)
        stats = L.sbuf("stats", [T, GROUP, 6])
        moments = L.sbuf("moments", [T, GROUP, 2])
        pad = L.sbuf("pad", [T, 1])
        rstd = L.sbuf("rstd", [T, GROUP])
        h = L.sbuf("h", [T, GROUP, D])
        h_t = L.sbuf("h_t", [D, GROUP * T])
        padded = L.sbuf("padded", [T, NC, GROUP, T + TAPS - 1])
        conv = L.sbuf("conv", [T, 2, NC, GROUP, T])
        gate = L.sbuf("gate", [T, 2, 2, GROUP * T])
        dt_raw = L.sbuf("dt_raw", [T, GROUP, NH])
        dt = L.sbuf("dt", [T, 2, GROUP, NH])
        da = L.sbuf("da", [T, GROUP, 3, NH])
        neg_a = L.sbuf("neg_a", [T, NH])
        high = L.sbuf("high", [3 * NH, GROUP * T], BF16)
        rest = L.sbuf("rest", [3 * NH, GROUP * T])
        middle = L.sbuf("middle", [3 * NH, GROUP * T], BF16)
        parts = L.sbuf("parts", [3 * NH, 2, GROUP * T], BF16)
        pick = L.sbuf("pick", [3 * NH, NH, T], BF16)
        minus = L.sbuf("minus", [3 * NH, NH], BF16)
        cb = L.sbuf("cb", [T, 2, GROUP, T])
        xs_t = L.sbuf("xs_t", [T, GROUP, 2 * T])
        ident_b = L.sbuf("ident_b", [T, T], BF16)
        future_b = L.sbuf("future_b", [T, T], BF16)
        xdt_own = L.sbuf("xdt_own", [T, 2, NH * T])
        decay = L.sbuf("decay", [T, 2, QH, T])
        mix = L.sbuf("mix", [T, 2, QH, T])
        y = L.sbuf("y", [T, 2, GROUP, T])
        sq = L.sbuf("sq", [T, 2, GROUP, T])
        out_w = L.sbuf("out_w", [T, 2, D])
        ones = L.sbuf("ones", [T, 2])
        ms = L.sbuf("ms", [T, GROUP])
        rms = L.sbuf("rms", [T, GROUP])
        o = L.sbuf("o", [T, GROUP, D])
        p_a = L.psum("p_a", [T, BANK])
        p_b = L.psum("p_b", [T, BANK])
        p_seg = [L.psum(f"p_seg{n}", [T, 2, BANK]) for n in range(2)]
        p_y = L.psum("p_y", [T, 2, BANK])
        stats_ready = L.sem("stats_ready")
        rstd_ready = L.sem("rstd_ready")
        normed = L.sem("normed")
        x_h = L.sem("x_h")
        trans = L.sem("trans")
        h_t_ready = L.sem("h_t_ready")
        conv_in = L.sem("conv_in")
        padded_ready = L.sem("padded_ready")
        convolved = L.sem("convolved")
        conv_ready = L.sem("conv_ready")
        z_done = L.sem("z_done")
        gate_ready = L.sem("gate_ready")
        dt_done = L.sem("dt_done")
        dt_in = L.sem("dt_in")
        dt_exp = L.sem("dt_exp")
        da_ready = L.sem("da_ready")
        cum_done = L.sem("cum_done")
        high_ready = L.sem("high_ready")
        parts_ready = L.sem("parts_ready")
        cb_done = L.sem("cb_done")
        cb_ready = L.sem("cb_ready")
        x_turned = L.sem("x_turned")
        xs_half = L.sem("xs_half")
        xs_ready = L.sem("xs_ready")
        own_ready = L.sem("own_ready")
        seg_done = L.sem("seg_done")
        decay_ready = L.sem("decay_ready")
        mix_ready = L.sem("mix_ready")
        mixed = L.sem("mixed")
        y_ready = L.sem("y_ready")
        sq_ready = L.sem("sq_ready")
        ms_done = L.sem("ms_done")
        ms_ready = L.sem("ms_ready")
        rms_ready = L.sem("rms_ready")
        out_done = L.sem("out_done")
        o_scaled = L.sem("o_scaled")
        o_stats_ready = L.sem("o_stats_ready")
        o_rstd_ready = L.sem("o_rstd_ready")
        o_ready = L.sem("o_ready")
        o_order = L.sem("o_order")
        dve_order = L.sem("dve_order")
        setup = L.sem("setup")
        started = lambda i: not (isinstance(i, int) and i == 0)

        with nc.Block() as block:
            @block.tensor
            def _(pe):
                pe.wait_ge(loaded, w["n"])
                pe.wait_ge(setup, 4)

                def turn_h(j):
                    pe.wait_ge(normed, j + 1)
                    if started(j):
                        pe.wait_ge(xs_ready, j)
                    for u in range(GROUP):
                        last = nc.tensor.transpose(p_a[:, u * T:(u + 1) * T], h[:, u, :], const["ident"][:, :])
                    last.then_inc(trans, 1)

                def project(j, c):
                    if c < 2:
                        pe.wait_ge(h_t_ready, j + 1)
                    else:
                        pe.wait_ge(padded_ready, NC * j + c - 1)
                    nc.tensor.matmul((p_b, p_a)[c % 2][:, :], w["conv_in"][:, c * T:(c + 1) * T], h_t[:, :],
                                     start=True, stop=True).then_inc(conv_in, 1)

                def time_steps(j, after_output):
                    if after_output:
                        pe.wait_ge(ms_ready, j - 1)
                    else:
                        pe.wait_ge(padded_ready, NC * j + 3)
                    for u in range(GROUP):
                        last = nc.tensor.matmul(p_b[:, u * NH:(u + 1) * NH], h_t[:, u * T:(u + 1) * T], w["dt_in"][:, :],
                                                start=True, stop=True)
                    last.then_inc(dt_done, 1)

                def running_sums(j):
                    pe.wait_ge(da_ready, j + 1)
                    for u in range(GROUP):
                        last = nc.tensor.matmul(p_b[0:3 * NH, u * T:(u + 1) * T], da[:, u, :, :].rearrange("p r h -> p (r h)"),
                                                w["upto"][:, :], start=True, stop=True)
                    last.then_inc(cum_done, 1)

                def gates(j, b, after_output):
                    if b == 1:
                        pe.wait_ge(parts_ready, j + 1)
                    elif after_output:
                        pe.wait_ge(o_scaled, j - 1)
                    else:
                        pe.wait_ge(padded_ready, NC * j + 4)
                    nc.tensor.matmul((p_a, p_b)[b][:, :], w["z_in"][:, b * T:(b + 1) * T], h_t[:, :], start=True, stop=True)\
                        .then_inc(z_done, 1)

                def products(j, q):
                    pe.wait_ge(gate_ready, 2 * j + 2)
                    pe.wait_ge(conv_ready, j + 1)
                    for u in range(GROUP):
                        last = nc.tensor.matmul(p_a[:, u * T:(u + 1) * T], conv[:, q, 2, u, :], conv[:, q, 3, u, :],
                                                start=True, stop=True)
                    last.then_inc(cb_done, 1)

                def turn_x(j, q, b):
                    if b == 1:
                        pe.wait_ge(cb_ready, j + 1)
                    for u in range(GROUP):
                        last = nc.tensor.transpose((p_b, p_a)[b][:, u * T:(u + 1) * T], conv[:, q, b, u, :],
                                                   const["ident"][:, :])
                    last.then_inc(x_turned, 1)

                def segments(i, n, q):
                    u, part, g = n // 4, n % 4, i * NU + n
                    if n == 0:
                        pe.wait_ge(parts_ready, i + 1)
                    if not isinstance(g, int) or g >= 2:
                        pe.wait_ge(decay_ready, g - 1)
                    for half in range(2):
                        first = part * QH + 4 * half
                        out = p_seg[n % 2][:, half, :]
                        nc.tensor.matmul(out, ident_b[:, :], bcast(future_b[:, :], [T, 4, T], 1), start=True, stop=False)
                        nc.tensor.matmul(out, parts[:, q, u * T:(u + 1) * T], bcast(minus[:, first:first + 4], [3 * NH, 4, T], 2),
                                         start=False, stop=False)
                        for k in range(4):
                            last = nc.tensor.matmul(out[:, k * T:(k + 1) * T], pick[:, first + k, :],
                                                    parts[:, q, u * T:(u + 1) * T], start=False, stop=(k == 3))
                    last.then_inc(seg_done, 1)

                def mixing(i, n):
                    u, part = n // 4, n % 4
                    pe.wait_ge(mix_ready, i * NU + n + 1)
                    if part == 0:
                        pe.wait_ge(own_ready, i * GROUP + u + 1)
                        if u >= 2 or not isinstance(i, int) or i > 0:
                            pe.wait_ge(y_ready, i * GROUP + u - 1)
                    for k in range(QH):
                        head = part * QH + k
                        block_of = part // 2
                        last = nc.tensor.matmul(p_y[:, u % 2, block_of * T:(block_of + 1) * T],
                                                xdt_own[:, u % 2, head * T:(head + 1) * T], mix[:, n % 2, k, :],
                                                start=(head % 16 == 0), stop=(head % 16 == 15))
                    last.then_inc(mixed, 1)

                def output(j):
                    pe.wait_ge(sq_ready, GROUP * (j + 1))
                    for u in range(GROUP):
                        for b in range(2):
                            last = nc.tensor.matmul(p_b[:, 2 * u:2 * u + 2], sq[:, b, u, :], ones[:, :],
                                                    start=(b == 0), stop=(b == 1))
                    last.then_inc(ms_done, 1)
                    for u in range(GROUP):
                        for b in range(2):
                            last = nc.tensor.matmul(p_a[:, u * D:(u + 1) * D], y[:, b, u, :], out_w[:, b, :],
                                                    start=(b == 0), stop=(b == 1))
                    last.then_inc(out_done, 1)

                def start():
                    turn_h(0)
                    for c in range(NC):
                        project(0, c)
                    time_steps(0, False)
                    running_sums(0)
                    gates(0, 0, False)
                    gates(0, 1, False)
                    products(0, 0)
                    turn_x(0, 0, 0)
                    turn_x(0, 0, 1)
                    segments(0, 0, 0)

                def body(i, p, last_group):
                    j, q = i + 1, 1 - p
                    for n in range(NU):
                        if n + 1 < NU:
                            segments(i, n + 1, p)
                        elif not last_group:
                            segments(j, 0, q)
                        mixing(i, n)
                        if not last_group:
                            if n == 1:
                                turn_h(j)
                            if n == 2:
                                project(j, 0)
                                project(j, 1)
                            if n == 3:
                                project(j, 2)
                                project(j, 3)
                        if n == 4 and started(i):
                            if not last_group:
                                pe.wait_ge(padded_ready, NC * (j + 1))
                            output(i - 1)
                        if not last_group:
                            if n == 5:
                                time_steps(j, started(i))
                            if n == 9:
                                running_sums(j)
                            if n == 10:
                                gates(j, 0, started(i))
                            if n == 11:
                                gates(j, 1, started(i))
                            if n == 13:
                                products(j, q)
                                turn_x(j, q, 0)
                            if n == 14:
                                turn_x(j, q, 1)
                pipelined(pe, None, start, body)
                pe.wait_ge(o_scaled, NG - 1)
                output(NG - 1)

            @block.scalar
            def _(act):
                act.wait_ge(loaded, w["n"])
                nc.scalar.activation(neg_a[:, :], w["a_log"][:, :], ACT.Exp).then_inc(setup, 1)
                act.wait_ge(setup, 4)

                def copy_h(j):
                    act.wait_ge(trans, j + 1)
                    nc.scalar.copy(h_t[:, :], p_a[:, :]).then_inc(h_t_ready, 1)

                def pad_block(j, q, c):
                    act.wait_ge(conv_in, NC * j + c + 1)
                    source = (p_b, p_a)[c % 2][:, :].rearrange("p (u t) -> p u t", t=T)
                    nc.scalar.copy(padded[:, c, :, TAPS - 1:], source)
                    nc.scalar.activation(conv[:, q, c, :, :], source, ACT.Identity, bias=w["conv_b"][:, c:c + 1],
                                         scale=w["conv_w"][:, c, TAPS - 1:TAPS]).then_inc(padded_ready, 1)

                def time_exp(j):
                    act.wait_ge(dt_in, j + 1)
                    nc.scalar.activation(dt_raw[:, :, :], dt_raw[:, :, :], ACT.Exp, scale=-1.0).then_inc(dt_exp, 1)

                def split(j, q):
                    act.wait_ge(cum_done, j + 1)
                    split_high(nc, p_b, high, parts[:, q, :]).then_inc(high_ready, 1)

                def silus(j, q):
                    act.wait_ge(convolved, 2 * j + 2)
                    for c in (2, 3, 0, 1):
                        last = nc.scalar.activation(conv[:, q, c, :, :], conv[:, q, c, :, :], ACT.Silu)
                    last.then_inc(conv_ready, 1)
                    for b in range(2):
                        act.wait_ge(z_done, 2 * j + b + 1)
                        nc.scalar.activation(gate[:, q, b, :], (p_a, p_b)[b][:, :], ACT.Silu).then_inc(gate_ready, 1)

                def square(i, u):
                    act.wait_ge(y_ready, GROUP * i + u + 1)
                    nc.scalar.activation(sq[:, :, u, :], y[:, :, u, :], ACT.Square).then_inc(sq_ready, 1)

                def start():
                    copy_h(0)
                    for c in range(NC):
                        pad_block(0, 0, c)
                    time_exp(0)
                    split(0, 0)
                    silus(0, 0)

                def body(i, p, last_group):
                    j, q = i + 1, 1 - p
                    for n in range(NU):
                        g = i * NU + n
                        act.wait_ge(seg_done, g + 1)
                        if not isinstance(g, int) or g >= 2:
                            act.wait_ge(mix_ready, g - 1)
                        nc.scalar.activation(decay[:, n % 2, :, :], p_seg[n % 2][:, :, :], ACT.Exp).then_inc(decay_ready, 1)
                        if n == 2 and started(i):
                            square(i - 1, GROUP - 1)
                        if n in (7, 11, 14):
                            square(i, (n - 6) // 4)
                        if last_group:
                            continue
                        if n == 2:
                            copy_h(j)
                        if n in (3, 4):
                            pad_block(j, q, 2 * (n - 3))
                            pad_block(j, q, 2 * (n - 3) + 1)
                        if n == 7:
                            time_exp(j)
                        if n == 10:
                            split(j, q)
                        if n == 12:
                            silus(j, q)
                pipelined(act, None, start, body)
                square(NG - 1, GROUP - 1)

            @block.vector
            def _(dve):
                order = Order(dve, dve_order)
                dve.wait_ge(loaded, w["n"])
                nc.vector.memset(ones[:, :], 1.0)
                nc.vector.tensor_copy(ident_b[:, :], const["ident"][:, :])
                nc.vector.tensor_copy(pick[:, :, :], bcast(w["head_row"][:, :], [3 * NH, NH, T], 2))
                nc.vector.tensor_scalar(minus[:, :], w["head_row"][:, :], -1.0, None, ALU.mult)
                nc.vector.tensor_scalar(future_b[:, :], w["upto"][:, :], 1.0, -NEG, ALU.subtract, ALU.mult)
                nc.vector.memset(padded[:, :, :, :].rearrange("p c u t -> p (c u t)"), 0.0)
                nc.vector.tensor_tensor(out_w[:, :, :], w["out_w"][:, :, :], bcast(w["norm_w"][:, :], [T, 2, D], 2), ALU.mult)\
                    .then_inc(setup, 1)
                dve.wait_ge(setup, 3)
                nc.vector.tensor_scalar(neg_a[:, :], neg_a[:, :], -1.0, None, ALU.mult).then_inc(setup, 1)
                dve.wait_ge(setup, 4)

                def norm(j):
                    if started(j):
                        dve.wait_ge(trans, j)
                        dve.wait_ge(x_h, j)
                    layernorm_stats(nc, dve, order, x, j, stats, moments, pad).then_inc(stats_ready, 1)
                    dve.wait_ge(rstd_ready, j + 1)
                    layernorm_apply(nc, x, j, moments, rstd, h).then_inc(normed, 1)

                def tap(j, q, pair, k):
                    if k == 0:
                        dve.wait_ge(padded_ready, NC * j + 2 * pair + 2)
                    for c in (2 * pair, 2 * pair + 1):
                        last = nc.vector.scalar_tensor_tensor(conv[:, q, c, :, :], padded[:, c, :, k:k + T],
                                                              w["conv_w"][:, c, k:k + 1], conv[:, q, c, :, :],
                                                              ALU.mult, ALU.add)
                    if k < TAPS - 2:
                        order.then(last)
                    else:
                        last.then_inc(convolved, 1)

                def time_bias(j):
                    dve.wait_ge(dt_done, j + 1)
                    nc.vector.tensor_tensor(dt_raw[:, :, :], p_b[:, 0:GROUP * NH].rearrange("p (u h) -> p u h", h=NH),
                                            bcast(w["dt_bias"][:, :], [T, GROUP, NH], 1), ALU.add).then_inc(dt_in, 1)

                def time_step(j, q):
                    dve.wait_ge(dt_exp, j + 1)
                    order.then(nc.vector.tensor_scalar(dt_raw[:, :, :], dt_raw[:, :, :], 1.0, None, ALU.add))
                    order.then(nc.vector.reciprocal(dt_raw[:, :, :], dt_raw[:, :, :]))
                    order.then(nc.vector.tensor_scalar(dt[:, q, :, :], dt_raw[:, :, :], 0.1 - 0.001, 0.001, ALU.mult, ALU.add))
                    for r in range(3):
                        last = nc.vector.tensor_tensor(da[:, :, r, :], dt[:, q, :, :], bcast(neg_a[:, :], [T, GROUP, NH], 1), ALU.mult)
                    last.then_inc(da_ready, 1)

                def split(j, q):
                    dve.wait_ge(high_ready, j + 1)
                    split_rest(nc, order, p_b, high, rest, middle, parts[:, q, :]).then_inc(parts_ready, 1)

                def copy_products(j, q):
                    dve.wait_ge(cb_done, j + 1)
                    nc.vector.tensor_copy(cb[:, q, :, :], p_a[:, :]).then_inc(cb_ready, 1)

                def copy_x(j, b):
                    dve.wait_ge(x_turned, 2 * j + b + 1)
                    if b == 0 and started(j):
                        dve.wait_ge(own_ready, GROUP * j)
                    nc.vector.tensor_copy(xs_t[:, :, b * T:(b + 1) * T],
                                          (p_b, p_a)[b][:, :].rearrange("p (u c) -> p u c", u=GROUP))\
                        .then_inc((xs_half, xs_ready)[b], 1)

                def combine(i, n, p):
                    u, g = n // 4, i * NU + n
                    dve.wait_ge(decay_ready, g + 1)
                    if not isinstance(g, int) or g >= 2:
                        dve.wait_ge(mixed, g - 1)
                    nc.vector.tensor_tensor(mix[:, n % 2, :, :], decay[:, n % 2, :, :],
                                            bcast(cb[:, p, u, :], [T, QH, T], 1), ALU.mult).then_inc(mix_ready, 1)

                def gated(i, u, p):
                    dve.wait_ge(mixed, i * NU + 4 * (u + 1))
                    if u == 0:
                        dve.wait_ge(gate_ready, 2 * i + 2)
                        if started(i):
                            dve.wait_ge(out_done, i)
                    for b in range(2):
                        last = nc.vector.scalar_tensor_tensor(y[:, b, u, :], conv[:, p, b, u, :], w["d_skip"][:, b:b + 1],
                                                              p_y[:, u % 2, b * T:(b + 1) * T], ALU.mult, ALU.add)
                    order.then(last)
                    nc.vector.tensor_tensor(y[:, :, u, :], y[:, :, u, :], gate[:, p, :, u * T:(u + 1) * T], ALU.mult)\
                        .then_inc(y_ready, 1)

                def mean_square(j):
                    dve.wait_ge(ms_done, j + 1)
                    nc.vector.tensor_scalar(ms[:, :], p_b[:, 0:2 * GROUP].rearrange("p (u two) -> p u two", two=2)[:, :, 0],
                                            1.0 / 256.0, 1e-5, ALU.mult, ALU.add).then_inc(ms_ready, 1)

                def norm_output(j):
                    dve.wait_ge(out_done, j + 1)
                    dve.wait_ge(rms_ready, j + 1)
                    nc.vector.tensor_tensor(o[:, :, :], p_a[:, :].rearrange("p (u d) -> p u d", d=D),
                                            bcast(rms[:, :], [T, GROUP, D], 2), ALU.mult).then_inc(o_scaled, 1)
                    dve.wait_ge(o_scaled, j + 1)
                    layernorm_stats(nc, dve, order, o, 0, stats, moments, pad).then_inc(o_stats_ready, 1)
                    dve.wait_ge(o_rstd_ready, j + 1)
                    layernorm_apply(nc, o, 0, moments, rstd, o).then_inc(o_ready, 1)

                def start():
                    norm(0)
                    for k in range(TAPS - 1):
                        tap(0, 0, 0, k)
                    time_bias(0)
                    time_step(0, 0)
                    for k in range(TAPS - 1):
                        tap(0, 0, 1, k)
                    split(0, 0)
                    copy_products(0, 0)
                    copy_x(0, 0)
                    copy_x(0, 1)

                def body(i, p, last_group):
                    j, q = i + 1, 1 - p
                    dve.wait_ge(cb_ready, i + 1)
                    for n in range(NU):
                        combine(i, n, p)
                        if n == 0 and not last_group:
                            norm(j)
                        if n == 1 and started(i):
                            gated(i - 1, GROUP - 1, q)
                        if n == 5 and started(i):
                            mean_square(i - 1)
                        if n in (6, 10, 13):
                            gated(i, (n - 6 + 1) // 4, p)
                        if n == 7 and started(i):
                            norm_output(i - 1)
                        if last_group:
                            continue
                        if n in (4, 5, 6):
                            tap(j, q, 0, n - 4)
                        if n == 6:
                            time_bias(j)
                        if n == 8:
                            time_step(j, q)
                        if n in (8, 9, 10):
                            tap(j, q, 1, n - 8)
                        if n == 11:
                            split(j, q)
                        if n == 14:
                            copy_products(j, q)
                            copy_x(j, 0)
                        if n == 15:
                            copy_x(j, 1)
                pipelined(dve, order, start, body, per=2 + 4 + 2 + 4 + 3 + 2)
                gated(NG - 1, GROUP - 1, 1)
                mean_square(NG - 1)
                norm_output(NG - 1)

            @block.gpsimd
            def _(pool):
                nc.gpsimd.memset(xdt_own[:, :, :].rearrange("p a b -> p (a b)"), 0.0).then_inc(setup, 1)
                pool.wait_ge(setup, 4)

                def add_h(j):
                    pool.wait_ge(normed, j + 1)
                    xs = x[:, bass.ts(j, GROUP), :]
                    nc.gpsimd.tensor_tensor(xs, xs, h[:, :, :], ALU.add).then_inc(x_h, 1)

                def own(i, u, p):
                    if u == 0:
                        pool.wait_ge(xs_ready, i + 1)
                    if u >= 2 or not isinstance(i, int) or i > 0:
                        pool.wait_ge(mixed, i * NU + 4 * (u - 1))
                    for b in range(2):
                        dst = xdt_own[:, u % 2, b * 16 * T:(b + 1) * 16 * T]
                        dst = bass.AP(dst.tensor, dst.offset, [dst.ap[0], [T + P8, 16], [1, P8]])
                        last = nc.gpsimd.tensor_tensor(
                            dst, xs_t[:, u, b * T:(b + 1) * T].rearrange("p (h d) -> p h d", d=P8),
                            bcast(dt[:, p, u, 16 * b:16 * b + 16], [T, 16, P8], 2), ALU.mult)
                    last.then_inc(own_ready, 1)

                def rms_scale(j):
                    pool.wait_ge(ms_ready, j + 1)
                    nc.gpsimd.tensor_tensor(rms[:, :], ms[:, :], const["minus_half"][:, 0:GROUP], ALU.pow).then_inc(rms_ready, 1)

                def norm_scale(j):
                    layernorm_rstd(nc, pool, stats_ready, j, const["minus_half"], moments, rstd).then_inc(rstd_ready, 1)

                def output_scale(j):
                    layernorm_rstd(nc, pool, o_stats_ready, j, const["minus_half"], moments, rstd).then_inc(o_rstd_ready, 1)

                def add_output(j):
                    pool.wait_ge(o_ready, j + 1)
                    nc.gpsimd.tensor_tensor(o[:, :, :], o[:, :, :], bcast(w["ln_w"][:, :], [T, GROUP, D], 1), ALU.mult)\
                        .then_inc(o_order, 1)
                    pool.wait_ge(o_order, 2 * j + 1)
                    nc.gpsimd.tensor_tensor(o[:, :, :], o[:, :, :], bcast(w["ln_b"][:, :], [T, GROUP, D], 1), ALU.add)\
                        .then_inc(o_order, 1)
                    pool.wait_ge(o_order, 2 * j + 2)
                    xs = x[:, bass.ts(j, GROUP), :]
                    nc.gpsimd.tensor_tensor(xs, xs, o[:, :, :], ALU.add)

                def start():
                    norm_scale(0)
                    add_h(0)
                    own(0, 0, 0)

                def body(i, p, last_group):
                    if not last_group:
                        norm_scale(i + 1)
                    own(i, 1, p)
                    if not last_group:
                        add_h(i + 1)
                    own(i, 2, p)
                    if started(i):
                        rms_scale(i - 1)
                        output_scale(i - 1)
                        add_output(i - 1)
                    own(i, 3, p)
                    if not last_group:
                        own(i + 1, 0, 1 - p)
                pipelined(pool, None, start, body)
                rms_scale(NG - 1)
                output_scale(NG - 1)
                add_output(NG - 1)


def sparse_attention(nc, name, x, const, w, loaded):
    S = 32
    ROWS = GROUP * HEADS
    LI = 16
    scale = float(HD) ** -0.5
    with ExitStack() as ctx:
        L = Layer(nc, ctx, name)
        stats = L.sbuf("stats", [T, GROUP, 6])
        moments = L.sbuf("moments", [T, GROUP, 2])
        pad = L.sbuf("pad", [T, 1])
        rstd = L.sbuf("rstd", [T, GROUP])
        h = L.sbuf("h", [T, GROUP, D])
        h_t = L.sbuf("h_t", [D, GROUP * T])
        q_t = L.sbuf("q_t", [D, GROUP * T])
        scaled_bq = L.sbuf("scaled_bq", [D, 1])
        k_t = L.sbuf("k_t", [D, S])
        k_rep = L.sbuf("k_rep", [D, 4, S])
        keys = L.sbuf("keys", [D, HEADS, S])
        vals = L.sbuf("vals", [T, D])
        vals_own = L.sbuf("vals_own", [T, 4, D])
        z = L.sbuf("z", [T, ROWS, S])
        srt = [L.sbuf(f"srt{n}", [T, ROWS, S]) for n in range(2)]
        starts = L.sbuf("starts", [T, ROWS, S])
        tau = L.sbuf("tau", [T, ROWS])
        a_t = L.sbuf("a_t", [T, 4, GROUP * T])
        o_t = L.sbuf("o_t", [D, GROUP * T])
        apart = L.sbuf("apart", [D, 2, LI, T])
        out = L.sbuf("out", [T, GROUP, D])
        p_misc = L.psum("p_misc", [T, BANK])
        p_q = L.psum("p_q", [T, BANK])
        p_out = L.psum("p_out", [T, GROUP, D])
        p_s = [L.psum(f"p_s{n}", [T, BANK]) for n in range(4)]
        stats_ready = L.sem("stats_ready")
        rstd_ready = L.sem("rstd_ready")
        normed = L.sem("normed")
        trans = L.sem("trans")
        h_t_ready = L.sem("h_t_ready")
        proj = L.sem("proj")
        q_ready = L.sem("q_ready")
        scored = L.sem("scored")
        z_ready = L.sem("z_ready")
        shifted = L.sem("shifted")
        clipped = L.sem("clipped")
        turned = L.sem("turned")
        turned_out = L.sem("turned_out")
        weighed = L.sem("weighed")
        o_t_ready = L.sem("o_t_ready")
        apart_ready = L.sem("apart_ready")
        out_done = L.sem("out_done")
        added = L.sem("added")
        dve_order = L.sem("dve_order")
        kv_done = L.sem("kv_done")
        kv_ready = L.sem("kv_ready")

        def blocks(t, size):
            return t[:, :, :].rearrange("p r s -> p (r s)").rearrange("p (b e) -> p b e", e=size)

        with nc.Block() as block:
            @block.tensor
            def _(pe):
                pe.wait_ge(loaded, w["n"])
                nc.tensor.matmul(p_misc[:, 0:S], w["wk"][:, :], w["key_t"][:, :], start=True, stop=True)\
                    .then_inc(kv_done, 1)
                pe.wait_ge(kv_ready, 2)
                nc.tensor.matmul(p_misc[:, 0:D], k_rep[:, :, :], w["wv"][:, :], start=True, stop=True).then_inc(kv_done, 1)
                pe.wait_ge(kv_ready, 3)

                def body(i, first):
                    pe.wait_ge(normed, i + 1)
                    if not first:
                        pe.wait_ge(added, i)
                    for u in range(GROUP):
                        last = nc.tensor.transpose(p_misc[:, u * T:(u + 1) * T], h[:, u, :], const["ident"][:, :])
                    last.then_inc(trans, 1)
                    pe.wait_ge(h_t_ready, i + 1)
                    nc.tensor.matmul(p_q[:, :], w["wq"][:, :], h_t[:, :], start=True, stop=True).then_inc(proj, 1)
                    pe.wait_ge(q_ready, i + 1)
                    for u in range(GROUP):
                        nc.tensor.matmul(p_s[u][:, :], q_t[:, u * T:(u + 1) * T], keys[:, :, :], start=True, stop=True)\
                            .then_inc(scored, 1)
                    pe.wait_ge(clipped, i + 1)
                    for b in range(4):
                        for u in range(GROUP):
                            row = u * HEADS + 4 * b
                            last = nc.tensor.transpose(p_s[b][:, u * T:(u + 1) * T], z[:, row:row + 4, :],
                                                       const["ident"][:, :])
                        last.then_inc(turned, 1)
                    for b in range(4):
                        pe.wait_ge(turned_out, 4 * i + b + 1)
                        last = nc.tensor.matmul(p_q[:, :], vals_own[:, b, :], a_t[:, b, :], start=(b == 0), stop=(b == 3))
                    last.then_inc(weighed, 1)
                    for u in range(GROUP):
                        pe.wait_ge(apart_ready, GROUP * i + u + 1)
                        for li in range(LI):
                            last = nc.tensor.matmul(p_out[:, u, :], apart[:, u % 2, li, :], w["wo"][:, li, :],
                                                    start=(li == 0), stop=(li == LI - 1))
                        last.then_inc(out_done, 1)
                groups(pe, None, body)

            @block.scalar
            def _(act):
                act.wait_ge(kv_ready, 3)

                def body(i, first):
                    act.wait_ge(trans, i + 1)
                    nc.scalar.copy(h_t[:, :], p_misc[:, :]).then_inc(h_t_ready, 1)
                    act.wait_ge(proj, i + 1)
                    nc.scalar.activation(q_t[:, :], p_q[:, :], ACT.Identity, bias=scaled_bq[:, 0:1], scale=scale)\
                        .then_inc(q_ready, 1)
                    for u in range(GROUP):
                        act.wait_ge(scored, GROUP * i + u + 1)
                        nc.scalar.copy(z[:, u * HEADS:(u + 1) * HEADS, :], p_s[u][:, :]).then_inc(z_ready, 1)
                    act.wait_ge(shifted, i + 1)
                    nc.scalar.activation(z[:, :, :], z[:, :, :], ACT.Relu).then_inc(clipped, 1)
                    for b in range(4):
                        act.wait_ge(turned, 4 * i + b + 1)
                        nc.scalar.copy(a_t[:, b, :], p_s[b][:, :]).then_inc(turned_out, 1)
                    act.wait_ge(weighed, i + 1)
                    nc.scalar.copy(o_t[:, :], p_q[:, :]).then_inc(o_t_ready, 1)
                groups(act, None, body)

            @block.vector
            def _(dve):
                order = Order(dve, dve_order)
                dve.wait_ge(loaded, w["n"])
                nc.vector.tensor_scalar(scaled_bq[:, :], w["bq"][:, :], scale, None, ALU.mult)
                nc.vector.memset(starts[:, :, :], 1.0).then_inc(kv_ready, 1)
                dve.wait_ge(kv_ready, 1)
                nc.vector.memset(starts[:, :, 0:1], 0.0)
                dve.wait_ge(kv_done, 1)
                order.then(nc.vector.tensor_scalar(k_t[:, :], p_misc[:, 0:S], w["bk"][:, 0:1], None, ALU.add))
                nc.vector.tensor_copy(k_rep[:, :, :], bcast(k_t[:, :], [D, 4, S], 1)).then_inc(kv_ready, 1)
                nc.vector.tensor_tensor(keys[:, :, :], bcast(k_t[:, :], [D, HEADS, S], 1),
                                        bcast(const["head_of"][:, :], [D, HEADS, S], 2), ALU.mult)
                dve.wait_ge(kv_done, 2)
                order.then(nc.vector.tensor_tensor(vals[:, :], p_misc[:, 0:D], w["bv"][:, :], ALU.add))
                nc.vector.tensor_tensor(vals_own[:, :, :], bcast(vals[:, :], [T, 4, D], 1), w["own"][:, :, :], ALU.mult)\
                    .then_inc(kv_ready, 1)
                setup_steps = order.n
                order.n = 0

                def body(i, first):
                    order.base = order.base + setup_steps
                    if not first:
                        dve.wait_ge(added, i)
                        dve.wait_ge(trans, i)
                    layernorm_stats(nc, dve, order, x, i, stats, moments, pad).then_inc(stats_ready, 1)
                    dve.wait_ge(rstd_ready, i + 1)
                    layernorm_apply(nc, x, i, moments, rstd, h).then_inc(normed, 1)
                    dve.wait_ge(z_ready, GROUP * (i + 1))
                    src, dst, at = z, srt[0], 0
                    size = 2
                    while size <= S:
                        step = size // 2
                        while step:
                            if 2 * step == size:
                                a, b = blocks(src, size)[:, :, 0:step], blocks(src, size)[:, :, size - 1:step - 1:-1]
                                da, db = blocks(dst, size)[:, :, 0:step], blocks(dst, size)[:, :, size - 1:step - 1:-1]
                            else:
                                a, b = blocks(src, 2 * step)[:, :, 0:step], blocks(src, 2 * step)[:, :, step:2 * step]
                                da, db = blocks(dst, 2 * step)[:, :, 0:step], blocks(dst, 2 * step)[:, :, step:2 * step]
                            nc.vector.tensor_tensor(da, a, b, ALU.max)
                            order.then(nc.vector.tensor_tensor(db, a, b, ALU.min))
                            at = 1 - at
                            src, dst = dst, srt[at]
                            step //= 2
                        size *= 2
                    flat = lambda t: t[:, :, :].rearrange("p r s -> p (r s)")
                    order.then(nc.vector.tensor_tensor_scan(flat(dst), flat(starts), flat(src), 0.0, ALU.mult, ALU.add))
                    order.then(nc.vector.scalar_tensor_tensor(src[:, :, :], dst[:, :, :], 1.0,
                                                              bcast(w["inv"][:, :], [T, ROWS, S], 1),
                                                              ALU.subtract, ALU.mult))
                    order.then(nc.vector.tensor_reduce(tau[:, :], src[:, :, :], AX.X, ALU.max))
                    nc.vector.tensor_tensor(z[:, :, :], z[:, :, :], bcast(tau[:, :], [T, ROWS, S], 2), ALU.subtract)\
                        .then_inc(shifted, 1)
                    dve.wait_ge(out_done, GROUP * (i + 1))
                    order.then(nc.vector.tensor_tensor(out[:, :, :], p_out[:, :, :], bcast(w["bo"][:, :], [T, GROUP, D], 1),
                                                       ALU.add))
                    xs = x[:, bass.ts(i, GROUP), :]
                    nc.vector.tensor_tensor(xs, xs, out[:, :, :], ALU.add).then_inc(added, 1)
                groups(dve, order, body)

            @block.gpsimd
            def _(pool):
                def body(i, first):
                    layernorm_rstd(nc, pool, stats_ready, i, const["minus_half"], moments, rstd).then_inc(rstd_ready, 1)
                    pool.wait_ge(o_t_ready, i + 1)
                    for u in range(GROUP):
                        if not first:
                            pool.wait_ge(out_done, GROUP * i + u - 1)
                        elif u >= 2:
                            pool.wait_ge(out_done, u - 1)
                        nc.gpsimd.tensor_tensor(
                            apart[:, u % 2, :, :].rearrange("p l (h o) -> p l h o", h=HEADS),
                            o_t[:, u * T:(u + 1) * T].rearrange("p (o l) -> p l o", l=LI).unsqueeze(2)
                            .broadcast_to([D, LI, HEADS, T // LI]),
                            const["head_of"][:, :].unsqueeze(1).unsqueeze(3).broadcast_to([D, LI, HEADS, T // LI]),
                            ALU.mult).then_inc(apart_ready, 1)
                groups(pool, None, body)


def quantized(nc, name, x, const, w, loaded):
    MAGIC = 12582912.0
    with ExitStack() as ctx:
        L = Layer(nc, ctx, name)
        stats = L.sbuf("stats", [T, GROUP, 6])
        moments = L.sbuf("moments", [T, GROUP, 2])
        pad = L.sbuf("pad", [T, 1])
        rstd = L.sbuf("rstd", [T, GROUP])
        h = L.sbuf("h", [T, GROUP, D])
        mag = L.sbuf("mag", [T, GROUP, D])
        q = L.sbuf("q", [T, GROUP, D])
        q_t = L.sbuf("q_t", [D, GROUP * T], BF16)
        wq = L.sbuf("wq", [D, D], BF16)
        amax = L.sbuf("amax", [T, GROUP])
        scale = L.sbuf("scale", [T, GROUP])
        out = L.sbuf("out", [T, GROUP, D])
        p_t = L.psum("p_t", [T, BANK])
        p_out = L.psum("p_out", [T, GROUP, D])
        stats_ready = L.sem("stats_ready")
        rstd_ready = L.sem("rstd_ready")
        normed = L.sem("normed")
        mag_ready = L.sem("mag_ready")
        rounded = L.sem("rounded")
        trans = L.sem("trans")
        q_t_ready = L.sem("q_t_ready")
        out_done = L.sem("out_done")
        added = L.sem("added")
        dve_order = L.sem("dve_order")
        setup = L.sem("setup")
        with nc.Block() as block:
            @block.tensor
            def _(pe):
                pe.wait_ge(setup, 1)

                def body(i, first):
                    pe.wait_ge(rounded, i + 1)
                    for u in range(GROUP):
                        last = nc.tensor.transpose(p_t[:, u * T:(u + 1) * T], q[:, u, :], const["ident"][:, :])
                    last.then_inc(trans, 1)
                    pe.wait_ge(q_t_ready, i + 1)
                    if not first:
                        pe.wait_ge(added, i)
                    for u in range(GROUP):
                        last = nc.tensor.matmul(p_out[:, u, :], q_t[:, u * T:(u + 1) * T], wq[:, :], start=True, stop=True)
                    last.then_inc(out_done, 1)
                groups(pe, None, body)

            @block.scalar
            def _(act):
                def body(i, first):
                    act.wait_ge(normed, i + 1)
                    nc.scalar.activation(mag[:, :, :], h[:, :, :], ACT.Abs).then_inc(mag_ready, 1)
                    act.wait_ge(trans, i + 1)
                    nc.scalar.copy(q_t[:, :], p_t[:, :]).then_inc(q_t_ready, 1)
                groups(act, None, body)

            @block.vector
            def _(dve):
                order = Order(dve, dve_order)
                dve.wait_ge(loaded, w["n"])
                nc.vector.tensor_copy(wq[:, :], w["wq"][:, :]).then_inc(setup, 1)

                def body(i, first):
                    if not first:
                        dve.wait_ge(added, i)
                        dve.wait_ge(trans, i)
                    layernorm_stats(nc, dve, order, x, i, stats, moments, pad).then_inc(stats_ready, 1)
                    dve.wait_ge(rstd_ready, i + 1)
                    layernorm_apply(nc, x, i, moments, rstd, h).then_inc(normed, 1)
                    dve.wait_ge(mag_ready, i + 1)
                    order.then(nc.vector.tensor_reduce(amax[:, :], mag[:, :, :], AX.X, ALU.max))
                    order.then(nc.vector.tensor_scalar(amax[:, :], amax[:, :], 1e-6, None, ALU.max))
                    order.then(nc.vector.tensor_scalar(scale[:, :], amax[:, :], 1.0 / 127.0, None, ALU.mult))
                    order.then(nc.vector.reciprocal(amax[:, :], scale[:, :]))
                    order.then(nc.vector.tensor_tensor(q[:, :, :], h[:, :, :], bcast(amax[:, :], [T, GROUP, D], 2),
                                                       ALU.mult))
                    order.then(nc.vector.tensor_scalar(q[:, :, :], q[:, :, :], MAGIC, MAGIC, ALU.add, ALU.subtract))
                    nc.vector.tensor_scalar(q[:, :, :], q[:, :, :], 127.0, -128.0, ALU.min, ALU.max).then_inc(rounded, 1)
                    dve.wait_ge(out_done, i + 1)
                    order.then(nc.vector.tensor_tensor(out[:, :, :], p_out[:, :, :], bcast(scale[:, :], [T, GROUP, D], 2),
                                                       ALU.mult))
                    order.then(nc.vector.tensor_tensor(out[:, :, :], out[:, :, :], bcast(w["scale"][:, :], [T, GROUP, D], 1),
                                                       ALU.mult))
                    order.then(nc.vector.tensor_tensor(out[:, :, :], out[:, :, :], bcast(w["bias"][:, :], [T, GROUP, D], 1),
                                                       ALU.add))
                    xs = x[:, bass.ts(i, GROUP), :]
                    nc.vector.tensor_tensor(xs, xs, out[:, :, :], ALU.add).then_inc(added, 1)
                groups(dve, order, body)

            @block.gpsimd
            def _(pool):
                def body(i, first):
                    layernorm_rstd(nc, pool, stats_ready, i, const["minus_half"], moments, rstd).then_inc(rstd_ready, 1)
                groups(pool, None, body)


def layer3(nc, x, const, w, loaded, aps):
    attention16(nc, "l3", x, {**const, "causal": w["causal"]}, w, loaded, latent=True, causal=True)


def layer4(nc, x, const, w, loaded, aps):
    attention16(nc, "l4", x, const, w, loaded, ctx_t=aps["ctx_t"], key_mask=True, qkv_bias=True, out_bias=True)


def layer7(nc, x, const, w, loaded, aps):
    with ExitStack() as ctx:
        rel = ctx.enter_context(nc.sbuf_tensor("l7_rel", [T, HEADS, T], F32))
        table = aps["rel_table"]
        rel_in = ctx.enter_context(nc.semaphore("rel_in"))
        with nc.Block() as block:
            @block.sync
            def _(sp):
                for head in range(HEADS):
                    src = bass.AP(table.tensor, head * 511 + 128, [[1, T], [1, T]])
                    sp.dma_start(rel[:, head, :], src).then_inc(rel_in, 16)
                sp.wait_ge(rel_in, 16 * HEADS)
        attention16(nc, "l7", x, {**const, "flip": w["flip"]}, {**w, "rel": rel}, loaded, ctx_t=aps["ctx_t"],
                    rel_bias=True, out_bias=True)


def layer2(nc, x, const, w, loaded, aps):
    experts(nc, "l2", x, const, w, loaded, "groups")


def layer5(nc, x, const, w, loaded, aps):
    experts(nc, "l5", x, const, w, loaded, "top2")


def layer8(nc, x, const, w, loaded, aps):
    experts(nc, "l8", x, const, w, loaded, "top1")


def layer1(nc, x, const, w, loaded, aps):
    attention8(nc, "l1", x, const, w, loaded, aps["ctx_t"])


def layer6(nc, x, const, w, loaded, aps):
    attention1(nc, "l6", x, const, w, loaded, aps, cross=False)


def layer10(nc, x, const, w, loaded, aps):
    attention1(nc, "l10", x, const, w, loaded, aps, cross=True)


def layer11(nc, x, const, w, loaded, aps):
    quantized(nc, "l11", x, const, w, loaded)


def layer0(nc, x, const, w, loaded, aps):
    state_space(nc, "l0", x, const, w, loaded)


def layer9(nc, x, const, w, loaded, aps):
    sparse_attention(nc, "l9", x, const, w, loaded)


LAYERS = {0: layer0, 9: layer9, 1: layer1, 6: layer6, 10: layer10, 11: layer11, 2: layer2, 3: layer3, 4: layer4, 5: layer5, 7: layer7, 8: layer8}


TABLE = [
    (-1, "ident", "ident", 0, False),
    (-1, "head_of", "head_of", 0, False),
    (-1, "minus_half", "minus_half", 0, False),
    (-1, "falling4", "falling4", T, True),
    (-1, "falling8", "falling8", T, True),
    (-1, "falling16", "falling16", T, True),
    (0, "conv_in", "mam_conv_in", 0, False),
    (0, "z_in", "mam_z_in", 0, False),
    (0, "dt_in", "mam_dt_in", 0, False),
    (0, "conv_w", "mam_conv_w", 0, False),
    (0, "conv_b", "mam_conv_b", 0, False),
    (0, "dt_bias", "mam_dt_bias", T, True),
    (0, "a_log", "mam_a_log", T, True),
    (0, "d_skip", "mam_d_skip", 0, False),
    (0, "norm_w", "mam_norm_w", 0, False),
    (0, "out_w", "mam_out_w", 0, False),
    (0, "ln_w", "mam_ln_w", T, True),
    (0, "ln_b", "mam_ln_b", T, True),
    (0, "upto", "mam_upto", 0, False),
    (0, "head_row", "mam_head_row", 0, False),
    (9, "key_t", "l3a_key", 0, False),
    (9, "wq", "L3_attn_Wq", 0, False),
    (9, "wk", "L3_attn_Wk", 0, False),
    (9, "wv", "L3_attn_Wv", 0, False),
    (9, "wo", "l3a_wo", 0, False),
    (9, "bq", "l3a_bq", 0, False),
    (9, "bk", "l3a_bk", 0, False),
    (9, "bv", "l3a_bv", T, True),
    (9, "bo", "l3a_bo", T, True),
    (9, "own", "l3a_own", 0, False),
    (9, "inv", "l3a_inv", T, True),
    (1, "wq", "L0_xattn_Wq1", 0, False),
    (1, "wk1", "L0_xattn_Wk1", 0, False),
    (1, "wk2", "L0_xattn_Wk2", 0, False),
    (1, "wv1", "L0_xattn_Wv1", 0, False),
    (1, "wv2", "L0_xattn_Wv2", 0, False),
    (1, "wo", "l0x_wo", 0, False),
    (1, "bo", "l0x_bo", T, True),
    (2, "router", "l0f_router", 0, False),
    (2, "gate_bias", "l0f_bias", T, True),
    (2, "pick", "l0f_pick", 0, False),
    (2, "wg", "l0f_wg", 0, False),
    (2, "wu", "l0f_wu", 0, False),
    (2, "wd", "l0f_wd", 0, False),
    (5, "rw1", "L1_ffn_rw1", 0, False),
    (5, "rb1", "l1f_rb1", 0, False),
    (5, "router", "L1_ffn_rw2", 0, False),
    (5, "rb2", "l1f_rb2", T, True),
    (5, "pick", "pick8", 0, False),
    (5, "wg", "l1f_w1", 0, False),
    (5, "eb1", "l1f_eb1", 0, False),
    (5, "wd", "l1f_w2", 0, False),
    (5, "eb2", "L1_ffn_eb2", 0, False),
    (6, "wq", "l2a_wq", 0, False),
    (6, "wk", "l2a_wk", 0, False),
    (6, "wv", "l2a_wv", 0, False),
    (6, "bq", "l2a_bq", 0, False),
    (6, "bk", "l2a_bk", 0, False),
    (6, "bv", "l2a_bv", T, True),
    (10, "wo", "l3x_wo", 0, False),
    (10, "bo", "l3x_bo", T, True),
    (11, "wq", "l3f_wq", 0, False),
    (11, "scale", "l3f_scale", T, True),
    (11, "bias", "l3f_bias", T, True),
    (8, "router", "L2_ffn_Wr", 0, False),
    (8, "pick", "pick7", 0, False),
    (8, "wg", "l2f_wg", 0, False),
    (8, "wu", "l2f_wu", 0, False),
    (8, "wd", "l2f_wd", 0, False),
    (3, "causal", "causal", 0, False),
    (3, "down", "L1_attn_Wc_down", 0, False),
    (3, "wq", "L1_attn_Wq_up", 0, False),
    (3, "wk", "l1_wk", 0, False),
    (3, "wv", "l1_wv", 0, False),
    (3, "wo", "L1_attn_Wc_proj", 0, False),
    (4, "wq", "l1x_wq", 0, False),
    (4, "wk", "l1x_wk", 0, False),
    (4, "wv", "l1x_wv", 0, False),
    (4, "wo", "l1x_wo", 0, False),
    (4, "bq", "l1x_bq", 0, False),
    (4, "bk", "l1x_bk", 0, False),
    (4, "bv", "l1x_bv", T, True),
    (4, "bo", "l1x_bo", T, True),
    (4, "mask", "mask", 0, False),
    (7, "wq", "l2x_wq", 0, False),
    (7, "wk", "l2x_wk", 0, False),
    (7, "wv", "l2x_wv", 0, False),
    (7, "wo", "l2x_wo", 0, False),
    (7, "bo", "l2x_bo", T, True),
    (7, "flip", "flip", 0, False),
]


def lay_out(a):
    c = np.ascontiguousarray
    a = {k: np.asarray(v) for k, v in a.items()}
    o = {"x": c(a["x"].transpose(1, 0, 2)), "ctx_t": c(a["ctx_1024"].transpose(2, 0, 1).reshape(D, NB * T))}
    o["ident"] = np.eye(T, dtype=np.float32)
    o["minus_half"] = np.full((T, 8), -0.5, np.float32)
    o["flip"] = c(np.eye(T, dtype=np.float32)[::-1])
    o["causal"] = np.where(np.tril(np.ones((T, T), bool)), 0.0, -1e30).astype(np.float32)
    o["head_of"] = c(np.repeat(np.eye(HEADS, dtype=np.float32), HD, axis=0))
    for n in ("L1_attn_Wc_down", "L1_attn_Wq_up", "L1_attn_Wc_proj"):
        o[n] = a[n]
    o["l1_wk"] = np.tile(a["L1_attn_Wkv_up"][:, :HD], (1, HEADS))
    o["l1_wv"] = np.tile(a["L1_attn_Wkv_up"][:, HD:], (1, HEADS))
    for n in "qkvo":
        o[f"l1x_w{n}"] = c(a[f"L1_xattn_W{n}"].T)
    o["l1x_bq"], o["l1x_bk"] = a["L1_xattn_bq"].reshape(D, 1), a["L1_xattn_bk"].reshape(D, 1)
    o["l1x_bv"], o["l1x_bo"] = a["L1_xattn_bv"].reshape(1, D), a["L1_xattn_bo"].reshape(1, D)
    o["mask"] = a["mask_BxS2_ik0"].reshape(1, NB * T)
    for n in "qkv":
        o[f"l2x_w{n}"] = c(a[f"L2_xattn_w{n}"].T)
    o["l2x_wo"], o["l2x_bo"] = c(a["L2_xattn_fc_w"].T), a["L2_xattn_fc_b"].reshape(1, D)
    o["rel_table"] = c(a["L2_xattn_rel_table"].T)
    for n in (4, 8, 16):
        o[f"falling{n}"] = np.arange(n, 0, -1, dtype=np.float32).reshape(1, n)
    rows = lambda e: np.tile(np.pad(e, ((0, 32 - e.shape[0]), (0, 0), (0, 0))), (3, 1, 1))
    o["pick8"] = rows(np.repeat(np.eye(8, dtype=np.float32)[:, :, None], T, axis=2))
    o["pick7"] = c(o["pick8"][:, :7])
    o["l0f_pick"] = rows(np.repeat(np.eye(16, dtype=np.float32), 64, axis=1).reshape(16, 8, T))
    o["l0f_router"] = c(a["L0_ffn_gate_w"].T)
    o["l0f_bias"] = a["L0_ffn_gate_bias"].reshape(1, 16)
    for n, s in (("g", "Ws_g"), ("u", "Ws_u")):
        both = np.concatenate([a[f"L0_ffn_W{n}"].reshape(8, T, D), a[f"L0_ffn_{s}"][None]])
        o[f"l0f_w{n}"] = c(both.transpose(2, 0, 1))
    both = np.concatenate([a["L0_ffn_Wd"].transpose(0, 2, 1).reshape(8, T, D), a["L0_ffn_Ws_d"].T[None]])
    o["l0f_wd"] = c(both.transpose(1, 0, 2))
    for n in ("L1_ffn_rw1", "L1_ffn_rw2", "L1_ffn_eb2", "L2_ffn_Wr"):
        o[n] = a[n]
    o["l1f_rb1"], o["l1f_rb2"] = a["L1_ffn_rb1"].reshape(D, 1), a["L1_ffn_rb2"].reshape(1, 8)
    o["l1f_w1"] = c(a["L1_ffn_ew1"].transpose(1, 0, 2).reshape(D, 16, T))
    o["l1f_eb1"] = c(a["L1_ffn_eb1"].reshape(16, T).T)
    o["l1f_w2"] = c(a["L1_ffn_ew2"].reshape(16, T, D).transpose(1, 0, 2))
    for n in "gu":
        both = np.concatenate([a[f"L2_ffn_W{n}"], a[f"L2_ffn_W{n}_s"][None]])
        o[f"l2f_w{n}"] = c(both.transpose(1, 0, 2).reshape(D, 32, T))
    both = np.concatenate([a["L2_ffn_Wd"], a["L2_ffn_Wd_s"][None]])
    o["l2f_wd"] = c(both.reshape(32, T, D).transpose(1, 0, 2))
    for n in ("Wq1", "Wk1", "Wk2", "Wv1", "Wv2"):
        o[f"L0_xattn_{n}"] = a[f"L0_xattn_{n}"]
    o["l0x_wo"], o["l0x_bo"] = c(a["L0_xattn_Wo"].reshape(4, T, D).transpose(1, 0, 2)), a["L0_xattn_bo"].reshape(1, D)
    for n in "qkv":
        o[f"l2a_w{n}"] = c(a[f"L2_attn_w{n}"].T)
    o["l2a_bq"], o["l2a_bk"] = a["L2_attn_bq"].reshape(D, 1), a["L2_attn_bk"].reshape(D, 1)
    o["l2a_bv"] = a["L2_attn_bv"].reshape(1, D)
    o["l3x_wo"], o["l3x_bo"] = c(a["L3_xattn_Wout"].T), a["L3_xattn_bout"].reshape(1, D)
    o["ctx"] = c(a["ctx_1024"].transpose(1, 0, 2))
    o["drop"] = c(a["mask_BxSxS2_fk0"].transpose(1, 0, 2))
    o["l3f_wq"] = c(a["L3_ffn_weight_q"].T.astype(np.int32))
    o["l3f_scale"], o["l3f_bias"] = a["L3_ffn_weight_scale"].reshape(1, D), a["L3_ffn_bias"].reshape(1, D)
    w_in = a["L0_attn_in_proj_w"].T
    o["mam_z_in"], o["mam_conv_in"], o["mam_dt_in"] = c(w_in[:, :256]), c(w_in[:, 256:768]), c(w_in[:, 768:])
    o["mam_conv_w"] = c(a["L0_attn_conv_w"].reshape(4, T, 4).transpose(1, 0, 2))
    o["mam_conv_b"] = c(a["L0_attn_conv_b"].reshape(4, T).T)
    o["mam_dt_bias"], o["mam_a_log"] = a["L0_attn_dt_bias"].reshape(1, 32), a["L0_attn_A_log"].reshape(1, 32)
    o["mam_d_skip"] = c(np.repeat(a["L0_attn_D_skip"], 8).reshape(2, T).T)
    o["mam_norm_w"] = c(a["L0_attn_norm_w"].reshape(2, T).T)
    o["mam_out_w"] = c(a["L0_attn_out_proj_w"].T.reshape(2, T, D).transpose(1, 0, 2))
    o["mam_ln_w"], o["mam_ln_b"] = a["L0_attn_ln_w"].reshape(1, D), a["L0_attn_ln_b"].reshape(1, D)
    o["mam_upto"] = np.triu(np.ones((T, T), np.float32))
    o["mam_head_row"] = np.tile(np.eye(32, dtype=np.float32), (3, 1))
    o["l3a_key"] = c(a["L3_attn_key_param"][0].T)
    for n in "qkv":
        o[f"L3_attn_W{n}"] = a[f"L3_attn_W{n}"]
    o["l3a_wo"] = c(np.tile(a["L3_attn_Wo"].reshape(16, HD, D).transpose(1, 0, 2), (HEADS, 1, 1)))
    o["l3a_bq"], o["l3a_bk"] = a["L3_attn_bq"].reshape(D, 1), a["L3_attn_bk"].reshape(D, 1)
    o["l3a_bv"], o["l3a_bo"] = a["L3_attn_bv"].reshape(1, D), a["L3_attn_bo"].reshape(1, D)
    head = np.arange(T)[:, None, None] // 32 + 4 * np.arange(4)[None, :, None]
    o["l3a_own"] = (head == np.arange(D)[None, None, :] // HD).astype(np.float32)
    o["l3a_inv"] = (1.0 / np.arange(1, 33)).astype(np.float32).reshape(1, 32)
    return o


def load(nc, aps, table, ctx, layers, x=None):
    tiles, loaded, counts = {}, {}, {}
    jobs = []
    for layer, key, name, parts, wide in table:
        if layer not in layers:
            continue
        ap = aps[name]
        dt = ap.dtype
        shape = [parts if wide else ap.shape[0]] + list(ap.shape[1:])
        t = ctx.enter_context(nc.sbuf_tensor(f"w{layer}_{key}", shape, dt))
        tiles.setdefault(layer, {})[key] = t
        counts[layer] = counts.get(layer, 0) + 16
        jobs.append((layer, t, ap, wide))
    for layer in counts:
        loaded[layer] = ctx.enter_context(nc.semaphore(f"loaded{layer}"))
        tiles[layer]["n"] = counts[layer]
    with nc.Block() as block:
        @block.sync
        def _(sp):
            if x is not None:
                sp.dma_start(x[:, :, :], aps["x"]).then_inc(loaded[-1], 16)
            for layer, t, ap, wide in jobs:
                src = ap
                if wide:
                    src = ap.partition_broadcast(T)
                    src = src.rearrange("p o d -> p (o d)") if len(src.shape) == 3 else src
                sp.dma_start(t[tuple(slice(None) for _ in t.shape)], src).then_inc(loaded[layer], 16)
            if x is not None:
                sp.wait_ge(loaded[-1], counts[-1] + 16)
    return tiles, loaded


ACTS = ((0, 1, 2), (3, 4, 5), (6, 7, 8), (9, 10, 11))


def build(nc, aps, phases=tuple(range(12))):
    with ExitStack() as ctx:
        x = ctx.enter_context(nc.sbuf_tensor("x_res", [T, NB, D], F32))
        tiles, _ = load(nc, aps, TABLE, ctx, (-1,), x)
        const = tiles[-1]
        for act in ACTS:
            act = [p for p in act if p in phases]
            if act:
                with ExitStack() as act_ctx:
                    tiles, loaded = load(nc, aps, TABLE, act_ctx, act)
                    for p in act:
                        LAYERS[p](nc, x, const, tiles[p], loaded[p], aps)
        done = ctx.enter_context(nc.semaphore("done"))
        with nc.Block() as block:
            @block.sync
            def _(sp):
                sp.dma_start(aps["out"], x[:, :, :]).then_inc(done, 16)
                sp.wait_ge(done, 16)


def kernel(**inputs):
    import concourse.bacc as bacc
    from concourse.bass_utils import run_bass_kernel_spmd

    arrays = lay_out(inputs)
    used = {row[2] for row in TABLE} | {"x", "ctx_t", "ctx", "drop", "rel_table"}
    nc = bacc.Bacc("TRN2", target_bir_lowering=False, num_devices=1)
    ins, aps = {}, {}
    for name in sorted(used):
        array = np.ascontiguousarray(arrays[name])
        ins[f"in_{name}"] = array
        aps[name] = nc.dram_tensor(f"in_{name}", array.shape, mybir.dt.from_np(array.dtype), kind="ExternalInput").ap()
    aps["out"] = nc.dram_tensor("out", (T, NB, D), F32, kind="ExternalOutput").ap()
    build(nc, aps)
    result = run_bass_kernel_spmd(nc, [ins], core_ids=[0])
    return np.ascontiguousarray(result.results[0]["out"].transpose(1, 0, 2))
```

```python
import concourse.bass as bass
import concourse.mybir as mybir
import numpy as np
from contextlib import ExitStack

F32 = mybir.dt.float32
BF16 = mybir.dt.bfloat16
ALU = mybir.AluOpType
ACT = mybir.ActivationFunctionType
AX = mybir.AxisListType

NB = 32
T = 128
D = 128
GROUP = 4
NG = NB // GROUP
BANK = 512
LN_EPS = 1e-5
NEG = -1e30
MASKED = -1e20


class Layer:

    def __init__(self, nc, ctx, name):
        self.nc, self.ctx, self.name, self.sems = nc, ctx, name, []
        ctx.callback(self.close)

    def close(self):
        self.nc.clear_and_free_semaphores(self.sems)
        self.nc.all_engine_barrier()

    def sbuf(self, name, shape, dtype=F32):
        return self.ctx.enter_context(self.nc.sbuf_tensor(f"{self.name}_{name}", shape, dtype))

    def psum(self, name, shape, dtype=F32):
        return self.ctx.enter_context(self.nc.psum_tensor(f"{self.name}_{name}", shape, dtype))

    def sem(self, name):
        handle = self.nc.alloc_semaphore(f"{self.name}_{name}")
        self.sems.append(handle)
        return handle


class Order:

    def __init__(self, eng, sem):
        self.eng, self.sem, self.n, self.base = eng, sem, 0, 0

    def then(self, ins):
        self.n += 1
        ins.then_inc(self.sem, 1)
        self.eng.wait_ge(self.sem, self.base + self.n)


def groups(eng, order, body, n=NG):
    body(0, True)
    if order is not None:
        per, order.n = order.n, 0
    with eng.Fori(1, n) as i:
        if order is not None:
            order.base = i * per
            order.n = 0
        body(i, False)


def pipelined(eng, order, start, body, per=None):
    start()
    before = order.n if order is not None else 0
    body(0, 0, False)
    if order is not None:
        base = order.n
        per = base - before if per is None else per
    with eng.Fori(0, NG // 2 - 1) as k:
        if order is not None:
            order.base, order.n = base + k * (2 * per), 0
        body(k * 2 + 1, 1, False)
        body(k * 2 + 2, 0, False)
        assert order is None or order.n == 2 * per
    if order is not None:
        order.base, order.n = base + (NG // 2 - 1) * 2 * per, 0
    body(NG - 1, 1, True)


def split_high(nc, src, high, parts):
    nc.scalar.copy(high[:, :], src[0:96, :])
    return nc.scalar.copy(parts[0:32, :], src[0:32, :])


def split_rest(nc, order, src, high, rest, middle, parts):
    order.then(nc.vector.tensor_tensor(rest[:, :], src[0:96, :], high[:, :], ALU.subtract))
    nc.vector.tensor_copy(parts[32:64, :], rest[32:64, :])
    order.then(nc.vector.tensor_copy(middle[64:96, :], rest[64:96, :]))
    return nc.vector.tensor_tensor(parts[64:96, :], rest[64:96, :], middle[64:96, :], ALU.subtract)


def bcast(ap, shape, axis):
    return ap.unsqueeze(axis).broadcast_to(shape)


def layernorm_stats(nc, dve, order, x, i, stats, moments, pad, count=GROUP):
    for u in range(count):
        last = nc.vector.bn_stats(stats[:, u, :], x[:, i * count + u, :])
    order.then(last)
    nc.vector.memset(pad[:, :], 0.0)
    for u in range(count):
        last = nc.vector.bn_aggr(moments[:, u, :], stats[:, u, :])
    order.then(last)
    return nc.vector.tensor_scalar(moments[:, :, 1], moments[:, :, 1], LN_EPS, None, ALU.add)


def layernorm_rstd(nc, pool, stats_ready, i, minus_half, moments, rstd):
    pool.wait_ge(stats_ready, i + 1)
    return nc.gpsimd.tensor_tensor(rstd[:, :], moments[:, :, 1], minus_half[:, 0:moments.shape[1]], ALU.pow)


def layernorm_apply(nc, x, i, moments, rstd, h, count=GROUP):
    for u in range(count):
        last = nc.vector.tensor_scalar(h[:, u, :], x[:, i * count + u, :], moments[:, u, 0:1], rstd[:, u:u + 1],
                                       ALU.subtract, ALU.mult)
    return last
HEADS = 16
HD = D // HEADS
HALF = HEADS // 2
UNITS = 2 * GROUP


def attention16(nc, name, x, const, w, loaded, ctx_t=None, latent=False, causal=False, key_mask=None,
                rel_bias=False, qkv_bias=False, out_bias=False):
    scale = float(HD) ** -0.5
    with ExitStack() as ctx:
        L = Layer(nc, ctx, name)
        stats = L.sbuf("stats", [T, GROUP, 6])
        moments = L.sbuf("moments", [T, GROUP, 2])
        pad = L.sbuf("pad", [T, 1])
        rstd = L.sbuf("rstd", [T, GROUP])
        h = L.sbuf("h", [T, GROUP, D])
        h_t = L.sbuf("h_t", [D, GROUP * T])
        lat_t = L.sbuf("lat_t", [64, GROUP * T])
        q_t = L.sbuf("q_t", [D, 2, GROUP * T])
        k_t = L.sbuf("k_t", [D, 2, GROUP * T])
        c_t = L.sbuf("c_t", [D, GROUP * T])
        v = L.sbuf("v", [T, 2 * GROUP, HEADS, HD + 1])
        spread = L.sbuf("spread", [D, 2, HEADS, T])
        probs = L.sbuf("probs", [T, 2, HALF, T])
        probs_t = L.sbuf("probs_t", [T, 2, HALF, T])
        top = L.sbuf("top", [T, 2, HALF])
        rec = L.sbuf("rec", [T, HALF])
        heads_out = L.sbuf("heads_out", [T, 2 * GROUP, D])
        heads_t = L.sbuf("heads_t", [D, GROUP * T])
        update = L.sbuf("update", [T, GROUP, D])
        p_score = [L.psum(f"p_score{n}", [T, 2, 4, T]) for n in range(2)]
        p_trans = L.psum("p_trans", [T, 2, 4, T])
        p_pv = L.psum("p_pv", [T, BANK])
        p_misc = L.psum("p_misc", [T, BANK])

        ctx_in = L.sem("ctx_in")
        stats_ready = L.sem("stats_ready")
        rstd_ready = L.sem("rstd_ready")
        normed = L.sem("normed")
        trans = L.sem("trans")
        h_t_ready = L.sem("h_t_ready")
        lat_done = L.sem("lat_done")
        lat_ready = L.sem("lat_ready")
        proj = L.sem("proj")
        q_ready = L.sem("q_ready")
        k_ready = L.sem("k_ready")
        v_ready = L.sem("v_ready")
        spread_ready = L.sem("spread_ready")
        scored = L.sem("scored")
        shifted = L.sem("shifted")
        expd = L.sem("expd")
        turned = L.sem("turned")
        turned_out = L.sem("turned_out")
        weighed = L.sem("weighed")
        divided = L.sem("divided")
        out_t = L.sem("out_t")
        out_t_ready = L.sem("out_t_ready")
        out_done = L.sem("out_done")
        added = L.sem("added")
        biased = L.sem("biased")
        dve_order = L.sem("dve_order")
        setup = L.sem("setup")
        flipped = L.sem("flipped")
        scaled_bq = L.sbuf("scaled_bq", [D, 1])
        if rel_bias:
            bias = L.sbuf("bias", [T, HEADS, T])
        if causal:
            causal_b = L.sbuf("causal_b", [T, T], BF16)
            ident_b = L.sbuf("ident_b", [T, T], BF16)
        if key_mask is not None:
            mask_f = L.sbuf("mask_f", [1, 2, GROUP * T], BF16)
            ones_b = L.sbuf("ones_b", [1, T], BF16)

        masks = causal or key_mask is not None
        started = lambda i: not (isinstance(i, int) and i == 0)
        if latent:
            TURN_H, LATENT, QUERIES, KEYS, VALUES, TURN_OUT, PROJECT = 0, 2, 3, 4, 5, 6, 7
        else:
            TURN_H, LATENT, QUERIES, KEYS, VALUES, TURN_OUT, PROJECT = 1, None, 2, 3, 4, 5, 6

        with nc.Block() as block:
            if ctx_t is not None:
                @block.sync
                def _(sp):
                    def body(i, first):
                        if not first:
                            sp.wait_ge(proj, 3 * i)
                        sp.dma_start(c_t[:, :], ctx_t[:, bass.ts(i, GROUP * T)]).then_inc(ctx_in, 16)
                    groups(sp, None, body)

            @block.tensor
            def _(pe):
                pe.wait_ge(loaded, w["n"])
                if rel_bias:
                    for n in range(4):
                        last = nc.tensor.matmul(p_score[n // 2][:, n % 2, :, :], const["flip"][:, :],
                                                w["rel"][:, 4 * n:4 * n + 4, :], start=True, stop=True)
                    last.then_inc(flipped, 1)
                pe.wait_ge(setup, 1)
                source_kv, kd = (c_t, D) if ctx_t is not None else (lat_t, 64) if latent else (h_t, D)
                source_q = lat_t if latent else h_t

                def turn_h(j):
                    pe.wait_ge(normed, j + 1)
                    for u in range(GROUP):
                        last = nc.tensor.transpose(p_misc[:, u * T:(u + 1) * T], h[:, u, :], const["ident"][:, :])
                    last.then_inc(trans, 1)

                def latent_down(j):
                    pe.wait_ge(h_t_ready, j + 1)
                    nc.tensor.matmul(p_misc[0:64, :], w["down"][:, :], h_t[:, :], start=True, stop=True)\
                        .then_inc(lat_done, 1)

                def queries(j):
                    pe.wait_ge(lat_ready if latent else h_t_ready, j + 1)
                    nc.tensor.matmul(p_misc[:, :], w["wq"][0:kd, :], source_q[0:kd, :], start=True, stop=True)\
                        .then_inc(proj, 1)

                def keys(j):
                    pe.wait_ge(q_ready, j + 1)
                    if ctx_t is not None:
                        pe.wait_ge(ctx_in, (j + 1) * 16)
                    nc.tensor.matmul(p_misc[:, :], w["wk"][0:kd, :], source_kv[0:kd, :], start=True, stop=True)\
                        .then_inc(proj, 1)

                def value_rows(j):
                    pe.wait_ge(k_ready, j + 1)
                    for u in range(GROUP):
                        last = nc.tensor.matmul(p_misc[:, u * T:(u + 1) * T], source_kv[0:kd, u * T:(u + 1) * T],
                                                w["wv"][0:kd, :], start=True, stop=True)
                    last.then_inc(proj, 1)

                def turn_out(j, q):
                    pe.wait_ge(divided, (j + 1) * UNITS)
                    for u in range(GROUP):
                        last = nc.tensor.transpose(p_misc[:, u * T:(u + 1) * T], heads_out[:, q * GROUP + u, :],
                                                   const["ident"][:, :])
                    last.then_inc(out_t, 1)

                def project(j):
                    pe.wait_ge(out_t_ready, j + 1)
                    for u in range(GROUP):
                        last = nc.tensor.matmul(p_misc[:, u * D:(u + 1) * D], heads_t[:, u * T:(u + 1) * T],
                                                w["wo"][:, :], start=True, stop=True)
                    last.then_inc(out_done, 1)

                def scores(i, n, q):
                    u, half, g = n // 2, n % 2, i * UNITS + n
                    pe.wait_ge(spread_ready, i * GROUP + u + 1)
                    if not isinstance(g, int) or g >= 2:
                        pe.wait_ge(shifted, g - 1)
                    for j in range(2):
                        out = p_score[n % 2][:, j, :, :]
                        if causal:
                            nc.tensor.matmul(out, ident_b[:, :], bcast(causal_b[:, :], [T, 4, T], 1), start=True, stop=False)
                        if key_mask is not None:
                            nc.tensor.matmul(out, ones_b[0:1, :], bcast(mask_f[0:1, q, u * T:(u + 1) * T], [1, 4, T], 1),
                                             start=True, stop=False)
                        head = half * HALF + 4 * j
                        last = nc.tensor.matmul(out, q_t[:, q, u * T:(u + 1) * T], spread[:, u % 2, head:head + 4, :],
                                                start=not masks, stop=True)
                    last.then_inc(scored, 1)

                def transposes(i, n):
                    g = i * UNITS + n
                    pe.wait_ge(expd, g + 1)
                    if not isinstance(g, int) or g >= 1:
                        pe.wait_ge(turned_out, g)
                    for k in range(HALF):
                        last = nc.tensor.transpose(p_trans[:, k // 4, k % 4, :], probs[:, n % 2, k, :], const["ident"][:, :])
                    last.then_inc(turned, 1)

                def values(i, n, q):
                    u, half, g = n // 2, n % 2, i * UNITS + n
                    pe.wait_ge(turned_out, g + 1)
                    if not isinstance(g, int) or g >= 1:
                        pe.wait_ge(divided, g)
                    for k in range(HALF):
                        last = nc.tensor.matmul(p_pv[:, k * (HD + 1):(k + 1) * (HD + 1)], probs_t[:, n % 2, k, :],
                                                v[:, q * GROUP + u, half * HALF + k, :], start=True, stop=True)
                    last.then_inc(weighed, 1)

                def start():
                    turn_h(0)
                    if latent:
                        latent_down(0)
                    queries(0)
                    keys(0)
                    value_rows(0)
                    pe.wait_ge(v_ready, 1)
                    scores(0, 0, 0)

                def body(i, p, last_group):
                    for n in range(UNITS):
                        if n + 1 < UNITS:
                            scores(i, n + 1, p)
                        elif not last_group:
                            pe.wait_ge(v_ready, i + 2)
                            scores(i + 1, 0, 1 - p)
                        if n >= 1:
                            values(i, n - 1, p)
                        elif started(i):
                            values(i - 1, UNITS - 1, 1 - p)
                        transposes(i, n)
                        if not last_group:
                            if n == TURN_H:
                                pe.wait_ge(shifted, i * UNITS + 1)
                                turn_h(i + 1)
                            if n == LATENT and latent:
                                latent_down(i + 1)
                            if n == QUERIES:
                                queries(i + 1)
                            if n == KEYS:
                                keys(i + 1)
                            if n == VALUES:
                                value_rows(i + 1)
                        if n == TURN_OUT and started(i):
                            if not last_group:
                                pe.wait_ge(v_ready, i + 2)
                            else:
                                pe.wait_ge(added, i - 1)
                            turn_out(i - 1, 1 - p)
                        if n == PROJECT and started(i):
                            project(i - 1)
                pipelined(pe, None, start, body)
                values(NG - 1, UNITS - 1, 1)
                pe.wait_ge(added, NG - 1)
                turn_out(NG - 1, 1)
                project(NG - 1)

            @block.scalar
            def _(act):
                act.wait_ge(loaded, w["n"])
                act.wait_ge(setup, 1)

                def copy_h(j):
                    act.wait_ge(trans, j + 1)
                    nc.scalar.copy(h_t[:, :], p_misc[:, :]).then_inc(h_t_ready, 1)

                def copy_latent(j):
                    act.wait_ge(lat_done, j + 1)
                    nc.scalar.copy(lat_t[:, :], p_misc[0:64, :]).then_inc(lat_ready, 1)

                def copy_queries(j, q):
                    act.wait_ge(proj, j * 3 + 1)
                    if qkv_bias:
                        nc.scalar.activation(q_t[:, q, :], p_misc[:, :], ACT.Identity, bias=scaled_bq[:, 0:1], scale=scale)\
                            .then_inc(q_ready, 1)
                    else:
                        nc.scalar.activation(q_t[:, q, :], p_misc[:, :], ACT.Copy, scale=scale).then_inc(q_ready, 1)

                def copy_keys(j, q):
                    act.wait_ge(proj, j * 3 + 2)
                    if qkv_bias:
                        nc.scalar.activation(k_t[:, q, :], p_misc[:, :], ACT.Identity, bias=w["bk"][:, 0:1]).then_inc(k_ready, 1)
                    else:
                        nc.scalar.copy(k_t[:, q, :], p_misc[:, :]).then_inc(k_ready, 1)

                def copy_turned(i, n):
                    g = i * UNITS + n
                    act.wait_ge(turned, g + 1)
                    if not isinstance(g, int) or g >= 2:
                        act.wait_ge(weighed, g - 1)
                    nc.scalar.copy(probs_t[:, n % 2, 0:4, :], p_trans[:, 0, :, :])
                    nc.scalar.copy(probs_t[:, n % 2, 4:8, :], p_trans[:, 1, :, :]).then_inc(turned_out, 1)

                def copy_out(j):
                    act.wait_ge(out_t, j + 1)
                    nc.scalar.copy(heads_t[:, :], p_misc[:, :]).then_inc(out_t_ready, 1)

                def start():
                    copy_h(0)
                    if latent:
                        copy_latent(0)
                    copy_queries(0, 0)
                    copy_keys(0, 0)

                def body(i, p, last_group):
                    for n in range(UNITS):
                        act.wait_ge(shifted, i * UNITS + n + 1)
                        nc.scalar.activation(probs[:, n % 2, :, :], probs[:, n % 2, :, :], ACT.Exp).then_inc(expd, 1)
                        if n >= 1:
                            copy_turned(i, n - 1)
                        elif started(i):
                            copy_turned(i - 1, UNITS - 1)
                        if not last_group:
                            if n == TURN_H + 1:
                                copy_h(i + 1)
                            if latent and n == LATENT + 1:
                                copy_latent(i + 1)
                            if n == QUERIES + 1:
                                copy_queries(i + 1, 1 - p)
                            if n == KEYS + 1:
                                copy_keys(i + 1, 1 - p)
                        if n == TURN_OUT + 1 and started(i):
                            copy_out(i - 1)
                pipelined(act, None, start, body)
                copy_turned(NG - 1, UNITS - 1)
                copy_out(NG - 1)

            @block.vector
            def _(dve):
                order = Order(dve, dve_order)
                dve.wait_ge(loaded, w["n"])
                if causal:
                    nc.vector.tensor_copy(causal_b[:, :], const["causal"][:, :])
                    nc.vector.tensor_copy(ident_b[:, :], const["ident"][:, :])
                if key_mask is not None:
                    nc.vector.memset(ones_b[:, :], 1.0)
                if qkv_bias:
                    nc.vector.tensor_scalar(scaled_bq[:, :], w["bq"][:, :], scale, None, ALU.mult)
                if rel_bias:
                    dve.wait_ge(flipped, 1)
                    for n in range(4):
                        nc.vector.tensor_copy(bias[:, 4 * n:4 * n + 4, :], p_score[n // 2][:, n % 2, :, :])
                nc.vector.memset(v[:, :, :, :], 1.0).then_inc(setup, 1)
                dve.wait_ge(setup, 1)

                def norm_stats(j):
                    layernorm_stats(nc, dve, order, x, j, stats, moments, pad).then_inc(stats_ready, 1)

                def norm_apply(j):
                    dve.wait_ge(rstd_ready, j + 1)
                    layernorm_apply(nc, x, j, moments, rstd, h).then_inc(normed, 1)

                def copy_values(j, q):
                    if key_mask is not None:
                        nc.vector.tensor_scalar(mask_f[:, q, :], w["mask"][0:1, bass.ts(j, GROUP * T)], 0.0, MASKED,
                                                ALU.is_equal, ALU.mult)
                    dve.wait_ge(proj, 3 * j + 3)
                    dst = v[:, q * GROUP:(q + 1) * GROUP, :, 0:HD]
                    src = p_misc[:, :].rearrange("p (u h d) -> p u h d", u=GROUP, d=HD)
                    if qkv_bias:
                        nc.vector.tensor_tensor(dst, src, bcast(w["bv"][:, :].rearrange("p (h d) -> p h d", d=HD),
                                                                [T, GROUP, HEADS, HD], 1), ALU.add).then_inc(v_ready, 1)
                    else:
                        nc.vector.tensor_copy(dst, src).then_inc(v_ready, 1)

                def shift(i, n):
                    u, half, g = n // 2, n % 2, i * UNITS + n
                    dve.wait_ge(scored, g + 1)
                    if not isinstance(g, int) or g >= 2:
                        dve.wait_ge(turned, g - 1)
                    s = p_score[n % 2][:, :, :, :].rearrange("p a b k -> p (a b) k")
                    p = probs[:, n % 2, :, :]
                    if rel_bias:
                        order.then(nc.vector.tensor_tensor(p, s, bias[:, half * HALF:(half + 1) * HALF, :], ALU.add))
                        s = p
                    order.then(nc.vector.tensor_reduce(top[:, n % 2, :], s, AX.X, ALU.max))
                    nc.vector.tensor_tensor(p, s, bcast(top[:, n % 2, :], [T, HALF, T], 2), ALU.subtract)\
                        .then_inc(shifted, 1)

                def divide(i, n, q):
                    u, half, g = n // 2, n % 2, i * UNITS + n
                    dve.wait_ge(weighed, g + 1)
                    o = p_pv[:, 0:HALF * (HD + 1)].rearrange("p (h d) -> p h d", d=HD + 1)
                    order.then(nc.vector.reciprocal(rec[:, :], o[:, :, HD]))
                    nc.vector.tensor_tensor(
                        heads_out[:, q * GROUP + u, half * (D // 2):(half + 1) * (D // 2)].rearrange("p (h d) -> p h d", d=HD),
                        o[:, :, 0:HD], bcast(rec[:, :], [T, HALF, HD], 2), ALU.mult).then_inc(divided, 1)

                def add_output(j):
                    dve.wait_ge(out_done, j + 1)
                    out = p_misc[:, :].rearrange("p (u d) -> p u d", d=D)
                    xs = x[:, bass.ts(j, GROUP), :]
                    if out_bias:
                        nc.vector.tensor_tensor(update[:, :, :], out, bcast(w["bo"][:, :], [T, GROUP, D], 1), ALU.add)\
                            .then_inc(biased, 1)
                        dve.wait_ge(biased, j + 1)
                        out = update[:, :, :]
                    nc.vector.tensor_tensor(xs, xs, out, ALU.add).then_inc(added, 1)

                def start():
                    norm_stats(0)
                    norm_apply(0)
                    copy_values(0, 0)

                def body(i, p, last_group):
                    for n in range(UNITS):
                        shift(i, n)
                        if n >= 2:
                            divide(i, n - 2, p)
                        elif started(i):
                            divide(i - 1, UNITS - 2 + n, 1 - p)
                        if n == 0 and not last_group:
                            norm_stats(i + 1)
                            norm_apply(i + 1)
                        if n == VALUES + 1 and not last_group:
                            copy_values(i + 1, 1 - p)
                        if n == UNITS - 1 and started(i):
                            add_output(i - 1)
                pipelined(dve, order, start, body, per=2 + UNITS * (3 if rel_bias else 2))
                divide(NG - 1, UNITS - 2, 1)
                divide(NG - 1, UNITS - 1, 1)
                add_output(NG - 1)

            @block.gpsimd
            def _(pool):
                def norm_scale(j):
                    layernorm_rstd(nc, pool, stats_ready, j, const["minus_half"], moments, rstd).then_inc(rstd_ready, 1)

                def spread_keys(i, u, q):
                    if not isinstance(i, int) or i > 0:
                        pool.wait_ge(scored, i * UNITS + 2 * u - 2)
                    elif u >= 2:
                        pool.wait_ge(scored, 2 * u - 2)
                    nc.gpsimd.tensor_tensor(spread[:, u % 2, :, :], bcast(k_t[:, q, u * T:(u + 1) * T], [D, HEADS, T], 1),
                                            bcast(const["head_of"][:, :], [D, HEADS, T], 2), ALU.mult)\
                        .then_inc(spread_ready, 1)

                def start():
                    norm_scale(0)
                    pool.wait_ge(k_ready, 1)
                    spread_keys(0, 0, 0)
                    spread_keys(0, 1, 0)

                def body(i, p, last_group):
                    if not last_group:
                        norm_scale(i + 1)
                    spread_keys(i, 2, p)
                    spread_keys(i, 3, p)
                    if not last_group:
                        pool.wait_ge(k_ready, i + 2)
                        spread_keys(i + 1, 0, 1 - p)
                        spread_keys(i + 1, 1, 1 - p)
                pipelined(pool, None, start, body)


def attention8(nc, name, x, const, w, loaded, ctx_t):
    HEADS8, HD8, KEYS, BLOCKS = 8, 64, 2 * T, 4
    with ExitStack() as ctx:
        L = Layer(nc, ctx, name)
        stats = L.sbuf("stats", [T, GROUP, 6])
        moments = L.sbuf("moments", [T, GROUP, 2])
        pad = L.sbuf("pad", [T, 1])
        rstd = L.sbuf("rstd", [T, GROUP])
        h = L.sbuf("h", [T, GROUP, D])
        h_t = L.sbuf("h_t", [D, 2, GROUP * T])
        c_t = L.sbuf("c_t", [D, 2, GROUP * T])
        q_t = L.sbuf("q_t", [T, 2, BLOCKS, T])
        keys = L.sbuf("keys", [T, 2, BLOCKS, 2, KEYS])
        v = L.sbuf("v", [T, 2, 2, HEADS8, HD8 + 1])
        probs = L.sbuf("probs", [T, 2, 4, KEYS])
        probs_t = L.sbuf("probs_t", [T, 2, 8, T])
        top = L.sbuf("top", [T, 2, 4])
        rec = L.sbuf("rec", [T, 4])
        heads_out = L.sbuf("heads_out", [T, GROUP, BLOCKS, T])
        heads_t = L.sbuf("heads_t", [T, BLOCKS, T])
        update = L.sbuf("update", [T, D])
        p_score = [L.psum(f"p_score{n}", [T, 2, BANK]) for n in range(2)]
        p_trans = L.psum("p_trans", [T, 2, 4, T])
        p_pv = L.psum("p_pv", [T, BANK])
        p_misc = L.psum("p_misc", [T, BANK])

        ctx_in = [L.sem(f"ctx_in{n}") for n in range(2)]
        stats_ready = L.sem("stats_ready")
        rstd_ready = L.sem("rstd_ready")
        normed = L.sem("normed")
        trans = L.sem("trans")
        h_t_ready = L.sem("h_t_ready")
        qk_done = L.sem("qk_done")
        qk_ready = L.sem("qk_ready")
        v_done = L.sem("v_done")
        v_ready = L.sem("v_ready")
        scored = L.sem("scored")
        shifted = L.sem("shifted")
        expd = L.sem("expd")
        turned = L.sem("turned")
        turned_out = L.sem("turned_out")
        weighed = L.sem("weighed")
        divided = L.sem("divided")
        out_t = L.sem("out_t")
        out_t_ready = L.sem("out_t_ready")
        out_done = L.sem("out_done")
        update_ready = L.sem("update_ready")
        biased = L.sem("biased")
        added = L.sem("added")
        dve_order = L.sem("dve_order")
        setup = L.sem("setup")
        started = lambda i: not (isinstance(i, int) and i == 0)
        positive = lambda count: not isinstance(count, int) or count > 0


        def other(i, u, p, last_group, ahead):
            if 0 <= u + ahead < GROUP:
                return i, u + ahead, p
            if ahead > 0:
                return None if last_group else (i + 1, u + ahead - GROUP, 1 - p)
            return (i - 1, u + ahead + GROUP, 1 - p) if started(i) else None

        with nc.Block() as block:
            @block.sync
            def _(sp):
                def load_group(j, q):
                    sp.dma_start(c_t[:, q, :], ctx_t[:, bass.ts(j, GROUP * T)]).then_inc(ctx_in[q], 16)

                def body(i, p, last_group):
                    if not last_group:
                        if started(i):
                            sp.wait_ge(v_done, 2 * GROUP * i)
                        load_group(i + 1, 1 - p)
                pipelined(sp, None, lambda: load_group(0, 0), body)

            @block.tensor
            def _(pe):
                pe.wait_ge(loaded, w["n"])
                pe.wait_ge(setup, 2)

                def turn_h(j):
                    pe.wait_ge(normed, j + 1)
                    for u in range(GROUP):
                        last = nc.tensor.transpose(p_misc[:, u * T:(u + 1) * T], h[:, u, :], const["ident"][:, :])
                    last.then_inc(trans, 1)

                def project_qk(j, u, q, what):
                    if what == 0 and u == 0:
                        pe.wait_ge(h_t_ready, j + 1)
                    if what == 2 and u == 0:
                        pe.wait_ge(ctx_in[q], (j - q) * 8 + 16)
                    if what:
                        pe.wait_ge(qk_ready, 3 * (GROUP * j + u) + what)
                    weights = (w["wq"], w["wk1"], w["wk2"])[what]
                    source = (h_t, h_t, c_t)[what][:, q, u * T:(u + 1) * T]
                    for b in range(BLOCKS):
                        last = nc.tensor.matmul(p_misc[:, b * T:(b + 1) * T], weights[:, b * T:(b + 1) * T], source,
                                                start=True, stop=True)
                    last.then_inc(qk_done, 1)

                def project_v(j, u, q, of_ctx):
                    nc.tensor.matmul(p_misc[:, :], (h_t, c_t)[of_ctx][:, q, u * T:(u + 1) * T],
                                     (w["wv1"], w["wv2"])[of_ctx][:, :], start=True, stop=True).then_inc(v_done, 1)

                def scores(i, n):
                    u, half, g = n // 2, n % 2, i * UNITS + n
                    if half == 0:
                        pe.wait_ge(qk_ready, 3 * (GROUP * i + u + 1))
                    if positive(g - 1):
                        pe.wait_ge(shifted, g - 1)
                    for j in range(2):
                        b = 2 * half + j
                        last = nc.tensor.matmul(p_score[n % 2][:, j, :], q_t[:, u % 2, b, :], keys[:, u % 2, b, :, :],
                                                start=True, stop=True)
                    last.then_inc(scored, 1)

                def transposes(i, n):
                    g = i * UNITS + n
                    pe.wait_ge(expd, g + 1)
                    if positive(g):
                        pe.wait_ge(turned_out, g)
                    for k in range(8):
                        last = nc.tensor.transpose(p_trans[:, k // 4, k % 4, :],
                                                   probs[:, n % 2, k // 2, (k % 2) * T:(k % 2 + 1) * T],
                                                   const["ident"][:, :])
                    last.then_inc(turned, 1)

                def values(i, n):
                    u, half, g = n // 2, n % 2, i * UNITS + n
                    pe.wait_ge(turned_out, g + 1)
                    if half == 0:
                        pe.wait_ge(v_ready, 2 * (GROUP * i + u + 1))
                    if positive(g):
                        pe.wait_ge(divided, g)
                    for k in range(8):
                        head, part = k // 2, k % 2
                        last = nc.tensor.matmul(p_pv[:, head * (HD8 + 1):(head + 1) * (HD8 + 1)],
                                                probs_t[:, n % 2, k, :], v[:, u % 2, part, 4 * half + head, :],
                                                start=(part == 0), stop=(part == 1))
                    last.then_inc(weighed, 1)

                def turn_out(i, u):
                    pe.wait_ge(divided, 2 * (GROUP * i + u + 1))
                    for b in range(BLOCKS):
                        last = nc.tensor.transpose(p_misc[:, b * T:(b + 1) * T], heads_out[:, u, b, :], const["ident"][:, :])
                    last.then_inc(out_t, 1)

                def output(i, u):
                    pe.wait_ge(out_t_ready, GROUP * i + u + 1)
                    for b in range(BLOCKS):
                        last = nc.tensor.matmul(p_misc[:, 0:D], heads_t[:, b, :], w["wo"][:, b, :],
                                                start=(b == 0), stop=(b == BLOCKS - 1))
                    last.then_inc(out_done, 1)

                def start():
                    turn_h(0)
                    for what in range(3):
                        project_qk(0, 0, 0, what)
                    pe.wait_ge(qk_ready, 3)
                    project_v(0, 0, 0, 0)
                    pe.wait_ge(v_ready, 1)
                    project_v(0, 0, 0, 1)
                    pe.wait_ge(v_ready, 2)
                    project_qk(0, 1, 0, 0)
                    scores(0, 0)

                def body(i, p, last_group):
                    for n in range(UNITS):
                        u, s = n // 2, GROUP * i + n // 2
                        following = other(i, u, p, last_group, 1)
                        if n % 2 == 0:
                            scores(i, n + 1)
                            done = other(i, u, p, last_group, -3)
                            pe.wait_ge(v_ready, 2 * (s + 1))
                            if following:
                                pe.wait_ge(qk_ready, 3 * (s + 1) + 1)
                            if n == 4 and not last_group:
                                pe.wait_ge(h_t_ready, i + 2)
                            if done:
                                output(*done[:2])
                            if following:
                                if done:
                                    pe.wait_ge(update_ready, s - 2)
                                project_qk(*following, 1)
                            if n:
                                values(i, n - 1)
                            elif started(i):
                                values(i - 1, UNITS - 1)
                            if following:
                                project_qk(*following, 2)
                            transposes(i, n)
                        else:
                            if n + 1 < UNITS:
                                scores(i, n + 1)
                            elif not last_group:
                                scores(i + 1, 0)
                            if following:
                                pe.wait_ge(qk_ready, 3 * (s + 2))
                                project_v(*following, 0)
                            values(i, n - 1)
                            done = other(i, u, p, last_group, -2)
                            if done:
                                if following:
                                    pe.wait_ge(v_ready, 2 * (s + 1) + 1)
                                else:
                                    pe.wait_ge(update_ready, s - 2)
                                turn_out(*done[:2])
                            transposes(i, n)
                            if following:
                                if done:
                                    pe.wait_ge(out_t_ready, s - 1)
                                else:
                                    pe.wait_ge(v_ready, 2 * (s + 1) + 1)
                                project_v(*following, 1)
                            after = other(i, u, p, last_group, 2)
                            if after:
                                pe.wait_ge(v_ready, 2 * (s + 2))
                                project_qk(*after, 0)
                            if n == 3 and not last_group:
                                pe.wait_ge(qk_ready, 3 * (s + 2) + 1)
                                turn_h(i + 1)
                pipelined(pe, None, start, body)
                values(NG - 1, UNITS - 1)
                for u in range(1, GROUP):
                    if u > 1:
                        pe.wait_ge(update_ready, GROUP * (NG - 1) + u)
                        turn_out(NG - 1, u)
                    output(NG - 1, u)

            @block.scalar
            def _(act):
                act.wait_ge(loaded, w["n"])
                act.wait_ge(setup, 2)

                def copy_h(j, q):
                    act.wait_ge(trans, j + 1)
                    nc.scalar.copy(h_t[:, q, :], p_misc[:, :]).then_inc(h_t_ready, 1)

                def copy_qk(j, u, what):
                    act.wait_ge(qk_done, 3 * (GROUP * j + u) + what + 1)
                    if what == 0:
                        nc.scalar.activation(q_t[:, u % 2, :, :], p_misc[:, :], ACT.Copy, scale=float(HD8) ** -0.5)\
                            .then_inc(qk_ready, 1)
                    else:
                        for half in range(2):
                            part = slice(64 * half, 64 * half + 64)
                            last = nc.scalar.copy(keys[part, u % 2, :, half, (what - 1) * T:what * T],
                                                  p_misc[part, :].rearrange("p (b k) -> p b k", k=T))
                        last.then_inc(qk_ready, 1)

                def exponent(i, n):
                    act.wait_ge(shifted, i * UNITS + n + 1)
                    nc.scalar.activation(probs[:, n % 2, :, :], probs[:, n % 2, :, :], ACT.Exp).then_inc(expd, 1)

                def copy_turned(i, n):
                    g = i * UNITS + n
                    act.wait_ge(turned, g + 1)
                    if positive(g - 1):
                        act.wait_ge(weighed, g - 1)
                    nc.scalar.copy(probs_t[:, n % 2, 0:4, :], p_trans[:, 0, :, :])
                    nc.scalar.copy(probs_t[:, n % 2, 4:8, :], p_trans[:, 1, :, :]).then_inc(turned_out, 1)

                def copy_out(i, u):
                    act.wait_ge(out_t, GROUP * i + u + 1)
                    nc.scalar.copy(heads_t[:, :, :], p_misc[:, :]).then_inc(out_t_ready, 1)

                def copy_v(j, u, of_ctx):
                    act.wait_ge(v_done, 2 * (GROUP * j + u) + of_ctx + 1)
                    nc.scalar.copy(v[:, u % 2, of_ctx, :, 0:HD8], p_misc[:, :].rearrange("p (h d) -> p h d", d=HD8))\
                        .then_inc(v_ready, 1)

                def copy_output(i, u):
                    s = GROUP * i + u
                    act.wait_ge(out_done, s + 1)
                    if positive(s):
                        act.wait_ge(added, s)
                    nc.scalar.copy(update[:, :], p_misc[:, 0:D]).then_inc(update_ready, 1)

                def start():
                    copy_h(0, 0)
                    for what in range(3):
                        copy_qk(0, 0, what)
                    for of_ctx in range(2):
                        copy_v(0, 0, of_ctx)
                    copy_qk(0, 1, 0)

                def body(i, p, last_group):
                    for n in range(UNITS):
                        u = n // 2
                        following = other(i, u, p, last_group, 1)
                        if n % 2 == 0:
                            done = other(i, u, p, last_group, -3)
                            if done:
                                copy_output(*done[:2])
                            if following:
                                copy_qk(*following[:2], 1)
                            exponent(i, n)
                            if following:
                                copy_qk(*following[:2], 2)
                        else:
                            copy_turned(i, n - 1)
                            exponent(i, n)
                            if following:
                                copy_v(*following[:2], 0)
                            done = other(i, u, p, last_group, -2)
                            if done:
                                copy_out(*done[:2])
                            if following:
                                copy_v(*following[:2], 1)
                            copy_turned(i, n)
                            after = other(i, u, p, last_group, 2)
                            if after:
                                copy_qk(*after[:2], 0)
                            if n == 3 and not last_group:
                                copy_h(i + 1, 1 - p)
                pipelined(act, None, start, body)
                for u in range(1, GROUP):
                    if u > 1:
                        copy_out(NG - 1, u)
                    copy_output(NG - 1, u)

            @block.vector
            def _(dve):
                order = Order(dve, dve_order)
                dve.wait_ge(loaded, w["n"])
                nc.vector.memset(v[:, :, :, :, :].rearrange("p a b c d -> p (a b c d)"), 1.0).then_inc(setup, 1)
                dve.wait_ge(setup, 2)

                def norm(j):
                    if started(j):
                        dve.wait_ge(trans, j)
                    layernorm_stats(nc, dve, order, x, j, stats, moments, pad).then_inc(stats_ready, 1)
                    dve.wait_ge(rstd_ready, j + 1)
                    layernorm_apply(nc, x, j, moments, rstd, h).then_inc(normed, 1)

                def shift(i, n):
                    g = i * UNITS + n
                    dve.wait_ge(scored, g + 1)
                    if positive(g - 1):
                        dve.wait_ge(turned, g - 1)
                    s = p_score[n % 2][:, :, :].rearrange("p a (b k) -> p (a b) k", k=KEYS)
                    order.then(nc.vector.tensor_reduce(top[:, n % 2, :], s, AX.X, ALU.max))
                    nc.vector.tensor_tensor(probs[:, n % 2, :, :], s, bcast(top[:, n % 2, :], [T, 4, KEYS], 2),
                                            ALU.subtract).then_inc(shifted, 1)

                def divide(i, n):
                    u, half, g = n // 2, n % 2, i * UNITS + n
                    dve.wait_ge(weighed, g + 1)
                    o = p_pv[:, 0:4 * (HD8 + 1)].rearrange("p (h d) -> p h d", d=HD8 + 1)
                    order.then(nc.vector.reciprocal(rec[:, :], o[:, :, HD8]))
                    out = heads_out[:, u, 2 * half:2 * half + 2, :].rearrange("p b (h d) -> p (b h) d", d=HD8)
                    nc.vector.tensor_tensor(out, o[:, :, 0:HD8], bcast(rec[:, :], [T, 4, HD8], 2), ALU.mult)\
                        .then_inc(divided, 1)

                def body(i, p, last_group):
                    for n in range(UNITS):
                        shift(i, n)
                        if n >= 2:
                            divide(i, n - 2)
                        elif started(i):
                            divide(i - 1, UNITS - 2 + n)
                        if n == 2 and not last_group:
                            norm(i + 1)
                pipelined(dve, order, lambda: norm(0), body, per=2 + 2 * UNITS)
                divide(NG - 1, UNITS - 2)
                divide(NG - 1, UNITS - 1)

            @block.gpsimd
            def _(pool):
                nc.gpsimd.memset(keys[:, :, :, :, :].rearrange("p a b c d -> p (a b c d)"), 0.0).then_inc(setup, 1)

                def norm_scale(j):
                    layernorm_rstd(nc, pool, stats_ready, j, const["minus_half"], moments, rstd).then_inc(rstd_ready, 1)

                def add_output(i, u):
                    s = GROUP * i + u
                    pool.wait_ge(update_ready, s + 1)
                    nc.gpsimd.tensor_tensor(update[:, :], update[:, :], w["bo"][:, :], ALU.add).then_inc(biased, 1)
                    pool.wait_ge(biased, s + 1)
                    nc.gpsimd.tensor_tensor(x[:, s, :], x[:, s, :], update[:, :], ALU.add).then_inc(added, 1)

                def body(i, p, last_group):
                    if started(i):
                        add_output(i - 1, 1)
                        add_output(i - 1, 2)
                    if not last_group:
                        norm_scale(i + 1)
                    if started(i):
                        add_output(i - 1, 3)
                    add_output(i, 0)
                pipelined(pool, None, lambda: norm_scale(0), body)
                for u in range(1, GROUP):
                    add_output(NG - 1, u)


def pick_first_largest(nc, order, vals, falling, best, best_rank, chosen):
    shape = list(vals.shape)
    axis = len(shape) - 1
    order.then(nc.vector.tensor_reduce(best, vals, AX.X, ALU.max))
    order.then(nc.vector.tensor_tensor(chosen, vals, bcast(best, shape, axis), ALU.is_equal))
    order.then(nc.vector.tensor_tensor(chosen, chosen, falling, ALU.mult))
    order.then(nc.vector.tensor_reduce(best_rank, chosen, AX.X, ALU.max))
    order.then(nc.vector.tensor_tensor(chosen, chosen, bcast(best_rank, shape, axis), ALU.is_equal))


def experts(nc, name, x, const, w, loaded, kind):
    gated = kind != "top2"
    n_exp = 16 if kind == "groups" else 8
    per = {"groups": 1, "top2": 2, "top1": 4}[kind]
    n_weights = {"groups": 8, "top2": 8, "top1": 7}[kind]
    shared = {"groups": 1, "top2": 0, "top1": 4}[kind]
    steps = n_weights * per + shared
    at = {"groups": dict(r1=0, logits=0, route=(1, 1, 2, 2, 3, 3, 4, 4), act_h=0, act_r1=0, act_route=1, turn=5),
          "top2": dict(r1=0, logits=1, route=(3, 5, 7, 8), act_h=0, act_r1=1, act_route=4, turn=10),
          "top1": dict(r1=0, logits=3, route=(5, 7, 10), act_h=1, act_r1=0, act_route=7, turn=12)}[kind]
    turn_at = at["turn"]
    with ExitStack() as ctx:
        L = Layer(nc, ctx, name)
        stats = L.sbuf("stats", [T, GROUP, 6])
        moments = L.sbuf("moments", [T, GROUP, 2])
        pad = L.sbuf("pad", [T, 1])
        rstd = L.sbuf("rstd", [T, GROUP])
        h = L.sbuf("h", [T, GROUP, D])
        h_t = L.sbuf("h_t", [D, 2, GROUP * T])
        r1 = L.sbuf("r1", [D, GROUP * T]) if kind == "top2" else None
        score = L.sbuf("score", [T, GROUP, n_exp])
        left = L.sbuf("left", [T, GROUP, n_exp])
        raw = L.sbuf("raw", [T, GROUP, n_exp])
        chosen = L.sbuf("chosen", [T, GROUP, n_exp])
        picked = L.sbuf("picked", [T, GROUP, n_exp])
        best = L.sbuf("best", [T, GROUP, 4])
        best_rank = L.sbuf("best_rank", [T, GROUP, 4])
        g_score = L.sbuf("g_score", [T, GROUP, 4])
        g_chosen = L.sbuf("g_chosen", [T, GROUP, 4])
        g_picked = L.sbuf("g_picked", [T, GROUP, 4])
        total = L.sbuf("total", [T, GROUP])
        weight = L.sbuf("weight", [T, GROUP, n_exp])
        weight3 = L.sbuf("weight3", [T, GROUP, 3, 32])
        high = L.sbuf("high", [96, GROUP * T], BF16)
        rest = L.sbuf("rest", [96, GROUP * T])
        middle = L.sbuf("middle", [96, GROUP * T], BF16)
        parts = [L.sbuf(f"parts{n}", [96, GROUP * T], BF16) for n in range(2)]
        pick = L.sbuf("pick", [96, n_weights, T], BF16)
        weight_t = L.sbuf("weight_t", [n_exp, 2, GROUP * T]) if kind == "top2" else None
        h_w = L.sbuf("h_w", [D, 2, GROUP * T])
        act_out = L.sbuf("act_out", [D, 2, GROUP * T])
        prod = L.sbuf("prod", [D, 2, GROUP * T]) if kind == "groups" else None
        hidden = L.sbuf("hidden", [D, 2, GROUP * T])
        out_t = L.sbuf("out_t", [D, GROUP * T])
        p_misc = L.psum("p_misc", [T, BANK])
        p_route = L.psum("p_route", [T, BANK])
        p_spread = L.psum("p_spread", [T, BANK])
        p_out = L.psum("p_out", [T, BANK])
        p_gate = [L.psum(f"p_gate{n}", [T, BANK]) for n in range(2)]
        p_up = [L.psum(f"p_up{n}", [T, BANK]) for n in range(2)] if gated else None

        stats_ready = L.sem("stats_ready")
        rstd_ready = L.sem("rstd_ready")
        normed = L.sem("normed")
        x_h = L.sem("x_h")
        trans = L.sem("trans")
        h_t_ready = L.sem("h_t_ready")
        r1_done = L.sem("r1_done")
        r1_ready = L.sem("r1_ready")
        logits = L.sem("logits")
        route_in = L.sem("route_in")
        route_out = L.sem("route_out")
        routed = L.sem("routed")
        routed_t = L.sem("routed_t")
        high_ready = L.sem("high_ready")
        parts_ready = L.sem("parts_ready")
        spread = L.sem("spread")
        spread_used = L.sem("spread_used")
        gate = L.sem("gate")
        acted = L.sem("acted")
        hidden_ready = L.sem("hidden_ready")
        down = L.sem("down")
        out_t_ready = L.sem("out_t_ready")
        out_done = L.sem("out_done")
        added = L.sem("added")
        dve_order = L.sem("dve_order")
        setup = L.sem("setup")
        weighs_input = kind == "top1"
        n_down = steps + (kind == "top2")

        with nc.Block() as block:
            @block.tensor
            def _(pe):
                pe.wait_ge(loaded, w["n"])
                pe.wait_ge(setup, 1)

                def turn_h(j, q):
                    pe.wait_ge(normed, j + 1)
                    for u in range(GROUP):
                        last = nc.tensor.transpose(p_route[:, u * T:(u + 1) * T], h[:, u, :], const["ident"][:, :])
                    last.then_inc(trans, 1)

                def route_first(j, q):
                    pe.wait_ge(h_t_ready, j + 1)
                    nc.tensor.matmul(p_route[:, :], w["rw1"][:, :], h_t[:, q, :], start=True, stop=True)\
                        .then_inc(r1_done, 1)

                def route_logits(j, q):
                    source = h_t[:, q, :]
                    if kind == "top2":
                        pe.wait_ge(r1_ready, j + 1)
                        source = r1[:, :]
                    else:
                        pe.wait_ge(h_t_ready, j + 1)
                    for u in range(GROUP):
                        last = nc.tensor.matmul(p_route[:, u * n_exp:(u + 1) * n_exp], source[:, u * T:(u + 1) * T],
                                                w["router"][:, :], start=True, stop=True)
                    last.then_inc(logits, 1)

                def turn_weights(j):
                    pe.wait_ge(routed, j + 1)
                    if not isinstance(j, int) or j >= 2:
                        pe.wait_ge(added, j - 1)
                    for u in range(GROUP):
                        last = nc.tensor.transpose(p_misc[0:96, u * T:(u + 1) * T],
                                                   weight3[:, u, :, :].rearrange("p r e -> p (r e)"), const["ident"][:, :])
                    last.then_inc(routed_t, 1)

                def start():
                    turn_h(0, 0)
                    if kind == "top2":
                        route_first(0, 0)
                    route_logits(0, 0)
                    turn_weights(0)

                def output(i):
                    pe.wait_ge(out_t_ready, i + 1)
                    for u in range(GROUP):
                        last = nc.tensor.transpose(p_misc[:, u * D:(u + 1) * D], out_t[:, u * T:(u + 1) * T],
                                                   const["ident"][:, :])
                    last.then_inc(out_done, 1)

                def body(i, p, last_group):
                    pe.wait_ge(parts_ready, i + 1)

                    def spread_weight(e):
                        if e >= 1:
                            pe.wait_ge(spread_used, i * n_weights + e)
                        nc.tensor.matmul(p_spread[:, :], pick[:, e, :], parts[p][:, :], start=True, stop=True)\
                            .then_inc(spread, 1)

                    def gate_step(s):
                        e = s // per
                        if e < n_weights and s % per == 0:
                            if weighs_input:
                                if e == 0:
                                    spread_weight(0)
                                if e + 1 < n_weights:
                                    spread_weight(e + 1)
                                pe.wait_ge(spread_used, i * n_weights + e + 1)
                        if s >= 2:
                            pe.wait_ge(acted, i * steps + s - 1)
                        out = nc.tensor.matmul(p_gate[s % 2][:, :], w["wg"][:, s, :], h_t[:, p, :], start=True, stop=True)
                        if gated:
                            if s >= 2:
                                pe.wait_ge(hidden_ready, i * steps + s - 1)
                            source = h_w[:, e % 2, :] if weighs_input and e < n_weights else h_t[:, p, :]
                            out = nc.tensor.matmul(p_up[s % 2][:, :], w["wu"][:, s, :], source, start=True, stop=True)
                        out.then_inc(gate, 1)
                        if e < n_weights and s % per == 0 and not weighs_input:
                            spread_weight(e)

                    def down_step(s):
                        pe.wait_ge(hidden_ready, i * steps + s + 1)
                        nc.tensor.matmul(p_out[:, :], w["wd"][:, s, :], hidden[:, s % 2, :], start=(s == 0),
                                         stop=(s == steps - 1 and kind != "top2")).then_inc(down, 1)

                    gate_step(0)
                    for s in range(steps):
                        if s + 1 < steps:
                            gate_step(s + 1)
                        if s == 0 and not last_group:
                            turn_h(i + 1, 1 - p)
                        if s == 0 and not (isinstance(i, int) and i == 0):
                            pe.wait_ge(out_t_ready, i)
                        down_step(s)
                        if s == 0 and not (isinstance(i, int) and i == 0):
                            output(i - 1)
                        if last_group:
                            continue
                        if kind == "top2" and s == at["r1"]:
                            route_first(i + 1, 1 - p)
                        if s == at["logits"]:
                            route_logits(i + 1, 1 - p)
                        if s == turn_at:
                            turn_weights(i + 1)
                    if kind == "top2":
                        nc.tensor.matmul(p_out[:, :], w["eb2"][:, :], weight_t[:, p, :], start=False, stop=True)\
                            .then_inc(down, 1)
                pipelined(pe, None, start, body)
                output(NG - 1)

            @block.scalar
            def _(act):
                act.wait_ge(loaded, w["n"])

                def copy_h(j, q):
                    act.wait_ge(trans, j + 1)
                    nc.scalar.copy(h_t[:, q, :], p_route[:, :]).then_inc(h_t_ready, 1)

                def route_first(j):
                    act.wait_ge(r1_done, j + 1)
                    nc.scalar.activation(r1[:, :], p_route[:, :], ACT.Silu, bias=w["rb1"][:, 0:1]).then_inc(r1_ready, 1)

                def route_function(j):
                    if kind == "groups":
                        act.wait_ge(logits, j + 1)
                        nc.scalar.activation(score[:, :, :], p_route[:, 0:GROUP * n_exp], ACT.Sigmoid)\
                            .then_inc(route_out, 1)
                    else:
                        act.wait_ge(route_in, j + 1)
                        nc.scalar.activation(score[:, :, :], left[:, :, :], ACT.Exp).then_inc(route_out, 1)

                def split(j, q):
                    act.wait_ge(routed_t, j + 1)
                    if kind == "top2":
                        nc.scalar.copy(weight_t[:, q, :], p_misc[0:n_exp, :])
                    split_high(nc, p_misc, high, parts[q]).then_inc(high_ready, 1)

                def start():
                    copy_h(0, 0)
                    if kind == "top2":
                        route_first(0)
                    route_function(0)
                    split(0, 0)

                def body(i, p, last_group):
                    for s in range(steps):
                        act.wait_ge(gate, i * steps + s + 1)
                        if s >= 2:
                            act.wait_ge(hidden_ready, i * steps + s - 1)
                        bias = {"bias": w["eb1"][:, s:s + 1]} if kind == "top2" else {}
                        nc.scalar.activation(act_out[:, s % 2, :], p_gate[s % 2][:, :], ACT.Silu, **bias)\
                            .then_inc(acted, 1)
                        if last_group:
                            continue
                        if s == at["act_h"]:
                            copy_h(i + 1, 1 - p)
                        if kind == "top2" and s == at["act_r1"]:
                            route_first(i + 1)
                        if s == at["act_route"]:
                            route_function(i + 1)
                        if s == turn_at + 1:
                            split(i + 1, 1 - p)
                    act.wait_ge(down, (i + 1) * n_down)
                    nc.scalar.copy(out_t[:, :], p_out[:, :]).then_inc(out_t_ready, 1)
                    if not last_group and turn_at + 1 >= steps:
                        split(i + 1, 1 - p)
                pipelined(act, None, start, body)

            @block.vector
            def _(dve):
                order = Order(dve, dve_order)
                dve.wait_ge(loaded, w["n"])
                nc.vector.memset(weight3[:, :, :, :].rearrange("p u r e -> p (u r e)"), 0.0)
                nc.vector.tensor_copy(pick[:, :, :], w["pick"][:, :, :]).then_inc(setup, 1)
                dve.wait_ge(setup, 1)

                def route_groups(j, part):
                    falling = bcast(const["falling16"][:, :], [T, GROUP, n_exp], 1)
                    by_group = lambda t: t[:, :, :].rearrange("p u (g e) -> p (u g) e", e=4)
                    flat = lambda t: t[:, :, :].rearrange("p u g -> p (u g)")
                    if part == 0:
                        dve.wait_ge(route_out, j + 1)
                        order.then(nc.vector.tensor_tensor(raw[:, :, :], score[:, :, :],
                                                           bcast(w["gate_bias"][:, :], [T, GROUP, n_exp], 1), ALU.add))
                        fall4 = bcast(const["falling4"][:, :], [T, 4 * GROUP, 4], 1)
                        pick_first_largest(nc, order, by_group(raw), fall4, flat(best), flat(best_rank), by_group(chosen))
                        order.then(nc.vector.scalar_tensor_tensor(left[:, :, :], chosen[:, :, :], NEG, raw[:, :, :],
                                                                  ALU.mult, ALU.add))
                        order.then(nc.vector.tensor_reduce(flat(g_score), by_group(left), AX.X, ALU.max))
                        order.then(nc.vector.tensor_tensor(flat(g_score), flat(g_score), flat(best), ALU.add))
                    elif part in (1, 2):
                        pick_first_largest(nc, order, g_score[:, :, :], bcast(const["falling4"][:, :], [T, GROUP, 4], 1),
                                           best[:, :, 0], best_rank[:, :, 0], g_chosen[:, :, :])
                        if part == 1:
                            order.then(nc.vector.tensor_copy(g_picked[:, :, :], g_chosen[:, :, :]))
                            order.then(nc.vector.scalar_tensor_tensor(g_score[:, :, :], g_chosen[:, :, :], NEG,
                                                                      g_score[:, :, :], ALU.mult, ALU.add))
                        else:
                            order.then(nc.vector.tensor_tensor(g_picked[:, :, :], g_picked[:, :, :], g_chosen[:, :, :],
                                                               ALU.add))
                            order.then(nc.vector.tensor_scalar(g_picked[:, :, :], g_picked[:, :, :], 1.0, -NEG,
                                                               ALU.subtract, ALU.mult))
                            order.then(nc.vector.tensor_tensor(by_group(left), by_group(raw),
                                                               bcast(flat(g_picked), [T, 4 * GROUP, 4], 2), ALU.add))
                    elif part < 7:
                        pick_first_largest(nc, order, left[:, :, :], falling, best[:, :, 0], best_rank[:, :, 0],
                                           chosen[:, :, :])
                        if part == 3:
                            order.then(nc.vector.tensor_copy(picked[:, :, :], chosen[:, :, :]))
                        else:
                            order.then(nc.vector.tensor_tensor(picked[:, :, :], picked[:, :, :], chosen[:, :, :], ALU.add))
                        if part < 6:
                            order.then(nc.vector.scalar_tensor_tensor(left[:, :, :], chosen[:, :, :], 2 * NEG,
                                                                      left[:, :, :], ALU.mult, ALU.add))
                    else:
                        order.then(nc.vector.tensor_tensor(weight[:, :, :], score[:, :, :], picked[:, :, :], ALU.mult))
                        order.then(nc.vector.tensor_reduce(total[:, :], weight[:, :, :], AX.X, ALU.add))
                        order.then(nc.vector.tensor_scalar(total[:, :], total[:, :], 1e-20, None, ALU.add))
                        order.then(nc.vector.reciprocal(total[:, :], total[:, :]))
                        order.then(nc.vector.tensor_scalar(total[:, :], total[:, :], 2.5, None, ALU.mult))
                        write_weights()

                def route_top(j, part, count):
                    falling = bcast(const["falling8"][:, :], [T, GROUP, n_exp], 1)
                    if part == 0:
                        dve.wait_ge(logits, j + 1)
                        p_logit = p_route[:, 0:GROUP * n_exp].rearrange("p (u e) -> p u e", e=n_exp)
                        if kind == "top2":
                            order.then(nc.vector.tensor_tensor(raw[:, :, :], p_logit,
                                                               bcast(w["rb2"][:, :], [T, GROUP, n_exp], 1), ALU.add))
                        else:
                            order.then(nc.vector.tensor_copy(raw[:, :, :], p_logit))
                        order.then(nc.vector.tensor_reduce(best[:, :, 0], raw[:, :, :], AX.X, ALU.max))
                        nc.vector.tensor_tensor(left[:, :, :], raw[:, :, :], bcast(best[:, :, 0], [T, GROUP, n_exp], 2),
                                                ALU.subtract).then_inc(route_in, 1)
                    elif part <= count:
                        pick_first_largest(nc, order, raw[:, :, :], falling, best[:, :, 1], best_rank[:, :, 1],
                                           chosen[:, :, :])
                        if part == 1:
                            order.then(nc.vector.tensor_copy(picked[:, :, :], chosen[:, :, :]))
                            if count == 2:
                                order.then(nc.vector.scalar_tensor_tensor(raw[:, :, :], chosen[:, :, :], NEG, raw[:, :, :],
                                                                          ALU.mult, ALU.add))
                        else:
                            order.then(nc.vector.tensor_tensor(picked[:, :, :], picked[:, :, :], chosen[:, :, :], ALU.add))
                    else:
                        dve.wait_ge(route_out, j + 1)
                        order.then(nc.vector.tensor_tensor(weight[:, :, :], score[:, :, :], picked[:, :, :], ALU.mult))
                        over = weight if count == 2 else score
                        order.then(nc.vector.tensor_reduce(total[:, :], over[:, :, :], AX.X, ALU.add))
                        order.then(nc.vector.reciprocal(total[:, :], total[:, :]))
                        if count == 1:
                            order.then(nc.vector.tensor_scalar(total[:, :], total[:, :], 2.0, None, ALU.mult))
                        write_weights()

                def write_weights():
                    order.then(nc.vector.tensor_tensor(weight[:, :, :], weight[:, :, :],
                                                       bcast(total[:, :], [T, GROUP, n_exp], 2), ALU.mult))
                    nc.vector.tensor_copy(weight3[:, :, :, 0:n_exp], weight[:, :, :].unsqueeze(2)
                                          .broadcast_to([T, GROUP, 3, n_exp])).then_inc(routed, 1)

                def route(j, part):
                    if kind == "groups":
                        route_groups(j, part)
                    else:
                        route_top(j, part, 2 if kind == "top2" else 1)

                def norm_stats(j):
                    layernorm_stats(nc, dve, order, x, j, stats, moments, pad).then_inc(stats_ready, 1)

                def norm_apply(j):
                    dve.wait_ge(rstd_ready, j + 1)
                    layernorm_apply(nc, x, j, moments, rstd, h).then_inc(normed, 1)
                    if kind != "top1":
                        dve.wait_ge(normed, j + 1)
                        xs = x[:, bass.ts(j, GROUP), :]
                        nc.vector.tensor_tensor(xs, xs, h[:, :, :], ALU.add).then_inc(x_h, 1)

                def split(j, q):
                    dve.wait_ge(high_ready, j + 1)
                    split_rest(nc, order, p_misc, high, rest, middle, parts[q]).then_inc(parts_ready, 1)

                def start():
                    norm_stats(0)
                    norm_apply(0)
                    for part in range(len(at["route"])):
                        route(0, part)
                    split(0, 0)

                def add_output(i):
                    dve.wait_ge(out_done, i + 1)
                    if kind != "top1":
                        dve.wait_ge(x_h, i + 1)
                    xs = x[:, bass.ts(i, GROUP), :]
                    nc.vector.tensor_tensor(xs, xs, p_misc[:, :].rearrange("p (u d) -> p u d", d=D), ALU.add)\
                        .then_inc(added, 1)

                def body(i, p, last_group):
                    def weigh_input(e):
                        dve.wait_ge(spread, i * n_weights + e + 1)
                        if e >= 2:
                            dve.wait_ge(gate, i * steps + (e - 1) * per)
                        nc.vector.tensor_tensor(h_w[:, e % 2, :], h_t[:, p, :], p_spread[:, :], ALU.mult)\
                            .then_inc(spread_used, 1)

                    if not last_group:
                        norm_stats(i + 1)
                    if weighs_input:
                        dve.wait_ge(h_t_ready, i + 1)
                        weigh_input(0)
                        weigh_input(1)
                    if not last_group:
                        norm_apply(i + 1)
                    for s in range(steps):
                        e = s // per
                        dve.wait_ge(acted, i * steps + s + 1)
                        if s >= 2:
                            dve.wait_ge(down, i * n_down + s - 1)
                        if weighs_input or e >= n_weights:
                            nc.vector.tensor_tensor(hidden[:, s % 2, :], act_out[:, s % 2, :], p_up[s % 2][:, :], ALU.mult)\
                                .then_inc(hidden_ready, 1)
                            if weighs_input and s % per == per - 1 and e + 2 < n_weights:
                                weigh_input(e + 2)
                        else:
                            a = act_out[:, s % 2, :]
                            if gated:
                                order.then(nc.vector.tensor_tensor(prod[:, s % 2, :], a, p_up[s % 2][:, :], ALU.mult))
                                a = prod[:, s % 2, :]
                            dve.wait_ge(spread, i * n_weights + e + 1)
                            nc.vector.tensor_tensor(hidden[:, s % 2, :], a, p_spread[:, :], ALU.mult)\
                                .then_inc(hidden_ready, 1)
                            if s % per == per - 1:
                                nc.vector.memset(pad[:, :], 0.0).then_inc(spread_used, 1)
                        if s == 0 and not (isinstance(i, int) and i == 0):
                            add_output(i - 1)
                        if last_group:
                            continue
                        for part, where in enumerate(at["route"]):
                            if s == where:
                                route(i + 1, part)
                        if s == turn_at + 2:
                            split(i + 1, 1 - p)
                    if not last_group and turn_at + 2 >= steps:
                        split(i + 1, 1 - p)
                pipelined(dve, order, start, body)
                add_output(NG - 1)

            @block.gpsimd
            def _(pool):
                def body(i, first):
                    layernorm_rstd(nc, pool, stats_ready, i, const["minus_half"], moments, rstd).then_inc(rstd_ready, 1)
                groups(pool, None, body)


def attention1(nc, name, x, const, w, loaded, aps, cross):
    scale = 1.0 / 32.0 if cross else float(D) ** -0.5
    with ExitStack() as ctx:
        L = Layer(nc, ctx, name)
        stats = L.sbuf("stats", [T, GROUP, 6])
        moments = L.sbuf("moments", [T, GROUP, 2])
        pad = L.sbuf("pad", [T, 1])
        first_pad = L.sbuf("first_pad", [T, 1])
        rstd = L.sbuf("rstd", [T, GROUP])
        h = L.sbuf("h", [T, GROUP, D])
        h_t = L.sbuf("h_t", [D, GROUP * T])
        q_t = L.sbuf("q_t", [D, GROUP * T])
        k_t = L.sbuf("k_t", [D, 2, GROUP * T])
        v = L.sbuf("v", [T, 2, GROUP, D])
        drop = L.sbuf("drop", [T, 2, GROUP, T]) if cross else None
        probs = L.sbuf("probs", [T, 2, GROUP, T])
        probs_t = L.sbuf("probs_t", [T, GROUP * T])
        top = L.sbuf("top", [T, GROUP])
        total = L.sbuf("total", [T, 2, GROUP])
        att = L.sbuf("att", [T, GROUP, D])
        att_t = L.sbuf("att_t", [D, GROUP * T])
        update = L.sbuf("update", [T, GROUP, D]) if cross else None
        p_misc = L.psum("p_misc", [T, BANK])
        p_q = L.psum("p_q", [T, BANK])
        p_k = L.psum("p_k", [T, BANK])
        p_v = L.psum("p_v", [T, BANK])
        p_score = L.psum("p_score", [T, GROUP, T])
        p_trans = L.psum("p_trans", [T, BANK])
        p_out = L.psum("p_out", [T, GROUP, D])

        k_in = [L.sem(f"k_in{n}") for n in range(2)]
        drop_in = [L.sem(f"drop_in{n}") for n in range(2)]
        v_in = [L.sem(f"v_in{n}") for n in range(2)]
        stats_ready = L.sem("stats_ready")
        rstd_ready = L.sem("rstd_ready")
        normed = L.sem("normed")
        trans = L.sem("trans")
        h_t_ready = L.sem("h_t_ready")
        proj = L.sem("proj")
        q_ready = L.sem("q_ready")
        k_ready = L.sem("k_ready")
        v_ready = L.sem("v_ready")
        scored = L.sem("scored")
        shifted = L.sem("shifted")
        expd = L.sem("expd")
        masked = L.sem("masked")
        turned = L.sem("turned")
        turned_out = L.sem("turned_out")
        weighed = L.sem("weighed")
        divided = L.sem("divided")
        att_turned = L.sem("att_turned")
        att_t_ready = L.sem("att_t_ready")
        out_done = L.sem("out_done")
        added = L.sem("added")
        dve_order = L.sem("dve_order")
        started = lambda i: not (isinstance(i, int) and i == 0)

        loads = lambda i, p: (i - p) * 8 + 16

        with nc.Block() as block:
            if cross:
                @block.sync
                def _(sp):
                    def load_group(j, q):
                        group, columns = bass.ts(j, GROUP), bass.ts(j, GROUP * T)
                        if not isinstance(j, int) or j >= 2:
                            sp.wait_ge(scored, j - 1)
                        sp.dma_start(k_t[:, q, :], aps["ctx_t"][:, columns]).then_inc(k_in[q], 16)
                        if not isinstance(j, int) or j >= 2:
                            sp.wait_ge(masked, j - 1)
                        sp.dma_start(drop[:, q, :, :], aps["drop"][:, group, :]).then_inc(drop_in[q], 16)
                        if not isinstance(j, int) or j >= 2:
                            sp.wait_ge(weighed, j - 1)
                        sp.dma_start(v[:, q, :, :], aps["ctx"][:, group, :]).then_inc(v_in[q], 16)

                    def body(i, p, last_group):
                        if not last_group:
                            load_group(i + 1, 1 - p)
                    pipelined(sp, None, lambda: load_group(0, 0), body)

            @block.tensor
            def _(pe):
                pe.wait_ge(loaded, w["n"])

                def turn_h(j):
                    pe.wait_ge(normed, j + 1)
                    for u in range(GROUP):
                        last = nc.tensor.transpose(p_misc[:, u * T:(u + 1) * T], h[:, u, :], const["ident"][:, :])
                    last.then_inc(trans, 1)

                def project(j):
                    if cross:
                        return
                    pe.wait_ge(h_t_ready, j + 1)
                    nc.tensor.matmul(p_q[:, :], w["wq"][:, :], h_t[:, :], start=True, stop=True).then_inc(proj, 1)
                    nc.tensor.matmul(p_k[:, :], w["wk"][:, :], h_t[:, :], start=True, stop=True).then_inc(proj, 1)
                    for u in range(GROUP):
                        last = nc.tensor.matmul(p_v[:, u * D:(u + 1) * D], h_t[:, u * T:(u + 1) * T], w["wv"][:, :],
                                                start=True, stop=True)
                    last.then_inc(proj, 1)

                def scores(i, p):
                    if cross:
                        pe.wait_ge(h_t_ready, i + 1)
                        pe.wait_ge(k_in[p], loads(i, p))
                    else:
                        pe.wait_ge(q_ready, i + 1)
                        pe.wait_ge(k_ready, i + 1)
                    queries, keys = (h_t, k_t[:, p, :]) if cross else (q_t, k_t[:, 0, :])
                    for u in range(GROUP):
                        last = nc.tensor.matmul(p_score[:, u, :], queries[:, u * T:(u + 1) * T],
                                                keys[:, u * T:(u + 1) * T], start=True, stop=True)
                    last.then_inc(scored, 1)

                def transposes(j, q):
                    if cross:
                        pe.wait_ge(masked, j + 1)
                    else:
                        pe.wait_ge(expd, j + 1)
                    for u in range(GROUP):
                        last = nc.tensor.transpose(p_trans[:, u * T:(u + 1) * T], probs[:, q, u, :], const["ident"][:, :])
                    last.then_inc(turned, 1)

                def values(j, q):
                    pe.wait_ge(turned_out, j + 1)
                    if cross:
                        pe.wait_ge(v_in[q], loads(j, q))
                    else:
                        pe.wait_ge(v_ready, j + 1)
                    pe.wait_ge(divided, j + 1)
                    for u in range(GROUP):
                        last = nc.tensor.matmul(p_out[:, u, :], probs_t[:, u * T:(u + 1) * T], v[:, q, u, :],
                                                start=True, stop=True)
                    last.then_inc(weighed, 1)

                def output(j):
                    if not cross:
                        return
                    pe.wait_ge(divided, j + 2)
                    for u in range(GROUP):
                        last = nc.tensor.transpose(p_q[:, u * T:(u + 1) * T], att[:, u, :], const["ident"][:, :])
                    last.then_inc(att_turned, 1)
                    pe.wait_ge(att_t_ready, j + 1)
                    pe.wait_ge(added, j + 1)
                    for u in range(GROUP):
                        last = nc.tensor.matmul(p_k[:, u * D:(u + 1) * D], att_t[:, u * T:(u + 1) * T],
                                                w["wo"][:, :], start=True, stop=True)
                    last.then_inc(out_done, 1)

                def start():
                    turn_h(0)
                    project(0)

                def body(i, p, last_group):
                    if started(i):
                        transposes(i - 1, 1 - p)
                    scores(i, p)
                    if not last_group:
                        turn_h(i + 1)
                    if started(i):
                        values(i - 1, 1 - p)
                    if not last_group:
                        project(i + 1)
                    if started(i):
                        output(i - 1)
                pipelined(pe, None, start, body)
                transposes(NG - 1, 1)
                values(NG - 1, 1)
                output(NG - 1)

            @block.scalar
            def _(act):
                act.wait_ge(loaded, w["n"])

                def copy_h(j):
                    act.wait_ge(trans, j + 1)
                    nc.scalar.copy(h_t[:, :], p_misc[:, :]).then_inc(h_t_ready, 1)

                def project(j):
                    if cross:
                        return
                    act.wait_ge(proj, 3 * j + 1)
                    nc.scalar.activation(q_t[:, :], p_q[:, :], ACT.Identity, bias=w["bq"][:, 0:1]).then_inc(q_ready, 1)
                    act.wait_ge(proj, 3 * j + 2)
                    nc.scalar.activation(k_t[:, 0, :], p_k[:, :], ACT.Identity, bias=w["bk"][:, 0:1]).then_inc(k_ready, 1)

                def exponent(i, p):
                    act.wait_ge(shifted, i + 1)
                    nc.scalar.activation(probs[:, p, :, :], probs[:, p, :, :], ACT.Exp, scale=scale).then_inc(expd, 1)

                def copy_turned(j):
                    act.wait_ge(turned, j + 1)
                    nc.scalar.copy(probs_t[:, :], p_trans[:, :]).then_inc(turned_out, 1)

                def copy_att(j):
                    if cross:
                        act.wait_ge(att_turned, j + 1)
                        nc.scalar.copy(att_t[:, :], p_q[:, :]).then_inc(att_t_ready, 1)

                def start():
                    copy_h(0)
                    project(0)

                def body(i, p, last_group):
                    if started(i):
                        copy_turned(i - 1)
                    if not last_group:
                        copy_h(i + 1)
                    exponent(i, p)
                    if not last_group:
                        project(i + 1)
                    if started(i):
                        copy_att(i - 1)
                pipelined(act, None, start, body)
                copy_turned(NG - 1)
                copy_att(NG - 1)

            @block.vector
            def _(dve):
                order = Order(dve, dve_order)
                dve.wait_ge(loaded, w["n"])
                nc.vector.memset(pad[:, :], 0.0).then_inc(divided, 1)
                nc.vector.memset(first_pad[:, :], 0.0).then_inc(added, 1)

                def norm(j):
                    if started(j):
                        dve.wait_ge(trans, j)
                    layernorm_stats(nc, dve, order, x, j, stats, moments, pad).then_inc(stats_ready, 1)
                    dve.wait_ge(rstd_ready, j + 1)
                    layernorm_apply(nc, x, j, moments, rstd, h).then_inc(normed, 1)

                def copy_v(j, q):
                    if not cross:
                        dve.wait_ge(proj, 3 * j + 3)
                        nc.vector.tensor_tensor(v[:, q, :, :], p_v[:, :].rearrange("p (u d) -> p u d", d=D),
                                                bcast(w["bv"][:, :], [T, GROUP, D], 1), ALU.add).then_inc(v_ready, 1)

                def shift(i, p):
                    dve.wait_ge(scored, i + 1)
                    order.then(nc.vector.tensor_reduce(top[:, :], p_score[:, :, :], AX.X, ALU.max))
                    nc.vector.tensor_tensor(probs[:, p, :, :], p_score[:, :, :], bcast(top[:, :], [T, GROUP, T], 2),
                                            ALU.subtract).then_inc(shifted, 1)

                def sums(i, p):
                    dve.wait_ge(expd, i + 1)
                    order.then(nc.vector.tensor_reduce(total[:, p, :], probs[:, p, :, :], AX.X, ALU.add))
                    if cross:
                        dve.wait_ge(drop_in[p], loads(i, p))
                        nc.vector.tensor_tensor(probs[:, p, :, :], probs[:, p, :, :], drop[:, p, :, :], ALU.mult)\
                            .then_inc(masked, 1)
                    order.then(nc.vector.reciprocal(total[:, p, :], total[:, p, :]))

                def divide(j, q):
                    dve.wait_ge(weighed, j + 1)
                    dve.wait_ge(added, j + 1)
                    nc.vector.tensor_tensor(att[:, :, :], p_out[:, :, :], bcast(total[:, q, :], [T, GROUP, D], 2),
                                            ALU.mult).then_inc(divided, 1)

                def add_output(j):
                    xs = x[:, bass.ts(j, GROUP), :]
                    if cross:
                        dve.wait_ge(out_done, j + 1)
                        order.then(nc.vector.tensor_tensor(update[:, :, :], p_k[:, :].rearrange("p (u d) -> p u d", d=D),
                                                           bcast(w["bo"][:, :], [T, GROUP, D], 1), ALU.add))
                        nc.vector.tensor_tensor(xs, xs, update[:, :, :], ALU.add).then_inc(added, 1)
                    else:
                        dve.wait_ge(divided, j + 2)
                        nc.vector.tensor_tensor(xs, xs, att[:, :, :], ALU.add).then_inc(added, 1)

                def start():
                    norm(0)
                    copy_v(0, 0)

                def body(i, p, last_group):
                    if not last_group:
                        norm(i + 1)
                    shift(i, p)
                    if started(i):
                        divide(i - 1, 1 - p)
                    sums(i, p)
                    if not last_group:
                        copy_v(i + 1, 1 - p)
                    if started(i):
                        add_output(i - 1)
                pipelined(dve, order, start, body, per=6 if cross else 5)
                divide(NG - 1, 1)
                add_output(NG - 1)

            @block.gpsimd
            def _(pool):
                def norm_scale(j):
                    layernorm_rstd(nc, pool, stats_ready, j, const["minus_half"], moments, rstd).then_inc(rstd_ready, 1)

                def body(i, p, last_group):
                    if not last_group:
                        norm_scale(i + 1)
                pipelined(pool, None, lambda: norm_scale(0), body)


def state_space(nc, name, x, const, w, loaded):
    NH, P8, NC = 32, 8, 4
    QH = 8
    NU = GROUP * NH // QH
    TAPS = 4
    with ExitStack() as ctx:
        L = Layer(nc, ctx, name)
        stats = L.sbuf("stats", [T, GROUP, 6])
        moments = L.sbuf("moments", [T, GROUP, 2])
        pad = L.sbuf("pad", [T, 1])
        rstd = L.sbuf("rstd", [T, GROUP])
        h = L.sbuf("h", [T, GROUP, D])
        h_t = L.sbuf("h_t", [D, GROUP * T])
        padded = L.sbuf("padded", [T, NC, GROUP, T + TAPS - 1])
        conv = L.sbuf("conv", [T, 2, NC, GROUP, T])
        gate = L.sbuf("gate", [T, 2, 2, GROUP * T])
        dt_raw = L.sbuf("dt_raw", [T, GROUP, NH])
        dt = L.sbuf("dt", [T, 2, GROUP, NH])
        da = L.sbuf("da", [T, GROUP, 3, NH])
        neg_a = L.sbuf("neg_a", [T, NH])
        high = L.sbuf("high", [3 * NH, GROUP * T], BF16)
        rest = L.sbuf("rest", [3 * NH, GROUP * T])
        middle = L.sbuf("middle", [3 * NH, GROUP * T], BF16)
        parts = L.sbuf("parts", [3 * NH, 2, GROUP * T], BF16)
        pick = L.sbuf("pick", [3 * NH, NH, T], BF16)
        minus = L.sbuf("minus", [3 * NH, NH], BF16)
        cb = L.sbuf("cb", [T, 2, GROUP, T])
        xs_t = L.sbuf("xs_t", [T, GROUP, 2 * T])
        ident_b = L.sbuf("ident_b", [T, T], BF16)
        future_b = L.sbuf("future_b", [T, T], BF16)
        xdt_own = L.sbuf("xdt_own", [T, 2, NH * T])
        decay = L.sbuf("decay", [T, 2, QH, T])
        mix = L.sbuf("mix", [T, 2, QH, T])
        y = L.sbuf("y", [T, 2, GROUP, T])
        sq = L.sbuf("sq", [T, 2, GROUP, T])
        out_w = L.sbuf("out_w", [T, 2, D])
        ones = L.sbuf("ones", [T, 2])
        ms = L.sbuf("ms", [T, GROUP])
        rms = L.sbuf("rms", [T, GROUP])
        o = L.sbuf("o", [T, GROUP, D])
        p_a = L.psum("p_a", [T, BANK])
        p_b = L.psum("p_b", [T, BANK])
        p_seg = [L.psum(f"p_seg{n}", [T, 2, BANK]) for n in range(2)]
        p_y = L.psum("p_y", [T, 2, BANK])
        stats_ready = L.sem("stats_ready")
        rstd_ready = L.sem("rstd_ready")
        normed = L.sem("normed")
        x_h = L.sem("x_h")
        trans = L.sem("trans")
        h_t_ready = L.sem("h_t_ready")
        conv_in = L.sem("conv_in")
        padded_ready = L.sem("padded_ready")
        convolved = L.sem("convolved")
        conv_ready = L.sem("conv_ready")
        z_done = L.sem("z_done")
        gate_ready = L.sem("gate_ready")
        dt_done = L.sem("dt_done")
        dt_in = L.sem("dt_in")
        dt_exp = L.sem("dt_exp")
        da_ready = L.sem("da_ready")
        cum_done = L.sem("cum_done")
        high_ready = L.sem("high_ready")
        parts_ready = L.sem("parts_ready")
        cb_done = L.sem("cb_done")
        cb_ready = L.sem("cb_ready")
        x_turned = L.sem("x_turned")
        xs_half = L.sem("xs_half")
        xs_ready = L.sem("xs_ready")
        own_ready = L.sem("own_ready")
        seg_done = L.sem("seg_done")
        decay_ready = L.sem("decay_ready")
        mix_ready = L.sem("mix_ready")
        mixed = L.sem("mixed")
        y_ready = L.sem("y_ready")
        sq_ready = L.sem("sq_ready")
        ms_done = L.sem("ms_done")
        ms_ready = L.sem("ms_ready")
        rms_ready = L.sem("rms_ready")
        out_done = L.sem("out_done")
        o_scaled = L.sem("o_scaled")
        o_stats_ready = L.sem("o_stats_ready")
        o_rstd_ready = L.sem("o_rstd_ready")
        o_ready = L.sem("o_ready")
        o_order = L.sem("o_order")
        dve_order = L.sem("dve_order")
        setup = L.sem("setup")
        started = lambda i: not (isinstance(i, int) and i == 0)

        with nc.Block() as block:
            @block.tensor
            def _(pe):
                pe.wait_ge(loaded, w["n"])
                pe.wait_ge(setup, 4)

                def turn_h(j):
                    pe.wait_ge(normed, j + 1)
                    if started(j):
                        pe.wait_ge(xs_ready, j)
                    for u in range(GROUP):
                        last = nc.tensor.transpose(p_a[:, u * T:(u + 1) * T], h[:, u, :], const["ident"][:, :])
                    last.then_inc(trans, 1)

                def project(j, c):
                    if c < 2:
                        pe.wait_ge(h_t_ready, j + 1)
                    else:
                        pe.wait_ge(padded_ready, NC * j + c - 1)
                    nc.tensor.matmul((p_b, p_a)[c % 2][:, :], w["conv_in"][:, c * T:(c + 1) * T], h_t[:, :],
                                     start=True, stop=True).then_inc(conv_in, 1)

                def time_steps(j, after_output):
                    if after_output:
                        pe.wait_ge(ms_ready, j - 1)
                    else:
                        pe.wait_ge(padded_ready, NC * j + 3)
                    for u in range(GROUP):
                        last = nc.tensor.matmul(p_b[:, u * NH:(u + 1) * NH], h_t[:, u * T:(u + 1) * T], w["dt_in"][:, :],
                                                start=True, stop=True)
                    last.then_inc(dt_done, 1)

                def running_sums(j):
                    pe.wait_ge(da_ready, j + 1)
                    for u in range(GROUP):
                        last = nc.tensor.matmul(p_b[0:3 * NH, u * T:(u + 1) * T], da[:, u, :, :].rearrange("p r h -> p (r h)"),
                                                w["upto"][:, :], start=True, stop=True)
                    last.then_inc(cum_done, 1)

                def gates(j, b, after_output):
                    if b == 1:
                        pe.wait_ge(parts_ready, j + 1)
                    elif after_output:
                        pe.wait_ge(o_scaled, j - 1)
                    else:
                        pe.wait_ge(padded_ready, NC * j + 4)
                    nc.tensor.matmul((p_a, p_b)[b][:, :], w["z_in"][:, b * T:(b + 1) * T], h_t[:, :], start=True, stop=True)\
                        .then_inc(z_done, 1)

                def products(j, q):
                    pe.wait_ge(gate_ready, 2 * j + 2)
                    pe.wait_ge(conv_ready, j + 1)
                    for u in range(GROUP):
                        last = nc.tensor.matmul(p_a[:, u * T:(u + 1) * T], conv[:, q, 2, u, :], conv[:, q, 3, u, :],
                                                start=True, stop=True)
                    last.then_inc(cb_done, 1)

                def turn_x(j, q, b):
                    if b == 1:
                        pe.wait_ge(cb_ready, j + 1)
                    for u in range(GROUP):
                        last = nc.tensor.transpose((p_b, p_a)[b][:, u * T:(u + 1) * T], conv[:, q, b, u, :],
                                                   const["ident"][:, :])
                    last.then_inc(x_turned, 1)

                def segments(i, n, q):
                    u, part, g = n // 4, n % 4, i * NU + n
                    if n == 0:
                        pe.wait_ge(parts_ready, i + 1)
                    if not isinstance(g, int) or g >= 2:
                        pe.wait_ge(decay_ready, g - 1)
                    for half in range(2):
                        first = part * QH + 4 * half
                        out = p_seg[n % 2][:, half, :]
                        nc.tensor.matmul(out, ident_b[:, :], bcast(future_b[:, :], [T, 4, T], 1), start=True, stop=False)
                        nc.tensor.matmul(out, parts[:, q, u * T:(u + 1) * T], bcast(minus[:, first:first + 4], [3 * NH, 4, T], 2),
                                         start=False, stop=False)
                        for k in range(4):
                            last = nc.tensor.matmul(out[:, k * T:(k + 1) * T], pick[:, first + k, :],
                                                    parts[:, q, u * T:(u + 1) * T], start=False, stop=(k == 3))
                    last.then_inc(seg_done, 1)

                def mixing(i, n):
                    u, part = n // 4, n % 4
                    pe.wait_ge(mix_ready, i * NU + n + 1)
                    if part == 0:
                        pe.wait_ge(own_ready, i * GROUP + u + 1)
                        if u >= 2 or not isinstance(i, int) or i > 0:
                            pe.wait_ge(y_ready, i * GROUP + u - 1)
                    for k in range(QH):
                        head = part * QH + k
                        block_of = part // 2
                        last = nc.tensor.matmul(p_y[:, u % 2, block_of * T:(block_of + 1) * T],
                                                xdt_own[:, u % 2, head * T:(head + 1) * T], mix[:, n % 2, k, :],
                                                start=(head % 16 == 0), stop=(head % 16 == 15))
                    last.then_inc(mixed, 1)

                def output(j):
                    pe.wait_ge(sq_ready, GROUP * (j + 1))
                    for u in range(GROUP):
                        for b in range(2):
                            last = nc.tensor.matmul(p_b[:, 2 * u:2 * u + 2], sq[:, b, u, :], ones[:, :],
                                                    start=(b == 0), stop=(b == 1))
                    last.then_inc(ms_done, 1)
                    for u in range(GROUP):
                        for b in range(2):
                            last = nc.tensor.matmul(p_a[:, u * D:(u + 1) * D], y[:, b, u, :], out_w[:, b, :],
                                                    start=(b == 0), stop=(b == 1))
                    last.then_inc(out_done, 1)

                def start():
                    turn_h(0)
                    for c in range(NC):
                        project(0, c)
                    time_steps(0, False)
                    running_sums(0)
                    gates(0, 0, False)
                    gates(0, 1, False)
                    products(0, 0)
                    turn_x(0, 0, 0)
                    turn_x(0, 0, 1)
                    segments(0, 0, 0)

                def body(i, p, last_group):
                    j, q = i + 1, 1 - p
                    for n in range(NU):
                        if n + 1 < NU:
                            segments(i, n + 1, p)
                        elif not last_group:
                            segments(j, 0, q)
                        mixing(i, n)
                        if not last_group:
                            if n == 1:
                                turn_h(j)
                            if n == 2:
                                project(j, 0)
                                project(j, 1)
                            if n == 3:
                                project(j, 2)
                                project(j, 3)
                        if n == 4 and started(i):
                            if not last_group:
                                pe.wait_ge(padded_ready, NC * (j + 1))
                            output(i - 1)
                        if not last_group:
                            if n == 5:
                                time_steps(j, started(i))
                            if n == 9:
                                running_sums(j)
                            if n == 10:
                                gates(j, 0, started(i))
                            if n == 11:
                                gates(j, 1, started(i))
                            if n == 13:
                                products(j, q)
                                turn_x(j, q, 0)
                            if n == 14:
                                turn_x(j, q, 1)
                pipelined(pe, None, start, body)
                pe.wait_ge(o_scaled, NG - 1)
                output(NG - 1)

            @block.scalar
            def _(act):
                act.wait_ge(loaded, w["n"])
                nc.scalar.activation(neg_a[:, :], w["a_log"][:, :], ACT.Exp).then_inc(setup, 1)
                act.wait_ge(setup, 4)

                def copy_h(j):
                    act.wait_ge(trans, j + 1)
                    nc.scalar.copy(h_t[:, :], p_a[:, :]).then_inc(h_t_ready, 1)

                def pad_block(j, q, c):
                    act.wait_ge(conv_in, NC * j + c + 1)
                    source = (p_b, p_a)[c % 2][:, :].rearrange("p (u t) -> p u t", t=T)
                    nc.scalar.copy(padded[:, c, :, TAPS - 1:], source)
                    nc.scalar.activation(conv[:, q, c, :, :], source, ACT.Identity, bias=w["conv_b"][:, c:c + 1],
                                         scale=w["conv_w"][:, c, TAPS - 1:TAPS]).then_inc(padded_ready, 1)

                def time_exp(j):
                    act.wait_ge(dt_in, j + 1)
                    nc.scalar.activation(dt_raw[:, :, :], dt_raw[:, :, :], ACT.Exp, scale=-1.0).then_inc(dt_exp, 1)

                def split(j, q):
                    act.wait_ge(cum_done, j + 1)
                    split_high(nc, p_b, high, parts[:, q, :]).then_inc(high_ready, 1)

                def silus(j, q):
                    act.wait_ge(convolved, 2 * j + 2)
                    for c in (2, 3, 0, 1):
                        last = nc.scalar.activation(conv[:, q, c, :, :], conv[:, q, c, :, :], ACT.Silu)
                    last.then_inc(conv_ready, 1)
                    for b in range(2):
                        act.wait_ge(z_done, 2 * j + b + 1)
                        nc.scalar.activation(gate[:, q, b, :], (p_a, p_b)[b][:, :], ACT.Silu).then_inc(gate_ready, 1)

                def square(i, u):
                    act.wait_ge(y_ready, GROUP * i + u + 1)
                    nc.scalar.activation(sq[:, :, u, :], y[:, :, u, :], ACT.Square).then_inc(sq_ready, 1)

                def start():
                    copy_h(0)
                    for c in range(NC):
                        pad_block(0, 0, c)
                    time_exp(0)
                    split(0, 0)
                    silus(0, 0)

                def body(i, p, last_group):
                    j, q = i + 1, 1 - p
                    for n in range(NU):
                        g = i * NU + n
                        act.wait_ge(seg_done, g + 1)
                        if not isinstance(g, int) or g >= 2:
                            act.wait_ge(mix_ready, g - 1)
                        nc.scalar.activation(decay[:, n % 2, :, :], p_seg[n % 2][:, :, :], ACT.Exp).then_inc(decay_ready, 1)
                        if n == 2 and started(i):
                            square(i - 1, GROUP - 1)
                        if n in (7, 11, 14):
                            square(i, (n - 6) // 4)
                        if last_group:
                            continue
                        if n == 2:
                            copy_h(j)
                        if n in (3, 4):
                            pad_block(j, q, 2 * (n - 3))
                            pad_block(j, q, 2 * (n - 3) + 1)
                        if n == 7:
                            time_exp(j)
                        if n == 10:
                            split(j, q)
                        if n == 12:
                            silus(j, q)
                pipelined(act, None, start, body)
                square(NG - 1, GROUP - 1)

            @block.vector
            def _(dve):
                order = Order(dve, dve_order)
                dve.wait_ge(loaded, w["n"])
                nc.vector.memset(ones[:, :], 1.0)
                nc.vector.tensor_copy(ident_b[:, :], const["ident"][:, :])
                nc.vector.tensor_copy(pick[:, :, :], bcast(w["head_row"][:, :], [3 * NH, NH, T], 2))
                nc.vector.tensor_scalar(minus[:, :], w["head_row"][:, :], -1.0, None, ALU.mult)
                nc.vector.tensor_scalar(future_b[:, :], w["upto"][:, :], 1.0, -NEG, ALU.subtract, ALU.mult)
                nc.vector.memset(padded[:, :, :, :].rearrange("p c u t -> p (c u t)"), 0.0)
                nc.vector.tensor_tensor(out_w[:, :, :], w["out_w"][:, :, :], bcast(w["norm_w"][:, :], [T, 2, D], 2), ALU.mult)\
                    .then_inc(setup, 1)
                dve.wait_ge(setup, 3)
                nc.vector.tensor_scalar(neg_a[:, :], neg_a[:, :], -1.0, None, ALU.mult).then_inc(setup, 1)
                dve.wait_ge(setup, 4)

                def norm(j):
                    if started(j):
                        dve.wait_ge(trans, j)
                        dve.wait_ge(x_h, j)
                    layernorm_stats(nc, dve, order, x, j, stats, moments, pad).then_inc(stats_ready, 1)
                    dve.wait_ge(rstd_ready, j + 1)
                    layernorm_apply(nc, x, j, moments, rstd, h).then_inc(normed, 1)

                def tap(j, q, pair, k):
                    if k == 0:
                        dve.wait_ge(padded_ready, NC * j + 2 * pair + 2)
                    for c in (2 * pair, 2 * pair + 1):
                        last = nc.vector.scalar_tensor_tensor(conv[:, q, c, :, :], padded[:, c, :, k:k + T],
                                                              w["conv_w"][:, c, k:k + 1], conv[:, q, c, :, :],
                                                              ALU.mult, ALU.add)
                    if k < TAPS - 2:
                        order.then(last)
                    else:
                        last.then_inc(convolved, 1)

                def time_bias(j):
                    dve.wait_ge(dt_done, j + 1)
                    nc.vector.tensor_tensor(dt_raw[:, :, :], p_b[:, 0:GROUP * NH].rearrange("p (u h) -> p u h", h=NH),
                                            bcast(w["dt_bias"][:, :], [T, GROUP, NH], 1), ALU.add).then_inc(dt_in, 1)

                def time_step(j, q):
                    dve.wait_ge(dt_exp, j + 1)
                    order.then(nc.vector.tensor_scalar(dt_raw[:, :, :], dt_raw[:, :, :], 1.0, None, ALU.add))
                    order.then(nc.vector.reciprocal(dt_raw[:, :, :], dt_raw[:, :, :]))
                    order.then(nc.vector.tensor_scalar(dt[:, q, :, :], dt_raw[:, :, :], 0.1 - 0.001, 0.001, ALU.mult, ALU.add))
                    for r in range(3):
                        last = nc.vector.tensor_tensor(da[:, :, r, :], dt[:, q, :, :], bcast(neg_a[:, :], [T, GROUP, NH], 1), ALU.mult)
                    last.then_inc(da_ready, 1)

                def split(j, q):
                    dve.wait_ge(high_ready, j + 1)
                    split_rest(nc, order, p_b, high, rest, middle, parts[:, q, :]).then_inc(parts_ready, 1)

                def copy_products(j, q):
                    dve.wait_ge(cb_done, j + 1)
                    nc.vector.tensor_copy(cb[:, q, :, :], p_a[:, :]).then_inc(cb_ready, 1)

                def copy_x(j, b):
                    dve.wait_ge(x_turned, 2 * j + b + 1)
                    if b == 0 and started(j):
                        dve.wait_ge(own_ready, GROUP * j)
                    nc.vector.tensor_copy(xs_t[:, :, b * T:(b + 1) * T],
                                          (p_b, p_a)[b][:, :].rearrange("p (u c) -> p u c", u=GROUP))\
                        .then_inc((xs_half, xs_ready)[b], 1)

                def combine(i, n, p):
                    u, g = n // 4, i * NU + n
                    dve.wait_ge(decay_ready, g + 1)
                    if not isinstance(g, int) or g >= 2:
                        dve.wait_ge(mixed, g - 1)
                    nc.vector.tensor_tensor(mix[:, n % 2, :, :], decay[:, n % 2, :, :],
                                            bcast(cb[:, p, u, :], [T, QH, T], 1), ALU.mult).then_inc(mix_ready, 1)

                def gated(i, u, p):
                    dve.wait_ge(mixed, i * NU + 4 * (u + 1))
                    if u == 0:
                        dve.wait_ge(gate_ready, 2 * i + 2)
                        if started(i):
                            dve.wait_ge(out_done, i)
                    for b in range(2):
                        last = nc.vector.scalar_tensor_tensor(y[:, b, u, :], conv[:, p, b, u, :], w["d_skip"][:, b:b + 1],
                                                              p_y[:, u % 2, b * T:(b + 1) * T], ALU.mult, ALU.add)
                    order.then(last)
                    nc.vector.tensor_tensor(y[:, :, u, :], y[:, :, u, :], gate[:, p, :, u * T:(u + 1) * T], ALU.mult)\
                        .then_inc(y_ready, 1)

                def mean_square(j):
                    dve.wait_ge(ms_done, j + 1)
                    nc.vector.tensor_scalar(ms[:, :], p_b[:, 0:2 * GROUP].rearrange("p (u two) -> p u two", two=2)[:, :, 0],
                                            1.0 / 256.0, 1e-5, ALU.mult, ALU.add).then_inc(ms_ready, 1)

                def norm_output(j):
                    dve.wait_ge(out_done, j + 1)
                    dve.wait_ge(rms_ready, j + 1)
                    nc.vector.tensor_tensor(o[:, :, :], p_a[:, :].rearrange("p (u d) -> p u d", d=D),
                                            bcast(rms[:, :], [T, GROUP, D], 2), ALU.mult).then_inc(o_scaled, 1)
                    dve.wait_ge(o_scaled, j + 1)
                    layernorm_stats(nc, dve, order, o, 0, stats, moments, pad).then_inc(o_stats_ready, 1)
                    dve.wait_ge(o_rstd_ready, j + 1)
                    layernorm_apply(nc, o, 0, moments, rstd, o).then_inc(o_ready, 1)

                def start():
                    norm(0)
                    for k in range(TAPS - 1):
                        tap(0, 0, 0, k)
                    time_bias(0)
                    time_step(0, 0)
                    for k in range(TAPS - 1):
                        tap(0, 0, 1, k)
                    split(0, 0)
                    copy_products(0, 0)
                    copy_x(0, 0)
                    copy_x(0, 1)

                def body(i, p, last_group):
                    j, q = i + 1, 1 - p
                    dve.wait_ge(cb_ready, i + 1)
                    for n in range(NU):
                        combine(i, n, p)
                        if n == 0 and not last_group:
                            norm(j)
                        if n == 1 and started(i):
                            gated(i - 1, GROUP - 1, q)
                        if n == 5 and started(i):
                            mean_square(i - 1)
                        if n in (6, 10, 13):
                            gated(i, (n - 6 + 1) // 4, p)
                        if n == 7 and started(i):
                            norm_output(i - 1)
                        if last_group:
                            continue
                        if n in (4, 5, 6):
                            tap(j, q, 0, n - 4)
                        if n == 6:
                            time_bias(j)
                        if n == 8:
                            time_step(j, q)
                        if n in (8, 9, 10):
                            tap(j, q, 1, n - 8)
                        if n == 11:
                            split(j, q)
                        if n == 14:
                            copy_products(j, q)
                            copy_x(j, 0)
                        if n == 15:
                            copy_x(j, 1)
                pipelined(dve, order, start, body, per=2 + 4 + 2 + 4 + 3 + 2)
                gated(NG - 1, GROUP - 1, 1)
                mean_square(NG - 1)
                norm_output(NG - 1)

            @block.gpsimd
            def _(pool):
                nc.gpsimd.memset(xdt_own[:, :, :].rearrange("p a b -> p (a b)"), 0.0).then_inc(setup, 1)
                pool.wait_ge(setup, 4)

                def add_h(j):
                    pool.wait_ge(normed, j + 1)
                    xs = x[:, bass.ts(j, GROUP), :]
                    nc.gpsimd.tensor_tensor(xs, xs, h[:, :, :], ALU.add).then_inc(x_h, 1)

                def own(i, u, p):
                    if u == 0:
                        pool.wait_ge(xs_ready, i + 1)
                    if u >= 2 or not isinstance(i, int) or i > 0:
                        pool.wait_ge(mixed, i * NU + 4 * (u - 1))
                    for b in range(2):
                        dst = xdt_own[:, u % 2, b * 16 * T:(b + 1) * 16 * T]
                        dst = bass.AP(dst.tensor, dst.offset, [dst.ap[0], [T + P8, 16], [1, P8]])
                        last = nc.gpsimd.tensor_tensor(
                            dst, xs_t[:, u, b * T:(b + 1) * T].rearrange("p (h d) -> p h d", d=P8),
                            bcast(dt[:, p, u, 16 * b:16 * b + 16], [T, 16, P8], 2), ALU.mult)
                    last.then_inc(own_ready, 1)

                def rms_scale(j):
                    pool.wait_ge(ms_ready, j + 1)
                    nc.gpsimd.tensor_tensor(rms[:, :], ms[:, :], const["minus_half"][:, 0:GROUP], ALU.pow).then_inc(rms_ready, 1)

                def norm_scale(j):
                    layernorm_rstd(nc, pool, stats_ready, j, const["minus_half"], moments, rstd).then_inc(rstd_ready, 1)

                def output_scale(j):
                    layernorm_rstd(nc, pool, o_stats_ready, j, const["minus_half"], moments, rstd).then_inc(o_rstd_ready, 1)

                def add_output(j):
                    pool.wait_ge(o_ready, j + 1)
                    nc.gpsimd.tensor_tensor(o[:, :, :], o[:, :, :], bcast(w["ln_w"][:, :], [T, GROUP, D], 1), ALU.mult)\
                        .then_inc(o_order, 1)
                    pool.wait_ge(o_order, 2 * j + 1)
                    nc.gpsimd.tensor_tensor(o[:, :, :], o[:, :, :], bcast(w["ln_b"][:, :], [T, GROUP, D], 1), ALU.add)\
                        .then_inc(o_order, 1)
                    pool.wait_ge(o_order, 2 * j + 2)
                    xs = x[:, bass.ts(j, GROUP), :]
                    nc.gpsimd.tensor_tensor(xs, xs, o[:, :, :], ALU.add)

                def start():
                    norm_scale(0)
                    add_h(0)
                    own(0, 0, 0)

                def body(i, p, last_group):
                    if not last_group:
                        norm_scale(i + 1)
                    own(i, 1, p)
                    if not last_group:
                        add_h(i + 1)
                    own(i, 2, p)
                    if started(i):
                        rms_scale(i - 1)
                        output_scale(i - 1)
                        add_output(i - 1)
                    own(i, 3, p)
                    if not last_group:
                        own(i + 1, 0, 1 - p)
                pipelined(pool, None, start, body)
                rms_scale(NG - 1)
                output_scale(NG - 1)
                add_output(NG - 1)


def sparse_attention(nc, name, x, const, w, loaded):
    S = 32
    ROWS = GROUP * HEADS
    LI = 16
    scale = float(HD) ** -0.5
    with ExitStack() as ctx:
        L = Layer(nc, ctx, name)
        stats = L.sbuf("stats", [T, GROUP, 6])
        moments = L.sbuf("moments", [T, GROUP, 2])
        pad = L.sbuf("pad", [T, 1])
        rstd = L.sbuf("rstd", [T, GROUP])
        h = L.sbuf("h", [T, GROUP, D])
        h_t = L.sbuf("h_t", [D, GROUP * T])
        q_t = L.sbuf("q_t", [D, GROUP * T])
        scaled_bq = L.sbuf("scaled_bq", [D, 1])
        k_t = L.sbuf("k_t", [D, S])
        k_rep = L.sbuf("k_rep", [D, 4, S])
        keys = L.sbuf("keys", [D, HEADS, S])
        vals = L.sbuf("vals", [T, D])
        vals_own = L.sbuf("vals_own", [T, 4, D])
        z = L.sbuf("z", [T, 2, ROWS, S])
        srt = [L.sbuf(f"srt{n}", [T, ROWS, S]) for n in range(2)]
        starts = L.sbuf("starts", [T, ROWS, S])
        tau = L.sbuf("tau", [T, ROWS])
        a_t = L.sbuf("a_t", [T, 4, GROUP * T])
        o_t = L.sbuf("o_t", [D, GROUP * T])
        apart = L.sbuf("apart", [D, 2, LI, T])
        out = L.sbuf("out", [T, GROUP, D])
        p_misc = L.psum("p_misc", [T, BANK])
        p_q = L.psum("p_q", [T, BANK])
        p_out = L.psum("p_out", [T, GROUP, D])
        p_s = [L.psum(f"p_s{n}", [T, BANK]) for n in range(4)]
        stats_ready = L.sem("stats_ready")
        rstd_ready = L.sem("rstd_ready")
        normed = L.sem("normed")
        trans = L.sem("trans")
        h_t_ready = L.sem("h_t_ready")
        proj = L.sem("proj")
        q_ready = L.sem("q_ready")
        scored = L.sem("scored")
        z_ready = L.sem("z_ready")
        shifted = L.sem("shifted")
        clipped = L.sem("clipped")
        turned = L.sem("turned")
        turned_out = L.sem("turned_out")
        weighed = L.sem("weighed")
        o_t_ready = L.sem("o_t_ready")
        apart_ready = L.sem("apart_ready")
        out_done = L.sem("out_done")
        dve_order = L.sem("dve_order")
        kv_done = L.sem("kv_done")
        kv_ready = L.sem("kv_ready")

        started = lambda i: not (isinstance(i, int) and i == 0)
        SORT_STEPS = 15

        def blocks(t, size):
            return t.rearrange("p r s -> p (r s)").rearrange("p (b e) -> p b e", e=size)

        with nc.Block() as block:
            @block.tensor
            def _(pe):
                pe.wait_ge(loaded, w["n"])
                nc.tensor.matmul(p_misc[:, 0:S], w["wk"][:, :], w["key_t"][:, :], start=True, stop=True)\
                    .then_inc(kv_done, 1)
                pe.wait_ge(kv_ready, 2)
                nc.tensor.matmul(p_misc[:, 0:D], k_rep[:, :, :], w["wv"][:, :], start=True, stop=True).then_inc(kv_done, 1)
                pe.wait_ge(kv_ready, 3)

                def before(j):
                    pe.wait_ge(normed, j + 1)
                    for u in range(GROUP):
                        last = nc.tensor.transpose(p_misc[:, u * T:(u + 1) * T], h[:, u, :], const["ident"][:, :])
                    last.then_inc(trans, 1)
                    pe.wait_ge(h_t_ready, j + 1)
                    nc.tensor.matmul(p_q[:, :], w["wq"][:, :], h_t[:, :], start=True, stop=True).then_inc(proj, 1)
                    pe.wait_ge(q_ready, j + 1)
                    for u in range(GROUP):
                        nc.tensor.matmul(p_s[u][:, :], q_t[:, u * T:(u + 1) * T], keys[:, :, :], start=True, stop=True)\
                            .then_inc(scored, 1)

                def behind(j, q):
                    pe.wait_ge(clipped, j + 1)
                    for b in range(4):
                        for u in range(GROUP):
                            row = u * HEADS + 4 * b
                            last = nc.tensor.transpose(p_s[b][:, u * T:(u + 1) * T], z[:, q, row:row + 4, :],
                                                       const["ident"][:, :])
                        last.then_inc(turned, 1)
                    for b in range(4):
                        pe.wait_ge(turned_out, 4 * j + b + 1)
                        last = nc.tensor.matmul(p_q[:, :], vals_own[:, b, :], a_t[:, b, :], start=(b == 0), stop=(b == 3))
                    last.then_inc(weighed, 1)
                    for u in range(GROUP):
                        pe.wait_ge(apart_ready, GROUP * j + u + 1)
                        for li in range(LI):
                            last = nc.tensor.matmul(p_out[:, u, :], apart[:, u % 2, li, :], w["wo"][:, li, :],
                                                    start=(li == 0), stop=(li == LI - 1))
                        last.then_inc(out_done, 1)

                def body(i, p, last_group):
                    if started(i):
                        pe.wait_ge(z_ready, GROUP * (i + 1))
                        behind(i - 1, 1 - p)
                    if not last_group:
                        if started(i):
                            pe.wait_ge(o_t_ready, i)
                        else:
                            pe.wait_ge(z_ready, GROUP)
                        before(i + 1)
                pipelined(pe, None, lambda: before(0), body)
                behind(NG - 1, 1)

            @block.scalar
            def _(act):
                act.wait_ge(kv_ready, 3)

                def before(j, q):
                    act.wait_ge(trans, j + 1)
                    nc.scalar.copy(h_t[:, :], p_misc[:, :]).then_inc(h_t_ready, 1)
                    act.wait_ge(proj, j + 1)
                    nc.scalar.activation(q_t[:, :], p_q[:, :], ACT.Identity, bias=scaled_bq[:, 0:1], scale=scale)\
                        .then_inc(q_ready, 1)
                    for u in range(GROUP):
                        act.wait_ge(scored, GROUP * j + u + 1)
                        nc.scalar.copy(z[:, q, u * HEADS:(u + 1) * HEADS, :], p_s[u][:, :]).then_inc(z_ready, 1)

                def behind(j, q):
                    act.wait_ge(shifted, j + 1)
                    nc.scalar.activation(z[:, q, :, :], z[:, q, :, :], ACT.Relu).then_inc(clipped, 1)
                    for b in range(4):
                        act.wait_ge(turned, 4 * j + b + 1)
                        nc.scalar.copy(a_t[:, b, :], p_s[b][:, :]).then_inc(turned_out, 1)
                    act.wait_ge(weighed, j + 1)
                    nc.scalar.copy(o_t[:, :], p_q[:, :]).then_inc(o_t_ready, 1)

                def body(i, p, last_group):
                    if started(i):
                        behind(i - 1, 1 - p)
                    if not last_group:
                        before(i + 1, 1 - p)
                pipelined(act, None, lambda: before(0, 0), body)
                behind(NG - 1, 1)

            @block.vector
            def _(dve):
                order = Order(dve, dve_order)
                dve.wait_ge(loaded, w["n"])
                nc.vector.tensor_scalar(scaled_bq[:, :], w["bq"][:, :], scale, None, ALU.mult)
                nc.vector.memset(starts[:, :, :], 1.0).then_inc(kv_ready, 1)
                dve.wait_ge(kv_ready, 1)
                nc.vector.memset(starts[:, :, 0:1], 0.0)
                dve.wait_ge(kv_done, 1)
                order.then(nc.vector.tensor_scalar(k_t[:, :], p_misc[:, 0:S], w["bk"][:, 0:1], None, ALU.add))
                nc.vector.tensor_copy(k_rep[:, :, :], bcast(k_t[:, :], [D, 4, S], 1)).then_inc(kv_ready, 1)
                nc.vector.tensor_tensor(keys[:, :, :], bcast(k_t[:, :], [D, HEADS, S], 1),
                                        bcast(const["head_of"][:, :], [D, HEADS, S], 2), ALU.mult)
                dve.wait_ge(kv_done, 2)
                order.then(nc.vector.tensor_tensor(vals[:, :], p_misc[:, 0:D], w["bv"][:, :], ALU.add))
                nc.vector.tensor_tensor(vals_own[:, :, :], bcast(vals[:, :], [T, 4, D], 1), w["own"][:, :, :], ALU.mult)\
                    .then_inc(kv_ready, 1)

                def norm(j):
                    if started(j):
                        dve.wait_ge(trans, j)
                    layernorm_stats(nc, dve, order, x, j, stats, moments, pad).then_inc(stats_ready, 1)
                    dve.wait_ge(rstd_ready, j + 1)
                    layernorm_apply(nc, x, j, moments, rstd, h).then_inc(normed, 1)

                def threshold(i, p):
                    dve.wait_ge(z_ready, GROUP * (i + 1))
                    src, dst, at = z[:, p, :, :], srt[0][:, :, :], 0
                    size = 2
                    while size <= S:
                        step = size // 2
                        while step:
                            if 2 * step == size:
                                a, b = blocks(src, size)[:, :, 0:step], blocks(src, size)[:, :, size - 1:step - 1:-1]
                                da, db = blocks(dst, size)[:, :, 0:step], blocks(dst, size)[:, :, size - 1:step - 1:-1]
                            else:
                                a, b = blocks(src, 2 * step)[:, :, 0:step], blocks(src, 2 * step)[:, :, step:2 * step]
                                da, db = blocks(dst, 2 * step)[:, :, 0:step], blocks(dst, 2 * step)[:, :, step:2 * step]
                            nc.vector.tensor_tensor(da, a, b, ALU.max)
                            order.then(nc.vector.tensor_tensor(db, a, b, ALU.min))
                            at = 1 - at
                            src, dst = dst, srt[at][:, :, :]
                            step //= 2
                        size *= 2
                    flat = lambda t: t.rearrange("p r s -> p (r s)")
                    order.then(nc.vector.tensor_tensor_scan(flat(dst), flat(starts[:, :, :]), flat(src), 0.0, ALU.mult, ALU.add))
                    order.then(nc.vector.scalar_tensor_tensor(src, dst, 1.0,
                                                              bcast(w["inv"][:, :], [T, ROWS, S], 1),
                                                              ALU.subtract, ALU.mult))
                    order.then(nc.vector.tensor_reduce(tau[:, :], src, AX.X, ALU.max))

                def add_output(j):
                    dve.wait_ge(out_done, GROUP * (j + 1))
                    order.then(nc.vector.tensor_tensor(out[:, :, :], p_out[:, :, :], bcast(w["bo"][:, :], [T, GROUP, D], 1),
                                                       ALU.add))
                    xs = x[:, bass.ts(j, GROUP), :]
                    nc.vector.tensor_tensor(xs, xs, out[:, :, :], ALU.add)

                def body(i, p, last_group):
                    if not last_group:
                        norm(i + 1)
                    threshold(i, p)
                    if started(i):
                        add_output(i - 1)
                    nc.vector.tensor_tensor(z[:, p, :, :], z[:, p, :, :], bcast(tau[:, :], [T, ROWS, S], 2), ALU.subtract)\
                        .then_inc(shifted, 1)
                pipelined(dve, order, lambda: norm(0), body, per=2 + SORT_STEPS + 3 + 1)
                add_output(NG - 1)

            @block.gpsimd
            def _(pool):
                def norm_scale(j):
                    layernorm_rstd(nc, pool, stats_ready, j, const["minus_half"], moments, rstd).then_inc(rstd_ready, 1)

                def spread(j):
                    pool.wait_ge(o_t_ready, j + 1)
                    for u in range(GROUP):
                        if u >= 2:
                            pool.wait_ge(out_done, GROUP * j + u - 1)
                        nc.gpsimd.tensor_tensor(
                            apart[:, u % 2, :, :].rearrange("p l (h o) -> p l h o", h=HEADS),
                            o_t[:, u * T:(u + 1) * T].rearrange("p (o l) -> p l o", l=LI).unsqueeze(2)
                            .broadcast_to([D, LI, HEADS, T // LI]),
                            const["head_of"][:, :].unsqueeze(1).unsqueeze(3).broadcast_to([D, LI, HEADS, T // LI]),
                            ALU.mult).then_inc(apart_ready, 1)

                def body(i, p, last_group):
                    if not last_group:
                        norm_scale(i + 1)
                    if started(i):
                        spread(i - 1)
                pipelined(pool, None, lambda: norm_scale(0), body)
                spread(NG - 1)


def quantized(nc, name, x, const, w, loaded):
    MAGIC = 12582912.0
    with ExitStack() as ctx:
        L = Layer(nc, ctx, name)
        stats = L.sbuf("stats", [T, GROUP, 6])
        moments = L.sbuf("moments", [T, GROUP, 2])
        pad = L.sbuf("pad", [T, 1])
        rstd = L.sbuf("rstd", [T, GROUP])
        h = L.sbuf("h", [T, GROUP, D])
        mag = L.sbuf("mag", [T, GROUP, D])
        q = L.sbuf("q", [T, GROUP, D])
        q_t = L.sbuf("q_t", [D, GROUP * T], BF16)
        wq = L.sbuf("wq", [D, D], BF16)
        amax = L.sbuf("amax", [T, GROUP])
        scale = L.sbuf("scale", [T, 2, GROUP])
        out = L.sbuf("out", [T, GROUP, D])
        p_t = L.psum("p_t", [T, BANK])
        p_out = L.psum("p_out", [T, GROUP, D])
        stats_ready = L.sem("stats_ready")
        rstd_ready = L.sem("rstd_ready")
        normed = L.sem("normed")
        mag_ready = L.sem("mag_ready")
        rounded = L.sem("rounded")
        trans = L.sem("trans")
        q_t_ready = L.sem("q_t_ready")
        out_done = L.sem("out_done")
        scaled = L.sem("scaled")
        scaled_columns = L.sem("scaled_columns")
        biased = L.sem("biased")
        added = L.sem("added")
        dve_order = L.sem("dve_order")
        setup = L.sem("setup")
        started = lambda i: not (isinstance(i, int) and i == 0)

        with nc.Block() as block:
            @block.tensor
            def _(pe):
                pe.wait_ge(setup, 1)

                def turn(j):
                    pe.wait_ge(rounded, j + 1)
                    for u in range(GROUP):
                        last = nc.tensor.transpose(p_t[:, u * T:(u + 1) * T], q[:, u, :], const["ident"][:, :])
                    last.then_inc(trans, 1)

                def product(i):
                    pe.wait_ge(q_t_ready, i + 1)
                    if started(i):
                        pe.wait_ge(scaled, i)
                    for u in range(GROUP):
                        last = nc.tensor.matmul(p_out[:, u, :], q_t[:, u * T:(u + 1) * T], wq[:, :], start=True, stop=True)
                    last.then_inc(out_done, 1)

                def body(i, p, last_group):
                    product(i)
                    if not last_group:
                        turn(i + 1)
                pipelined(pe, None, lambda: turn(0), body)

            @block.scalar
            def _(act):
                def start():
                    magnitude(0)
                    copy_turned(0)

                def magnitude(j):
                    act.wait_ge(normed, j + 1)
                    nc.scalar.activation(mag[:, :, :], h[:, :, :], ACT.Abs).then_inc(mag_ready, 1)

                def copy_turned(j):
                    act.wait_ge(trans, j + 1)
                    if started(j):
                        act.wait_ge(out_done, j)
                    nc.scalar.copy(q_t[:, :], p_t[:, :]).then_inc(q_t_ready, 1)

                def body(i, p, last_group):
                    if not last_group:
                        magnitude(i + 1)
                        copy_turned(i + 1)
                pipelined(act, None, start, body)

            @block.vector
            def _(dve):
                order = Order(dve, dve_order)
                dve.wait_ge(loaded, w["n"])
                nc.vector.tensor_copy(wq[:, :], w["wq"][:, :]).then_inc(setup, 1)

                def steps_before(j, s):
                    def norm_stats():
                        layernorm_stats(nc, dve, order, x, j, stats, moments, pad).then_inc(stats_ready, 1)

                    def norm_apply():
                        dve.wait_ge(rstd_ready, j + 1)
                        layernorm_apply(nc, x, j, moments, rstd, h).then_inc(normed, 1)

                    def largest():
                        dve.wait_ge(mag_ready, j + 1)
                        order.then(nc.vector.tensor_reduce(amax[:, :], mag[:, :, :], AX.X, ALU.max))
                        order.then(nc.vector.tensor_scalar(amax[:, :], amax[:, :], 1e-6, None, ALU.max))
                        order.then(nc.vector.tensor_scalar(scale[:, s, :], amax[:, :], 1.0 / 127.0, None, ALU.mult))
                        order.then(nc.vector.reciprocal(amax[:, :], scale[:, s, :]))

                    def round_h():
                        if started(j):
                            dve.wait_ge(trans, j)
                        order.then(nc.vector.tensor_tensor(q[:, :, :], h[:, :, :], bcast(amax[:, :], [T, GROUP, D], 2),
                                                           ALU.mult))
                        order.then(nc.vector.tensor_scalar(q[:, :, :], q[:, :, :], MAGIC, MAGIC, ALU.add, ALU.subtract))
                        nc.vector.tensor_scalar(q[:, :, :], q[:, :, :], 127.0, -128.0, ALU.min, ALU.max).then_inc(rounded, 1)
                    return norm_stats, norm_apply, largest, round_h

                def scale_output(i, s):
                    dve.wait_ge(out_done, i + 1)
                    if started(i):
                        dve.wait_ge(added, i)
                    nc.vector.tensor_tensor(out[:, :, :], p_out[:, :, :], bcast(scale[:, s, :], [T, GROUP, D], 2),
                                            ALU.mult).then_inc(scaled, 1)

                def scale_columns(i):
                    dve.wait_ge(scaled, i + 1)
                    nc.vector.tensor_tensor(out[:, :, :], out[:, :, :], bcast(w["scale"][:, :], [T, GROUP, D], 1),
                                            ALU.mult).then_inc(scaled_columns, 1)

                def start():
                    for step in steps_before(0, 0):
                        step()

                def body(i, p, last_group):
                    if last_group:
                        scale_output(i, p)
                        scale_columns(i)
                    else:
                        norm_stats, norm_apply, largest, round_h = steps_before(i + 1, 1 - p)
                        norm_stats()
                        scale_output(i, p)
                        norm_apply()
                        scale_columns(i)
                        largest()
                        round_h()
                pipelined(dve, order, start, body)

            @block.gpsimd
            def _(pool):
                def norm_scale(j):
                    layernorm_rstd(nc, pool, stats_ready, j, const["minus_half"], moments, rstd).then_inc(rstd_ready, 1)

                def add_output(i):
                    pool.wait_ge(scaled_columns, i + 1)
                    nc.gpsimd.tensor_tensor(out[:, :, :], out[:, :, :], bcast(w["bias"][:, :], [T, GROUP, D], 1),
                                            ALU.add).then_inc(biased, 1)
                    pool.wait_ge(biased, i + 1)
                    xs = x[:, bass.ts(i, GROUP), :]
                    nc.gpsimd.tensor_tensor(xs, xs, out[:, :, :], ALU.add).then_inc(added, 1)

                def body(i, p, last_group):
                    if not last_group:
                        norm_scale(i + 1)
                    add_output(i)
                pipelined(pool, None, lambda: norm_scale(0), body)


def layer3(nc, x, const, w, loaded, aps):
    attention16(nc, "l3", x, {**const, "causal": w["causal"]}, w, loaded, latent=True, causal=True)


def layer4(nc, x, const, w, loaded, aps):
    attention16(nc, "l4", x, const, w, loaded, ctx_t=aps["ctx_t"], key_mask=True, qkv_bias=True, out_bias=True)


def layer7(nc, x, const, w, loaded, aps):
    with ExitStack() as ctx:
        rel = ctx.enter_context(nc.sbuf_tensor("l7_rel", [T, HEADS, T], F32))
        table = aps["rel_table"]
        rel_in = ctx.enter_context(nc.semaphore("rel_in"))
        with nc.Block() as block:
            @block.sync
            def _(sp):
                for head in range(HEADS):
                    src = bass.AP(table.tensor, head * 511 + 128, [[1, T], [1, T]])
                    sp.dma_start(rel[:, head, :], src).then_inc(rel_in, 16)
                sp.wait_ge(rel_in, 16 * HEADS)
        attention16(nc, "l7", x, {**const, "flip": w["flip"]}, {**w, "rel": rel}, loaded, ctx_t=aps["ctx_t"],
                    rel_bias=True, out_bias=True)


def layer2(nc, x, const, w, loaded, aps):
    experts(nc, "l2", x, const, w, loaded, "groups")


def layer5(nc, x, const, w, loaded, aps):
    experts(nc, "l5", x, const, w, loaded, "top2")


def layer8(nc, x, const, w, loaded, aps):
    experts(nc, "l8", x, const, w, loaded, "top1")


def layer1(nc, x, const, w, loaded, aps):
    attention8(nc, "l1", x, const, w, loaded, aps["ctx_t"])


def layer6(nc, x, const, w, loaded, aps):
    attention1(nc, "l6", x, const, w, loaded, aps, cross=False)


def layer10(nc, x, const, w, loaded, aps):
    attention1(nc, "l10", x, const, w, loaded, aps, cross=True)


def layer11(nc, x, const, w, loaded, aps):
    quantized(nc, "l11", x, const, w, loaded)


def layer0(nc, x, const, w, loaded, aps):
    state_space(nc, "l0", x, const, w, loaded)


def layer9(nc, x, const, w, loaded, aps):
    sparse_attention(nc, "l9", x, const, w, loaded)


LAYERS = {0: layer0, 9: layer9, 1: layer1, 6: layer6, 10: layer10, 11: layer11, 2: layer2, 3: layer3, 4: layer4, 5: layer5, 7: layer7, 8: layer8}


TABLE = [
    (-1, "ident", "ident", 0, False),
    (-1, "head_of", "head_of", 0, False),
    (-1, "minus_half", "minus_half", 0, False),
    (-1, "falling4", "falling4", T, True),
    (-1, "falling8", "falling8", T, True),
    (-1, "falling16", "falling16", T, True),
    (0, "conv_in", "mam_conv_in", 0, False),
    (0, "z_in", "mam_z_in", 0, False),
    (0, "dt_in", "mam_dt_in", 0, False),
    (0, "conv_w", "mam_conv_w", 0, False),
    (0, "conv_b", "mam_conv_b", 0, False),
    (0, "dt_bias", "mam_dt_bias", T, True),
    (0, "a_log", "mam_a_log", T, True),
    (0, "d_skip", "mam_d_skip", 0, False),
    (0, "norm_w", "mam_norm_w", 0, False),
    (0, "out_w", "mam_out_w", 0, False),
    (0, "ln_w", "mam_ln_w", T, True),
    (0, "ln_b", "mam_ln_b", T, True),
    (0, "upto", "mam_upto", 0, False),
    (0, "head_row", "mam_head_row", 0, False),
    (9, "key_t", "l3a_key", 0, False),
    (9, "wq", "L3_attn_Wq", 0, False),
    (9, "wk", "L3_attn_Wk", 0, False),
    (9, "wv", "L3_attn_Wv", 0, False),
    (9, "wo", "l3a_wo", 0, False),
    (9, "bq", "l3a_bq", 0, False),
    (9, "bk", "l3a_bk", 0, False),
    (9, "bv", "l3a_bv", T, True),
    (9, "bo", "l3a_bo", T, True),
    (9, "own", "l3a_own", 0, False),
    (9, "inv", "l3a_inv", T, True),
    (1, "wq", "L0_xattn_Wq1", 0, False),
    (1, "wk1", "L0_xattn_Wk1", 0, False),
    (1, "wk2", "L0_xattn_Wk2", 0, False),
    (1, "wv1", "L0_xattn_Wv1", 0, False),
    (1, "wv2", "L0_xattn_Wv2", 0, False),
    (1, "wo", "l0x_wo", 0, False),
    (1, "bo", "l0x_bo", T, True),
    (2, "router", "l0f_router", 0, False),
    (2, "gate_bias", "l0f_bias", T, True),
    (2, "pick", "l0f_pick", 0, False),
    (2, "wg", "l0f_wg", 0, False),
    (2, "wu", "l0f_wu", 0, False),
    (2, "wd", "l0f_wd", 0, False),
    (5, "rw1", "L1_ffn_rw1", 0, False),
    (5, "rb1", "l1f_rb1", 0, False),
    (5, "router", "L1_ffn_rw2", 0, False),
    (5, "rb2", "l1f_rb2", T, True),
    (5, "pick", "pick8", 0, False),
    (5, "wg", "l1f_w1", 0, False),
    (5, "eb1", "l1f_eb1", 0, False),
    (5, "wd", "l1f_w2", 0, False),
    (5, "eb2", "L1_ffn_eb2", 0, False),
    (6, "wq", "l2a_wq", 0, False),
    (6, "wk", "l2a_wk", 0, False),
    (6, "wv", "l2a_wv", 0, False),
    (6, "bq", "l2a_bq", 0, False),
    (6, "bk", "l2a_bk", 0, False),
    (6, "bv", "l2a_bv", T, True),
    (10, "wo", "l3x_wo", 0, False),
    (10, "bo", "l3x_bo", T, True),
    (11, "wq", "l3f_wq", 0, False),
    (11, "scale", "l3f_scale", T, True),
    (11, "bias", "l3f_bias", T, True),
    (8, "router", "L2_ffn_Wr", 0, False),
    (8, "pick", "pick7", 0, False),
    (8, "wg", "l2f_wg", 0, False),
    (8, "wu", "l2f_wu", 0, False),
    (8, "wd", "l2f_wd", 0, False),
    (3, "causal", "causal", 0, False),
    (3, "down", "L1_attn_Wc_down", 0, False),
    (3, "wq", "L1_attn_Wq_up", 0, False),
    (3, "wk", "l1_wk", 0, False),
    (3, "wv", "l1_wv", 0, False),
    (3, "wo", "L1_attn_Wc_proj", 0, False),
    (4, "wq", "l1x_wq", 0, False),
    (4, "wk", "l1x_wk", 0, False),
    (4, "wv", "l1x_wv", 0, False),
    (4, "wo", "l1x_wo", 0, False),
    (4, "bq", "l1x_bq", 0, False),
    (4, "bk", "l1x_bk", 0, False),
    (4, "bv", "l1x_bv", T, True),
    (4, "bo", "l1x_bo", T, True),
    (4, "mask", "mask", 0, False),
    (7, "wq", "l2x_wq", 0, False),
    (7, "wk", "l2x_wk", 0, False),
    (7, "wv", "l2x_wv", 0, False),
    (7, "wo", "l2x_wo", 0, False),
    (7, "bo", "l2x_bo", T, True),
    (7, "flip", "flip", 0, False),
]


def lay_out(a):
    c = np.ascontiguousarray
    a = {k: np.asarray(v) for k, v in a.items()}
    o = {"x": c(a["x"].transpose(1, 0, 2)), "ctx_t": c(a["ctx_1024"].transpose(2, 0, 1).reshape(D, NB * T))}
    o["ident"] = np.eye(T, dtype=np.float32)
    o["minus_half"] = np.full((T, 8), -0.5, np.float32)
    o["flip"] = c(np.eye(T, dtype=np.float32)[::-1])
    o["causal"] = np.where(np.tril(np.ones((T, T), bool)), 0.0, -1e30).astype(np.float32)
    o["head_of"] = c(np.repeat(np.eye(HEADS, dtype=np.float32), HD, axis=0))
    for n in ("L1_attn_Wc_down", "L1_attn_Wq_up", "L1_attn_Wc_proj"):
        o[n] = a[n]
    o["l1_wk"] = np.tile(a["L1_attn_Wkv_up"][:, :HD], (1, HEADS))
    o["l1_wv"] = np.tile(a["L1_attn_Wkv_up"][:, HD:], (1, HEADS))
    for n in "qkvo":
        o[f"l1x_w{n}"] = c(a[f"L1_xattn_W{n}"].T)
    o["l1x_bq"], o["l1x_bk"] = a["L1_xattn_bq"].reshape(D, 1), a["L1_xattn_bk"].reshape(D, 1)
    o["l1x_bv"], o["l1x_bo"] = a["L1_xattn_bv"].reshape(1, D), a["L1_xattn_bo"].reshape(1, D)
    o["mask"] = a["mask_BxS2_ik0"].reshape(1, NB * T)
    for n in "qkv":
        o[f"l2x_w{n}"] = c(a[f"L2_xattn_w{n}"].T)
    o["l2x_wo"], o["l2x_bo"] = c(a["L2_xattn_fc_w"].T), a["L2_xattn_fc_b"].reshape(1, D)
    o["rel_table"] = c(a["L2_xattn_rel_table"].T)
    for n in (4, 8, 16):
        o[f"falling{n}"] = np.arange(n, 0, -1, dtype=np.float32).reshape(1, n)
    rows = lambda e: np.tile(np.pad(e, ((0, 32 - e.shape[0]), (0, 0), (0, 0))), (3, 1, 1))
    o["pick8"] = rows(np.repeat(np.eye(8, dtype=np.float32)[:, :, None], T, axis=2))
    o["pick7"] = c(o["pick8"][:, :7])
    o["l0f_pick"] = rows(np.repeat(np.eye(16, dtype=np.float32), 64, axis=1).reshape(16, 8, T))
    o["l0f_router"] = c(a["L0_ffn_gate_w"].T)
    o["l0f_bias"] = a["L0_ffn_gate_bias"].reshape(1, 16)
    for n, s in (("g", "Ws_g"), ("u", "Ws_u")):
        both = np.concatenate([a[f"L0_ffn_W{n}"].reshape(8, T, D), a[f"L0_ffn_{s}"][None]])
        o[f"l0f_w{n}"] = c(both.transpose(2, 0, 1))
    both = np.concatenate([a["L0_ffn_Wd"].transpose(0, 2, 1).reshape(8, T, D), a["L0_ffn_Ws_d"].T[None]])
    o["l0f_wd"] = c(both.transpose(1, 0, 2))
    for n in ("L1_ffn_rw1", "L1_ffn_rw2", "L1_ffn_eb2", "L2_ffn_Wr"):
        o[n] = a[n]
    o["l1f_rb1"], o["l1f_rb2"] = a["L1_ffn_rb1"].reshape(D, 1), a["L1_ffn_rb2"].reshape(1, 8)
    o["l1f_w1"] = c(a["L1_ffn_ew1"].transpose(1, 0, 2).reshape(D, 16, T))
    o["l1f_eb1"] = c(a["L1_ffn_eb1"].reshape(16, T).T)
    o["l1f_w2"] = c(a["L1_ffn_ew2"].reshape(16, T, D).transpose(1, 0, 2))
    for n in "gu":
        both = np.concatenate([a[f"L2_ffn_W{n}"], a[f"L2_ffn_W{n}_s"][None]])
        o[f"l2f_w{n}"] = c(both.transpose(1, 0, 2).reshape(D, 32, T))
    both = np.concatenate([a["L2_ffn_Wd"], a["L2_ffn_Wd_s"][None]])
    o["l2f_wd"] = c(both.reshape(32, T, D).transpose(1, 0, 2))
    for n in ("Wq1", "Wk1", "Wk2", "Wv1", "Wv2"):
        o[f"L0_xattn_{n}"] = a[f"L0_xattn_{n}"]
    o["l0x_wo"], o["l0x_bo"] = c(a["L0_xattn_Wo"].reshape(4, T, D).transpose(1, 0, 2)), a["L0_xattn_bo"].reshape(1, D)
    for n in "qkv":
        o[f"l2a_w{n}"] = c(a[f"L2_attn_w{n}"].T)
    o["l2a_bq"], o["l2a_bk"] = a["L2_attn_bq"].reshape(D, 1), a["L2_attn_bk"].reshape(D, 1)
    o["l2a_bv"] = a["L2_attn_bv"].reshape(1, D)
    o["l3x_wo"], o["l3x_bo"] = c(a["L3_xattn_Wout"].T), a["L3_xattn_bout"].reshape(1, D)
    o["ctx"] = c(a["ctx_1024"].transpose(1, 0, 2))
    o["drop"] = c(a["mask_BxSxS2_fk0"].transpose(1, 0, 2))
    o["l3f_wq"] = c(a["L3_ffn_weight_q"].T.astype(np.int32))
    o["l3f_scale"], o["l3f_bias"] = a["L3_ffn_weight_scale"].reshape(1, D), a["L3_ffn_bias"].reshape(1, D)
    w_in = a["L0_attn_in_proj_w"].T
    o["mam_z_in"], o["mam_conv_in"], o["mam_dt_in"] = c(w_in[:, :256]), c(w_in[:, 256:768]), c(w_in[:, 768:])
    o["mam_conv_w"] = c(a["L0_attn_conv_w"].reshape(4, T, 4).transpose(1, 0, 2))
    o["mam_conv_b"] = c(a["L0_attn_conv_b"].reshape(4, T).T)
    o["mam_dt_bias"], o["mam_a_log"] = a["L0_attn_dt_bias"].reshape(1, 32), a["L0_attn_A_log"].reshape(1, 32)
    o["mam_d_skip"] = c(np.repeat(a["L0_attn_D_skip"], 8).reshape(2, T).T)
    o["mam_norm_w"] = c(a["L0_attn_norm_w"].reshape(2, T).T)
    o["mam_out_w"] = c(a["L0_attn_out_proj_w"].T.reshape(2, T, D).transpose(1, 0, 2))
    o["mam_ln_w"], o["mam_ln_b"] = a["L0_attn_ln_w"].reshape(1, D), a["L0_attn_ln_b"].reshape(1, D)
    o["mam_upto"] = np.triu(np.ones((T, T), np.float32))
    o["mam_head_row"] = np.tile(np.eye(32, dtype=np.float32), (3, 1))
    o["l3a_key"] = c(a["L3_attn_key_param"][0].T)
    for n in "qkv":
        o[f"L3_attn_W{n}"] = a[f"L3_attn_W{n}"]
    o["l3a_wo"] = c(np.tile(a["L3_attn_Wo"].reshape(16, HD, D).transpose(1, 0, 2), (HEADS, 1, 1)))
    o["l3a_bq"], o["l3a_bk"] = a["L3_attn_bq"].reshape(D, 1), a["L3_attn_bk"].reshape(D, 1)
    o["l3a_bv"], o["l3a_bo"] = a["L3_attn_bv"].reshape(1, D), a["L3_attn_bo"].reshape(1, D)
    head = np.arange(T)[:, None, None] // 32 + 4 * np.arange(4)[None, :, None]
    o["l3a_own"] = (head == np.arange(D)[None, None, :] // HD).astype(np.float32)
    o["l3a_inv"] = (1.0 / np.arange(1, 33)).astype(np.float32).reshape(1, 32)
    return o


def load(nc, aps, table, ctx, layers, x=None):
    tiles, loaded, counts = {}, {}, {}
    jobs = []
    for layer, key, name, parts, wide in table:
        if layer not in layers:
            continue
        ap = aps[name]
        dt = ap.dtype
        shape = [parts if wide else ap.shape[0]] + list(ap.shape[1:])
        t = ctx.enter_context(nc.sbuf_tensor(f"w{layer}_{key}", shape, dt))
        tiles.setdefault(layer, {})[key] = t
        counts[layer] = counts.get(layer, 0) + 16
        jobs.append((layer, t, ap, wide))
    for layer in counts:
        loaded[layer] = ctx.enter_context(nc.semaphore(f"loaded{layer}"))
        tiles[layer]["n"] = counts[layer]
    with nc.Block() as block:
        @block.sync
        def _(sp):
            if x is not None:
                sp.dma_start(x[:, :, :], aps["x"]).then_inc(loaded[-1], 16)
            for layer, t, ap, wide in jobs:
                src = ap
                if wide:
                    src = ap.partition_broadcast(T)
                    src = src.rearrange("p o d -> p (o d)") if len(src.shape) == 3 else src
                sp.dma_start(t[tuple(slice(None) for _ in t.shape)], src).then_inc(loaded[layer], 16)
            if x is not None:
                sp.wait_ge(loaded[-1], counts[-1] + 16)
    return tiles, loaded


ACTS = ((0, 1, 2), (3, 4, 5), (6, 7, 8), (9, 10, 11))


def build(nc, aps, phases=tuple(range(12))):
    with ExitStack() as ctx:
        x = ctx.enter_context(nc.sbuf_tensor("x_res", [T, NB, D], F32))
        tiles, _ = load(nc, aps, TABLE, ctx, (-1,), x)
        const = tiles[-1]
        for act in ACTS:
            act = [p for p in act if p in phases]
            if act:
                with ExitStack() as act_ctx:
                    tiles, loaded = load(nc, aps, TABLE, act_ctx, act)
                    for p in act:
                        LAYERS[p](nc, x, const, tiles[p], loaded[p], aps)
        done = ctx.enter_context(nc.semaphore("done"))
        with nc.Block() as block:
            @block.sync
            def _(sp):
                sp.dma_start(aps["out"], x[:, :, :]).then_inc(done, 16)
                sp.wait_ge(done, 16)


def kernel(**inputs):
    import concourse.bacc as bacc
    from concourse.bass_utils import run_bass_kernel_spmd

    arrays = lay_out(inputs)
    used = {row[2] for row in TABLE} | {"x", "ctx_t", "ctx", "drop", "rel_table"}
    nc = bacc.Bacc("TRN2", target_bir_lowering=False, num_devices=1)
    ins, aps = {}, {}
    for name in sorted(used):
        array = np.ascontiguousarray(arrays[name])
        ins[f"in_{name}"] = array
        aps[name] = nc.dram_tensor(f"in_{name}", array.shape, mybir.dt.from_np(array.dtype), kind="ExternalInput").ap()
    aps["out"] = nc.dram_tensor("out", (T, NB, D), F32, kind="ExternalOutput").ap()
    build(nc, aps)
    result = run_bass_kernel_spmd(nc, [ins], core_ids=[0])
    return np.ascontiguousarray(result.results[0]["out"].transpose(1, 0, 2))
```
